# Optimizing a Trainium2 kernel written in Bass

```python
import numpy as np
import jax
import jax.numpy as jnp

def _softmax(x, axis=-1):
    return jax.nn.softmax(x, axis=axis)

def _gelu(x):
    return jax.nn.gelu(x, approximate=True)

def _silu(x):
    return jax.nn.silu(x)

def _sigmoid(x):
    return jax.nn.sigmoid(x)

def _layernorm(x, axis=-1, eps=1e-05):
    m = jnp.mean(x, axis=axis, keepdims=True)
    v = jnp.var(x, axis=axis, keepdims=True)
    return (x - m) / jnp.sqrt(v + eps)

def _scatter_add(tgt, idx, src, axis=0):
    return tgt.at[idx].add(src)

def _segment_sum(src, seg, n):
    return jax.ops.segment_sum(src, seg, n)
kernel_name = 'mk_xattn_ffn_d4_seqx_r8_934bdd'

def setup_inputs(seed: int=0):
    np.random.seed(seed)
    _w = jnp.asarray

    def _rec_inputs():
        import jax
        import jax.numpy as jnp
        _rk = jax.random.key(seed)
        x = -0.000125 + 0.9999 * jax.random.normal(jax.random.fold_in(_rk, 1), (8, 128, 512), jnp.float32)
        _lenS = 128 - jax.random.randint(jax.random.fold_in(_rk, 7), (8,), 0, max(1, 128 // 4) + 1, jnp.int32)
        _lenS2 = 128 - jax.random.randint(jax.random.fold_in(_rk, 8), (8,), 0, max(1, 128 // 4) + 1, jnp.int32)
        _ctx_4096P = jax.random.normal(jax.random.fold_in(_rk, 11), (8, 16, 512), jnp.float32)
        _ctx_4096c = jax.random.dirichlet(jax.random.fold_in(_rk, 511), 0.3 * jnp.ones((16,), jnp.float32), (8, 128))
        _ctx_4096t = jnp.einsum('bsk,bkd->bsd', _ctx_4096c, _ctx_4096P)
        _ctx_4096t = _ctx_4096t * jax.lax.rsqrt(jnp.mean(jnp.square(_ctx_4096t)) + 1e-12) * 0.953939
        ctx_4096 = -1.52775e-05 + 0.999936 * (_ctx_4096t + 0.3 * jax.random.normal(jax.random.fold_in(_rk, 611), (8, 128, 512), jnp.float32))
        _validS = jnp.arange(128)[None, :] < _lenS[:, None]
        _validS2 = jnp.arange(128)[None, :] < _lenS2[:, None]
        _causal = jnp.tril(jnp.ones((128, 128), dtype=bool))
        mask_Bx1x4096_ff1 = jnp.where(jnp.ones((8, 1, 512), dtype=bool), 1.0, 0.0).astype(jnp.float32)
        return (x, ctx_4096, mask_Bx1x4096_ff1)
    x, ctx_4096, mask_Bx1x4096_ff1 = _rec_inputs()

    def _L0_xattn_setup():
        import jax, jax.numpy as jnp
        import numpy as np
        W = 128
        H = 8
        D = 128
        DK = D // 2

        def _to_patches(x):
            b, d, s = x.shape
            np_ = s // W
            return x.reshape(b, d, np_, W).transpose(0, 2, 1, 3).reshape(b * np_, d, W)
        key = jax.random.key(seed)
        ks = jax.random.split(key, 10)
        B, S = (8, 512)
        qk = jax.random.normal(ks[0], (B, D, S), dtype=jnp.float32)
        v = jax.random.normal(ks[1], (B, D, S), dtype=jnp.float32)
        masks = jnp.ones((B, 1, S), dtype=jnp.float32)
        sc = 1.0 / np.sqrt(D)
        Wq = jax.random.normal(ks[2], (DK, D), dtype=jnp.float32) * sc
        bq = jnp.zeros((DK,), dtype=jnp.float32)
        Wk = jax.random.normal(ks[3], (DK, D), dtype=jnp.float32) * sc
        bk = jnp.zeros((DK,), dtype=jnp.float32)
        Wv = jax.random.normal(ks[4], (DK, D), dtype=jnp.float32) * sc
        bv = jnp.zeros((DK,), dtype=jnp.float32)
        Wo = jax.random.normal(ks[5], (D, DK), dtype=jnp.float32) * (1.0 / np.sqrt(DK))
        bo = jnp.zeros((D,), dtype=jnp.float32)
        return dict(qk=qk, v=v, masks=masks, Wq=Wq, bq=bq, Wk=Wk, bk=bk, Wv=Wv, bv=bv, Wo=Wo, bo=bo)
    _L0_xattn_all = _L0_xattn_setup()
    _L0_xattn_in = {k: v for k, v in _L0_xattn_all.items() if k in ('Wq', 'bq', 'Wk', 'bk', 'Wv', 'bv', 'Wo', 'bo')}
    del _L0_xattn_all

    def _L0_ffn_setup():
        import jax, jax.numpy as jnp
        import numpy as np
        H = 512
        I = 256
        E = 16
        TOPK = 4
        SI = 256
        key = jax.random.key(seed)
        ks = jax.random.split(key, 9)
        s = 0.02
        return {'hidden_states': jax.random.normal(ks[0], (2, 256, H), dtype=jnp.float32), 'gate_w': jax.random.normal(ks[1], (E, H), dtype=jnp.float32) * s, 'bias': jnp.zeros((E,), dtype=jnp.float32), 'Wg': jax.random.normal(ks[2], (E, I, H), dtype=jnp.float32) * s, 'Wu': jax.random.normal(ks[3], (E, I, H), dtype=jnp.float32) * s, 'Wd': jax.random.normal(ks[4], (E, H, I), dtype=jnp.float32) * s, 'Sg': jax.random.normal(ks[5], (SI, H), dtype=jnp.float32) * s, 'Su': jax.random.normal(ks[6], (SI, H), dtype=jnp.float32) * s, 'Sd': jax.random.normal(ks[7], (H, SI), dtype=jnp.float32) * s}
    _L0_ffn_all = _L0_ffn_setup()
    _L0_ffn_in = {k: v for k, v in _L0_ffn_all.items() if k in ('gate_w', 'bias', 'Wg', 'Wu', 'Wd', 'Sg', 'Su', 'Sd')}
    del _L0_ffn_all

    def _L1_xattn_setup():
        import jax, jax.numpy as jnp
        import numpy as np
        TEXT_DIM = 512
        FEATURE_DIM = 512

        def _xavier_uniform(key, shape):
            fan_in, fan_out = (shape[1], shape[0])
            limit = float(np.sqrt(6.0 / (fan_in + fan_out)))
            return jax.random.uniform(key, shape, jnp.float32, -limit, limit)
        key = jax.random.key(seed)
        k1, k2, k3, k4 = jax.random.split(key, 4)
        text = jax.random.normal(k1, (8, 256, TEXT_DIM), jnp.float32)
        features = jax.random.normal(k2, (8, 72, FEATURE_DIM), jnp.float32)
        Wq = _xavier_uniform(k3, (FEATURE_DIM, TEXT_DIM))
        bq = jnp.zeros((FEATURE_DIM,), jnp.float32)
        Wk = _xavier_uniform(k4, (FEATURE_DIM, FEATURE_DIM))
        bk = jnp.zeros((FEATURE_DIM,), jnp.float32)
        return {'text': text, 'features': features, 'Wq': Wq, 'bq': bq, 'Wk': Wk, 'bk': bk}
    _L1_xattn_all = _L1_xattn_setup()
    _L1_xattn_in = {k: v for k, v in _L1_xattn_all.items() if k in ('Wq', 'bq', 'Wk', 'bk')}
    del _L1_xattn_all

    def _L1_ffn_setup():
        import jax, jax.numpy as jnp
        import numpy as np
        QW = 127.0
        QA = 255.0
        key = jax.random.key(seed)
        k1, k2, k3, k4, k5 = jax.random.split(key, 5)
        B, S, D_IN, D_OUT = (4, 256, 512, 512)
        x = jax.random.normal(k1, (B, S, D_IN), dtype=jnp.float32)
        W = jax.random.normal(k2, (D_OUT, D_IN), dtype=jnp.float32) * 0.02
        bias = jax.random.normal(k3, (D_OUT,), dtype=jnp.float32) * 0.1
        calib_min = -(jax.random.uniform(k4, (D_IN,), dtype=jnp.float32) * 3.0 + 0.1)
        calib_max = jax.random.uniform(k5, (D_IN,), dtype=jnp.float32) * 3.0 + 0.1
        return {'x': x, 'W': W, 'bias': bias, 'calib_min': calib_min, 'calib_max': calib_max}
    _L1_ffn_all = _L1_ffn_setup()
    _L1_ffn_in = {k: v for k, v in _L1_ffn_all.items() if k in ('W', 'bias', 'calib_min', 'calib_max')}
    del _L1_ffn_all

    def _L2_xattn_setup():
        import jax, jax.numpy as jnp
        import numpy as np
        DIM = 512
        NUM_HEADS = 32
        NUM_KV_HEADS = 8
        HEAD_DIM = DIM // NUM_HEADS
        KV_DIM = DIM // (NUM_HEADS // NUM_KV_HEADS)
        B, S = (1, 256)
        key = jax.random.key(seed)
        ks = jax.random.split(key, 7)
        w_scale = DIM ** (-0.5)
        return {'query': jax.random.normal(ks[0], (B, S, DIM), jnp.float32), 'key': jax.random.normal(ks[1], (B, S, DIM), jnp.float32), 'value': jax.random.normal(ks[2], (B, S, DIM), jnp.float32), 'Wq': jax.random.normal(ks[3], (DIM, DIM), jnp.float32) * w_scale, 'Wk': jax.random.normal(ks[4], (DIM, KV_DIM), jnp.float32) * w_scale, 'Wv': jax.random.normal(ks[5], (DIM, KV_DIM), jnp.float32) * w_scale, 'Wo': jax.random.normal(ks[6], (DIM, DIM), jnp.float32) * w_scale}
    _L2_xattn_all = _L2_xattn_setup()
    _L2_xattn_in = {k: v for k, v in _L2_xattn_all.items() if k in ('Wq', 'Wk', 'Wv', 'Wo')}
    del _L2_xattn_all

    def _L2_ffn_setup():
        import jax, jax.numpy as jnp
        import numpy as np
        ALPHA = 32
        R = 16
        SCALING = ALPHA / R
        key = jax.random.key(seed)
        k1, k2, k3, k4 = jax.random.split(key, 4)
        B_, S, D = (4, 256, 512)
        H, r, O = (8, R, 512)
        x = jax.random.normal(k1, (B_, S, D), dtype=jnp.float32)
        A = jax.random.normal(k2, (H, r, D), dtype=jnp.float32) * 0.02
        Bm = jax.random.normal(k3, (H, O, r), dtype=jnp.float32) * 0.02
        Wr = jax.random.normal(k4, (H, D), dtype=jnp.float32) * 0.02
        br = jnp.zeros((H,), dtype=jnp.float32)
        return {'x': x, 'A': A, 'B': Bm, 'Wr': Wr, 'br': br}
    _L2_ffn_all = _L2_ffn_setup()
    _L2_ffn_in = {k: v for k, v in _L2_ffn_all.items() if k in ('A', 'B', 'Wr', 'br')}
    del _L2_ffn_all

    def _L3_xattn_setup():
        import jax, jax.numpy as jnp
        import numpy as np
        B, C, N = (8, 64, 512)
        key = jax.random.key(seed)
        k1, k2, k3 = jax.random.split(key, 3)
        k = jax.random.normal(k1, (B, C, N), dtype=jnp.float32)
        q = jax.random.normal(k2, (B, C, N), dtype=jnp.float32)
        v = jax.random.normal(k3, (B, C, N), dtype=jnpp.float32) if False else jax.random.normal(k3, (B, C, N), dtype=jnp.float32)
        return {'k': k, 'q': q, 'v': v}
    _L3_xattn_all = _L3_xattn_setup()
    _L3_xattn_in = {k: v for k, v in _L3_xattn_all.items() if k in ()}
    del _L3_xattn_all

    def _L3_ffn_setup():
        import jax, jax.numpy as jnp
        import numpy as np
        HID, INT, LAT, NE, K = (512, 1024, 256, 8, 2)
        LN_EPS = 1e-05

        def _layernorm(x, gamma, beta):
            mu = jnp.mean(x, axis=-1, keepdims=True)
            var = jnp.var(x, axis=-1, keepdims=True)
            return (x - mu) * jax.lax.rsqrt(var + LN_EPS) * gamma + beta
        key = jax.random.key(seed)
        ks = jax.random.split(key, 8)
        s = lambda d: 1.0 / np.sqrt(d)
        return {'hidden_states': jax.random.normal(ks[0], (4, 256, HID), jnp.float32), 'gate_w': jax.random.normal(ks[1], (HID, NE), jnp.float32) * s(HID), 'up_w': jax.random.normal(ks[2], (HID, INT), jnp.float32) * s(HID), 'down_w': jax.random.normal(ks[3], (INT, HID), jnp.float32) * s(INT), 'fc1_w': jax.random.normal(ks[4], (HID, LAT), jnp.float32) * s(HID), 'fc2_w': jax.random.normal(ks[5], (LAT, HID), jnp.float32) * s(LAT), 'expert_w': jax.random.normal(ks[6], (LAT, LAT), jnp.float32), 'ln_gamma': jnp.ones((HID,), jnp.float32), 'ln_beta': jnp.zeros((HID,), jnp.float32)}
    _L3_ffn_all = _L3_ffn_setup()
    _L3_ffn_in = {k: v for k, v in _L3_ffn_all.items() if k in ('gate_w', 'up_w', 'down_w', 'fc1_w', 'fc2_w', 'expert_w', 'ln_gamma', 'ln_beta')}
    del _L3_ffn_all
    return {'x': x, 'ctx_4096': ctx_4096, 'mask_Bx1x4096_ff1': mask_Bx1x4096_ff1, 'L0_xattn_Wq': _L0_xattn_in['Wq'], 'L0_xattn_bq': _L0_xattn_in['bq'], 'L0_xattn_Wk': _L0_xattn_in['Wk'], 'L0_xattn_bk': _L0_xattn_in['bk'], 'L0_xattn_Wv': _L0_xattn_in['Wv'], 'L0_xattn_bv': _L0_xattn_in['bv'], 'L0_xattn_Wo': _L0_xattn_in['Wo'], 'L0_xattn_bo': _L0_xattn_in['bo'], 'L0_ffn_gate_w': _L0_ffn_in['gate_w'], 'L0_ffn_bias': _L0_ffn_in['bias'], 'L0_ffn_Wg': _L0_ffn_in['Wg'], 'L0_ffn_Wu': _L0_ffn_in['Wu'], 'L0_ffn_Wd': _L0_ffn_in['Wd'], 'L0_ffn_Sg': _L0_ffn_in['Sg'], 'L0_ffn_Su': _L0_ffn_in['Su'], 'L0_ffn_Sd': _L0_ffn_in['Sd'], 'L1_xattn_Wq': _L1_xattn_in['Wq'], 'L1_xattn_bq': _L1_xattn_in['bq'], 'L1_xattn_Wk': _L1_xattn_in['Wk'], 'L1_xattn_bk': _L1_xattn_in['bk'], 'L1_ffn_W': _L1_ffn_in['W'], 'L1_ffn_bias': _L1_ffn_in['bias'], 'L1_ffn_calib_min': _L1_ffn_in['calib_min'], 'L1_ffn_calib_max': _L1_ffn_in['calib_max'], 'L2_xattn_Wq': _L2_xattn_in['Wq'], 'L2_xattn_Wk': _L2_xattn_in['Wk'], 'L2_xattn_Wv': _L2_xattn_in['Wv'], 'L2_xattn_Wo': _L2_xattn_in['Wo'], 'L2_ffn_A': _L2_ffn_in['A'], 'L2_ffn_B': _L2_ffn_in['B'], 'L2_ffn_Wr': _L2_ffn_in['Wr'], 'L2_ffn_br': _L2_ffn_in['br'], 'L3_ffn_gate_w': _L3_ffn_in['gate_w'], 'L3_ffn_up_w': _L3_ffn_in['up_w'], 'L3_ffn_down_w': _L3_ffn_in['down_w'], 'L3_ffn_fc1_w': _L3_ffn_in['fc1_w'], 'L3_ffn_fc2_w': _L3_ffn_in['fc2_w'], 'L3_ffn_expert_w': _L3_ffn_in['expert_w'], 'L3_ffn_ln_gamma': _L3_ffn_in['ln_gamma'], 'L3_ffn_ln_beta': _L3_ffn_in['ln_beta']}

def reference(x, ctx_4096, mask_Bx1x4096_ff1, L0_xattn_Wq, L0_xattn_bq, L0_xattn_Wk, L0_xattn_bk, L0_xattn_Wv, L0_xattn_bv, L0_xattn_Wo, L0_xattn_bo, L0_ffn_gate_w, L0_ffn_bias, L0_ffn_Wg, L0_ffn_Wu, L0_ffn_Wd, L0_ffn_Sg, L0_ffn_Su, L0_ffn_Sd, L1_xattn_Wq, L1_xattn_bq, L1_xattn_Wk, L1_xattn_bk, L1_ffn_W, L1_ffn_bias, L1_ffn_calib_min, L1_ffn_calib_max, L2_xattn_Wq, L2_xattn_Wk, L2_xattn_Wv, L2_xattn_Wo, L2_ffn_A, L2_ffn_B, L2_ffn_Wr, L2_ffn_br, L3_ffn_gate_w, L3_ffn_up_w, L3_ffn_down_w, L3_ffn_fc1_w, L3_ffn_fc2_w, L3_ffn_expert_w, L3_ffn_ln_gamma, L3_ffn_ln_beta):
    import jax
    import jax.numpy as jnp

    def _L0_xattn_ref(qk, v, masks, Wq, bq, Wk, bk, Wv, bv, Wo, bo):
        import jax, jax.numpy as jnp
        import numpy as np
        W = 128
        H = 8
        D = 128
        DK = D // 2

        def _to_patches(x):
            b, d, s = x.shape
            np_ = s // W
            return x.reshape(b, d, np_, W).transpose(0, 2, 1, 3).reshape(b * np_, d, W)
        B, _, S = qk.shape
        np_ = S // W
        qp = _to_patches(qk)
        vp = _to_patches(v)
        mp = _to_patches(masks)
        q = jnp.einsum('ed,bdw->bew', Wq, qp) + bq[:, None]
        k = jnp.einsum('ed,bdw->bew', Wk, qp) + bk[:, None]
        val = jnp.einsum('ed,bdw->bew', Wv, vp) + bv[:, None]
        BN = q.shape[0]
        dh = DK // H
        qh = q.reshape(BN, H, dh, W)
        kh = k.reshape(BN, H, dh, W)
        vh = val.reshape(BN, H, dh, W)
        scores = jnp.einsum('bhdi,bhdj->bhij', qh, kh) / jnp.sqrt(jnp.asarray(dh, qh.dtype))
        scores = jnp.where(mp[:, :, None, :] > 0, scores, jnp.asarray(-1000000000.0, scores.dtype))
        attn = jax.nn.softmax(scores, axis=-1)
        o = jnp.einsum('bhij,bhdj->bhdi', attn, vh).reshape(BN, DK, W)
        o = jax.nn.gelu(o, approximate=False)
        out = jnp.einsum('de,bew->bdw', Wo, o) + bo[:, None]
        out = out.reshape(B, np_, D, W).transpose(0, 2, 1, 3).reshape(B, D, S)
        out = out * masks
        return out

    def _L0_ffn_ref(hidden_states, gate_w, bias, Wg, Wu, Wd, Sg, Su, Sd):
        import jax, jax.numpy as jnp
        import numpy as np
        H = 512
        I = 256
        E = 16
        TOPK = 4
        SI = 256
        orig_shape = hidden_states.shape
        x = hidden_states.reshape(-1, orig_shape[-1])
        scores = jax.nn.sigmoid(x @ gate_w.T) + bias
        topk_w, topk_idx = jax.lax.top_k(scores, TOPK)
        topk_w = topk_w / (jnp.sum(topk_w, axis=-1, keepdims=True) + 1e-20)
        cw = jnp.sum(jax.nn.one_hot(topk_idx, E, dtype=x.dtype) * topk_w[..., None], axis=1)
        g = jnp.einsum('th,eih->eti', x, Wg)
        u = jnp.einsum('th,eih->eti', x, Wu)
        z = jax.nn.silu(g) * u
        zw = z * cw.T[:, :, None]
        out = jnp.einsum('eti,ehi->th', zw, Wd)
        out = out + jax.nn.silu(x @ Sg.T) * (x @ Su.T) @ Sd.T
        return out.reshape(orig_shape)

    def _L1_xattn_ref(text, features, Wq, bq, Wk, bk):
        import jax, jax.numpy as jnp
        import numpy as np
        TEXT_DIM = 512
        FEATURE_DIM = 512

        def _xavier_uniform(key, shape):
            fan_in, fan_out = (shape[1], shape[0])
            limit = float(np.sqrt(6.0 / (fan_in + fan_out)))
            return jax.random.uniform(key, shape, jnp.float32, -limit, limit)
        Q = jnp.einsum('btx,dx->btd', text, Wq) + bq
        K = jnp.einsum('bpx,dx->bpd', features, Wk) + bk
        scale = 1.0 / jnp.sqrt(jnp.asarray(K.shape[-1], K.dtype))
        scores = jnp.einsum('btd,bpd->btp', Q, K) * scale
        attn = jax.nn.softmax(scores, axis=-1)
        attended = jnp.einsum('btp,bpd->btd', attn, features)
        return attended

    def _L1_ffn_ref(x, W, bias, calib_min, calib_max):
        import jax, jax.numpy as jnp
        import numpy as np
        QW = 127.0
        QA = 255.0
        B, S, D = x.shape
        Xf = x.reshape(-1, D)
        row_scales = jnp.max(jnp.abs(W), axis=1) / QW
        Wq = jnp.clip(jnp.round(W / row_scales[:, None]), -QW, QW).astype(jnp.int32)
        Xc = jnp.clip(Xf, calib_min[None, :], calib_max[None, :])
        mn = jnp.min(Xc, axis=1)
        mx = jnp.max(Xc, axis=1)
        col_scales = (mx - mn) / QA
        col_scales = jnp.where(col_scales > 0, col_scales, jnp.float32(1.0))
        col_zps = jnp.round(-128.0 - mn / col_scales)
        Xq = jnp.clip(jnp.round(Xc / col_scales[:, None]) + col_zps[:, None], -128.0, 127.0).astype(jnp.int32)
        acc = Xq @ Wq.T
        wsum = jnp.sum(Wq, axis=1)
        acc = acc - col_zps.astype(jnp.int32)[:, None] * wsum[None, :]
        Y = acc.astype(jnp.float32) * col_scales[:, None] * row_scales[None, :]
        Y = Y + bias[None, :]
        return Y.reshape(B, S, -1)

    def _L2_xattn_ref(query, key, value, Wq, Wk, Wv, Wo):
        import jax, jax.numpy as jnp
        import numpy as np
        DIM = 512
        NUM_HEADS = 32
        NUM_KV_HEADS = 8
        HEAD_DIM = DIM // NUM_HEADS
        KV_DIM = DIM // (NUM_HEADS // NUM_KV_HEADS)
        B, S = (1, 256)
        b, sq, _ = query.shape
        _, sk, _ = key.shape
        rep = NUM_HEADS // NUM_KV_HEADS
        q = (query @ Wq).reshape(b, sq, NUM_HEADS, HEAD_DIM).transpose(0, 2, 1, 3)
        k = (key @ Wk).reshape(b, sk, NUM_KV_HEADS, HEAD_DIM).transpose(0, 2, 1, 3)
        v = (value @ Wv).reshape(b, sk, NUM_KV_HEADS, HEAD_DIM).transpose(0, 2, 1, 3)
        k = jnp.repeat(k, rep, axis=1)
        v = jnp.repeat(v, rep, axis=1)
        scale = HEAD_DIM ** (-0.5)
        scores = jnp.einsum('bhqd,bhkd->bhqk', q, k) * scale
        probs = jax.nn.softmax(scores, axis=-1)
        out = jnp.einsum('bhqk,bhkd->bhqd', probs, v)
        out = out.transpose(0, 2, 1, 3).reshape(b, sq, DIM)
        return out @ Wo

    def _L2_ffn_ref(x, A, B, Wr, br):
        import jax, jax.numpy as jnp
        import numpy as np
        ALPHA = 32
        R = 16
        SCALING = ALPHA / R
        H = A.shape[0]
        router_logits = jnp.einsum('bsd,hd->bsh', x, Wr) + br
        scores = H * jax.nn.softmax(router_logits, axis=-1)
        low = jnp.einsum('bsd,hrd->bshr', x, A)
        out = jnp.einsum('bshr,hor,bsh->bso', low, B, scores)
        return SCALING * out

    def _L3_xattn_ref(k, q, v):
        import jax, jax.numpy as jnp
        import numpy as np
        B, C, N = (8, 64, 512)
        input_dim = k.shape[1]
        scores = jnp.einsum('bcn,bcm->bnm', k, q) / jnp.sqrt(jnp.float32(input_dim))
        attn = jax.nn.softmax(scores, axis=-1)
        out = jnp.einsum('bnm,bcm->bcn', attn, v)
        return out

    def _L3_ffn_ref(hidden_states, gate_w, up_w, down_w, fc1_w, fc2_w, expert_w, ln_gamma, ln_beta):
        import jax, jax.numpy as jnp
        import numpy as np
        HID, INT, LAT, NE, K = (512, 1024, 256, 8, 2)
        LN_EPS = 1e-05

        def _layernorm(x, gamma, beta):
            mu = jnp.mean(x, axis=-1, keepdims=True)
            var = jnp.var(x, axis=-1, keepdims=True)
            return (x - mu) * jax.lax.rsqrt(var + LN_EPS) * gamma + beta
        logits = jnp.einsum('bsh,he->bse', hidden_states, gate_w)
        routing_weights, selected_experts = jax.lax.top_k(logits, K)
        h = jax.nn.relu(jnp.einsum('bsh,hi->bsi', hidden_states, up_w)) ** 2
        shared_out = jnp.einsum('bsi,ih->bsh', h, down_w)
        x_latent = jnp.einsum('bsh,hl->bsl', hidden_states, fc1_w)
        expert_out = jnp.einsum('bsl,lm->bsm', x_latent, expert_w)
        moe_out = expert_out * jnp.sum(routing_weights, axis=-1, keepdims=True)
        routed_out = jnp.einsum('bsl,lh->bsh', moe_out, fc2_w)
        return _layernorm(shared_out + routed_out, ln_gamma, ln_beta)
    x = x + _L0_xattn_ref(_layernorm(x, axis=-1), ctx_4096, mask_Bx1x4096_ff1, L0_xattn_Wq, L0_xattn_bq, L0_xattn_Wk, L0_xattn_bk, L0_xattn_Wv, L0_xattn_bv, L0_xattn_Wo, L0_xattn_bo)
    x = x + _L0_ffn_ref(_layernorm(x, axis=-1), L0_ffn_gate_w, L0_ffn_bias, L0_ffn_Wg, L0_ffn_Wu, L0_ffn_Wd, L0_ffn_Sg, L0_ffn_Su, L0_ffn_Sd)
    x = x + _L1_xattn_ref(_layernorm(x, axis=-1), ctx_4096, L1_xattn_Wq, L1_xattn_bq, L1_xattn_Wk, L1_xattn_bk)
    x = x + _L1_ffn_ref(_layernorm(x, axis=-1), L1_ffn_W, L1_ffn_bias, L1_ffn_calib_min, L1_ffn_calib_max)
    x = x + _L2_xattn_ref(_layernorm(x, axis=-1), ctx_4096, ctx_4096, L2_xattn_Wq, L2_xattn_Wk, L2_xattn_Wv, L2_xattn_Wo)
    x = x + _L2_ffn_ref(_layernorm(x, axis=-1), L2_ffn_A, L2_ffn_B, L2_ffn_Wr, L2_ffn_br)
    x = x + _L3_xattn_ref(ctx_4096, _layernorm(x, axis=-1), ctx_4096)
    x = x + _L3_ffn_ref(_layernorm(x, axis=-1), L3_ffn_gate_w, L3_ffn_up_w, L3_ffn_down_w, L3_ffn_fc1_w, L3_ffn_fc2_w, L3_ffn_expert_w, L3_ffn_ln_gamma, L3_ffn_ln_beta)
    return x

_drawn_inputs = setup_inputs


def setup_inputs(seed=0):
    import zlib

    import numpy as np

    out = dict(_drawn_inputs(seed))
    spreads = {'L0_xattn_bq': (0.0, 0.8),
     'L0_xattn_bk': (0.0, 2.0),
     'L0_xattn_bv': (0.0, 0.281),
     'L0_xattn_bo': (0.0, 0.1),
     'L0_ffn_bias': (0.0, 0.77),
     'L1_xattn_bq': (0.0, 1.798),
     'L1_xattn_bk': (0.0, 2.0),
     'L2_ffn_br': (0.0, 2.0),
     'L3_ffn_ln_gamma': (1.0, 0.2),
     'L3_ffn_ln_beta': (0.0, 0.441)}
    factors = {'L0_ffn_gate_w': 6.408,
     'L0_ffn_Wg': 4.994,
     'L0_ffn_Wu': 4.607,
     'L0_ffn_Wd': 4.779,
     'L0_ffn_Sg': 4.695,
     'L0_ffn_Su': 4.615,
     'L0_ffn_Sd': 4.63,
     'L3_ffn_up_w': 3.472,
     'L3_ffn_down_w': 3.12,
     'L1_ffn_bias': 2.903,
     'L1_ffn_calib_min': 3.422,
     'L1_ffn_calib_max': 3.302,
     'L2_ffn_Wr': 3.196}
    for name, (base, spread) in spreads.items():
        noise = np.random.default_rng([zlib.crc32(name.encode()), seed]).standard_normal(out[name].shape)
        drawn = base * np.exp(spread * noise) if base else spread * noise
        out[name] = jnp.asarray(drawn.astype(out[name].dtype))
    for name, factor in factors.items():
        out[name] = (out[name] * factor).astype(out[name].dtype)
    return out
```

```python
import concourse.bass as bass
from concourse import mybir
from contextlib import ExitStack

F32 = mybir.dt.float32
F32R = mybir.dt.float32r
BF16 = mybir.dt.bfloat16
ALU = mybir.AluOpType
ACT = mybir.ActivationFunctionType
AX = mybir.AxisListType

P = 128
B = 8
D = 512
NC = D // P
T = B * P
HALVES = 2
BANK = 512
LN_EPS = 1e-5


class Core:

    def __init__(self, nc, ctx, dram):
        self.nc, self.ctx, self.dram, self.sems = nc, ctx, dram, []
        self.x = ctx.enter_context(nc.sbuf_tensor("x_res", [P, B, D], F32))
        self.ident = ctx.enter_context(nc.sbuf_tensor("ident", [P, P], F32))
        self.eps = ctx.enter_context(nc.sbuf_tensor("eps", [P, B], F32))
        self.neg_half = ctx.enter_context(nc.sbuf_tensor("neg_half", [P, B], F32))
        self.psum = ctx.enter_context(nc.psum_tensor("banks", [P, 8, BANK], F32))

    def sem(self, name):
        self.sems.append(self.nc.alloc_semaphore(name=name))
        return self.sems[-1]

    def retire_sems(self):
        self.nc.clear_and_free_semaphores(self.sems)
        self.nc.all_engine_barrier()
        self.sems = []


def sbuf(nc, scope, name, shape, dt=F32):
    return scope.enter_context(nc.sbuf_tensor(name, shape, dt))


class Norm:

    def __init__(self, core, scope, name):
        self.core = core
        self.stat = sbuf(core.nc, scope, f"{name}_stat", [P, B, 6])
        self.mv = sbuf(core.nc, scope, f"{name}_mv", [P, B, 2])
        self.ve = sbuf(core.nc, scope, f"{name}_var_eps", [P, B])
        self.rs = sbuf(core.nc, scope, f"{name}_rstd", [P, B])
        self.stat_ready = core.sem(f"{name}_stat_ready")
        self.mv_ready = core.sem(f"{name}_mv_ready")
        self.ve_ready = core.sem(f"{name}_ve_ready")
        self.rstd_ready = core.sem(f"{name}_rstd_ready")

    def stats(self, dve, b, src=None):
        src = self.core.x[:, b, :] if src is None else src
        dve.bn_stats(self.stat[:, b, :], src).then_inc(self.stat_ready, 1)
        dve.wait_ge(self.stat_ready, b + 1)
        dve.bn_aggr(self.mv[:, b, :], self.stat[:, b, :]).then_inc(self.mv_ready, 1)

    def scale(self, pool, b):
        pool.wait_ge(self.mv_ready, b + 1)
        pool.tensor_tensor(self.ve[:, b:b + 1], self.mv[:, b, 1:2], self.core.eps[:, 0:1],
                           ALU.add).then_inc(self.ve_ready, 1)
        pool.wait_ge(self.ve_ready, b + 1)
        pool.tensor_tensor(self.rs[:, b:b + 1], self.ve[:, b:b + 1], self.core.neg_half[:, 0:1],
                           ALU.pow).then_inc(self.rstd_ready, 1)

    def mean(self, b):
        return self.mv[:, b, 0:1]

    def rstd(self, b):
        return self.rs[:, b:b + 1]


def load_inputs(core):
    nc = core.nc
    loaded = core.sem("first_loaded")
    const_ready = core.sem("const_ready")
    with nc.Block() as block:
        @block.sync
        def _(sp):
            for b in range(B):
                sp.dma_start(core.x[:, b, :], core.dram["x"][b]).then_inc(loaded, 16)
            sp.wait_ge(loaded, 16 * B)

        @block.gpsimd
        def _(pool):
            pool.memset(core.ident[:, :], 0.0).then_inc(const_ready, 1)
            pool.memset(core.eps[:, :], LN_EPS)
            pool.memset(core.neg_half[:, :], -0.5)
            pool.wait_ge(const_ready, 1)
            pool.affine_select(out=core.ident[:, :], in_=core.ident[:, :],
                               compare_op=ALU.not_equal, fill=1.0, base=0,
                               pattern=[[-1, P]], channel_multiplier=1)


def store_output(core):
    stored = core.sem("stored")
    with core.nc.Block() as block:
        @block.sync
        def _(sp):
            for b in range(B):
                sp.dma_start(core.dram["out"][b], core.x[:, b, :]).then_inc(stored, 16)
            sp.wait_ge(stored, 16 * B)


class NormTurned:

    def __init__(self, core, scope, name, hi, lo):
        self.core, self.hi, self.lo = core, hi, lo
        self.norm = Norm(core, scope, name)
        self.xn = sbuf(core.nc, scope, f"{name}_turn_xn", [P, 2, D])
        self.xn_ready = core.sem(f"{name}_xn_ready")
        self.turned = core.sem(f"{name}_turned")
        self.hi_ready = core.sem(f"{name}_turned_hi_ready")
        self.lo_ready = core.sem(f"{name}_turned_lo_ready")

    def tile(self, part, b):
        return part[:, :, b * P:(b + 1) * P]

    def bank(self, b):
        return self.core.psum[:, b % 2, :].rearrange("p (c t) -> p c t", c=NC)

    def pool(self, pool, batches=range(B)):
        for b in batches:
            self.norm.scale(pool, b)

    def act(self, act, batches=range(B)):
        for b in batches:
            act.wait_ge(self.turned, b + 1)
            act.copy(self.tile(self.hi, b), self.bank(b)).then_inc(self.hi_ready, 1)

    def pe(self, pe, batches=range(B)):
        for b in batches:
            pe.wait_ge(self.xn_ready, b + 1)
            if b >= 2:
                pe.wait_ge(self.lo_ready, b - 1)
            for c in range(NC):
                mm = pe.transpose(self.core.psum[:, b % 2, c * P:(c + 1) * P],
                                  self.xn[:, b % 2, c * P:(c + 1) * P], self.core.ident[:, :])
            mm.then_inc(self.turned, 1)

    def dve(self, dve, batches=range(B)):
        for b in batches:
            if b == 0:
                self.norm.stats(dve, 0)
            if b + 1 < B:
                self.norm.stats(dve, b + 1)
            dve.wait_ge(self.norm.rstd_ready, b + 1)
            if b >= 2:
                dve.wait_ge(self.turned, b - 1)
            dve.tensor_scalar(self.xn[:, b % 2, :], self.core.x[:, b, :], self.norm.mean(b),
                              self.norm.rstd(b), ALU.subtract, ALU.mult)\
               .then_inc(self.xn_ready, 1)
            if b >= 1:
                self.rest(dve, b - 1)
            if b == B - 1:
                self.rest(dve, b)

    def rest(self, dve, b):
        dve.wait_ge(self.hi_ready, b + 1)
        dve.tensor_tensor(self.tile(self.lo, b), self.bank(b), self.tile(self.hi, b).bitcast(F32),
                          ALU.subtract).then_inc(self.lo_ready, 1)


RAW = 2048


class Weights:

    def __init__(self, core, scope, name, pieces, size=RAW):
        self.pieces = pieces
        self.raw = sbuf(core.nc, scope, f"{name}_raw", [P, 2, size])
        self.loaded = [core.sem(f"{name}_loaded_{i}") for i in range(2)]
        self.hi_ready = core.sem(f"{name}_w_hi_ready")
        self.lo_ready = core.sem(f"{name}_w_lo_ready")

    def load(self, sp):
        for i, (src, _, _) in enumerate(self.pieces):
            if i >= 2:
                sp.wait_ge(self.lo_ready, i - 1)
            sp.dma_start(self.raw[:, i % 2, 0:src.shape[1]], src).then_inc(self.loaded[i % 2], 16)

    def split_hi(self, act, pieces=None):
        for i in range(len(self.pieces)) if pieces is None else pieces:
            src, hi, _ = self.pieces[i]
            act.wait_ge(self.loaded[i % 2], 16 * (i // 2 + 1))
            act.copy(hi, self.raw[:, i % 2, 0:src.shape[1]]).then_inc(self.hi_ready, 1)

    def split_lo(self, pool, pieces=None):
        for i in range(len(self.pieces)) if pieces is None else pieces:
            src, hi, lo = self.pieces[i]
            pool.wait_ge(self.hi_ready, i + 1)
            if lo is None:
                pool.sem_inc(self.lo_ready, 1)
            else:
                pool.tensor_tensor(lo, self.raw[:, i % 2, 0:src.shape[1]], hi.bitcast(F32),
                                   ALU.subtract).then_inc(self.lo_ready, 1)

    def wait(self, pe, i):
        pe.wait_ge(self.lo_ready, i + 1)


def matmul_split(pe, out, w_hi, w_lo, m_hi, m_lo, start, stop):
    pe.matmul(out, w_hi, m_hi, start=start, stop=False)
    pe.matmul(out, w_hi, m_lo, start=False, stop=False)
    return pe.matmul(out, w_lo, m_hi, start=False, stop=stop)


A0_WIN, A0_HEADS, A0_DH = 128, 8, 8
A0_DK = A0_HEADS * A0_DH
A0_SLOT, A0_GROUPS = 32, 2
A0_PER_GROUP = A0_HEADS // A0_GROUPS
A0_WINS = D // A0_WIN
A0_MAX_ROW, A0_MASK_ROW = 24, 25
A0_OFF = -float(2 ** 31)
C_SELQ, C_SELK, C_MASKC, C_MASKA, C_BO = 0, 1, 2, 3, 4
C_BQ, C_SBQ, C_BK = 5, 7, 9
A0_COLS = 11


def l0_attention(core):
    nc, dram, ps = core.nc, core.dram, core.psum
    scale = float(A0_DH) ** -0.5
    with ExitStack() as lay:
        on_all = sbuf(nc, lay, "a0_on_all", [P, B, A0_WINS, A0_DK])
        wo = sbuf(nc, lay, "a0_wo", [A0_DK, P])
        out_mask = sbuf(nc, lay, "a0_out_mask", [P, B, D])
        gl = sbuf(nc, lay, "a0_gelu", [A0_DK, 2, D])
        tmp = sbuf(nc, lay, "a0_tmp", [P, 2, D])
        cols = sbuf(nc, lay, "a0_cols", [P, A0_COLS])
        loaded = core.sem("a0_loaded")
        ctx_loaded = [core.sem(f"a0_ctx_loaded_{h}") for h in range(HALVES)]
        mask_loaded = [core.sem(f"a0_mask_loaded_{h}") for h in range(HALVES)]
        out_mask_loaded = core.sem("a0_out_mask_loaded")
        with ExitStack() as part:
            wq = sbuf(nc, part, "a0_wq", [P, A0_GROUPS, P])
            wk = sbuf(nc, part, "a0_wk", [P, A0_GROUPS, P])
            wv = sbuf(nc, part, "a0_wv", [P, A0_DK])
            bv = sbuf(nc, part, "a0_bv", [P, A0_DK])
            ctx = sbuf(nc, part, "a0_ctx", [P, B, D])
            mask = sbuf(nc, part, "a0_mask", [P, B, D])
            xn = sbuf(nc, part, "a0_xn", [P, 2, D])
            q_lo = sbuf(nc, part, "a0_q_sel", [P, D], F32R)
            q = sbuf(nc, part, "a0_q", [P, 2, D], F32R)
            kf = sbuf(nc, part, "a0_kf", [P, 2, D])
            k_hi = sbuf(nc, part, "a0_k_sel", [P, 2, D], F32R)
            k = sbuf(nc, part, "a0_k", [P, 2, D], F32R)
            v = sbuf(nc, part, "a0_v", [P, 2, A0_WINS, A0_HEADS, A0_SLOT])
            mx = sbuf(nc, part, "a0_mx", [P, A0_WINS, P])
            e = sbuf(nc, part, "a0_e", [P, 2, A0_PER_GROUP, D])
            osb = sbuf(nc, part, "a0_osb", [P, 2, D])
            rec = sbuf(nc, part, "a0_rec", [P, A0_WINS, A0_PER_GROUP])
            norm = Norm(core, part, "a0")
            zeroed = core.sem("a0_zeroed")
            xn_ready = core.sem("a0_xn_ready")
            mask_ready = core.sem("a0_mask_ready")
            proj_done = core.sem("a0_proj_done")
            v_done = core.sem("a0_v_done")
            q_sel_ready = core.sem("a0_q_sel_ready")
            q_ready = core.sem("a0_q_ready")
            kf_ready = core.sem("a0_kf_ready")
            k_sel_ready = core.sem("a0_k_sel_ready")
            k_ready = core.sem("a0_k_ready")
            v_ready = core.sem("a0_v_ready")
            scores_done = core.sem("a0_scores_done")
            max_ready = core.sem("a0_max_ready")
            max_turned = core.sem("a0_max_turned")
            q_max_ready = core.sem("a0_q_max_ready")
            keyed_done = core.sem("a0_keyed_done")
            exp_ready = core.sem("a0_exp_ready")
            pv_done = core.sem("a0_pv_done")
            o_ready = core.sem("a0_o_ready")
            o_turned = core.sem("a0_o_turned")
            rec_ready = core.sem("a0_rec_ready")
            on_ready = core.sem("a0_on_ready")
            on_turned = core.sem("a0_on_turned")
            gelu_ready = core.sem("a0_gelu_ready")
            out_done = core.sem("a0_out_done")
            tmp_ready = core.sem("a0_tmp_ready")
            x_ready = core.sem("a0_x_ready")
            Q_BANK, K_BANK, V_BANK, M_BANK, S_BANK = 0, 1, 2, 3, 4
            GELU_BANK, OUT_BANK = 4, 6
            UNITS = B * A0_GROUPS

            def turned_o():
                return ps[:, M_BANK, :].rearrange("p (w r s) -> p w r s", w=A0_WINS, r=A0_PER_GROUP)

            with nc.Block() as block:
                @block.sync
                def _(sp):
                    for dst, name in ((wq, "a0_wq"), (wk, "a0_wk")):
                        sp.dma_start(dst[:, :, :], dram[name]).then_inc(loaded, 16)
                    for dst, name in ((cols, "a0_cols"), (wv, "a0_wv"), (bv, "a0_bv"), (wo, "a0_wo")):
                        sp.dma_start(dst[:, :], dram[name]).then_inc(loaded, 16)
                    for h in range(HALVES):
                        part_b = slice(h * B // HALVES, (h + 1) * B // HALVES)
                        sp.dma_start(mask[:, part_b, :], dram["mask"][part_b].partition_broadcast(P))\
                          .then_inc(mask_loaded[h], 16)
                        sp.dma_start(ctx[:, part_b, :], dram["ctx"][part_b].rearrange("b p s -> p b s"))\
                          .then_inc(ctx_loaded[h], 16)
                    sp.dma_start(out_mask[:, :, :], dram["mask"].partition_broadcast(P))\
                      .then_inc(out_mask_loaded, 16)

                @block.gpsimd
                def _(pool):
                    for i in range(2):
                        pool.memset(v[:, i, :, :, :], 0.0)
                    pool.memset(mx[:, :, :], 0.0).then_inc(zeroed, 1)
                    pool.wait_ge(zeroed, 1)
                    for i in range(2):
                        pool.memset(v[:, i, :, :, A0_DH:A0_DH + 1], 1.0).then_inc(zeroed, 1)
                    pool.wait_ge(loaded, 16 * 6)
                    norm.scale(pool, 0)
                    for b in range(B):
                        pool.wait_ge(mask_loaded[b * HALVES // B], 16)
                        pool.tensor_scalar(mask[:, b, :], mask[:, b, :], 0.0,
                                           cols[:, C_MASKC:C_MASKC + 1], ALU.is_gt,
                                           ALU.mult).then_inc(mask_ready, 1)
                        pool.wait_ge(mask_ready, 2 * b + 1)
                        pool.tensor_scalar(mask[:, b, :], mask[:, b, :],
                                           cols[:, C_MASKA:C_MASKA + 1], None,
                                           ALU.add).then_inc(mask_ready, 1)
                        if b + 1 < B:
                            norm.scale(pool, b + 1)
                        for g in range(A0_GROUPS):
                            u = A0_GROUPS * b + g
                            pool.wait_ge(k_sel_ready, u + 1)
                            if u >= 2:
                                pool.wait_ge(keyed_done, u - 1)
                            pool.tensor_tensor(k[:, u % 2, :], kf[:, u % 2, :],
                                               k_hi[:, u % 2, :].bitcast(F32),
                                               ALU.subtract).then_inc(k_ready, 1)

                @block.scalar
                def _(act):
                    act.wait_ge(loaded, 16 * 6)

                    def split(u):
                        g = u % A0_GROUPS
                        act.wait_ge(proj_done, u + 1)
                        if u >= 1:
                            act.wait_ge(q_ready, u)
                        act.activation(q_lo[:, :], ps[:, Q_BANK, :], ACT.Identity,
                                       bias=cols[:, C_SBQ + g:C_SBQ + g + 1],
                                       scale=cols[:, C_SELQ:C_SELQ + 1]).then_inc(q_sel_ready, 1)
                        act.wait_ge(kf_ready, u + 1)
                        if u >= 2:
                            act.wait_ge(k_ready, u - 1)
                        act.activation(k_hi[:, u % 2, :], kf[:, u % 2, :], ACT.Copy,
                                       scale=cols[:, C_SELK:C_SELK + 1]).then_inc(k_sel_ready, 1)

                    def take_out(u):
                        act.wait_ge(pv_done, u + 1)
                        if u >= 2:
                            act.wait_ge(o_turned, u - 1)
                        act.copy(osb[:, u % 2, :], ps[:, V_BANK, :]).then_inc(o_ready, 1)

                    split(0)
                    for u in range(UNITS):
                        if u + 1 < UNITS:
                            split(u + 1)
                        act.wait_ge(keyed_done, u + 1)
                        if u >= 2:
                            act.wait_ge(pv_done, u - 1)
                        act.activation(e[:, u % 2, :, :], ps[:, S_BANK:S_BANK + A0_PER_GROUP, :],
                                       ACT.Exp, scale=scale).then_inc(exp_ready, 1)
                        if u >= 1:
                            take_out(u - 1)
                    take_out(UNITS - 1)
                    for b in range(B):
                        act.wait_ge(on_turned, b + 1)
                        if b >= 2:
                            act.wait_ge(out_done, b - 1)
                        act.activation(gl[:, b % 2, :], ps[0:A0_DK, GELU_BANK + b % 2, :], ACT.Gelu)\
                           .then_inc(gelu_ready, 1)

                @block.vector
                def _(dve):
                    def normalise(b):
                        dve.wait_ge(norm.rstd_ready, b + 1)
                        if b >= 2:
                            dve.wait_ge(proj_done, A0_GROUPS * (b - 1))
                        dve.tensor_scalar(xn[:, b % 2, :], core.x[:, b, :], norm.mean(b),
                                          norm.rstd(b), ALU.subtract, ALU.mult).then_inc(xn_ready, 1)

                    def stack(u):
                        b, g = divmod(u, A0_GROUPS)
                        dve.wait_ge(proj_done, u + 1)
                        dve.wait_ge(mask_ready, 2 * b + 2)
                        if u >= 2:
                            dve.wait_ge(k_ready, u - 1)
                        dve.scalar_tensor_tensor(out=kf[:, u % 2, :], in0=ps[:, K_BANK, :],
                                                 scalar=cols[:, C_BK + g:C_BK + g + 1],
                                                 in1=mask[:, b, :], op0=ALU.add,
                                                 op1=ALU.mult).then_inc(kf_ready, 1)
                        dve.wait_ge(q_sel_ready, u + 1)
                        if u >= 2:
                            dve.wait_ge(keyed_done, u - 1)
                        dve.scalar_tensor_tensor(out=q[:, u % 2, :], in0=ps[:, Q_BANK, :],
                                                 scalar=cols[:, C_BQ + g:C_BQ + g + 1],
                                                 in1=q_lo[:, :].bitcast(F32), op0=ALU.add,
                                                 op1=ALU.subtract).then_inc(q_ready, 1)

                    def values_biased(b):
                        dve.wait_ge(v_done, b + 1)
                        dve.wait_ge(zeroed, 3)
                        if b >= 2:
                            dve.wait_ge(pv_done, A0_GROUPS * (b - 1))
                        dve.tensor_tensor(
                            v[:, b % 2, :, :, 0:A0_DH],
                            ps[:, V_BANK, 0:A0_WINS * A0_DK].rearrange(
                                "p (w h d) -> p w h d", w=A0_WINS, h=A0_HEADS),
                            bv[:, :].rearrange("p (h d) -> p h d", h=A0_HEADS).unsqueeze(1)
                            .broadcast_to([P, A0_WINS, A0_HEADS, A0_DH]),
                            ALU.add).then_inc(v_ready, 1)

                    def divide(u):
                        b, g = divmod(u, A0_GROUPS)
                        dve.wait_ge(o_turned, u + 1)
                        dve.reciprocal(rec[:, :, :], turned_o()[:, :, :, A0_DH]).then_inc(rec_ready, 1)
                        dve.wait_ge(rec_ready, u + 1)
                        dve.tensor_tensor(
                            on_all[:, b, :, :].rearrange("p w (h d) -> p w h d", h=A0_HEADS)
                            [:, :, A0_PER_GROUP * g:A0_PER_GROUP * (g + 1), :],
                            turned_o()[:, :, :, 0:A0_DH],
                            rec[:, :, :].unsqueeze(3).broadcast_to([P, A0_WINS, A0_PER_GROUP, A0_DH]),
                            ALU.mult).then_inc(on_ready, 1)

                    norm.stats(dve, 0)
                    norm.stats(dve, 1)
                    normalise(0)
                    dve.wait_ge(loaded, 16 * 6)
                    stack(0)
                    for u in range(UNITS):
                        b, g = divmod(u, A0_GROUPS)
                        dve.wait_ge(scores_done, u + 1)
                        dve.tensor_reduce(
                            mx[:, :, A0_MAX_ROW:P:A0_SLOT].rearrange("p w r -> p r w"),
                            ps[:, S_BANK:S_BANK + A0_PER_GROUP, :].rearrange(
                                "p r (w j) -> p r w j", w=A0_WINS),
                            AX.X, ALU.max, negate=True).then_inc(max_ready, 1)
                        dve.wait_ge(max_turned, u + 1)
                        dve.wait_ge(q_ready, u + 1)
                        dve.tensor_tensor(q[:, u % 2, :], ps[:, M_BANK, :],
                                          q[:, u % 2, :].bitcast(F32), ALU.add)\
                           .then_inc(q_max_ready, 1)
                        if u + 1 < UNITS:
                            stack(u + 1)
                        if g == 0:
                            values_biased(b)
                        if g == 0 and b + 1 < B:
                            if b + 2 < B:
                                norm.stats(dve, b + 2)
                            normalise(b + 1)
                        if u >= 2:
                            divide(u - 2)
                    divide(UNITS - 2)
                    divide(UNITS - 1)
                    dve.wait_ge(out_mask_loaded, 16)
                    for b in range(B):
                        dve.wait_ge(out_done, b + 1)
                        dve.scalar_tensor_tensor(out=tmp[:, b % 2, :], in0=ps[:, OUT_BANK + b % 2, :],
                                                 scalar=cols[:, C_BO:C_BO + 1], in1=out_mask[:, b, :],
                                                 op0=ALU.add, op1=ALU.mult).then_inc(tmp_ready, 1)
                        dve.wait_ge(tmp_ready, b + 1)
                        dve.tensor_tensor(core.x[:, b, :], core.x[:, b, :], tmp[:, b % 2, :],
                                          ALU.add).then_inc(x_ready, 1)

                @block.tensor
                def _(pe):
                    def project(u):
                        b, g = divmod(u, A0_GROUPS)
                        pe.wait_ge(xn_ready, b + 1)
                        if u >= 1:
                            pe.wait_ge(q_ready, u)
                            pe.wait_ge(kf_ready, u)
                        pe.matmul(ps[:, K_BANK, :], wk[:, g, :], xn[:, b % 2, :], start=True, stop=True)
                        pe.matmul(ps[:, Q_BANK, :], wq[:, g, :], xn[:, b % 2, :], start=True,
                                  stop=True).then_inc(proj_done, 1)

                    def project_values(b):
                        pe.wait_ge(ctx_loaded[b * HALVES // B], 16)
                        if b >= 1:
                            pe.wait_ge(o_ready, A0_GROUPS * b - 1)
                        for w in range(A0_WINS):
                            mm = pe.matmul(ps[:, V_BANK, w * A0_DK:(w + 1) * A0_DK],
                                           ctx[:, b, w * A0_WIN:(w + 1) * A0_WIN], wv[:, :],
                                           start=True, stop=True)
                        mm.then_inc(v_done, 1)

                    def scores(u):
                        pe.wait_ge(q_ready, u + 1)
                        pe.wait_ge(k_ready, u + 1)
                        if u >= 1:
                            pe.wait_ge(exp_ready, u)
                        for w in range(A0_WINS):
                            for r in range(A0_PER_GROUP):
                                rows = slice(A0_SLOT * r, A0_SLOT * (r + 1))
                                win = slice(w * A0_WIN, (w + 1) * A0_WIN)
                                mm = pe.matmul(ps[:, S_BANK + r, win], q[rows, u % 2, win],
                                               k[rows, u % 2, win], start=True, stop=True)
                        mm.then_inc(scores_done, 1)

                    def turn_max(u):
                        pe.wait_ge(max_ready, u + 1)
                        if u >= 3:
                            pe.wait_ge(on_ready, u - 2)
                        for w in range(A0_WINS):
                            mm = pe.transpose(ps[:, M_BANK, w * A0_WIN:(w + 1) * A0_WIN],
                                              mx[:, w, :], core.ident[:, :])
                        mm.then_inc(max_turned, 1)

                    def keyed(u):
                        pe.wait_ge(q_max_ready, u + 1)
                        for w in range(A0_WINS):
                            for r in range(A0_PER_GROUP):
                                rows = slice(A0_SLOT * r, A0_SLOT * (r + 1))
                                win = slice(w * A0_WIN, (w + 1) * A0_WIN)
                                mm = pe.matmul(ps[:, S_BANK + r, win], k[rows, u % 2, win],
                                               q[rows, u % 2, win], start=True, stop=True)
                        mm.then_inc(keyed_done, 1)

                    def values(u):
                        b, g = divmod(u, A0_GROUPS)
                        pe.wait_ge(exp_ready, u + 1)
                        pe.wait_ge(v_ready, b + 1)
                        if u >= 1:
                            pe.wait_ge(o_ready, u)
                        if u % A0_GROUPS == 1 and b + 1 < B:
                            pe.wait_ge(v_ready, b + 2)
                        for w in range(A0_WINS):
                            for r in range(A0_PER_GROUP):
                                win = slice(w * A0_WIN, (w + 1) * A0_WIN)
                                mm = pe.matmul(ps[A0_SLOT * r:A0_SLOT * (r + 1), V_BANK, win],
                                               v[:, b % 2, w, A0_PER_GROUP * g + r, :],
                                               e[:, u % 2, r, win], start=True, stop=True)
                        mm.then_inc(pv_done, 1)

                    def turn_outputs(u):
                        pe.wait_ge(o_ready, u + 1)
                        if u >= 1:
                            pe.wait_ge(on_ready, u)
                        for w in range(A0_WINS):
                            mm = pe.transpose(ps[:, M_BANK, w * A0_WIN:(w + 1) * A0_WIN],
                                              osb[:, u % 2, w * A0_WIN:(w + 1) * A0_WIN], core.ident[:, :])
                        mm.then_inc(o_turned, 1)

                    def turn_back(b):
                        pe.wait_ge(on_ready, A0_GROUPS * (b + 1))
                        if b >= 2:
                            pe.wait_ge(gelu_ready, b - 1)
                        for w in range(A0_WINS):
                            mm = pe.transpose(ps[0:A0_DK, GELU_BANK + b % 2, w * A0_WIN:(w + 1) * A0_WIN],
                                              on_all[:, b, w, :], core.ident[:, :])
                        mm.then_inc(on_turned, 1)

                    def project_out(b):
                        pe.wait_ge(gelu_ready, b + 1)
                        if b >= 2:
                            pe.wait_ge(tmp_ready, b - 1)
                        pe.matmul(ps[:, OUT_BANK + b % 2, :], wo[:, :], gl[:, b % 2, :], start=True,
                                  stop=True).then_inc(out_done, 1)

                    pe.wait_ge(loaded, 16 * 6)
                    project(0)
                    for u in range(UNITS):
                        scores(u)
                        if u + 1 < UNITS:
                            project(u + 1)
                        if u % A0_GROUPS == 0:
                            project_values(u // A0_GROUPS)
                        turn_max(u)
                        keyed(u)
                        if u >= 2:
                            turn_outputs(u - 2)
                        if u >= 1:
                            values(u - 1)
                    turn_outputs(UNITS - 2)
                    values(UNITS - 1)
                    turn_outputs(UNITS - 1)
                    turn_back(0)
                    for b in range(B):
                        if b + 1 < B:
                            turn_back(b + 1)
                        project_out(b)


F0_E, F0_TOPK, F0_I = 16, 4, 256
F0_ALL = F0_E + 1
F0_IC = F0_I // P
F0_HALF = T // 2
F0_GU = NC * 2 * F0_I
F0_JOBS = 2 * F0_IC
TAKEN = -1e30


def l0_ffn(core):
    nc, dram, ps = core.nc, core.dram, core.psum
    with ExitStack() as lay:
        hi = sbuf(nc, lay, "f0_xn_hi", [P, NC, T], F32R)
        lo = sbuf(nc, lay, "f0_xn_lo", [P, NC, T], F32R)
        weight = sbuf(nc, lay, "f0_weight", [P, B, F0_ALL])
        with ExitStack() as part:
            turned = NormTurned(core, part, "f0", hi, lo)
            gate = sbuf(nc, part, "f0_gate", [P, NC, F0_E])
            gate_hi = sbuf(nc, part, "f0_gate_hi", [P, NC, F0_E], F32R)
            gate_lo = sbuf(nc, part, "f0_gate_lo", [P, NC, F0_E], F32R)
            bias = sbuf(nc, part, "f0_bias", [P, F0_E])
            rank = sbuf(nc, part, "f0_rank", [P, F0_E])
            score = sbuf(nc, part, "f0_score", [P, B, F0_E])
            left = sbuf(nc, part, "f0_left", [P, B, F0_E])
            pick = sbuf(nc, part, "f0_pick", [P, B, F0_E])
            chosen = sbuf(nc, part, "f0_chosen", [P, B, F0_E])
            top = sbuf(nc, part, "f0_top", [P, B])
            loaded = core.sem("f0_gate_loaded")
            gate_hi_ready = core.sem("f0_gate_hi_ready")
            gate_lo_ready = core.sem("f0_gate_lo_ready")
            logits_done = core.sem("f0_logits_done")
            sigmoid_ready = core.sem("f0_sigmoid_ready")
            step = core.sem("f0_route_step")
            LOGITS = 2
            with nc.Block() as block:
                @block.sync
                def _(sp):
                    sp.dma_start(gate[:, :, :], dram["f0_gate"]).then_inc(loaded, 16)
                    sp.dma_start(bias[:, :], dram["f0_bias"]).then_inc(loaded, 16)
                    sp.dma_start(rank[:, :], dram["f0_rank"]).then_inc(loaded, 16)

                @block.gpsimd
                def _(pool):
                    turned.pool(pool)

                @block.scalar
                def _(act):
                    act.wait_ge(loaded, 48)
                    act.copy(gate_hi[:, :, :], gate[:, :, :]).then_inc(gate_hi_ready, 1)
                    turned.act(act)
                    act.wait_ge(logits_done, 1)
                    act.activation(left[:, :, :], ps[:, LOGITS, 0:B * F0_E].rearrange(
                        "p (b e) -> p b e", b=B), ACT.Sigmoid).then_inc(sigmoid_ready, 1)

                @block.tensor
                def _(pe):
                    turned.pe(pe)
                    pe.wait_ge(gate_lo_ready, 1)
                    pe.wait_ge(turned.lo_ready, B)
                    for b in range(B):
                        out = ps[:, LOGITS, b * F0_E:(b + 1) * F0_E]
                        rows = slice(b * P, (b + 1) * P)
                        for c in range(NC):
                            mm = matmul_split(pe, out, hi[:, c, rows], lo[:, c, rows],
                                              gate_hi[:, c, :], gate_lo[:, c, :], c == 0, c == NC - 1)
                    mm.then_inc(logits_done, 1)

                @block.vector
                def _(dve):
                    dve.wait_ge(gate_hi_ready, 1)
                    dve.tensor_tensor(gate_lo[:, :, :], gate[:, :, :], gate_hi[:, :, :].bitcast(F32),
                                      ALU.subtract).then_inc(gate_lo_ready, 1)
                    turned.dve(dve)
                    dve.memset(weight[:, :, :], 1.0)
                    steps = 0

                    def after(instruction):
                        nonlocal steps
                        steps += 1
                        instruction.then_inc(step, 1)
                        dve.wait_ge(step, steps)

                    def by_expert(row):
                        return row[:, :].unsqueeze(1).broadcast_to([P, B, F0_E])

                    def by_batch(col):
                        return col[:, :].unsqueeze(2).broadcast_to([P, B, F0_E])

                    dve.wait_ge(loaded, 48)
                    dve.wait_ge(sigmoid_ready, 1)
                    after(dve.tensor_tensor(score[:, :, :], left[:, :, :], by_expert(bias), ALU.add))
                    after(dve.tensor_copy(left[:, :, :], score[:, :, :]))
                    for k in range(F0_TOPK):
                        after(dve.tensor_reduce(top[:, :], left[:, :, :], AX.X, ALU.max))
                        after(dve.tensor_tensor(pick[:, :, :], left[:, :, :], by_batch(top), ALU.is_equal))
                        after(dve.tensor_tensor(pick[:, :, :], pick[:, :, :], by_expert(rank), ALU.mult))
                        after(dve.tensor_reduce(top[:, :], pick[:, :, :], AX.X, ALU.max))
                        after(dve.tensor_tensor(pick[:, :, :], by_expert(rank), by_batch(top), ALU.is_equal))
                        after(dve.scalar_tensor_tensor(out=left[:, :, :], in0=pick[:, :, :], scalar=TAKEN,
                                                       in1=left[:, :, :], op0=ALU.mult, op1=ALU.add))
                        if k == 0:
                            after(dve.tensor_copy(chosen[:, :, :], pick[:, :, :]))
                        else:
                            after(dve.tensor_tensor(chosen[:, :, :], chosen[:, :, :], pick[:, :, :], ALU.add))
                    after(dve.tensor_tensor(score[:, :, :], score[:, :, :], chosen[:, :, :], ALU.mult))
                    after(dve.tensor_reduce(top[:, :], score[:, :, :], AX.X, ALU.add))
                    after(dve.tensor_scalar(top[:, :], top[:, :], 1e-20, None, ALU.add))
                    after(dve.reciprocal(top[:, :], top[:, :]))
                    after(dve.tensor_tensor(weight[:, :, 0:F0_E], score[:, :, :], by_batch(top), ALU.mult))

        with ExitStack() as part:
            gu = sbuf(nc, part, "f0_gu", [P, F0_GU])
            gu_hi = sbuf(nc, part, "f0_gu_hi", [P, NC, 2, F0_I], F32R)
            gu_lo = sbuf(nc, part, "f0_gu_lo", [P, NC, 2, F0_I], F32R)
            dn = sbuf(nc, part, "f0_dn", [P, F0_IC * D])
            dn_hi = sbuf(nc, part, "f0_dn_hi", [P, F0_IC, D], F32R)
            dn_lo = sbuf(nc, part, "f0_dn_lo", [P, F0_IC, D], F32R)
            sil = sbuf(nc, part, "f0_sil", [P, 2, F0_HALF])
            z = sbuf(nc, part, "f0_z", [P, 2, F0_HALF])
            z_hi = sbuf(nc, part, "f0_z_hi", [P, F0_IC, T], F32R)
            z_lo = sbuf(nc, part, "f0_z_lo", [P, F0_IC, T], F32R)
            gu_loaded, dn_loaded = core.sem("f0_gu_loaded"), core.sem("f0_dn_loaded")
            gu_hi_ready, gu_lo_ready = core.sem("f0_gu_hi_ready"), core.sem("f0_gu_lo_ready")
            dn_hi_ready, dn_lo_ready = core.sem("f0_dn_hi_ready"), core.sem("f0_dn_lo_ready")
            gu_done = core.sem("f0_gu_done")
            sil_ready, z_ready = core.sem("f0_sil_ready"), core.sem("f0_z_ready")
            z_hi_ready, z_lo_ready = core.sem("f0_z_hi_ready"), core.sem("f0_z_lo_ready")
            y_done = core.sem("f0_y_done")
            y_added = core.sem("f0_y_added")
            Y_BANK, Y_BANKS = 4, 4

            def flat(w):
                return w[:, :, :, :].rearrange("p c g i -> p (c g i)")

            def flat_dn(w):
                return w[:, :, :].rearrange("p c n -> p (c n)")

            with nc.Block() as block:
                @block.sync
                def _(sp):
                    with sp.Fori(0, F0_ALL) as e:
                        sp.wait_ge(gu_lo_ready, e)
                        sp.dma_start(gu[:, :], dram["f0_gu"][bass.ds(e, 1)].rearrange("e p n -> p (e n)"))\
                          .then_inc(gu_loaded, 16)
                        sp.wait_ge(dn_lo_ready, e)
                        sp.dma_start(dn[:, :], dram["f0_dn"][bass.ds(e, 1)].rearrange("e p n -> p (e n)"))\
                          .then_inc(dn_loaded, 16)

                @block.scalar
                def _(act):
                    with act.Fori(0, F0_ALL) as e:
                        act.wait_ge(gu_loaded, 16 * e + 16)
                        act.wait_ge(gu_done, F0_JOBS * e)
                        act.copy(flat(gu_hi), gu[:, :]).then_inc(gu_hi_ready, 1)
                        for j in range(F0_JOBS):
                            half, ic = divmod(j, F0_IC)
                            cols = slice(half * F0_HALF, (half + 1) * F0_HALF)
                            act.wait_ge(gu_done, F0_JOBS * e + (j + 1))
                            if j >= 2:
                                act.wait_ge(z_ready, F0_JOBS * e + (j - 1))
                            act.activation(sil[:, j % 2, :], ps[:, 2 * (j % 2), :], ACT.Silu)\
                               .then_inc(sil_ready, 1)
                            if j == 0:
                                act.wait_ge(dn_loaded, 16 * e + 16)
                                act.copy(flat_dn(dn_hi), dn[:, :]).then_inc(dn_hi_ready, 1)
                            act.wait_ge(z_ready, F0_JOBS * e + (j + 1))
                            act.copy(z_hi[:, ic, cols], z[:, j % 2, :]).then_inc(z_hi_ready, 1)

                @block.gpsimd
                def _(pool):
                    with pool.Fori(0, F0_ALL) as e:
                        pool.wait_ge(gu_hi_ready, e + 1)
                        pool.tensor_tensor(flat(gu_lo), gu[:, :], flat(gu_hi).bitcast(F32),
                                           ALU.subtract).then_inc(gu_lo_ready, 1)
                        for j in range(F0_JOBS):
                            half, ic = divmod(j, F0_IC)
                            cols = slice(half * F0_HALF, (half + 1) * F0_HALF)
                            pool.wait_ge(z_hi_ready, F0_JOBS * e + (j + 1))
                            pool.tensor_tensor(z_lo[:, ic, cols], z[:, j % 2, :],
                                               z_hi[:, ic, cols].bitcast(F32),
                                               ALU.subtract).then_inc(z_lo_ready, 1)
                            if j == 0:
                                pool.wait_ge(dn_hi_ready, e + 1)
                                pool.tensor_tensor(flat_dn(dn_lo), dn[:, :], flat_dn(dn_hi).bitcast(F32),
                                                   ALU.subtract).then_inc(dn_lo_ready, 1)

                @block.vector
                def _(dve):
                    with dve.Fori(0, F0_ALL) as e:
                        for j in range(F0_JOBS):
                            dve.wait_ge(sil_ready, F0_JOBS * e + (j + 1))
                            if j >= 2:
                                dve.wait_ge(z_lo_ready, F0_JOBS * e + (j - 1))
                            dve.tensor_tensor(z[:, j % 2, :], sil[:, j % 2, :], ps[:, 2 * (j % 2) + 1, :],
                                              ALU.mult).then_inc(z_ready, 1)
                        for b in range(B):
                            dve.wait_ge(y_done, B * e + (b + 1))
                            dve.scalar_tensor_tensor(out=core.x[:, b, :], in0=ps[:, Y_BANK + b % Y_BANKS, :],
                                                     scalar=weight[:, b, bass.ds(e, 1)], in1=core.x[:, b, :],
                                                     op0=ALU.mult, op1=ALU.add).then_inc(y_added, 1)

                @block.tensor
                def _(pe):
                    with pe.Fori(0, F0_ALL) as e:
                        pe.wait_ge(gu_lo_ready, e + 1)
                        for j in range(F0_JOBS):
                            half, ic = divmod(j, F0_IC)
                            cols = slice(half * F0_HALF, (half + 1) * F0_HALF)
                            if j >= 2:
                                pe.wait_ge(z_ready, F0_JOBS * e + (j - 1))
                            for n in range(2):
                                out = ps[:, 2 * (j % 2) + n, :]
                                w = slice(ic * P, (ic + 1) * P)
                                for c in range(NC):
                                    mm = matmul_split(pe, out, gu_hi[:, c, n, w], gu_lo[:, c, n, w],
                                                      hi[:, c, cols], lo[:, c, cols], c == 0, c == NC - 1)
                            mm.then_inc(gu_done, 1)
                        pe.wait_ge(y_added, B * e)
                        pe.wait_ge(dn_lo_ready, e + 1)
                        for b in range(B):
                            if b % (B // 2) == 0:
                                pe.wait_ge(z_lo_ready, F0_JOBS * e + F0_IC * (b // (B // 2) + 1))
                            if b >= Y_BANKS:
                                pe.wait_ge(y_added, B * e + (b - Y_BANKS + 1))
                            rows = slice(b * P, (b + 1) * P)
                            for ic in range(F0_IC):
                                mm = matmul_split(pe, ps[:, Y_BANK + b % Y_BANKS, :], z_hi[:, ic, rows],
                                                  z_lo[:, ic, rows], dn_hi[:, ic, :], dn_lo[:, ic, :],
                                                  ic == 0, ic == F0_IC - 1)
                            mm.then_inc(y_done, 1)


HB = B // HALVES
HT = HB * P


def chunked(w):
    return w.rearrange("p c n -> p (c n)")


def l1_attention(core):
    nc, dram, ps = core.nc, core.dram, core.psum
    scale = float(D) ** -0.5
    with ExitStack() as lay:
        hi = sbuf(nc, lay, "a1_xn_hi", [P, NC, T], F32R)
        lo = sbuf(nc, lay, "a1_xn_lo", [P, NC, T], F32R)
        turned = NormTurned(core, lay, "a1", hi, lo)
        w_hi = [sbuf(nc, lay, f"a1_w{i}_hi", [P, NC, D], F32R) for i in range(2)]
        w_lo = [sbuf(nc, lay, f"a1_w{i}_lo", [P, NC, D], F32R) for i in range(2)]
        ct_hi = sbuf(nc, lay, "a1_ct_hi", [P, NC, HT], F32R)
        ct_lo = sbuf(nc, lay, "a1_ct_lo", [P, NC, HT], F32R)
        kq_hi = [sbuf(nc, lay, f"a1_kq{i}_hi", [P, NC, HT], F32R) for i in range(2)]
        kq_lo = [sbuf(nc, lay, f"a1_kq{i}_lo", [P, NC, HT], F32R) for i in range(2)]
        c_hi = sbuf(nc, lay, "a1_c_hi", [P, HB, D], F32R)
        c_lo = sbuf(nc, lay, "a1_c_lo", [P, HB, D], F32R)
        bias = sbuf(nc, lay, "a1_bias", [P, 2, NC])
        negmax = sbuf(nc, lay, "a1_negmax", [P, B])
        shift = sbuf(nc, lay, "a1_shift", [P, B])
        total = sbuf(nc, lay, "a1_total", [P, B])
        inv = sbuf(nc, lay, "a1_inv", [P, B])
        e = sbuf(nc, lay, "a1_e", [P, HB, P])
        at_hi = sbuf(nc, lay, "a1_at_hi", [P, HT], F32R)
        at_lo = sbuf(nc, lay, "a1_at_lo", [P, HT], F32R)
        pieces = [(dram["a1_wk"], chunked(w_hi[0][:, :, :]), chunked(w_lo[0][:, :, :])),
                  (dram["ctx_turned"][0], chunked(ct_hi[:, :, :]), chunked(ct_lo[:, :, :])),
                  (dram["a1_wq"], chunked(w_hi[1][:, :, :]), chunked(w_lo[1][:, :, :])),
                  (dram["ctx_rows"][0], chunked(c_hi[:, :, :]), chunked(c_lo[:, :, :])),
                  (dram["ctx_turned"][1], chunked(ct_hi[:, :, :]), chunked(ct_lo[:, :, :])),
                  (dram["ctx_rows"][1], chunked(c_hi[:, :, :]), chunked(c_lo[:, :, :]))]
        WK, CT0, WQ, C0, CT1, C1 = range(6)
        weights = Weights(core, lay, "a1", pieces)
        bias_loaded = core.sem("a1_bias_loaded")
        proj_done = core.sem("a1_proj_done")
        hi_ready, lo_ready = core.sem("a1_hi_ready"), core.sem("a1_lo_ready")
        scores_done = core.sem("a1_scores_done")
        negmax_ready, shift_ready = core.sem("a1_negmax_ready"), core.sem("a1_shift_ready")
        exp_ready, inv_ready = core.sem("a1_exp_ready"), core.sem("a1_inv_ready")
        attn_turned = core.sem("a1_attn_turned")
        at_hi_ready, at_lo_ready = core.sem("a1_at_hi_ready"), core.sem("a1_at_lo_ready")
        y_done, x_ready = core.sem("a1_y_done"), core.sem("a1_x_ready")
        S_BANK, T_BANK = 4, 5
        PER_HALF = 2 * NC

        with nc.Block() as block:
            @block.sync
            def _(sp):
                sp.dma_start(bias[:, :, :], dram["a1_bias"]).then_inc(bias_loaded, 16)
                weights.load(sp)

            @block.gpsimd
            def _(pool):
                weights.split_lo(pool, [WK])
                turned.pool(pool, range(0, 5))
                weights.split_lo(pool, [CT0])
                turned.pool(pool, range(5, B))
                weights.split_lo(pool, [WQ, C0, CT1, C1])

            @block.scalar
            def _(act):
                def proj_hi(n):
                    half, which, m = n // PER_HALF, n % PER_HALF // NC, n % NC
                    act.wait_ge(proj_done, n + 1)
                    if half:
                        act.wait_ge(scores_done, half)
                    act.activation(kq_hi[which][:, m, :], ps[:, 2 + n % 2, :], ACT.Identity,
                                   bias=bias[:, which, m:m + 1], scale=1.0).then_inc(hi_ready, 1)

                def softmax(half):
                    for i in range(HB):
                        b = half * HB + i
                        act.wait_ge(shift_ready, half + 1)
                        if half:
                            act.wait_ge(attn_turned, half)
                        act.activation(e[:, i, :], ps[:, S_BANK, i * P:(i + 1) * P], ACT.Exp,
                                       bias=shift[:, b:b + 1], scale=scale,
                                       accum_out=total[:, b:b + 1]).then_inc(exp_ready, 1)

                def attn_hi(half):
                    act.wait_ge(attn_turned, half + 1)
                    if half:
                        act.wait_ge(y_done, HB * half)
                    act.copy(at_hi[:, :], ps[:, T_BANK, :]).then_inc(at_hi_ready, 1)

                weights.split_hi(act, [WK, CT0])
                turned.act(act, range(0, 4))
                act.wait_ge(bias_loaded, 16)
                for n in range(NC):
                    proj_hi(n)
                weights.split_hi(act, [WQ])
                turned.act(act, range(4, B))
                weights.split_hi(act, [C0])
                for n in range(NC, 2 * NC):
                    proj_hi(n)
                act.wait_ge(proj_done, NC)
                weights.split_hi(act, [CT1])
                softmax(0)
                attn_hi(0)
                for n in range(2 * NC, 3 * NC):
                    proj_hi(n)
                act.wait_ge(y_done, HB)
                weights.split_hi(act, [C1])
                for n in range(3 * NC, 4 * NC):
                    proj_hi(n)
                softmax(1)
                attn_hi(1)

            @block.tensor
            def _(pe):
                def project(n):
                    half, which, m = n // PER_HALF, n % PER_HALF // NC, n % NC
                    if n >= 2:
                        pe.wait_ge(lo_ready, n - 1)
                    for c in range(NC):
                        if which == 0:
                            mov = ct_hi[:, c, :], ct_lo[:, c, :]
                        else:
                            rows = slice(half * HT, (half + 1) * HT)
                            mov = hi[:, c, rows], lo[:, c, rows]
                        mm = matmul_split(pe, ps[:, 2 + n % 2, :], w_hi[which][:, c, m * P:(m + 1) * P],
                                          w_lo[which][:, c, m * P:(m + 1) * P], *mov, c == 0, c == NC - 1)
                    mm.then_inc(proj_done, 1)

                def scores(half):
                    pe.wait_ge(lo_ready, PER_HALF * (half + 1))
                    if half:
                        pe.wait_ge(exp_ready, HB * half)
                    for i in range(HB):
                        rows = slice(i * P, (i + 1) * P)
                        for c in range(NC):
                            mm = matmul_split(pe, ps[:, S_BANK, rows], kq_hi[1][:, c, rows],
                                              kq_lo[1][:, c, rows], kq_hi[0][:, c, rows],
                                              kq_lo[0][:, c, rows], c == 0, c == NC - 1)
                    mm.then_inc(scores_done, 1)

                def turn(half):
                    pe.wait_ge(exp_ready, HB * (half + 1))
                    if half:
                        pe.wait_ge(at_lo_ready, half)
                    for i in range(HB):
                        mm = pe.transpose(ps[:, T_BANK, i * P:(i + 1) * P], e[:, i, :], core.ident[:, :])
                    mm.then_inc(attn_turned, 1)

                def attend(half):
                    pe.wait_ge(at_lo_ready, half + 1)
                    weights.wait(pe, C1 if half else C0)
                    for i in range(HB):
                        b = half * HB + i
                        if b >= 2:
                            pe.wait_ge(x_ready, b - 1)
                        matmul_split(pe, ps[:, 6 + b % 2, :], at_hi[:, i * P:(i + 1) * P],
                                     at_lo[:, i * P:(i + 1) * P], c_hi[:, i, :], c_lo[:, i, :],
                                     True, True).then_inc(y_done, 1)

                turned.pe(pe, range(0, 4))
                weights.wait(pe, CT0)
                for n in range(NC):
                    project(n)
                turned.pe(pe, range(4, B))
                weights.wait(pe, WQ)
                pe.wait_ge(turned.lo_ready, B)
                for n in range(NC, 2 * NC):
                    project(n)
                scores(0)
                weights.wait(pe, CT1)
                turn(0)
                for n in range(2 * NC, 3 * NC):
                    project(n)
                attend(0)
                for n in range(3 * NC, 4 * NC):
                    project(n)
                scores(1)
                turn(1)
                attend(1)

            @block.vector
            def _(dve):
                def proj_lo(n):
                    which, m = n % PER_HALF // NC, n % NC
                    dve.wait_ge(hi_ready, n + 1)
                    dve.scalar_tensor_tensor(out=kq_lo[which][:, m, :], in0=ps[:, 2 + n % 2, :],
                                             scalar=bias[:, which, m:m + 1],
                                             in1=kq_hi[which][:, m, :].bitcast(F32),
                                             op0=ALU.add, op1=ALU.subtract).then_inc(lo_ready, 1)

                def maxima(half):
                    cols = slice(half * HB, (half + 1) * HB)
                    dve.wait_ge(scores_done, half + 1)
                    dve.tensor_reduce(negmax[:, cols], ps[:, S_BANK, :].rearrange("p (b k) -> p b k", b=HB),
                                      AX.X, ALU.max, negate=True).then_inc(negmax_ready, 1)
                    dve.wait_ge(negmax_ready, half + 1)
                    dve.tensor_scalar(shift[:, cols], negmax[:, cols], scale, None, ALU.mult)\
                       .then_inc(shift_ready, 1)

                def attn_lo(half):
                    cols = slice(half * HB, (half + 1) * HB)
                    dve.wait_ge(exp_ready, HB * (half + 1))
                    dve.reciprocal(inv[:, cols], total[:, cols]).then_inc(inv_ready, 1)
                    dve.wait_ge(at_hi_ready, half + 1)
                    dve.tensor_tensor(at_lo[:, :], ps[:, T_BANK, :], at_hi[:, :].bitcast(F32),
                                      ALU.subtract).then_inc(at_lo_ready, 1)

                def add(half):
                    dve.wait_ge(inv_ready, half + 1)
                    for i in range(HB):
                        b = half * HB + i
                        dve.wait_ge(y_done, b + 1)
                        dve.scalar_tensor_tensor(out=core.x[:, b, :], in0=ps[:, 6 + b % 2, :],
                                                 scalar=inv[:, b:b + 1], in1=core.x[:, b, :],
                                                 op0=ALU.mult, op1=ALU.add).then_inc(x_ready, 1)

                turned.dve(dve, range(0, 5))
                for n in range(NC):
                    proj_lo(n)
                turned.dve(dve, range(5, B))
                for n in range(NC, 2 * NC):
                    proj_lo(n)
                maxima(0)
                attn_lo(0)
                for n in range(2 * NC, 3 * NC):
                    proj_lo(n)
                add(0)
                for n in range(3 * NC, 4 * NC):
                    proj_lo(n)
                maxima(1)
                attn_lo(1)
                add(1)


QW, QA = 127.0, 255.0
ROUND = 1.5 * 2.0 ** 23


def l1_ffn(core):
    nc, dram, ps = core.nc, core.dram, core.psum
    with ExitStack() as lay:
        w = sbuf(nc, lay, "f1_w", [P, NC, D])
        wr = sbuf(nc, lay, "f1_wr", [P, NC, D])
        wq = sbuf(nc, lay, "f1_wq", [P, NC, D], BF16)
        wt = sbuf(nc, lay, "f1_wt", [P, NC, D], BF16)
        wide = sbuf(nc, lay, "f1_wide", [P, NC, P])
        bias = sbuf(nc, lay, "f1_bias", [P, D])
        low = sbuf(nc, lay, "f1_low", [P, D])
        high = sbuf(nc, lay, "f1_high", [P, D])
        row_scale = sbuf(nc, lay, "f1_row_scale", [P, D])
        rs = sbuf(nc, lay, "f1_rs", [P, NC])
        rs_inv = sbuf(nc, lay, "f1_rs_inv", [P, NC])
        identb = sbuf(nc, lay, "f1_identb", [P, P], BF16)
        xn = sbuf(nc, lay, "f1_xn", [P, 2, D])
        xr = sbuf(nc, lay, "f1_xr", [P, D])
        xq = sbuf(nc, lay, "f1_xq", [P, 2, D], BF16)
        xt = sbuf(nc, lay, "f1_xt", [P, 2, NC, P], BF16)
        y = sbuf(nc, lay, "f1_y", [P, D])
        mn = sbuf(nc, lay, "f1_mn", [P, 2])
        mxm = sbuf(nc, lay, "f1_mx", [P, 2])
        cs = sbuf(nc, lay, "f1_cs", [P, B])
        flat_row = sbuf(nc, lay, "f1_flat_row", [P, 2])
        cs_inv = sbuf(nc, lay, "f1_cs_inv", [P, 2])
        zp = sbuf(nc, lay, "f1_zp", [P, 2])
        ends = sbuf(nc, lay, "f1_ends", [P, 2, 2])
        norm = Norm(core, lay, "f1")
        loaded = core.sem("f1_loaded")
        identb_ready = core.sem("f1_identb_ready")
        step = core.sem("f1_step")
        w_turned, wt_ready = core.sem("f1_w_turned"), core.sem("f1_wt_ready")
        wide_ready, rs_spread, rs_ready = (core.sem(f"f1_{n}") for n in ("wide_ready", "rs_spread", "rs_ready"))
        wq_ready = core.sem("f1_wq_ready")
        xq_ready, x_turned, xt_ready = (core.sem(f"f1_{n}") for n in ("xq_ready", "x_turned", "xt_ready"))
        y_done, y_taken = core.sem("f1_y_done"), core.sem("f1_y_taken")

        def turned_bank(i):
            return ps[:, i % 2, 0:D // 2].bitcast(BF16).rearrange("p (c n) -> p c n", c=NC)

        with nc.Block() as block:
            @block.sync
            def _(sp):
                sp.dma_start(w[:, :, :], dram["f1_w"]).then_inc(loaded, 16)
                for dst, name in ((bias, "f1_bias"), (low, "f1_low"), (high, "f1_high")):
                    sp.dma_start(dst[:, :], dram[name]).then_inc(loaded, 16)

            @block.gpsimd
            def _(pool):
                pool.tensor_copy(identb[:, :], core.ident[:, :]).then_inc(identb_ready, 1)
                for b in range(B):
                    norm.scale(pool, b)

            @block.tensor
            def _(pe):
                pe.wait_ge(identb_ready, 1)
                pe.wait_ge(wq_ready, 1)
                for c in range(NC):
                    if c >= 2:
                        pe.wait_ge(wt_ready, c - 1)
                    for m in range(NC):
                        mm = pe.transpose(turned_bank(c)[:, m, :], wq[:, m, c * P:(c + 1) * P], identb[:, :])
                    mm.then_inc(w_turned, 1)
                pe.wait_ge(wide_ready, 1)
                for m in range(NC):
                    mm = pe.matmul(ps[:, 2, m * P:(m + 1) * P], wide[:, m, :], core.ident[:, :],
                                   start=True, stop=True)
                mm.then_inc(rs_spread, 1)
                pe.wait_ge(wt_ready, NC)

                def product(b):
                    pe.wait_ge(xt_ready, b + 1)
                    if b >= 2:
                        pe.wait_ge(y_taken, b - 1)
                    for c in range(NC):
                        mm = pe.matmul(ps[:, 4 + b % 2, :], xt[:, b % 2, c, :], wt[:, c, :],
                                       start=(c == 0), stop=(c == NC - 1))
                    mm.then_inc(y_done, 1)

                for b in range(B):
                    pe.wait_ge(xq_ready, b + 1)
                    if b >= 2:
                        pe.wait_ge(xt_ready, b - 1)
                    for c in range(NC):
                        mm = pe.transpose(turned_bank(b)[:, c, :], xq[:, b % 2, c * P:(c + 1) * P], identb[:, :])
                    mm.then_inc(x_turned, 1)
                    if b >= 1:
                        product(b - 1)
                product(B - 1)

            @block.scalar
            def _(act):
                for c in range(NC):
                    act.wait_ge(w_turned, c + 1)
                    act.copy(wt[:, c, :].rearrange("p (m n) -> p m n", m=NC), turned_bank(c)).then_inc(wt_ready, 1)
                act.wait_ge(rs_spread, 1)
                act.copy(row_scale[:, :], ps[:, 2, :]).then_inc(rs_ready, 1)
                for b in range(B):
                    act.wait_ge(x_turned, b + 1)
                    if b >= 2:
                        act.wait_ge(y_done, b - 1)
                    act.copy(xt[:, b % 2, :, :], turned_bank(b)).then_inc(xt_ready, 1)

            @block.vector
            def _(dve):
                steps = 0

                def after(instruction):
                    nonlocal steps
                    steps += 1
                    instruction.then_inc(step, 1)
                    dve.wait_ge(step, steps)

                norm.stats(dve, 0)
                dve.wait_ge(loaded, 64)
                after(dve.tensor_reduce(rs[:, :], w[:, :, :], AX.X, ALU.max, apply_absolute_value=True))
                after(dve.tensor_scalar(rs[:, :], rs[:, :], 1.0 / QW, None, ALU.mult))
                after(dve.reciprocal(rs_inv[:, :], rs[:, :]))
                for m in range(NC):
                    after(dve.tensor_scalar(wr[:, m, :], w[:, m, :], rs_inv[:, m:m + 1], ROUND,
                                            ALU.mult, ALU.add))
                    after(dve.tensor_scalar(wr[:, m, :], wr[:, m, :], ROUND, QW, ALU.subtract, ALU.min))
                after(dve.tensor_scalar(wq[:, :, :], wr[:, :, :], -QW, None, ALU.max))
                dve.memset(wide[:, :, :], 1.0).then_inc(wq_ready, 1)
                dve.wait_ge(wq_ready, 1)
                for m in range(NC):
                    ins = dve.tensor_scalar(wide[:, m, :], wide[:, m, :], rs[:, m:m + 1], None, ALU.mult)
                ins.then_inc(wide_ready, 1)

                def quantise(b):
                    p = b % 2
                    one = slice(p, p + 1)
                    dve.wait_ge(norm.rstd_ready, b + 1)
                    after(dve.tensor_scalar(xn[:, p, :], core.x[:, b, :], norm.mean(b), norm.rstd(b),
                                            ALU.subtract, ALU.mult))
                    after(dve.tensor_tensor(xn[:, p, :], xn[:, p, :], low[:, :], ALU.max))
                    after(dve.tensor_tensor(xn[:, p, :], xn[:, p, :], high[:, :], ALU.min))
                    dve.tensor_reduce(mn[:, one], xn[:, p, :], AX.X, ALU.min)
                    after(dve.tensor_reduce(mxm[:, one], xn[:, p, :], AX.X, ALU.max))
                    after(dve.tensor_tensor(cs[:, b:b + 1], mxm[:, one], mn[:, one], ALU.subtract))
                    after(dve.tensor_scalar(cs[:, b:b + 1], cs[:, b:b + 1], 1.0 / QA, None, ALU.mult))
                    after(dve.tensor_scalar(flat_row[:, one], cs[:, b:b + 1], 0.0, None, ALU.is_le))
                    after(dve.tensor_tensor(cs[:, b:b + 1], cs[:, b:b + 1], flat_row[:, one], ALU.add))
                    after(dve.reciprocal(cs_inv[:, one], cs[:, b:b + 1]))
                    after(dve.tensor_tensor(zp[:, one], mn[:, one], cs_inv[:, one], ALU.mult))
                    after(dve.tensor_scalar(zp[:, one], zp[:, one], -1.0, -128.0, ALU.mult, ALU.add))
                    after(dve.tensor_scalar(zp[:, one], zp[:, one], ROUND, ROUND, ALU.add, ALU.subtract))
                    dve.tensor_scalar(ends[:, p, 0:1], zp[:, one], -1.0, -128.0, ALU.mult, ALU.add)
                    after(dve.tensor_scalar(ends[:, p, 1:2], zp[:, one], -1.0, 127.0, ALU.mult, ALU.add))
                    after(dve.tensor_scalar(xr[:, :], xn[:, p, :], cs_inv[:, one], ROUND, ALU.mult, ALU.add))
                    after(dve.tensor_scalar(xr[:, :], xr[:, :], ROUND, ends[:, p, 0:1], ALU.subtract, ALU.max))
                    if b >= 2:
                        dve.wait_ge(x_turned, b - 1)
                    dve.tensor_scalar(xq[:, p, :], xr[:, :], ends[:, p, 1:2], None, ALU.min).then_inc(xq_ready, 1)

                def finish(b):
                    dve.wait_ge(y_done, b + 1)
                    dve.scalar_tensor_tensor(out=y[:, :], in0=ps[:, 4 + b % 2, :], scalar=cs[:, b:b + 1],
                                             in1=row_scale[:, :], op0=ALU.mult, op1=ALU.mult)\
                       .then_inc(y_taken, 1)
                    dve.wait_ge(y_taken, b + 1)
                    after(dve.tensor_tensor(y[:, :], y[:, :], bias[:, :], ALU.add))
                    after(dve.tensor_tensor(core.x[:, b, :], core.x[:, b, :], y[:, :], ALU.add))

                for b in range(B):
                    if b + 1 < B:
                        norm.stats(dve, b + 1)
                    quantise(b)
                    if b == 1:
                        dve.wait_ge(rs_ready, 1)
                    if b >= 1:
                        finish(b - 1)
                finish(B - 1)


A2_KV, A2_REP, A2_DH = 8, 4, 16
A2_SLOT, A2_MAX_ROW = 64, 48
A2_PAIRS = A2_KV // 2
A2_KVD = A2_KV * A2_DH
A2_VSLOT = 32
A2_GROUPS, A2_PER_GROUP = 2, 4
A2_UNITS = B * A2_GROUPS
A2_RAW = 1024


def l2_attention(core):
    with ExitStack() as lay:
        nc = core.nc
        q_st = sbuf(nc, lay, "a2_q_st", [P, A2_PAIRS * A2_REP, T], F32R)
        k_st = sbuf(nc, lay, "a2_k_st", [P, A2_PAIRS, T], F32R)
        v = sbuf(nc, lay, "a2_v", [P, B, A2_KV, A2_VSLOT])
        l2_project(core, q_st, k_st, v)
        l2_attend(core, q_st, k_st, v)


def l2_project(core, q_st, k_st, v):
    nc, dram, ps = core.nc, core.dram, core.psum
    with ExitStack() as part:
        hi = sbuf(nc, part, "a2_xn_hi", [P, NC, T], F32R)
        lo = sbuf(nc, part, "a2_xn_lo", [P, NC, T], F32R)
        turned = NormTurned(core, part, "a2", hi, lo)
        ct_hi = sbuf(nc, part, "a2_ct_hi", [P, NC, HT], F32R)
        ct_lo = sbuf(nc, part, "a2_ct_lo", [P, NC, HT], F32R)
        wq_hi = sbuf(nc, part, "a2_wq_hi", [P, NC, D], F32R)
        wq_lo = sbuf(nc, part, "a2_wq_lo", [P, NC, D], F32R)
        wkv_hi = sbuf(nc, part, "a2_wkv_hi", [P, NC, 2 * A2_KVD], F32R)
        wkv_lo = sbuf(nc, part, "a2_wkv_lo", [P, NC, 2 * A2_KVD], F32R)
        sel_k = sbuf(nc, part, "a2_sel_k", [P, 2, A2_PAIRS, P], F32R)
        sel_q = sbuf(nc, part, "a2_sel_q", [P, 2, A2_REP, P], F32R)
        part_hi = sbuf(nc, part, "a2_part_hi", [P, 2, HT], F32R)
        part_lo = sbuf(nc, part, "a2_part_lo", [P, 2, HT], F32R)
        ones_row = sbuf(nc, part, "a2_ones_row", [P, 1])

        def flat(w, a, b):
            return chunked(w[:, a:b, :])

        ct, wq = dram["ctx_turned"], dram["a2_wq"]
        pieces = [(dram["a2_wkv"], flat(wkv_hi, 0, NC), flat(wkv_lo, 0, NC)),
                  (ct[0][:, 0:A2_RAW], flat(ct_hi, 0, 2), flat(ct_lo, 0, 2)),
                  (ct[0][:, A2_RAW:], flat(ct_hi, 2, NC), flat(ct_lo, 2, NC)),
                  (dram["a2_sel_k"], sel_k[:, :, :, :].rearrange("p a b c -> p (a b c)"), None),
                  (dram["a2_sel_q"], sel_q[:, :, :, :].rearrange("p a b c -> p (a b c)"), None),
                  (wq[:, 0:A2_RAW], flat(wq_hi, 0, 2), flat(wq_lo, 0, 2)),
                  (wq[:, A2_RAW:], flat(wq_hi, 2, NC), flat(wq_lo, 2, NC)),
                  (ct[1][:, 0:A2_RAW], flat(ct_hi, 0, 2), flat(ct_lo, 0, 2)),
                  (ct[1][:, A2_RAW:], flat(ct_hi, 2, NC), flat(ct_lo, 2, NC))]
        WKV, CT0A, CT0B, SELK, SELQ, WQA, WQB, CT1A, CT1B = range(9)
        weights = Weights(core, part, "a2", pieces, A2_RAW)
        jobs = [("k", 0, 0)] + [("q", h, m) for h in range(HALVES) for m in range(NC)] + [("k", 1, 0)]
        row_loaded = core.sem("a2_row_loaded")
        proj_done = core.sem("a2_proj_done")
        hi_ready, lo_ready = core.sem("a2_hi_ready"), core.sem("a2_lo_ready")
        stack_done = core.sem("a2_stack_done")
        even_ready, odd_ready = core.sem("a2_even_ready"), core.sem("a2_odd_ready")
        v_done, v_ready, v_zeroed = core.sem("a2_v_done"), core.sem("a2_v_ready"), core.sem("a2_v_zeroed")

        def stack_tile(n, i):
            kind, half, m = jobs[n]
            rows = slice(half * HT, (half + 1) * HT)
            return k_st[:, i, rows] if kind == "k" else q_st[:, m * A2_REP + i, rows]

        with nc.Block() as block:
            @block.sync
            def _(sp):
                sp.dma_start(ones_row[:, :], dram["a2_ones_row"]).then_inc(row_loaded, 16)
                weights.load(sp)

            @block.gpsimd
            def _(pool):
                for i, piece in enumerate((WKV, CT0A, CT0B, SELK)):
                    weights.split_lo(pool, [piece])
                    turned.pool(pool, range(2 * i, 2 * i + 2))
                weights.split_lo(pool, [SELQ, WQA, WQB])
                pool.memset(v[:, :, :, :], 0.0).then_inc(v_zeroed, 1)
                pool.wait_ge(v_zeroed, 1)
                pool.memset(v[:, :, :, A2_DH:A2_DH + 1], 1.0).then_inc(v_zeroed, 1)
                weights.split_lo(pool, [CT1A, CT1B])

            @block.scalar
            def _(act):
                def part_of(n):
                    act.wait_ge(proj_done, n + 1)
                    if n >= 2:
                        act.wait_ge(stack_done, 4 * (n - 1))
                    act.copy(part_hi[:, n % 2, :], ps[:, 2 + n % 2, :]).then_inc(hi_ready, 1)

                def stacks(n):
                    for i in (0, 2):
                        act.wait_ge(stack_done, 4 * n + i + 1)
                        if jobs[n][0] == "k":
                            ins = act.activation(stack_tile(n, i), ps[:, 4 + i, :], ACT.Identity,
                                                 bias=ones_row[:, 0:1], scale=1.0)
                        else:
                            ins = act.copy(stack_tile(n, i), ps[:, 4 + i, :])
                        ins.then_inc(even_ready, 1)

                weights.split_hi(act, [WKV, CT0A])
                turned.act(act, range(0, 2))
                weights.split_hi(act, [CT0B])
                turned.act(act, range(2, 4))
                weights.split_hi(act, [SELK])
                turned.act(act, range(4, 6))
                weights.split_hi(act, [SELQ])
                turned.act(act, range(6, B))
                weights.split_hi(act, [WQA, WQB])
                act.wait_ge(row_loaded, 16)
                for n in range(len(jobs)):
                    part_of(n)
                    if n >= 1:
                        stacks(n - 1)
                    if n == 1:
                        act.wait_ge(v_done, 1)
                        weights.split_hi(act, [CT1A, CT1B])
                stacks(len(jobs) - 1)

            @block.vector
            def _(dve):
                def part_of(n):
                    dve.wait_ge(hi_ready, n + 1)
                    dve.tensor_tensor(part_lo[:, n % 2, :], ps[:, 2 + n % 2, :],
                                      part_hi[:, n % 2, :].bitcast(F32), ALU.subtract)\
                       .then_inc(lo_ready, 1)

                def stacks(n):
                    for i in (1, 3):
                        dve.wait_ge(stack_done, 4 * n + i + 1)
                        if jobs[n][0] == "k":
                            ins = dve.tensor_scalar(stack_tile(n, i), ps[:, 4 + i, :], ones_row[:, 0:1],
                                                    None, ALU.add)
                        else:
                            ins = dve.tensor_copy(stack_tile(n, i), ps[:, 4 + i, :])
                        ins.then_inc(odd_ready, 1)

                def values(half):
                    dve.wait_ge(v_done, half + 1)
                    dve.wait_ge(v_zeroed, 2)
                    dve.tensor_copy(v[:, half * HB:(half + 1) * HB, :, 0:A2_DH].rearrange(
                                        "p b c d -> p (b c) d"),
                                    ps[:, half, :].rearrange("p (n d) -> p n d", d=A2_DH)).then_inc(v_ready, 1)

                turned.dve(dve)
                dve.wait_ge(row_loaded, 16)
                for n in range(len(jobs)):
                    part_of(n)
                    if n == 0:
                        values(0)
                    if n >= 1:
                        stacks(n - 1)
                values(1)
                stacks(len(jobs) - 1)

            @block.tensor
            def _(pe):
                def project(n):
                    kind, half, m = jobs[n]
                    if n >= 2:
                        pe.wait_ge(lo_ready, n - 1)
                    for c in range(NC):
                        w = slice(m * P, (m + 1) * P)
                        if kind == "k":
                            ops = wkv_hi[:, c, w], wkv_lo[:, c, w], ct_hi[:, c, :], ct_lo[:, c, :]
                        else:
                            rows = slice(half * HT, (half + 1) * HT)
                            ops = wq_hi[:, c, w], wq_lo[:, c, w], hi[:, c, rows], lo[:, c, rows]
                        mm = matmul_split(pe, ps[:, 2 + n % 2, :], *ops, c == 0, c == NC - 1)
                    mm.then_inc(proj_done, 1)

                def stacks(n):
                    kind = jobs[n][0]
                    pe.wait_ge(lo_ready, n + 1)
                    sel = sel_k if kind == "k" else sel_q
                    for i in range(4):
                        if n >= 1:
                            pe.wait_ge(odd_ready if i % 2 else even_ready, 2 * (n - 1) + i // 2 + 1)
                        pe.matmul(ps[:, 4 + i, :], sel[:, 0, i, :], part_hi[:, n % 2, :], start=True,
                                  stop=False)
                        pe.matmul(ps[:, 4 + i, :], sel[:, 1, i, :], part_lo[:, n % 2, :], start=False,
                                  stop=True).then_inc(stack_done, 1)

                def values(half):
                    for i in range(HB):
                        rows = slice(i * P, (i + 1) * P)
                        for c in range(NC):
                            mm = matmul_split(pe, ps[:, half, i * A2_KVD:(i + 1) * A2_KVD],
                                              ct_hi[:, c, rows], ct_lo[:, c, rows],
                                              wkv_hi[:, c, A2_KVD:], wkv_lo[:, c, A2_KVD:],
                                              c == 0, c == NC - 1)
                    mm.then_inc(v_done, 1)

                turned.pe(pe)
                weights.wait(pe, CT0B)
                project(0)
                pe.wait_ge(turned.lo_ready, B)
                values(0)
                weights.wait(pe, WQB)
                for n in range(1, len(jobs)):
                    if n == len(jobs) - 1:
                        weights.wait(pe, CT1B)
                    project(n)
                    if n == len(jobs) - 1:
                        values(1)
                    stacks(n - 1)
                stacks(len(jobs) - 1)


def l2_attend(core, q_st, k_st, v):
    nc, dram, ps = core.nc, core.dram, core.psum
    scale = float(A2_DH) ** -0.5
    with ExitStack() as part:
        e = sbuf(nc, part, "a2_e", [P, 2, A2_PER_GROUP, A2_REP * P])
        osb = sbuf(nc, part, "a2_osb", [P, 2, A2_REP * P])
        rec = sbuf(nc, part, "a2_rec", [P, A2_REP, A2_PER_GROUP])
        on = sbuf(nc, part, "a2_on", [P, 2, A2_KV, A2_REP, A2_DH])
        ot_hi = sbuf(nc, part, "a2_ot_hi", [P, NC, T], F32R)
        ot_lo = sbuf(nc, part, "a2_ot_lo", [P, NC, T], F32R)
        wo_hi = sbuf(nc, part, "a2_wo_hi", [P, NC, D], F32R)
        wo_lo = sbuf(nc, part, "a2_wo_lo", [P, NC, D], F32R)
        mx = sbuf(nc, part, "a2_mx", [P, 2 * A2_REP, P])
        wo = dram["a2_wo"]
        pieces = [(wo[:, 0:A2_RAW], chunked(wo_hi[:, 0:2, :]), chunked(wo_lo[:, 0:2, :])),
                  (wo[:, A2_RAW:], chunked(wo_hi[:, 2:, :]), chunked(wo_lo[:, 2:, :]))]
        weights = Weights(core, part, "a2o", pieces, A2_RAW)
        zeroed = core.sem("a2_zeroed")
        scores_done, max_ready = core.sem("a2_scores_done"), core.sem("a2_max_ready")
        max_turned, q_ready = core.sem("a2_max_turned"), core.sem("a2_q_ready")
        keyed_done, exp_ready = core.sem("a2_keyed_done"), core.sem("a2_exp_ready")
        pv_done, o_ready = core.sem("a2_pv_done"), core.sem("a2_o_ready")
        o_turned, rec_ready, on_ready = (core.sem(f"a2_{n}") for n in ("o_turned", "rec_ready", "on_ready"))
        on_turned, ot_hi_ready, ot_lo_ready = (core.sem(f"a2_{n}") for n in
                                               ("on_turned", "ot_hi_ready", "ot_lo_ready"))
        y_done, x_ready = core.sem("a2_y_done"), core.sem("a2_x_ready")
        M_BANK, O_BANK, S_BANK, ON_BANK = 0, 2, 4, 3

        def rows_of(b):
            return slice(b * P, (b + 1) * P)

        STEPS = 2 * A2_UNITS

        def s_bank(s):
            return S_BANK + 2 * (s % 2)

        def batch_pair(s):
            return divmod(s, A2_PAIRS)

        with nc.Block() as block:
            @block.sync
            def _(sp):
                weights.load(sp)

            @block.gpsimd
            def _(pool):
                pool.memset(mx[:, :, :], 0.0).then_inc(zeroed, 1)
                weights.split_lo(pool)

            @block.scalar
            def _(act):
                def take_out(u):
                    act.wait_ge(pv_done, u + 1)
                    if u >= 2:
                        act.wait_ge(o_turned, u - 1)
                    act.copy(osb[:, u % 2, :], ps[:, O_BANK + u % 2, :]).then_inc(o_ready, 1)

                def turned_hi(b):
                    act.wait_ge(on_turned, b + 1)
                    act.copy(ot_hi[:, :, rows_of(b)], ps[:, ON_BANK, :].rearrange("p (c t) -> p c t", c=NC))\
                       .then_inc(ot_hi_ready, 1)

                weights.split_hi(act)
                for s in range(STEPS + 4):
                    u = s // 2
                    if s < STEPS:
                        act.wait_ge(keyed_done, s + 1)
                        if u >= 2:
                            act.wait_ge(pv_done, u - 1)
                        act.activation(e[:, u % 2, 2 * (s % 2):2 * (s % 2) + 2, :],
                                       ps[:, s_bank(s):s_bank(s) + 2, :],
                                       ACT.Exp, scale=scale).then_inc(exp_ready, 1)
                    if s % 2 == 0 and 1 <= u <= A2_UNITS:
                        take_out(u - 1)
                    if s % A2_PAIRS == 2 and s >= 6:
                        turned_hi((s - 6) // A2_PAIRS)

            @block.vector
            def _(dve):
                def take_on(u):
                    b, g = divmod(u, A2_GROUPS)
                    dve.wait_ge(o_turned, u + 1)
                    if u >= 1:
                        dve.wait_ge(on_ready, u)
                    o = ps[:, O_BANK + u % 2, :].rearrange("p (m c d) -> p m c d", m=A2_REP, c=A2_PER_GROUP)
                    dve.reciprocal(rec[:, :, :], o[:, :, :, A2_DH]).then_inc(rec_ready, 1)
                    dve.wait_ge(rec_ready, u + 1)
                    if b >= 2:
                        dve.wait_ge(on_turned, b - 1)
                    dve.tensor_tensor(
                        on[:, b % 2, g * A2_PER_GROUP:(g + 1) * A2_PER_GROUP, :, :].rearrange(
                            "p c m d -> p m c d"),
                        o[:, :, :, 0:A2_DH],
                        rec[:, :, :].unsqueeze(3).broadcast_to([P, A2_REP, A2_PER_GROUP, A2_DH]),
                        ALU.mult).then_inc(on_ready, 1)

                def turned_lo(b):
                    dve.wait_ge(ot_hi_ready, b + 1)
                    dve.tensor_tensor(ot_lo[:, :, rows_of(b)],
                                      ps[:, ON_BANK, :].rearrange("p (c t) -> p c t", c=NC),
                                      ot_hi[:, :, rows_of(b)].bitcast(F32), ALU.subtract)\
                       .then_inc(ot_lo_ready, 1)

                def maximum(s):
                    dve.wait_ge(scores_done, s + 1)
                    tiles = slice(A2_REP * (s % 2), A2_REP * (s % 2 + 1))
                    dve.tensor_reduce(
                        mx[:, tiles, A2_MAX_ROW:P:A2_SLOT].rearrange("p m r -> p r m"),
                        ps[:, s_bank(s):s_bank(s) + 2, :].rearrange("p r (m j) -> p r m j", m=A2_REP),
                        AX.X, ALU.max, negate=True).then_inc(max_ready, 1)

                def lower(s):
                    b, pair = batch_pair(s)
                    dve.wait_ge(max_turned, s + 1)
                    tiles = q_st[:, pair * A2_REP:(pair + 1) * A2_REP, rows_of(b)]
                    dve.tensor_tensor(tiles, ps[:, M_BANK + s % 2, :].rearrange("p (m t) -> p m t", m=A2_REP),
                                      tiles.bitcast(F32), ALU.add).then_inc(q_ready, 1)

                dve.wait_ge(zeroed, 1)
                maximum(0)
                lower(0)
                maximum(1)
                for s in range(STEPS + 4):
                    if s + 1 < STEPS:
                        lower(s + 1)
                    if s % A2_PAIRS == 2 and s >= 6:
                        turned_lo((s - 6) // A2_PAIRS)
                    if s + 2 < STEPS:
                        maximum(s + 2)
                    if s % 2 == 1 and 3 <= s < STEPS + 2:
                        take_on((s - 3) // 2)
                for b in range(B):
                    dve.wait_ge(y_done, b + 1)
                    dve.tensor_tensor(core.x[:, b, :], ps[:, S_BANK + b % 4, :], core.x[:, b, :], ALU.add)\
                       .then_inc(x_ready, 1)
                dve.wait_ge(x_ready, B)

            @block.tensor
            def _(pe):
                def slot(i):
                    return slice(A2_SLOT * (i % 2), A2_SLOT * (i % 2 + 1))

                def scores(s):
                    b, pair = batch_pair(s)
                    if s >= 2:
                        pe.wait_ge(exp_ready, s - 1)
                    for m in range(A2_REP):
                        for i in range(2):
                            mm = pe.matmul(ps[:, s_bank(s) + i, m * P:(m + 1) * P],
                                           q_st[slot(i), pair * A2_REP + m, rows_of(b)],
                                           k_st[slot(i), pair, rows_of(b)], start=True, stop=True)
                    mm.then_inc(scores_done, 1)

                def turn_max(s):
                    pe.wait_ge(max_ready, s + 1)
                    if s >= 2:
                        pe.wait_ge(q_ready, s - 1)
                    for m in range(A2_REP):
                        mm = pe.transpose(ps[:, M_BANK + s % 2, m * P:(m + 1) * P],
                                          mx[:, A2_REP * (s % 2) + m, :], core.ident[:, :])
                    mm.then_inc(max_turned, 1)

                def keyed(s):
                    b, pair = batch_pair(s)
                    pe.wait_ge(q_ready, s + 1)
                    for i in range(2):
                        mm = pe.matmul(ps[:, s_bank(s) + i, :], k_st[slot(i), pair, rows_of(b)],
                                       q_st[slot(i), pair * A2_REP:(pair + 1) * A2_REP, rows_of(b)],
                                       start=True, stop=True)
                    mm.then_inc(keyed_done, 1)

                def values(s):
                    u = s // 2
                    b, g = divmod(u, A2_GROUPS)
                    pe.wait_ge(exp_ready, s + 1)
                    if u >= 2:
                        pe.wait_ge(on_ready, u - 1)
                    if u % 2 == 1 and b >= 1:
                        pe.wait_ge(ot_lo_ready, b)
                    for i in range(2 * (s % 2), 2 * (s % 2) + 2):
                        mm = pe.matmul(ps[A2_VSLOT * i:A2_VSLOT * (i + 1), O_BANK + u % 2, :],
                                       v[:, b, g * A2_PER_GROUP + i, :], e[:, u % 2, i, :],
                                       start=True, stop=True)
                    if s % 2 == 1:
                        mm.then_inc(pv_done, 1)

                def turn_o(u):
                    pe.wait_ge(o_ready, u + 1)
                    for m in range(A2_REP):
                        mm = pe.transpose(ps[:, O_BANK + u % 2, m * P:(m + 1) * P],
                                          osb[:, u % 2, m * P:(m + 1) * P], core.ident[:, :])
                    mm.then_inc(o_turned, 1)

                def turn_on(b):
                    pe.wait_ge(on_ready, A2_GROUPS * (b + 1))
                    rows = on[:, b % 2, :, :, :].rearrange("p c m d -> p (c m d)")
                    for c in range(NC):
                        mm = pe.transpose(ps[:, ON_BANK, c * P:(c + 1) * P], rows[:, c * P:(c + 1) * P],
                                          core.ident[:, :])
                    mm.then_inc(on_turned, 1)

                scores(0)
                turn_max(0)
                scores(1)
                for s in range(STEPS + 4):
                    if s < STEPS:
                        keyed(s)
                    if 1 <= s <= STEPS:
                        values(s - 1)
                    if s + 1 < STEPS:
                        turn_max(s + 1)
                    if s % 2 == 1 and 3 <= s < STEPS + 2:
                        turn_o((s - 3) // 2)
                    if s % A2_PAIRS == 2 and s >= 6:
                        turn_on((s - 6) // A2_PAIRS)
                    if s + 2 < STEPS:
                        scores(s + 2)
                weights.wait(pe, 1)
                pe.wait_ge(ot_lo_ready, B)
                for b in range(B):
                    if b >= 4:
                        pe.wait_ge(x_ready, b - 3)
                    for c in range(NC):
                        mm = matmul_split(pe, ps[:, S_BANK + b % 4, :], ot_hi[:, c, rows_of(b)],
                                          ot_lo[:, c, rows_of(b)], wo_hi[:, c, :], wo_lo[:, c, :],
                                          c == 0, c == NC - 1)
                    mm.then_inc(y_done, 1)


F2_H, F2_R = 8, 16
F2_HR = F2_H * F2_R
F2_N = F2_HR + F2_H
F2_SCALING = 2.0


def l2_ffn(core):
    nc, dram, ps = core.nc, core.dram, core.psum
    with ExitStack() as lay:
        hi = sbuf(nc, lay, "f2_xn_hi", [P, NC, T], F32R)
        lo = sbuf(nc, lay, "f2_xn_lo", [P, NC, T], F32R)
        turned = NormTurned(core, lay, "f2", hi, lo)
        a_hi = sbuf(nc, lay, "f2_a_hi", [P, NC, F2_N], F32R)
        a_lo = sbuf(nc, lay, "f2_a_lo", [P, NC, F2_N], F32R)
        b_hi = sbuf(nc, lay, "f2_b_hi", [P, D], F32R)
        b_lo = sbuf(nc, lay, "f2_b_lo", [P, D], F32R)
        br = sbuf(nc, lay, "f2_br", [P, F2_H])
        low = sbuf(nc, lay, "f2_low", [P, B, F2_HR])
        logit = sbuf(nc, lay, "f2_logit", [P, B, F2_H])
        weight = sbuf(nc, lay, "f2_weight", [P, B, F2_H])
        col = sbuf(nc, lay, "f2_col", [P, B])
        lt_hi = sbuf(nc, lay, "f2_lt_hi", [P, T], F32R)
        lt_lo = sbuf(nc, lay, "f2_lt_lo", [P, T], F32R)
        pieces = [(dram["f2_a"], chunked(a_hi[:, :, :]), chunked(a_lo[:, :, :])),
                  (dram["f2_b"], b_hi[:, :], b_lo[:, :])]
        weights = Weights(core, lay, "f2", pieces)
        br_loaded = core.sem("f2_br_loaded")
        low_done, low_ready, logit_ready = (core.sem(f"f2_{n}") for n in
                                            ("low_done", "low_ready", "logit_ready"))
        shifted_ready, exp_ready, step = (core.sem(f"f2_{n}") for n in ("shifted_ready", "exp_ready", "step"))
        scaled_ready, low_turned = core.sem("f2_scaled_ready"), core.sem("f2_low_turned")
        lt_hi_ready, lt_lo_ready = core.sem("f2_lt_hi_ready"), core.sem("f2_lt_lo_ready")
        y_done, x_ready = core.sem("f2_y_done"), core.sem("f2_x_ready")
        LOW_BANK, T_BANK, Y_BANK = 2, 4, 6

        with nc.Block() as block:
            @block.sync
            def _(sp):
                weights.load(sp)
                sp.dma_start(br[:, :], dram["f2_br"]).then_inc(br_loaded, 16)

            @block.gpsimd
            def _(pool):
                weights.split_lo(pool, [0])
                turned.pool(pool)
                weights.split_lo(pool, [1])

            @block.scalar
            def _(act):
                def take_low(b):
                    act.wait_ge(low_done, b + 1)
                    act.copy(low[:, b, :], ps[:, LOW_BANK + b % 2, 0:F2_HR]).then_inc(low_ready, 1)

                weights.split_hi(act)
                for b in range(B):
                    turned.act(act, [b])
                    if b >= 1:
                        take_low(b - 1)
                take_low(B - 1)
                act.wait_ge(shifted_ready, 1)
                act.activation(weight[:, :, :], weight[:, :, :], ACT.Exp).then_inc(exp_ready, 1)
                for h in range(HALVES):
                    act.wait_ge(low_turned, h + 1)
                    act.copy(lt_hi[:, h * HT:(h + 1) * HT], ps[:, T_BANK + h, :]).then_inc(lt_hi_ready, 1)

            @block.tensor
            def _(pe):
                def lower(b):
                    if b == 0:
                        weights.wait(pe, 0)
                    pe.wait_ge(turned.lo_ready, b + 1)
                    if b >= 2:
                        pe.wait_ge(logit_ready, b - 1)
                    rows = slice(b * P, (b + 1) * P)
                    for c in range(NC):
                        mm = matmul_split(pe, ps[:, LOW_BANK + b % 2, 0:F2_N], hi[:, c, rows], lo[:, c, rows],
                                          a_hi[:, c, :], a_lo[:, c, :], c == 0, c == NC - 1)
                    mm.then_inc(low_done, 1)

                for b in range(B):
                    turned.pe(pe, [b])
                    if b >= 1:
                        lower(b - 1)
                lower(B - 1)
                for h in range(HALVES):
                    pe.wait_ge(scaled_ready, h + 1)
                    for i in range(HB):
                        mm = pe.transpose(ps[:, T_BANK + h, i * P:(i + 1) * P], low[:, h * HB + i, :],
                                          core.ident[:, :])
                    mm.then_inc(low_turned, 1)
                weights.wait(pe, 1)
                for b in range(B):
                    pe.wait_ge(lt_lo_ready, b // HB + 1)
                    if b >= 2:
                        pe.wait_ge(x_ready, b - 1)
                    rows = slice(b * P, (b + 1) * P)
                    matmul_split(pe, ps[:, Y_BANK + b % 2, :], lt_hi[:, rows], lt_lo[:, rows], b_hi[:, :],
                                 b_lo[:, :], True, True).then_inc(y_done, 1)

            @block.vector
            def _(dve):
                steps = 0

                def after(instruction):
                    nonlocal steps
                    steps += 1
                    instruction.then_inc(step, 1)
                    dve.wait_ge(step, steps)

                def take_logit(b):
                    dve.wait_ge(low_ready, b + 1)
                    dve.tensor_tensor(logit[:, b, :], ps[:, LOW_BANK + b % 2, F2_HR:F2_N], br[:, :],
                                      ALU.add).then_inc(logit_ready, 1)

                def by_batch(c):
                    return c[:, :].unsqueeze(2).broadcast_to([P, B, F2_H])

                for b in range(B):
                    turned.dve(dve, [b])
                    if b == 1:
                        dve.wait_ge(br_loaded, 16)
                    if b >= 2:
                        take_logit(b - 2)
                take_logit(B - 2)
                take_logit(B - 1)
                dve.wait_ge(logit_ready, B)
                after(dve.tensor_reduce(col[:, :], logit[:, :, :], AX.X, ALU.max))
                dve.tensor_tensor(weight[:, :, :], logit[:, :, :], by_batch(col), ALU.subtract)\
                   .then_inc(shifted_ready, 1)
                dve.wait_ge(exp_ready, 1)
                after(dve.tensor_reduce(col[:, :], weight[:, :, :], AX.X, ALU.add))
                after(dve.reciprocal(col[:, :], col[:, :]))
                after(dve.scalar_tensor_tensor(out=weight[:, :, :], in0=weight[:, :, :],
                                               scalar=F2_SCALING * F2_H, in1=by_batch(col),
                                               op0=ALU.mult, op1=ALU.mult))
                for h in range(HALVES):
                    half = low[:, h * HB:(h + 1) * HB, :].rearrange("p b (h r) -> p (b h) r", h=F2_H)
                    w = weight[:, h * HB:(h + 1) * HB, :].rearrange("p b h -> p (b h)")
                    dve.tensor_tensor(half, half, w.unsqueeze(2).broadcast_to([P, HB * F2_H, F2_R]),
                                      ALU.mult).then_inc(scaled_ready, 1)
                for h in range(HALVES):
                    rows = slice(h * HT, (h + 1) * HT)
                    dve.wait_ge(lt_hi_ready, h + 1)
                    dve.tensor_tensor(lt_lo[:, rows], ps[:, T_BANK + h, :], lt_hi[:, rows].bitcast(F32),
                                      ALU.subtract).then_inc(lt_lo_ready, 1)
                for b in range(B):
                    dve.wait_ge(y_done, b + 1)
                    dve.tensor_tensor(core.x[:, b, :], ps[:, Y_BANK + b % 2, :], core.x[:, b, :], ALU.add)\
                       .then_inc(x_ready, 1)


A3_JOBS = B * NC


def l3_attention(core):
    nc, dram, ps = core.nc, core.dram, core.psum
    scale = float(P) ** -0.5
    with ExitStack() as lay:
        c_hi = sbuf(nc, lay, "a3_c_hi", [P, B, D], F32R)
        c_lo = sbuf(nc, lay, "a3_c_lo", [P, B, D], F32R)
        v_hi = [sbuf(nc, lay, f"a3_v{h}_hi", [P, NC, HT], F32R) for h in range(HALVES)]
        v_lo = [sbuf(nc, lay, f"a3_v{h}_lo", [P, NC, HT], F32R) for h in range(HALVES)]
        pieces = []
        for h in range(HALVES):
            batches = slice(h * HB, (h + 1) * HB)
            pieces += [(dram["ctx_rows"][h], chunked(c_hi[:, batches, :]), chunked(c_lo[:, batches, :])),
                       (dram["ctx_turned"][h], chunked(v_hi[h][:, :, :]), chunked(v_lo[h][:, :, :]))]
        weights = Weights(core, lay, "a3", pieces)
        xn = sbuf(nc, lay, "a3_xn", [P, 2, D])
        q_hi = sbuf(nc, lay, "a3_q_hi", [P, 2, D], F32R)
        q_lo = sbuf(nc, lay, "a3_q_lo", [P, 2, D], F32R)
        e = sbuf(nc, lay, "a3_e", [P, 2, D])
        et_hi = sbuf(nc, lay, "a3_et_hi", [P, 2, NC, D], F32R)
        et_lo = sbuf(nc, lay, "a3_et_lo", [P, 2, NC, D], F32R)
        negmax = sbuf(nc, lay, "a3_negmax", [P, A3_JOBS])
        shift = sbuf(nc, lay, "a3_shift", [P, A3_JOBS])
        total = sbuf(nc, lay, "a3_total", [P, A3_JOBS])
        inv = sbuf(nc, lay, "a3_inv", [P, A3_JOBS])
        norm = Norm(core, lay, "a3")
        xn_ready, q_hi_ready, q_lo_ready = (core.sem(f"a3_{n}") for n in ("xn_ready", "q_hi_ready", "q_lo_ready"))
        scores_done, negmax_ready, shift_ready = (core.sem(f"a3_{n}") for n in
                                                  ("scores_done", "negmax_ready", "shift_ready"))
        exp_ready, inv_ready, e_ready = (core.sem(f"a3_{n}") for n in ("exp_ready", "inv_ready", "e_ready"))
        e_turned, et_hi_ready, et_lo_ready = (core.sem(f"a3_{n}") for n in
                                              ("e_turned", "et_hi_ready", "et_lo_ready"))
        y_done, x_ready = core.sem("a3_y_done"), core.sem("a3_x_ready")
        S_BANK, T_BANK, Y_BANK = 0, 2, 4

        def turned_bank(j):
            return ps[:, T_BANK + j % 2, :].rearrange("p (m n) -> p m n", m=NC)

        def columns(part, j):
            b, n = divmod(j, NC)
            return part[:, b % 2, :, n * P:(n + 1) * P]

        with nc.Block() as block:
            @block.sync
            def _(sp):
                weights.load(sp)

            @block.gpsimd
            def _(pool):
                def query_lo(b):
                    pool.wait_ge(q_hi_ready, b + 1)
                    if b >= 2:
                        pool.wait_ge(scores_done, NC * (b - 1))
                    pool.tensor_tensor(q_lo[:, b % 2, :], xn[:, b % 2, :], q_hi[:, b % 2, :].bitcast(F32),
                                       ALU.subtract).then_inc(q_lo_ready, 1)

                norm.scale(pool, 0)
                weights.split_lo(pool, [0])
                query_lo(0)
                norm.scale(pool, 1)
                weights.split_lo(pool, [1])
                for b in range(1, B):
                    if b + 1 < B:
                        norm.scale(pool, b + 1)
                    query_lo(b)
                    if b <= HALVES:
                        weights.split_lo(pool, [1 + b])

            @block.scalar
            def _(act):
                def query_hi(b):
                    act.wait_ge(xn_ready, b + 1)
                    if b >= 2:
                        act.wait_ge(scores_done, NC * (b - 1))
                    act.copy(q_hi[:, b % 2, :], xn[:, b % 2, :]).then_inc(q_hi_ready, 1)

                def exp(j):
                    act.wait_ge(shift_ready, j + 1)
                    if j >= 2:
                        act.wait_ge(e_turned, j - 1)
                    act.activation(e[:, j % 2, :], ps[:, S_BANK + j % 2, :], ACT.Exp,
                                   bias=shift[:, j:j + 1], scale=scale,
                                   accum_out=total[:, j:j + 1]).then_inc(exp_ready, 1)

                def turned_hi(j):
                    act.wait_ge(e_turned, j + 1)
                    if j // NC >= 2:
                        act.wait_ge(y_done, j // NC - 1)
                    act.copy(columns(et_hi, j), turned_bank(j)).then_inc(et_hi_ready, 1)

                weights.split_hi(act, [0])
                query_hi(0)
                weights.split_hi(act, [1])
                for j in range(A3_JOBS):
                    exp(j)
                    if j >= 1:
                        turned_hi(j - 1)
                    if j % NC == 1 and j // NC + 1 < B:
                        query_hi(j // NC + 1)
                    if j in (0, 4):
                        weights.split_hi(act, [2 + j // 4])
                turned_hi(A3_JOBS - 1)

            @block.vector
            def _(dve):
                def query(b):
                    dve.wait_ge(norm.rstd_ready, b + 1)
                    if b >= 2:
                        dve.wait_ge(q_lo_ready, b - 1)
                    dve.tensor_scalar(xn[:, b % 2, :], core.x[:, b, :], norm.mean(b), norm.rstd(b),
                                      ALU.subtract, ALU.mult).then_inc(xn_ready, 1)

                def maximum(j):
                    dve.wait_ge(scores_done, j + 1)
                    dve.tensor_reduce(negmax[:, j:j + 1], ps[:, S_BANK + j % 2, :], AX.X, ALU.max,
                                      negate=True).then_inc(negmax_ready, 1)
                    dve.wait_ge(negmax_ready, j + 1)
                    dve.tensor_scalar(shift[:, j:j + 1], negmax[:, j:j + 1], scale, None, ALU.mult)\
                       .then_inc(shift_ready, 1)

                def invert(j):
                    dve.wait_ge(exp_ready, j + 1)
                    dve.reciprocal(inv[:, j:j + 1], total[:, j:j + 1]).then_inc(inv_ready, 1)

                def divide(j):
                    dve.wait_ge(inv_ready, j + 1)
                    dve.tensor_scalar(e[:, j % 2, :], e[:, j % 2, :], inv[:, j:j + 1], None, ALU.mult)\
                       .then_inc(e_ready, 1)

                def turned_lo(j):
                    dve.wait_ge(et_hi_ready, j + 1)
                    dve.tensor_tensor(columns(et_lo, j), turned_bank(j), columns(et_hi, j).bitcast(F32),
                                      ALU.subtract).then_inc(et_lo_ready, 1)

                def add(b):
                    dve.wait_ge(y_done, b + 1)
                    dve.tensor_tensor(core.x[:, b, :], ps[:, Y_BANK + b % 2, :], core.x[:, b, :], ALU.add)\
                       .then_inc(x_ready, 1)

                norm.stats(dve, 0)
                norm.stats(dve, 1)
                query(0)
                for j in range(A3_JOBS):
                    b, n = divmod(j, NC)
                    maximum(j)
                    if j >= 1:
                        invert(j - 1)
                        divide(j - 1)
                    if n == 0 and b + 1 < B:
                        if b + 2 < B:
                            norm.stats(dve, b + 2)
                        query(b + 1)
                    if j >= 2:
                        turned_lo(j - 2)
                    if n == 0 and b >= 2:
                        add(b - 2)
                invert(A3_JOBS - 1)
                divide(A3_JOBS - 1)
                turned_lo(A3_JOBS - 2)
                turned_lo(A3_JOBS - 1)
                add(B - 2)
                add(B - 1)

            @block.tensor
            def _(pe):
                def scores(j):
                    b, n = divmod(j, NC)
                    if n == 0:
                        pe.wait_ge(q_lo_ready, b + 1)
                        if b % HB == 0:
                            weights.wait(pe, 2 * (b // HB))
                    if j >= 2:
                        pe.wait_ge(exp_ready, j - 1)
                    cols = slice(n * P, (n + 1) * P)
                    matmul_split(pe, ps[:, S_BANK + j % 2, :], c_hi[:, b, cols], c_lo[:, b, cols],
                                 q_hi[:, b % 2, :], q_lo[:, b % 2, :], True, True).then_inc(scores_done, 1)

                def turn(j):
                    pe.wait_ge(e_ready, j + 1)
                    if j >= 2:
                        pe.wait_ge(et_lo_ready, j - 1)
                    for m in range(NC):
                        mm = pe.transpose(turned_bank(j)[:, m, :], e[:, j % 2, m * P:(m + 1) * P],
                                          core.ident[:, :])
                    mm.then_inc(e_turned, 1)

                def attend(b, chunks):
                    h, i = divmod(b, HB)
                    if i == 0:
                        weights.wait(pe, 2 * h + 1)
                    pe.wait_ge(et_lo_ready, NC * (b + 1))
                    if b >= 2:
                        pe.wait_ge(x_ready, b - 1)
                    for m in chunks:
                        mm = matmul_split(pe, ps[:, Y_BANK + b % 2, :], v_hi[h][:, m, i * P:(i + 1) * P],
                                          v_lo[h][:, m, i * P:(i + 1) * P], et_hi[:, b % 2, m, :],
                                          et_lo[:, b % 2, m, :], m == 0, m == NC - 1)
                    if NC - 1 in chunks:
                        mm.then_inc(y_done, 1)

                scores(0)
                for j in range(A3_JOBS):
                    if j + 1 < A3_JOBS:
                        scores(j + 1)
                    if j >= 1:
                        turn(j - 1)
                    if j % NC >= 2 and j // NC >= 1:
                        attend(j // NC - 1, (0, 1) if j % NC == 2 else (2, 3))
                turn(A3_JOBS - 1)
                attend(B - 1, range(NC))


F3_INT, F3_LAT, F3_E = 1024, 256, 8
F3_IC, F3_LC = F3_INT // P, F3_LAT // P
F3_RAW = 1024


def l3_ffn(core):
    nc, dram, ps = core.nc, core.dram, core.psum
    with ExitStack() as lay:
        hi = sbuf(nc, lay, "f3_xn_hi", [P, NC, T], F32R)
        lo = sbuf(nc, lay, "f3_xn_lo", [P, NC, T], F32R)
        turned = NormTurned(core, lay, "f3", hi, lo)

        def pair(name, shape):
            return (sbuf(nc, lay, f"f3_{name}_hi", shape, F32R), sbuf(nc, lay, f"f3_{name}_lo", shape, F32R))

        up, down = pair("up", [P, NC, F3_INT]), pair("down", [P, F3_IC, D])
        fc1, fc2 = pair("fc1", [P, NC, F3_LAT]), pair("fc2", [P, F3_LC, D])
        expert, gate = pair("expert", [P, F3_LC, F3_LAT]), pair("gate", [P, NC, F3_E])
        latent, routed = pair("latent", [P, F3_LC, HT]), pair("routed", [P, F3_LC, HT])
        h = pair("h", [P, F3_IC, HT])
        relu = sbuf(nc, lay, "f3_relu", [P, 2, HT])
        gamma = sbuf(nc, lay, "f3_gamma", [P, D])
        beta = sbuf(nc, lay, "f3_beta", [P, D])
        side = sbuf(nc, lay, "f3_side", [P, D])
        both = turned.xn
        top = sbuf(nc, lay, "f3_top", [P, B, F3_E])
        rw = sbuf(nc, lay, "f3_rw", [P, B])
        norm = Norm(core, lay, "f3o")

        def piece(name, parts, a, b):
            n = parts[0].shape[2]
            return (dram[name][:, a * n:b * n], chunked(parts[0][:, a:b, :]), chunked(parts[1][:, a:b, :]))

        pieces = [piece("f3_fc1", fc1, 0, NC), piece("f3_gate", gate, 0, NC),
                  piece("f3_expert", expert, 0, F3_LC)]
        pieces += [piece("f3_up", up, c, c + 1) for c in range(NC)]
        pieces += [piece("f3_fc2", fc2, 0, F3_LC)]
        pieces += [piece("f3_down", down, c, c + 2) for c in range(0, F3_IC, 2)]
        FC1, GATE, EXPERT, UP, FC2, DOWN = 0, 1, 2, 3, 3 + NC, 4 + NC
        LAST_UP, LAST = FC2 - 1, len(pieces) - 1
        weights = Weights(core, lay, "f3", pieces, F3_RAW)
        order = [("fc1", 0), ("fc1", 1), ("up", 0), ("expert", 0), ("expert", 1)]
        order += [("up", m) for m in range(1, F3_IC)]
        jobs = [(half, kind, m) for half in range(HALVES) for kind, m in order]
        PER_HALF = len(order)

        def before(n, kinds):
            return sum(k in kinds for _, k, _ in jobs[:n])

        cols_loaded = core.sem("f3_cols_loaded")
        logits_done, top_ready, rw_ready = (core.sem(f"f3_{n}") for n in ("logits_done", "top_ready", "rw_ready"))
        job_done = core.sem("f3_job_done")
        hi_ready, lo_ready = core.sem("f3_hi_ready"), core.sem("f3_lo_ready")
        relu_ready, square_ready = core.sem("f3_relu_ready"), core.sem("f3_square_ready")
        h_hi_ready, h_lo_ready = core.sem("f3_h_hi_ready"), core.sem("f3_h_lo_ready")
        side_done, side_ready = core.sem("f3_side_done"), core.sem("f3_side_ready")
        main_done, both_ready = core.sem("f3_main_done"), core.sem("f3_both_ready")
        unit_ready, gain_ready, out_ready = (core.sem(f"f3_{n}") for n in ("unit_ready", "gain_ready", "out_ready"))
        x_ready = core.sem("f3_x_ready")
        JOB_BANK, G_BANK, SIDE_BANK, MAIN_BANK = 2, 4, 5, 6
        SPLIT = ("fc1", "expert")

        def split_out(kind):
            return latent if kind == "fc1" else routed

        with nc.Block() as block:
            @block.sync
            def _(sp):
                weights.load(sp)
                sp.dma_start(gamma[:, :], dram["f3_gamma"]).then_inc(cols_loaded, 16)
                sp.dma_start(beta[:, :], dram["f3_beta"]).then_inc(cols_loaded, 16)

            @block.gpsimd
            def _(pool):
                for b in range(B):
                    weights.split_lo(pool, [b])
                    turned.pool(pool, [b])
                weights.split_lo(pool, range(B, len(pieces)))

                def square_lo(n):
                    i = before(n, ("up",))
                    pool.wait_ge(h_hi_ready, i + 1)
                    pool.tensor_tensor(h[1][:, jobs[n][2], :], relu[:, i % 2, :],
                                       h[0][:, jobs[n][2], :].bitcast(F32), ALU.subtract).then_inc(h_lo_ready, 1)

                def gain(b):
                    norm.scale(pool, b)
                    pool.wait_ge(unit_ready, b + 1)
                    pool.tensor_tensor(both[:, b % 2, :], both[:, b % 2, :], gamma[:, :], ALU.mult)\
                        .then_inc(gain_ready, 1)
                    pool.wait_ge(gain_ready, b + 1)
                    pool.tensor_tensor(both[:, b % 2, :], both[:, b % 2, :], beta[:, :], ALU.add)\
                        .then_inc(out_ready, 1)

                pool.wait_ge(cols_loaded, 32)
                for half in range(HALVES):
                    for n in range(half * PER_HALF, (half + 1) * PER_HALF):
                        if jobs[n][1] == "up":
                            square_lo(n)
                    for b in range(half * HB, (half + 1) * HB):
                        gain(b)

            @block.scalar
            def _(act):
                def evacuate(n):
                    half, kind, m = jobs[n]
                    act.wait_ge(job_done, n + 1)
                    if kind in SPLIT:
                        if half:
                            act.wait_ge(side_done, HB)
                        act.copy(split_out(kind)[0][:, m, :], ps[:, JOB_BANK + n % 2, :]).then_inc(hi_ready, 1)
                    else:
                        i = before(n, ("up",))
                        if i >= 2:
                            act.wait_ge(h_lo_ready, i - 1)
                        act.activation(relu[:, i % 2, :], ps[:, JOB_BANK + n % 2, :], ACT.Relu)\
                           .then_inc(relu_ready, 1)
                        act.wait_ge(square_ready, i + 1)
                        if half:
                            act.wait_ge(main_done, HB)
                        act.copy(h[0][:, m, :], relu[:, i % 2, :]).then_inc(h_hi_ready, 1)

                def take_side(b):
                    act.wait_ge(side_done, b + 1)
                    act.wait_ge(rw_ready, 1)
                    if b >= 1:
                        act.wait_ge(both_ready, b)
                    act.mul(side[:, :], ps[:, SIDE_BANK, :], rw[:, b:b + 1]).then_inc(side_ready, 1)

                for b in range(B):
                    weights.split_hi(act, [b])
                    turned.act(act, [b])
                weights.split_hi(act, range(B, len(pieces)))
                for half in range(HALVES):
                    for n in range(half * PER_HALF, (half + 1) * PER_HALF):
                        evacuate(n)
                    for b in range(half * HB, (half + 1) * HB):
                        take_side(b)

            @block.vector
            def _(dve):
                def evacuate(n):
                    half, kind, m = jobs[n]
                    if kind in SPLIT:
                        dve.wait_ge(hi_ready, before(n, SPLIT) + 1)
                        dve.tensor_tensor(split_out(kind)[1][:, m, :], ps[:, JOB_BANK + n % 2, :],
                                          split_out(kind)[0][:, m, :].bitcast(F32), ALU.subtract)\
                           .then_inc(lo_ready, 1)
                    else:
                        i = before(n, ("up",))
                        dve.wait_ge(relu_ready, i + 1)
                        dve.tensor_tensor(relu[:, i % 2, :], relu[:, i % 2, :], relu[:, i % 2, :], ALU.mult)\
                           .then_inc(square_ready, 1)

                def add_side(b):
                    dve.wait_ge(main_done, b + 1)
                    dve.wait_ge(side_ready, b + 1)
                    if b >= 2:
                        dve.wait_ge(x_ready, b - 1)
                    dve.tensor_tensor(both[:, b % 2, :], ps[:, MAIN_BANK + b % 2, :], side[:, :], ALU.add)\
                       .then_inc(both_ready, 1)
                    dve.wait_ge(both_ready, b + 1)
                    norm.stats(dve, b, both[:, b % 2, :])
                    dve.wait_ge(norm.rstd_ready, b + 1)
                    dve.tensor_scalar(both[:, b % 2, :], both[:, b % 2, :], norm.mean(b), norm.rstd(b),
                                      ALU.subtract, ALU.mult).then_inc(unit_ready, 1)

                def add_x(b):
                    dve.wait_ge(out_ready, b + 1)
                    dve.tensor_tensor(core.x[:, b, :], both[:, b % 2, :], core.x[:, b, :], ALU.add)\
                       .then_inc(x_ready, 1)

                turned.dve(dve)
                dve.wait_ge(logits_done, 1)
                for b in range(B):
                    ins = dve.max(top[:, b, :], ps[:, G_BANK, b * F3_E:(b + 1) * F3_E])
                ins.then_inc(top_ready, 1)
                dve.wait_ge(top_ready, 1)
                dve.tensor_tensor(rw[:, :], top[:, :, 0], top[:, :, 1], ALU.add).then_inc(rw_ready, 1)
                for half in range(HALVES):
                    for n in range(half * PER_HALF, (half + 1) * PER_HALF):
                        evacuate(n)
                    for b in range(half * HB, (half + 1) * HB):
                        add_side(b)
                        if b % HB >= 1:
                            add_x(b - 1)
                    add_x((half + 1) * HB - 1)

            @block.tensor
            def _(pe):
                def product(n):
                    half, kind, m = jobs[n]
                    if n >= 2:
                        if jobs[n - 2][1] in SPLIT:
                            pe.wait_ge(lo_ready, before(n - 2, SPLIT) + 1)
                        else:
                            pe.wait_ge(relu_ready, before(n - 2, ("up",)) + 1)
                    rows = slice(half * HT, (half + 1) * HT)
                    w = slice(m * P, (m + 1) * P)
                    if kind == "expert":
                        pe.wait_ge(lo_ready, F3_LC + 2 * F3_LC * half)
                    parts, count = {"fc1": (fc1, NC), "expert": (expert, F3_LC), "up": (up, NC)}[kind]
                    for c in range(count):
                        mov = ((latent[0][:, c, :], latent[1][:, c, :]) if kind == "expert"
                               else (hi[:, c, rows], lo[:, c, rows]))
                        mm = matmul_split(pe, ps[:, JOB_BANK + n % 2, :], parts[0][:, c, w], parts[1][:, c, w],
                                          *mov, c == 0, c == count - 1)
                    mm.then_inc(job_done, 1)

                def outputs(half):
                    pe.wait_ge(lo_ready, 2 * F3_LC * (half + 1))
                    for i in range(HB):
                        b = half * HB + i
                        rows = slice(i * P, (i + 1) * P)
                        if b >= 1:
                            pe.wait_ge(side_ready, b)
                        for c in range(F3_LC):
                            mm = matmul_split(pe, ps[:, SIDE_BANK, :], routed[0][:, c, rows],
                                              routed[1][:, c, rows], fc2[0][:, c, :], fc2[1][:, c, :],
                                              c == 0, c == F3_LC - 1)
                        mm.then_inc(side_done, 1)
                        if b >= 2:
                            pe.wait_ge(both_ready, b - 1)
                        if i == 0:
                            pe.wait_ge(h_lo_ready, F3_IC * (half + 1))
                        for c in range(F3_IC):
                            mm = matmul_split(pe, ps[:, MAIN_BANK + b % 2, :], h[0][:, c, rows], h[1][:, c, rows],
                                              down[0][:, c, :], down[1][:, c, :], c == 0, c == F3_IC - 1)
                        mm.then_inc(main_done, 1)

                turned.pe(pe)
                weights.wait(pe, GATE)
                pe.wait_ge(turned.lo_ready, B)
                for b in range(B):
                    rows = slice(b * P, (b + 1) * P)
                    for c in range(NC):
                        mm = matmul_split(pe, ps[:, G_BANK, b * F3_E:(b + 1) * F3_E], hi[:, c, rows],
                                          lo[:, c, rows], gate[0][:, c, :], gate[1][:, c, :],
                                          c == 0, c == NC - 1)
                mm.then_inc(logits_done, 1)
                for half in range(HALVES):
                    for n in range(half * PER_HALF, (half + 1) * PER_HALF):
                        if half == 0 and jobs[n][1] == "up" and jobs[n][2] == 0:
                            weights.wait(pe, LAST_UP)
                        product(n)
                    weights.wait(pe, LAST)
                    outputs(half)


def more_layouts(a, out, np):
    f32 = np.float32

    def rows(w):
        return w.reshape(-1, P, w.shape[1]).transpose(1, 0, 2).reshape(P, -1)

    wg = np.concatenate([a["L0_ffn_Wg"], a["L0_ffn_Sg"][None]])
    wu = np.concatenate([a["L0_ffn_Wu"], a["L0_ffn_Su"][None]])
    wd = np.concatenate([a["L0_ffn_Wd"], a["L0_ffn_Sd"][None]])
    gu = np.stack([wg, wu], 1).reshape(F0_ALL, 2, F0_I, NC, P)
    out["f0_gu"] = gu.transpose(0, 4, 3, 1, 2).reshape(F0_ALL, P, F0_GU)
    out["f0_dn"] = wd.transpose(0, 2, 1).reshape(F0_ALL, F0_IC, P, D).transpose(0, 2, 1, 3)\
        .reshape(F0_ALL, P, F0_IC * D)
    out["f0_gate"] = a["L0_ffn_gate_w"].T.reshape(NC, P, F0_E).transpose(1, 0, 2)
    out["f0_bias"] = np.broadcast_to(a["L0_ffn_bias"], (P, F0_E))
    out["f0_rank"] = np.broadcast_to(np.arange(F0_E, 0, -1, dtype=f32), (P, F0_E))

    halves = a["ctx_4096"].reshape(HALVES, HB, P, D)
    out["ctx_turned"] = np.stack([rows(h.reshape(HT, D).T) for h in halves])
    out["ctx_rows"] = halves.transpose(0, 2, 1, 3).reshape(HALVES, P, HB * D)
    out["a1_wk"], out["a1_wq"] = rows(a["L1_xattn_Wk"].T), rows(a["L1_xattn_Wq"].T)
    out["a1_bias"] = np.stack([a["L1_xattn_bk"].reshape(NC, P).T, a["L1_xattn_bq"].reshape(NC, P).T], 1)
    out["f1_w"] = a["L1_ffn_W"].reshape(NC, P, D).transpose(1, 0, 2)
    for name, key in (("f1_bias", "L1_ffn_bias"), ("f1_low", "L1_ffn_calib_min"), ("f1_high", "L1_ffn_calib_max")):
        out[name] = np.broadcast_to(a[key], (P, D))

    sel_k = np.zeros((A2_KV, A2_DH, 2, A2_PAIRS, 2, A2_SLOT), f32)
    sel_q = np.zeros((2, A2_REP, A2_DH, 2, A2_REP, 2, A2_SLOT), f32)
    for d in range(A2_DH):
        for part in range(3):
            for c in range(A2_KV):
                sel_k[c, d, int(part == 1), c // 2, c % 2, part * A2_DH + d] = 1.0
            for r in range(2):
                for m in range(A2_REP):
                    sel_q[r, m, d, int(part == 2), m, r, part * A2_DH + d] = 1.0
    out["a2_sel_k"], out["a2_sel_q"] = sel_k.reshape(P, -1), sel_q.reshape(P, -1)
    ones_row = np.zeros((2, A2_SLOT, 1), f32)
    ones_row[:, A2_MAX_ROW] = 1.0
    out["a2_ones_row"] = ones_row.reshape(P, 1)
    out["a2_wq"], out["a2_wo"] = rows(a["L2_xattn_Wq"]), rows(a["L2_xattn_Wo"])
    out["a2_wkv"] = rows(np.concatenate([a["L2_xattn_Wk"], a["L2_xattn_Wv"]], 1))

    out["f2_a"] = rows(np.concatenate([a["L2_ffn_A"].reshape(F2_HR, D), a["L2_ffn_Wr"]]).T)
    out["f2_b"] = a["L2_ffn_B"].transpose(0, 2, 1).reshape(F2_HR, D)
    out["f2_br"] = np.broadcast_to(a["L2_ffn_br"], (P, F2_H))
    for name, key in (("f3_up", "up_w"), ("f3_down", "down_w"), ("f3_fc1", "fc1_w"), ("f3_fc2", "fc2_w"),
                      ("f3_expert", "expert_w"), ("f3_gate", "gate_w")):
        out[name] = rows(a[f"L3_ffn_{key}"])
    for name in ("gamma", "beta"):
        out[f"f3_{name}"] = np.broadcast_to(a[f"L3_ffn_ln_{name}"], (P, D))


LAYERS = [l0_attention, l0_ffn, l1_attention, l1_ffn, l2_attention, l2_ffn,
          l3_attention, l3_ffn]


def build(nc, dram):
    with ExitStack() as ctx:
        core = Core(nc, ctx, dram)
        load_inputs(core)
        for layer in LAYERS:
            layer(core)
            core.retire_sems()
        store_output(core)


def laid_out(inputs):
    import numpy as np

    a = {k: np.asarray(v) for k, v in inputs.items()}
    f32 = np.float32
    out = {"x": a["x"], "ctx": a["ctx_4096"], "mask": a["mask_Bx1x4096_ff1"].reshape(B, D)}

    wq = np.zeros((P, A0_GROUPS, A0_PER_GROUP, A0_SLOT), f32)
    wk, cols = np.zeros_like(wq), np.zeros((A0_PER_GROUP, A0_SLOT, A0_COLS), f32)
    for h in range(A0_HEADS):
        g, r = divmod(h, A0_PER_GROUP)
        e = slice(h * A0_DH, (h + 1) * A0_DH)
        for part in range(3):
            rows = slice(part * A0_DH, (part + 1) * A0_DH)
            wq[:, g, r, rows] = a["L0_xattn_Wq"].T[:, e]
            wk[:, g, r, rows] = a["L0_xattn_Wk"].T[:, e]
            cols[r, rows, C_BQ + g] = a["L0_xattn_bq"][e]
            cols[r, rows, C_BK + g] = a["L0_xattn_bk"][e]
            if part == 2:
                cols[r, rows, C_SBQ + g] = a["L0_xattn_bq"][e]
    cols[:, 2 * A0_DH:3 * A0_DH, C_SELQ] = 1.0
    cols[:, A0_DH:2 * A0_DH, C_SELK] = 1.0
    cols[:, 0:3 * A0_DH, C_MASKC] = 1.0
    cols[:, A0_MAX_ROW, C_MASKA] = 1.0
    cols[:, A0_MASK_ROW, C_MASKC] = -1.0
    cols[:, A0_MASK_ROW, C_MASKA] = 1.0
    cols[:, A0_MAX_ROW, C_BK:C_BK + A0_GROUPS] = 1.0
    cols[:, A0_MASK_ROW, C_BK:C_BK + A0_GROUPS] = A0_OFF
    cols[:, A0_MASK_ROW, C_BQ:C_BQ + A0_GROUPS] = 1.0
    cols = cols.reshape(P, A0_COLS)
    cols[:, C_BO] = a["L0_xattn_bo"]
    out["a0_wq"], out["a0_wk"] = (w.reshape(P, A0_GROUPS, P) for w in (wq, wk))
    out["a0_wo"], out["a0_cols"] = a["L0_xattn_Wo"].T, cols
    out["a0_wv"] = a["L0_xattn_Wv"].T
    out["a0_bv"] = np.broadcast_to(a["L0_xattn_bv"], (P, A0_DK))
    more_layouts(a, out, np)
    return {k: np.ascontiguousarray(v) for k, v in out.items()}


def kernel(**inputs):
    import concourse.bacc as bacc
    from concourse.bass_utils import run_bass_kernel_spmd

    nc = bacc.Bacc("TRN2", target_bir_lowering=False, num_devices=1)
    arrays = {f"in_{k}": v for k, v in laid_out(inputs).items()}
    dram = {k[3:]: nc.dram_tensor(k, v.shape, mybir.dt.from_np(v.dtype), kind="ExternalInput").ap()
            for k, v in arrays.items()}
    dram["out"] = nc.dram_tensor("out", (B, P, D), F32, kind="ExternalOutput").ap()
    build(nc, dram)
    return run_bass_kernel_spmd(nc, [arrays], core_ids=[0]).results[0]["out"]
```

```python
import concourse.bass as bass
from concourse import mybir
from contextlib import ExitStack

F32 = mybir.dt.float32
F32R = mybir.dt.float32r
BF16 = mybir.dt.bfloat16
ALU = mybir.AluOpType
ACT = mybir.ActivationFunctionType
AX = mybir.AxisListType

P = 128
B = 8
D = 512
NC = D // P
T = B * P
HALVES = 2
BANK = 512
LN_EPS = 1e-5


class Core:

    def __init__(self, nc, ctx, dram):
        self.nc, self.ctx, self.dram, self.sems = nc, ctx, dram, []
        self.x = ctx.enter_context(nc.sbuf_tensor("x_res", [P, B, D], F32))
        self.ident = ctx.enter_context(nc.sbuf_tensor("ident", [P, P], F32))
        self.eps = ctx.enter_context(nc.sbuf_tensor("eps", [P, B], F32))
        self.neg_half = ctx.enter_context(nc.sbuf_tensor("neg_half", [P, B], F32))
        self.stat = ctx.enter_context(nc.sbuf_tensor("stat", [P, B, 6], F32))
        self.mv = [ctx.enter_context(nc.sbuf_tensor(f"mean_var_{i}", [P, B, 2], F32)) for i in range(2)]
        self.rs = [ctx.enter_context(nc.sbuf_tensor(f"rstd_{i}", [P, B], F32)) for i in range(2)]
        self.next = 0
        self.psum = ctx.enter_context(nc.psum_tensor("banks", [P, 8, BANK], F32))

    def sem(self, name):
        self.sems.append(self.nc.alloc_semaphore(name=name))
        return self.sems[-1]

    def mean(self, b):
        return self.mv[1 - self.next][:, b, 0:1]

    def means(self):
        return self.mv[1 - self.next][:, :, 0]

    def rstd(self, b):
        return self.rs[1 - self.next][:, b:b + 1]

    def end_layer(self):
        self.next = 1 - self.next
        self.nc.clear_and_free_semaphores(self.sems)
        self.nc.all_engine_barrier()
        self.sems = []


def sbuf(nc, scope, name, shape, dt=F32):
    return scope.enter_context(nc.sbuf_tensor(name, shape, dt))


class Norm:

    def __init__(self, core, scope, name, stat=None, mv=None, rs=None):
        self.core = core
        self.stat = sbuf(core.nc, scope, f"{name}_stat", [P, B, 6]) if stat is None else stat
        self.mv = sbuf(core.nc, scope, f"{name}_mv", [P, B, 2]) if mv is None else mv
        self.ve = sbuf(core.nc, scope, f"{name}_var_eps", [P, B])
        self.rs = sbuf(core.nc, scope, f"{name}_rstd", [P, B]) if rs is None else rs
        self.stat_ready = core.sem(f"{name}_stat_ready")
        self.mv_ready = core.sem(f"{name}_mv_ready")
        self.ve_ready = core.sem(f"{name}_ve_ready")
        self.rstd_ready = core.sem(f"{name}_rstd_ready")

    def stats(self, dve, b, src):
        dve.bn_stats(self.stat[:, b, :], src).then_inc(self.stat_ready, 1)
        dve.wait_ge(self.stat_ready, b + 1)
        dve.bn_aggr(self.mv[:, b, :], self.stat[:, b, :]).then_inc(self.mv_ready, 1)

    def scale(self, pool, b):
        pool.wait_ge(self.mv_ready, b + 1)
        pool.tensor_tensor(self.ve[:, b:b + 1], self.mv[:, b, 1:2], self.core.eps[:, 0:1],
                           ALU.add).then_inc(self.ve_ready, 1)
        pool.wait_ge(self.ve_ready, b + 1)
        pool.tensor_tensor(self.rs[:, b:b + 1], self.ve[:, b:b + 1], self.core.neg_half[:, 0:1],
                           ALU.pow).then_inc(self.rstd_ready, 1)

    def mean(self, b):
        return self.mv[:, b, 0:1]

    def rstd(self, b):
        return self.rs[:, b:b + 1]


class Ahead(Norm):

    def __init__(self, core, scope, name):
        super().__init__(core, scope, f"{name}_ahead", core.stat, core.mv[core.next], core.rs[core.next])

    def dve(self, dve, b):
        self.stats(dve, b, self.core.x[:, b, :])

    def pool(self, pool):
        for b in range(B):
            self.scale(pool, b)


def load_inputs(core):
    with ExitStack() as lay:
        load_inputs_in(core, lay)
    core.end_layer()


def load_inputs_in(core, lay):
    nc = core.nc
    ahead = Ahead(core, lay, "in")
    loaded = [core.sem(f"x_loaded_{b}") for b in range(B)]
    const_ready = core.sem("const_ready")
    with nc.Block() as block:
        @block.sync
        def _(sp):
            for b in range(B):
                sp.dma_start(core.x[:, b, :], core.dram["x"][b]).then_inc(loaded[b], 16)

        @block.vector
        def _(dve):
            for b in range(B):
                dve.wait_ge(loaded[b], 16)
                ahead.dve(dve, b)

        @block.gpsimd
        def _(pool):
            pool.memset(core.ident[:, :], 0.0).then_inc(const_ready, 1)
            pool.memset(core.eps[:, :], LN_EPS).then_inc(const_ready, 1)
            pool.memset(core.neg_half[:, :], -0.5).then_inc(const_ready, 1)
            pool.wait_ge(const_ready, 3)
            pool.affine_select(out=core.ident[:, :], in_=core.ident[:, :],
                               compare_op=ALU.not_equal, fill=1.0, base=0,
                               pattern=[[-1, P]], channel_multiplier=1)
            ahead.pool(pool)


def store_output(core):
    stored = core.sem("stored")
    with core.nc.Block() as block:
        @block.sync
        def _(sp):
            for b in range(B):
                sp.dma_start(core.dram["out"][b], core.x[:, b, :]).then_inc(stored, 16)
            sp.wait_ge(stored, 16 * B)


class NormTurned:

    def __init__(self, core, scope, name, hi, lo, bank=0):
        self.core, self.hi, self.lo, self.first_bank = core, hi, lo, bank
        self.xn = sbuf(core.nc, scope, f"{name}_turn_xn", [P, 2, D])
        self.xn_ready = core.sem(f"{name}_xn_ready")
        self.turned = core.sem(f"{name}_turned")
        self.hi_ready = core.sem(f"{name}_turned_hi_ready")
        self.lo_ready = core.sem(f"{name}_turned_lo_ready")

    def tile(self, part, b):
        return part[:, :, b * P:(b + 1) * P]

    def bank(self, b):
        return self.core.psum[:, self.first_bank + b % 2, :].rearrange("p (c t) -> p c t", c=NC)

    def act(self, act, batches=range(B)):
        for b in batches:
            act.wait_ge(self.turned, b + 1)
            act.copy(self.tile(self.hi, b), self.bank(b)).then_inc(self.hi_ready, 1)

    def pe(self, pe, batches=range(B)):
        for b in batches:
            pe.wait_ge(self.xn_ready, b + 1)
            if b >= 2:
                pe.wait_ge(self.lo_ready, b - 1)
            for c in range(NC):
                mm = pe.transpose(self.core.psum[:, self.first_bank + b % 2, c * P:(c + 1) * P],
                                  self.xn[:, b % 2, c * P:(c + 1) * P], self.core.ident[:, :])
            mm.then_inc(self.turned, 1)

    def dve(self, dve, batches=range(B)):
        for b in batches:
            if b >= 2:
                dve.wait_ge(self.turned, b - 1)
            dve.tensor_scalar(self.xn[:, b % 2, :], self.core.x[:, b, :], self.core.mean(b),
                              self.core.rstd(b), ALU.subtract, ALU.mult)\
               .then_inc(self.xn_ready, 1)
            if b >= 1:
                self.rest(dve, b - 1)
            if b == B - 1:
                self.rest(dve, b)

    def rest(self, dve, b):
        dve.wait_ge(self.hi_ready, b + 1)
        dve.tensor_tensor(self.tile(self.lo, b), self.bank(b), self.tile(self.hi, b).bitcast(F32),
                          ALU.subtract).then_inc(self.lo_ready, 1)


RAW = 2048


class Weights:

    def __init__(self, core, scope, name, pieces, size=RAW):
        self.pieces = pieces
        self.raw = sbuf(core.nc, scope, f"{name}_raw", [P, 2, size])
        self.loaded = [core.sem(f"{name}_loaded_{i}") for i in range(2)]
        self.hi_ready = core.sem(f"{name}_w_hi_ready")
        self.lo_ready = core.sem(f"{name}_w_lo_ready")

    def load(self, sp):
        for i, (src, _, _) in enumerate(self.pieces):
            if i >= 2:
                sp.wait_ge(self.lo_ready, i - 1)
            sp.dma_start(self.raw[:, i % 2, 0:src.shape[1]], src).then_inc(self.loaded[i % 2], 16)

    def split_hi(self, act, pieces=None):
        for i in range(len(self.pieces)) if pieces is None else pieces:
            src, hi, _ = self.pieces[i]
            act.wait_ge(self.loaded[i % 2], 16 * (i // 2 + 1))
            act.copy(hi, self.raw[:, i % 2, 0:src.shape[1]]).then_inc(self.hi_ready, 1)

    def split_lo(self, pool, pieces=None):
        for i in range(len(self.pieces)) if pieces is None else pieces:
            src, hi, lo = self.pieces[i]
            pool.wait_ge(self.hi_ready, i + 1)
            if lo is None:
                if i:
                    pool.wait_ge(self.lo_ready, i)
                pool.sem_inc(self.lo_ready, 1)
            else:
                pool.tensor_tensor(lo, self.raw[:, i % 2, 0:src.shape[1]], hi.bitcast(F32),
                                   ALU.subtract).then_inc(self.lo_ready, 1)

    def wait(self, pe, i):
        pe.wait_ge(self.lo_ready, i + 1)


def matmul_split(pe, out, w_hi, w_lo, m_hi, m_lo, start, stop):
    pe.matmul(out, w_hi, m_hi, start=start, stop=False)
    pe.matmul(out, w_hi, m_lo, start=False, stop=False)
    return pe.matmul(out, w_lo, m_hi, start=False, stop=stop)


A0_WIN, A0_HEADS, A0_DH = 128, 8, 8
A0_DK = A0_HEADS * A0_DH
A0_SLOT, A0_GROUPS = 32, 2
A0_PER_GROUP = A0_HEADS // A0_GROUPS
A0_WINS = D // A0_WIN
A0_MAX_ROW, A0_MASK_ROW = 24, 25
A0_OFF = -float(2 ** 31)
C_SELQ, C_SELK, C_MASKC, C_MASKA, C_BO = 0, 1, 2, 3, 4
C_BQ, C_SBQ, C_BK = 5, 7, 9
A0_COLS = 11


def l0_attention(core):
    nc, dram, ps = core.nc, core.dram, core.psum
    scale = float(A0_DH) ** -0.5
    with ExitStack() as lay:
        on_all = sbuf(nc, lay, "a0_on_all", [P, B, A0_WINS, A0_DK])
        wo = sbuf(nc, lay, "a0_wo", [A0_DK, P])
        out_mask = sbuf(nc, lay, "a0_out_mask", [P, B, D])
        gl = sbuf(nc, lay, "a0_gelu", [A0_DK, 2, D])
        tmp = sbuf(nc, lay, "a0_tmp", [P, 2, D])
        cols = sbuf(nc, lay, "a0_cols", [P, A0_COLS])
        loaded = core.sem("a0_loaded")
        ctx_loaded = [core.sem(f"a0_ctx_loaded_{h}") for h in range(HALVES)]
        mask_loaded = [core.sem(f"a0_mask_loaded_{h}") for h in range(HALVES)]
        out_mask_loaded = core.sem("a0_out_mask_loaded")
        with ExitStack() as part:
            wq = sbuf(nc, part, "a0_wq", [P, A0_GROUPS, P])
            wk = sbuf(nc, part, "a0_wk", [P, A0_GROUPS, P])
            wv = sbuf(nc, part, "a0_wv", [P, A0_DK])
            bv = sbuf(nc, part, "a0_bv", [P, A0_DK])
            ctx = sbuf(nc, part, "a0_ctx", [P, B, D])
            mask = sbuf(nc, part, "a0_mask", [P, B, D])
            xn = sbuf(nc, part, "a0_xn", [P, 2, D])
            q_lo = sbuf(nc, part, "a0_q_sel", [P, D], F32R)
            q = sbuf(nc, part, "a0_q", [P, 2, D], F32R)
            kf = sbuf(nc, part, "a0_kf", [P, 2, D])
            k_hi = sbuf(nc, part, "a0_k_sel", [P, 2, D], F32R)
            k = sbuf(nc, part, "a0_k", [P, 2, D], F32R)
            v = sbuf(nc, part, "a0_v", [P, 2, A0_WINS, A0_HEADS, A0_SLOT])
            mx = sbuf(nc, part, "a0_mx", [P, A0_WINS, P])
            e = sbuf(nc, part, "a0_e", [P, 2, A0_PER_GROUP, D])
            osb = sbuf(nc, part, "a0_osb", [P, 2, D])
            rec = sbuf(nc, part, "a0_rec", [P, A0_WINS, A0_PER_GROUP])
            ahead = Ahead(core, part, "a0")
            zeroed = core.sem("a0_zeroed")
            xn_ready = core.sem("a0_xn_ready")
            mask_ready = core.sem("a0_mask_ready")
            proj_done = core.sem("a0_proj_done")
            v_done = core.sem("a0_v_done")
            q_sel_ready = core.sem("a0_q_sel_ready")
            q_ready = core.sem("a0_q_ready")
            kf_ready = core.sem("a0_kf_ready")
            k_sel_ready = core.sem("a0_k_sel_ready")
            k_ready = core.sem("a0_k_ready")
            v_ready = core.sem("a0_v_ready")
            scores_done = core.sem("a0_scores_done")
            max_ready = core.sem("a0_max_ready")
            max_turned = core.sem("a0_max_turned")
            q_max_ready = core.sem("a0_q_max_ready")
            keyed_done = core.sem("a0_keyed_done")
            exp_ready = core.sem("a0_exp_ready")
            pv_done = core.sem("a0_pv_done")
            o_ready = core.sem("a0_o_ready")
            o_turned = core.sem("a0_o_turned")
            rec_ready = core.sem("a0_rec_ready")
            on_ready = core.sem("a0_on_ready")
            on_turned = core.sem("a0_on_turned")
            gelu_ready = core.sem("a0_gelu_ready")
            out_done = core.sem("a0_out_done")
            tmp_ready = core.sem("a0_tmp_ready")
            x_ready = core.sem("a0_x_ready")
            Q_BANK, K_BANK, V_BANK, M_BANK, S_BANK = 0, 1, 2, 3, 4
            GELU_BANK, OUT_BANK = 4, 6
            UNITS = B * A0_GROUPS

            def turned_o():
                return ps[:, M_BANK, :].rearrange("p (w r s) -> p w r s", w=A0_WINS, r=A0_PER_GROUP)

            with nc.Block() as block:
                @block.sync
                def _(sp):
                    for dst, name in ((wq, "a0_wq"), (wk, "a0_wk")):
                        sp.dma_start(dst[:, :, :], dram[name]).then_inc(loaded, 16)
                    for dst, name in ((cols, "a0_cols"), (wv, "a0_wv"), (bv, "a0_bv"), (wo, "a0_wo")):
                        sp.dma_start(dst[:, :], dram[name]).then_inc(loaded, 16)
                    for h in range(HALVES):
                        part_b = slice(h * B // HALVES, (h + 1) * B // HALVES)
                        sp.dma_start(mask[:, part_b, :], dram["mask"][part_b].partition_broadcast(P))\
                          .then_inc(mask_loaded[h], 16)
                        sp.dma_start(ctx[:, part_b, :], dram["ctx"][part_b].rearrange("b p s -> p b s"))\
                          .then_inc(ctx_loaded[h], 16)
                    sp.dma_start(out_mask[:, :, :], dram["mask"].partition_broadcast(P))\
                      .then_inc(out_mask_loaded, 16)

                @block.gpsimd
                def _(pool):
                    for i in range(2):
                        pool.memset(v[:, i, :, :, :], 0.0)
                    pool.memset(mx[:, :, :], 0.0).then_inc(zeroed, 1)
                    pool.wait_ge(zeroed, 1)
                    for i in range(2):
                        pool.memset(v[:, i, :, :, A0_DH:A0_DH + 1], 1.0).then_inc(zeroed, 1)
                    pool.wait_ge(loaded, 16 * 6)
                    for b in range(B):
                        pool.wait_ge(mask_loaded[b * HALVES // B], 16)
                        pool.tensor_scalar(mask[:, b, :], mask[:, b, :], 0.0,
                                           cols[:, C_MASKC:C_MASKC + 1], ALU.is_gt,
                                           ALU.mult).then_inc(mask_ready, 1)
                        pool.wait_ge(mask_ready, 2 * b + 1)
                        pool.tensor_scalar(mask[:, b, :], mask[:, b, :],
                                           cols[:, C_MASKA:C_MASKA + 1], None,
                                           ALU.add).then_inc(mask_ready, 1)
                        for g in range(A0_GROUPS):
                            u = A0_GROUPS * b + g
                            pool.wait_ge(k_sel_ready, u + 1)
                            if u >= 2:
                                pool.wait_ge(keyed_done, u - 1)
                            pool.tensor_tensor(k[:, u % 2, :], kf[:, u % 2, :],
                                               k_hi[:, u % 2, :].bitcast(F32),
                                               ALU.subtract).then_inc(k_ready, 1)
                    ahead.pool(pool)

                @block.scalar
                def _(act):
                    act.wait_ge(loaded, 16 * 6)

                    def split(u):
                        g = u % A0_GROUPS
                        act.wait_ge(proj_done, u + 1)
                        if u >= 1:
                            act.wait_ge(q_ready, u)
                        act.activation(q_lo[:, :], ps[:, Q_BANK, :], ACT.Identity,
                                       bias=cols[:, C_SBQ + g:C_SBQ + g + 1],
                                       scale=cols[:, C_SELQ:C_SELQ + 1]).then_inc(q_sel_ready, 1)
                        act.wait_ge(kf_ready, u + 1)
                        if u >= 2:
                            act.wait_ge(k_ready, u - 1)
                        act.activation(k_hi[:, u % 2, :], kf[:, u % 2, :], ACT.Copy,
                                       scale=cols[:, C_SELK:C_SELK + 1]).then_inc(k_sel_ready, 1)

                    def take_out(u):
                        act.wait_ge(pv_done, u + 1)
                        if u >= 2:
                            act.wait_ge(o_turned, u - 1)
                        act.copy(osb[:, u % 2, :], ps[:, V_BANK, :]).then_inc(o_ready, 1)

                    split(0)
                    for u in range(UNITS):
                        if u + 1 < UNITS:
                            split(u + 1)
                        act.wait_ge(keyed_done, u + 1)
                        if u >= 2:
                            act.wait_ge(pv_done, u - 1)
                        act.activation(e[:, u % 2, :, :], ps[:, S_BANK:S_BANK + A0_PER_GROUP, :],
                                       ACT.Exp, scale=scale).then_inc(exp_ready, 1)
                        if u >= 1:
                            take_out(u - 1)
                    take_out(UNITS - 1)
                    for b in range(B):
                        act.wait_ge(on_turned, b + 1)
                        if b >= 2:
                            act.wait_ge(out_done, b - 1)
                        act.activation(gl[:, b % 2, :], ps[0:A0_DK, GELU_BANK + b % 2, :], ACT.Gelu)\
                           .then_inc(gelu_ready, 1)

                @block.vector
                def _(dve):
                    def normalise(b):
                        if b >= 2:
                            dve.wait_ge(proj_done, A0_GROUPS * (b - 1))
                        dve.tensor_scalar(xn[:, b % 2, :], core.x[:, b, :], core.mean(b),
                                          core.rstd(b), ALU.subtract, ALU.mult).then_inc(xn_ready, 1)

                    def stack(u):
                        b, g = divmod(u, A0_GROUPS)
                        dve.wait_ge(proj_done, u + 1)
                        dve.wait_ge(mask_ready, 2 * b + 2)
                        if u >= 2:
                            dve.wait_ge(k_ready, u - 1)
                        dve.scalar_tensor_tensor(out=kf[:, u % 2, :], in0=ps[:, K_BANK, :],
                                                 scalar=cols[:, C_BK + g:C_BK + g + 1],
                                                 in1=mask[:, b, :], op0=ALU.add,
                                                 op1=ALU.mult).then_inc(kf_ready, 1)
                        dve.wait_ge(q_sel_ready, u + 1)
                        if u >= 2:
                            dve.wait_ge(keyed_done, u - 1)
                        dve.scalar_tensor_tensor(out=q[:, u % 2, :], in0=ps[:, Q_BANK, :],
                                                 scalar=cols[:, C_BQ + g:C_BQ + g + 1],
                                                 in1=q_lo[:, :].bitcast(F32), op0=ALU.add,
                                                 op1=ALU.subtract).then_inc(q_ready, 1)

                    def values_biased(b):
                        dve.wait_ge(v_done, b + 1)
                        dve.wait_ge(zeroed, 3)
                        if b >= 2:
                            dve.wait_ge(pv_done, A0_GROUPS * (b - 1))
                        dve.tensor_tensor(
                            v[:, b % 2, :, :, 0:A0_DH],
                            ps[:, V_BANK, 0:A0_WINS * A0_DK].rearrange(
                                "p (w h d) -> p w h d", w=A0_WINS, h=A0_HEADS),
                            bv[:, :].rearrange("p (h d) -> p h d", h=A0_HEADS).unsqueeze(1)
                            .broadcast_to([P, A0_WINS, A0_HEADS, A0_DH]),
                            ALU.add).then_inc(v_ready, 1)

                    def divide(u):
                        b, g = divmod(u, A0_GROUPS)
                        dve.wait_ge(o_turned, u + 1)
                        dve.reciprocal(rec[:, :, :], turned_o()[:, :, :, A0_DH]).then_inc(rec_ready, 1)
                        dve.wait_ge(rec_ready, u + 1)
                        dve.tensor_tensor(
                            on_all[:, b, :, :].rearrange("p w (h d) -> p w h d", h=A0_HEADS)
                            [:, :, A0_PER_GROUP * g:A0_PER_GROUP * (g + 1), :],
                            turned_o()[:, :, :, 0:A0_DH],
                            rec[:, :, :].unsqueeze(3).broadcast_to([P, A0_WINS, A0_PER_GROUP, A0_DH]),
                            ALU.mult).then_inc(on_ready, 1)

                    normalise(0)
                    dve.wait_ge(loaded, 16 * 6)
                    stack(0)
                    for u in range(UNITS):
                        b, g = divmod(u, A0_GROUPS)
                        dve.wait_ge(scores_done, u + 1)
                        dve.tensor_reduce(
                            mx[:, :, A0_MAX_ROW:P:A0_SLOT].rearrange("p w r -> p r w"),
                            ps[:, S_BANK:S_BANK + A0_PER_GROUP, :].rearrange(
                                "p r (w j) -> p r w j", w=A0_WINS),
                            AX.X, ALU.max, negate=True).then_inc(max_ready, 1)
                        dve.wait_ge(max_turned, u + 1)
                        dve.wait_ge(q_ready, u + 1)
                        dve.tensor_tensor(q[:, u % 2, :], ps[:, M_BANK, :],
                                          q[:, u % 2, :].bitcast(F32), ALU.add)\
                           .then_inc(q_max_ready, 1)
                        if u + 1 < UNITS:
                            stack(u + 1)
                        if g == 0:
                            values_biased(b)
                        if g == 0 and b + 1 < B:
                            normalise(b + 1)
                        if u >= 2:
                            divide(u - 2)
                    divide(UNITS - 2)
                    divide(UNITS - 1)
                    dve.wait_ge(out_mask_loaded, 16)
                    for b in range(B):
                        dve.wait_ge(out_done, b + 1)
                        dve.scalar_tensor_tensor(out=tmp[:, b % 2, :], in0=ps[:, OUT_BANK + b % 2, :],
                                                 scalar=cols[:, C_BO:C_BO + 1], in1=out_mask[:, b, :],
                                                 op0=ALU.add, op1=ALU.mult).then_inc(tmp_ready, 1)
                        dve.wait_ge(tmp_ready, b + 1)
                        dve.tensor_tensor(core.x[:, b, :], core.x[:, b, :], tmp[:, b % 2, :],
                                          ALU.add).then_inc(x_ready, 1)
                        dve.wait_ge(x_ready, b + 1)
                        ahead.dve(dve, b)

                @block.tensor
                def _(pe):
                    def project(u):
                        b, g = divmod(u, A0_GROUPS)
                        pe.wait_ge(xn_ready, b + 1)
                        if u >= 1:
                            pe.wait_ge(q_ready, u)
                            pe.wait_ge(kf_ready, u)
                        pe.matmul(ps[:, K_BANK, :], wk[:, g, :], xn[:, b % 2, :], start=True, stop=True)
                        pe.matmul(ps[:, Q_BANK, :], wq[:, g, :], xn[:, b % 2, :], start=True,
                                  stop=True).then_inc(proj_done, 1)

                    def project_values(b):
                        pe.wait_ge(ctx_loaded[b * HALVES // B], 16)
                        if b >= 1:
                            pe.wait_ge(o_ready, A0_GROUPS * b - 1)
                        for w in range(A0_WINS):
                            mm = pe.matmul(ps[:, V_BANK, w * A0_DK:(w + 1) * A0_DK],
                                           ctx[:, b, w * A0_WIN:(w + 1) * A0_WIN], wv[:, :],
                                           start=True, stop=True)
                        mm.then_inc(v_done, 1)

                    def scores(u):
                        pe.wait_ge(q_ready, u + 1)
                        pe.wait_ge(k_ready, u + 1)
                        if u >= 1:
                            pe.wait_ge(exp_ready, u)
                        for w in range(A0_WINS):
                            for r in range(A0_PER_GROUP):
                                rows = slice(A0_SLOT * r, A0_SLOT * (r + 1))
                                win = slice(w * A0_WIN, (w + 1) * A0_WIN)
                                mm = pe.matmul(ps[:, S_BANK + r, win], q[rows, u % 2, win],
                                               k[rows, u % 2, win], start=True, stop=True)
                        mm.then_inc(scores_done, 1)

                    def turn_max(u):
                        pe.wait_ge(max_ready, u + 1)
                        if u >= 3:
                            pe.wait_ge(on_ready, u - 2)
                        for w in range(A0_WINS):
                            mm = pe.transpose(ps[:, M_BANK, w * A0_WIN:(w + 1) * A0_WIN],
                                              mx[:, w, :], core.ident[:, :])
                        mm.then_inc(max_turned, 1)

                    def keyed(u):
                        pe.wait_ge(q_max_ready, u + 1)
                        for w in range(A0_WINS):
                            for r in range(A0_PER_GROUP):
                                rows = slice(A0_SLOT * r, A0_SLOT * (r + 1))
                                win = slice(w * A0_WIN, (w + 1) * A0_WIN)
                                mm = pe.matmul(ps[:, S_BANK + r, win], k[rows, u % 2, win],
                                               q[rows, u % 2, win], start=True, stop=True)
                        mm.then_inc(keyed_done, 1)

                    def values(u):
                        b, g = divmod(u, A0_GROUPS)
                        pe.wait_ge(exp_ready, u + 1)
                        pe.wait_ge(v_ready, b + 1)
                        if u >= 1:
                            pe.wait_ge(o_ready, u)
                        if u % A0_GROUPS == 1 and b + 1 < B:
                            pe.wait_ge(v_ready, b + 2)
                        for w in range(A0_WINS):
                            for r in range(A0_PER_GROUP):
                                win = slice(w * A0_WIN, (w + 1) * A0_WIN)
                                mm = pe.matmul(ps[A0_SLOT * r:A0_SLOT * (r + 1), V_BANK, win],
                                               v[:, b % 2, w, A0_PER_GROUP * g + r, :],
                                               e[:, u % 2, r, win], start=True, stop=True)
                        mm.then_inc(pv_done, 1)

                    def turn_outputs(u):
                        pe.wait_ge(o_ready, u + 1)
                        if u >= 1:
                            pe.wait_ge(on_ready, u)
                        for w in range(A0_WINS):
                            mm = pe.transpose(ps[:, M_BANK, w * A0_WIN:(w + 1) * A0_WIN],
                                              osb[:, u % 2, w * A0_WIN:(w + 1) * A0_WIN], core.ident[:, :])
                        mm.then_inc(o_turned, 1)

                    def turn_back(b):
                        pe.wait_ge(on_ready, A0_GROUPS * (b + 1))
                        if b >= 2:
                            pe.wait_ge(gelu_ready, b - 1)
                        for w in range(A0_WINS):
                            mm = pe.transpose(ps[0:A0_DK, GELU_BANK + b % 2, w * A0_WIN:(w + 1) * A0_WIN],
                                              on_all[:, b, w, :], core.ident[:, :])
                        mm.then_inc(on_turned, 1)

                    def project_out(b):
                        pe.wait_ge(gelu_ready, b + 1)
                        if b >= 2:
                            pe.wait_ge(tmp_ready, b - 1)
                        pe.matmul(ps[:, OUT_BANK + b % 2, :], wo[:, :], gl[:, b % 2, :], start=True,
                                  stop=True).then_inc(out_done, 1)

                    pe.wait_ge(loaded, 16 * 6)
                    project(0)
                    for u in range(UNITS):
                        scores(u)
                        if u + 1 < UNITS:
                            project(u + 1)
                        if u % A0_GROUPS == 0:
                            project_values(u // A0_GROUPS)
                        turn_max(u)
                        keyed(u)
                        if u >= 2:
                            turn_outputs(u - 2)
                        if u >= 1:
                            values(u - 1)
                    turn_outputs(UNITS - 2)
                    values(UNITS - 1)
                    turn_outputs(UNITS - 1)
                    turn_back(0)
                    for b in range(B):
                        if b + 1 < B:
                            turn_back(b + 1)
                        project_out(b)


F0_E, F0_TOPK, F0_I = 16, 4, 256
F0_ALL = F0_E + 1
F0_IC = F0_I // P
F0_HALF = T // 2
F0_GU = NC * 2 * F0_I
F0_JOBS = 2 * F0_IC
FIRST, LAST = 0, F0_ALL - 1
TAKEN = -1e30


def l0_ffn(core):
    nc, dram, ps = core.nc, core.dram, core.psum
    with ExitStack() as lay:
        hi = sbuf(nc, lay, "f0_xn_hi", [P, NC, T], F32R)
        lo = sbuf(nc, lay, "f0_xn_lo", [P, NC, T], F32R)
        weight = sbuf(nc, lay, "f0_weight", [P, B, F0_ALL])
        turned = NormTurned(core, lay, "f0", hi, lo, bank=4)
        ahead = Ahead(core, lay, "f0")
        gate = sbuf(nc, lay, "f0_gate", [P, NC, F0_E])
        gate_hi = sbuf(nc, lay, "f0_gate_hi", [P, NC, F0_E], F32R)
        gate_lo = sbuf(nc, lay, "f0_gate_lo", [P, NC, F0_E], F32R)
        bias = sbuf(nc, lay, "f0_bias", [P, F0_E])
        rank = sbuf(nc, lay, "f0_rank", [P, F0_E])
        score = sbuf(nc, lay, "f0_score", [P, B, F0_E])
        left = sbuf(nc, lay, "f0_left", [P, B, F0_E])
        pick = sbuf(nc, lay, "f0_pick", [P, B, F0_E])
        chosen = sbuf(nc, lay, "f0_chosen", [P, B, F0_E])
        top = sbuf(nc, lay, "f0_top", [P, B])
        gu = sbuf(nc, lay, "f0_gu", [P, F0_GU])
        gu_hi = sbuf(nc, lay, "f0_gu_hi", [P, NC, 2, F0_I], F32R)
        gu_lo = sbuf(nc, lay, "f0_gu_lo", [P, NC, 2, F0_I], F32R)
        dn = sbuf(nc, lay, "f0_dn", [P, F0_IC * D])
        dn_hi = sbuf(nc, lay, "f0_dn_hi", [P, F0_IC, D], F32R)
        dn_lo = sbuf(nc, lay, "f0_dn_lo", [P, F0_IC, D], F32R)
        sil = sbuf(nc, lay, "f0_sil", [P, 2, F0_HALF])
        z = sbuf(nc, lay, "f0_z", [P, 2, F0_HALF])
        z_hi = sbuf(nc, lay, "f0_z_hi", [P, F0_IC, T], F32R)
        z_lo = sbuf(nc, lay, "f0_z_lo", [P, F0_IC, T], F32R)
        loaded = core.sem("f0_gate_loaded")
        gate_hi_ready = core.sem("f0_gate_hi_ready")
        gate_lo_ready = core.sem("f0_gate_lo_ready")
        logits_done = core.sem("f0_logits_done")
        sigmoid_ready = core.sem("f0_sigmoid_ready")
        step = core.sem("f0_route_step")
        gu_loaded, dn_loaded = core.sem("f0_gu_loaded"), core.sem("f0_dn_loaded")
        gu_hi_ready, gu_lo_ready = core.sem("f0_gu_hi_ready"), core.sem("f0_gu_lo_ready")
        dn_hi_ready, dn_lo_ready = core.sem("f0_dn_hi_ready"), core.sem("f0_dn_lo_ready")
        gu_done = core.sem("f0_gu_done")
        sil_ready, z_ready = core.sem("f0_sil_ready"), core.sem("f0_z_ready")
        z_hi_ready, z_lo_ready = core.sem("f0_z_hi_ready"), core.sem("f0_z_lo_ready")
        y_done = core.sem("f0_y_done")
        y_added = core.sem("f0_y_added")
        Y_BANK, Y_BANKS, LOGITS = 4, 4, 7

        def flat(w):
            return w[:, :, :, :].rearrange("p c g i -> p (c g i)")

        def flat_dn(w):
            return w[:, :, :].rearrange("p c n -> p (c n)")

        def job_place(j):
            half, ic = divmod(j, F0_IC)
            return ic, slice(half * F0_HALF, (half + 1) * F0_HALF)

        with nc.Block() as block:
            @block.sync
            def _(sp):
                def load(e):
                    if e is not FIRST:
                        sp.wait_ge(gu_lo_ready, e)
                    sp.dma_start(gu[:, :], dram["f0_gu"][bass.ds(e, 1)].rearrange("e p n -> p (e n)"))\
                      .then_inc(gu_loaded, 16)
                    if e is not FIRST:
                        sp.wait_ge(dn_lo_ready, e)
                    sp.dma_start(dn[:, :], dram["f0_dn"][bass.ds(e, 1)].rearrange("e p n -> p (e n)"))\
                      .then_inc(dn_loaded, 16)

                sp.dma_start(gate[:, :, :], dram["f0_gate"]).then_inc(loaded, 16)
                sp.dma_start(bias[:, :], dram["f0_bias"]).then_inc(loaded, 16)
                sp.dma_start(rank[:, :], dram["f0_rank"]).then_inc(loaded, 16)
                load(FIRST)
                with sp.Fori(1, F0_ALL) as e:
                    load(e)

            @block.scalar
            def _(act):
                def gu_split(e):
                    act.wait_ge(gu_loaded, 16 * e + 16)
                    if e is not FIRST:
                        act.wait_ge(gu_done, F0_JOBS * e)
                    act.copy(flat(gu_hi), gu[:, :]).then_inc(gu_hi_ready, 1)

                def job(e, j):
                    ic, cols = job_place(j)
                    act.wait_ge(gu_done, F0_JOBS * e + (j + 1))
                    if j >= 2:
                        act.wait_ge(z_ready, F0_JOBS * e + (j - 1))
                    act.activation(sil[:, j % 2, :], ps[:, 2 * (j % 2), :], ACT.Silu)\
                       .then_inc(sil_ready, 1)
                    if j == 0:
                        act.wait_ge(dn_loaded, 16 * e + 16)
                        act.copy(flat_dn(dn_hi), dn[:, :]).then_inc(dn_hi_ready, 1)
                    act.wait_ge(z_ready, F0_JOBS * e + (j + 1))
                    act.copy(z_hi[:, ic, cols], z[:, j % 2, :]).then_inc(z_hi_ready, 1)

                def expert(e):
                    gu_split(e)
                    for j in range(F0_JOBS):
                        job(e, j)

                gu_split(FIRST)
                turned.act(act, range(0, 2))
                act.wait_ge(loaded, 48)
                act.copy(gate_hi[:, :, :], gate[:, :, :]).then_inc(gate_hi_ready, 1)
                turned.act(act, range(2, HB))
                job(FIRST, 0)
                job(FIRST, 1)
                turned.act(act, range(HB, B))
                act.wait_ge(logits_done, 1)
                act.activation(left[:, :, :], ps[:, LOGITS, 0:B * F0_E].rearrange(
                    "p (b e) -> p b e", b=B), ACT.Sigmoid).then_inc(sigmoid_ready, 1)
                job(FIRST, 2)
                job(FIRST, 3)
                with act.Fori(1, F0_ALL) as e:
                    expert(e)

            @block.gpsimd
            def _(pool):
                def expert(e):
                    pool.wait_ge(gu_hi_ready, e + 1)
                    pool.tensor_tensor(flat(gu_lo), gu[:, :], flat(gu_hi).bitcast(F32),
                                       ALU.subtract).then_inc(gu_lo_ready, 1)
                    for j in range(F0_JOBS):
                        ic, cols = job_place(j)
                        pool.wait_ge(z_hi_ready, F0_JOBS * e + (j + 1))
                        pool.tensor_tensor(z_lo[:, ic, cols], z[:, j % 2, :],
                                           z_hi[:, ic, cols].bitcast(F32),
                                           ALU.subtract).then_inc(z_lo_ready, 1)
                        if j == 0:
                            pool.wait_ge(dn_hi_ready, e + 1)
                            pool.tensor_tensor(flat_dn(dn_lo), dn[:, :], flat_dn(dn_hi).bitcast(F32),
                                               ALU.subtract).then_inc(dn_lo_ready, 1)

                expert(FIRST)
                with pool.Fori(1, F0_ALL) as e:
                    expert(e)
                ahead.pool(pool)

            @block.vector
            def _(dve):
                def gated(e, j):
                    dve.wait_ge(sil_ready, F0_JOBS * e + (j + 1))
                    if j >= 2:
                        dve.wait_ge(z_lo_ready, F0_JOBS * e + (j - 1))
                    dve.tensor_tensor(z[:, j % 2, :], sil[:, j % 2, :], ps[:, 2 * (j % 2) + 1, :],
                                      ALU.mult).then_inc(z_ready, 1)

                def add(e, b):
                    dve.wait_ge(y_done, B * e + (b + 1))
                    dve.scalar_tensor_tensor(out=core.x[:, b, :], in0=ps[:, Y_BANK + b % Y_BANKS, :],
                                             scalar=weight[:, b, bass.ds(e, 1)], in1=core.x[:, b, :],
                                             op0=ALU.mult, op1=ALU.add).then_inc(y_added, 1)

                steps = 0

                def after(instruction):
                    nonlocal steps
                    steps += 1
                    instruction.then_inc(step, 1)
                    dve.wait_ge(step, steps)

                def by_expert(row):
                    return row[:, :].unsqueeze(1).broadcast_to([P, B, F0_E])

                def by_batch(col):
                    return col[:, :].unsqueeze(2).broadcast_to([P, B, F0_E])

                def biased():
                    dve.wait_ge(sigmoid_ready, 1)
                    after(dve.tensor_tensor(score[:, :, :], left[:, :, :], by_expert(bias), ALU.add))
                    after(dve.tensor_copy(left[:, :, :], score[:, :, :]))

                def choose(k):
                    after(dve.tensor_reduce(top[:, :], left[:, :, :], AX.X, ALU.max))
                    after(dve.tensor_tensor(pick[:, :, :], left[:, :, :], by_batch(top), ALU.is_equal))
                    after(dve.tensor_tensor(pick[:, :, :], pick[:, :, :], by_expert(rank), ALU.mult))
                    after(dve.tensor_reduce(top[:, :], pick[:, :, :], AX.X, ALU.max))
                    after(dve.tensor_tensor(pick[:, :, :], by_expert(rank), by_batch(top), ALU.is_equal))
                    after(dve.scalar_tensor_tensor(out=left[:, :, :], in0=pick[:, :, :], scalar=TAKEN,
                                                   in1=left[:, :, :], op0=ALU.mult, op1=ALU.add))
                    if k == 0:
                        after(dve.tensor_copy(chosen[:, :, :], pick[:, :, :]))
                    else:
                        after(dve.tensor_tensor(chosen[:, :, :], chosen[:, :, :], pick[:, :, :], ALU.add))

                def weigh():
                    after(dve.tensor_tensor(score[:, :, :], score[:, :, :], chosen[:, :, :], ALU.mult))
                    after(dve.tensor_reduce(top[:, :], score[:, :, :], AX.X, ALU.add))
                    after(dve.tensor_scalar(top[:, :], top[:, :], 1e-20, None, ALU.add))
                    after(dve.reciprocal(top[:, :], top[:, :]))
                    after(dve.tensor_tensor(weight[:, :, 1:], score[:, :, :], by_batch(top), ALU.mult))

                turned.dve(dve, range(0, HB + 1))
                dve.wait_ge(gate_hi_ready, 1)
                dve.tensor_tensor(gate_lo[:, :, :], gate[:, :, :], gate_hi[:, :, :].bitcast(F32),
                                  ALU.subtract).then_inc(gate_lo_ready, 1)
                after(dve.memset(weight[:, :, 0:1], 1.0))
                dve.wait_ge(loaded, 48)
                gated(FIRST, 0)
                gated(FIRST, 1)
                turned.dve(dve, range(HB + 1, B))
                biased()
                choose(0)
                gated(FIRST, 2)
                choose(1)
                gated(FIRST, 3)
                for b in range(B):
                    add(FIRST, b)
                    if b % HB == HB - 1:
                        choose(2 + b // HB)
                weigh()
                with dve.Fori(1, F0_ALL - 1) as e:
                    for j in range(F0_JOBS):
                        gated(e, j)
                    for b in range(B):
                        add(e, b)
                for j in range(F0_JOBS):
                    gated(LAST, j)
                for b in range(B):
                    add(LAST, b)
                    dve.wait_ge(y_added, B * LAST + b + 1)
                    ahead.dve(dve, b)

            @block.tensor
            def _(pe):
                def job(e, j):
                    ic, cols = job_place(j)
                    if j >= 2:
                        pe.wait_ge(z_ready, F0_JOBS * e + (j - 1))
                    for n in range(2):
                        out = ps[:, 2 * (j % 2) + n, :]
                        w = slice(ic * P, (ic + 1) * P)
                        for c in range(NC):
                            mm = matmul_split(pe, out, gu_hi[:, c, n, w], gu_lo[:, c, n, w],
                                              hi[:, c, cols], lo[:, c, cols], c == 0, c == NC - 1)
                    mm.then_inc(gu_done, 1)

                def down(e):
                    if e is not FIRST:
                        pe.wait_ge(y_added, B * e)
                    pe.wait_ge(dn_lo_ready, e + 1)
                    for b in range(B):
                        if b % (B // 2) == 0:
                            pe.wait_ge(z_lo_ready, F0_JOBS * e + F0_IC * (b // (B // 2) + 1))
                        if b >= Y_BANKS:
                            pe.wait_ge(y_added, B * e + (b - Y_BANKS + 1))
                        rows = slice(b * P, (b + 1) * P)
                        for ic in range(F0_IC):
                            mm = matmul_split(pe, ps[:, Y_BANK + b % Y_BANKS, :], z_hi[:, ic, rows],
                                              z_lo[:, ic, rows], dn_hi[:, ic, :], dn_lo[:, ic, :],
                                              ic == 0, ic == F0_IC - 1)
                        mm.then_inc(y_done, 1)

                def logits():
                    pe.wait_ge(gate_lo_ready, 1)
                    pe.wait_ge(turned.lo_ready, B)
                    for b in range(B):
                        out = ps[:, LOGITS, b * F0_E:(b + 1) * F0_E]
                        rows = slice(b * P, (b + 1) * P)
                        for c in range(NC):
                            mm = matmul_split(pe, out, hi[:, c, rows], lo[:, c, rows],
                                              gate_hi[:, c, :], gate_lo[:, c, :], c == 0, c == NC - 1)
                    mm.then_inc(logits_done, 1)

                turned.pe(pe, range(0, HB))
                pe.wait_ge(gu_lo_ready, 1)
                pe.wait_ge(turned.lo_ready, HB)
                job(FIRST, 0)
                job(FIRST, 1)
                turned.pe(pe, range(HB, B))
                logits()
                job(FIRST, 2)
                job(FIRST, 3)
                pe.wait_ge(sigmoid_ready, 1)
                down(FIRST)
                with pe.Fori(1, F0_ALL) as e:
                    pe.wait_ge(gu_lo_ready, e + 1)
                    for j in range(F0_JOBS):
                        job(e, j)
                    down(e)


HB = B // HALVES
HT = HB * P


def chunked(w):
    return w.rearrange("p c n -> p (c n)")


def l1_attention(core):
    nc, dram, ps = core.nc, core.dram, core.psum
    scale = float(D) ** -0.5
    with ExitStack() as lay:
        hi = sbuf(nc, lay, "a1_xn_hi", [P, NC, T], F32R)
        lo = sbuf(nc, lay, "a1_xn_lo", [P, NC, T], F32R)
        turned = NormTurned(core, lay, "a1", hi, lo)
        w_hi = [sbuf(nc, lay, f"a1_w{i}_hi", [P, NC, D], F32R) for i in range(2)]
        w_lo = [sbuf(nc, lay, f"a1_w{i}_lo", [P, NC, D], F32R) for i in range(2)]
        ct_hi = sbuf(nc, lay, "a1_ct_hi", [P, NC, HT], F32R)
        ct_lo = sbuf(nc, lay, "a1_ct_lo", [P, NC, HT], F32R)
        kq_hi = [sbuf(nc, lay, f"a1_kq{i}_hi", [P, NC, HT], F32R) for i in range(2)]
        kq_lo = [sbuf(nc, lay, f"a1_kq{i}_lo", [P, NC, HT], F32R) for i in range(2)]
        c_hi = sbuf(nc, lay, "a1_c_hi", [P, HB, D], F32R)
        c_lo = sbuf(nc, lay, "a1_c_lo", [P, HB, D], F32R)
        bias = sbuf(nc, lay, "a1_bias", [P, 2, NC])
        negmax = sbuf(nc, lay, "a1_negmax", [P, B])
        shift = sbuf(nc, lay, "a1_shift", [P, B])
        total = sbuf(nc, lay, "a1_total", [P, B])
        inv = sbuf(nc, lay, "a1_inv", [P, B])
        e = sbuf(nc, lay, "a1_e", [P, HB, P])
        at_hi = sbuf(nc, lay, "a1_at_hi", [P, HT], F32R)
        at_lo = sbuf(nc, lay, "a1_at_lo", [P, HT], F32R)
        pieces = [(dram["a1_wk"], chunked(w_hi[0][:, :, :]), chunked(w_lo[0][:, :, :])),
                  (dram["ctx_turned"][0], chunked(ct_hi[:, :, :]), chunked(ct_lo[:, :, :])),
                  (dram["a1_wq"], chunked(w_hi[1][:, :, :]), chunked(w_lo[1][:, :, :])),
                  (dram["ctx_rows"][0], chunked(c_hi[:, :, :]), chunked(c_lo[:, :, :])),
                  (dram["ctx_turned"][1], chunked(ct_hi[:, :, :]), chunked(ct_lo[:, :, :])),
                  (dram["ctx_rows"][1], chunked(c_hi[:, :, :]), chunked(c_lo[:, :, :]))]
        WK, CT0, WQ, C0, CT1, C1 = range(6)
        weights = Weights(core, lay, "a1", pieces)
        ahead = Ahead(core, lay, "a1")
        bias_loaded = core.sem("a1_bias_loaded")
        proj_done = core.sem("a1_proj_done")
        hi_ready, lo_ready = core.sem("a1_hi_ready"), core.sem("a1_lo_ready")
        scores_done = core.sem("a1_scores_done")
        negmax_ready, shift_ready = core.sem("a1_negmax_ready"), core.sem("a1_shift_ready")
        exp_ready, inv_ready = core.sem("a1_exp_ready"), core.sem("a1_inv_ready")
        attn_turned = core.sem("a1_attn_turned")
        at_hi_ready, at_lo_ready = core.sem("a1_at_hi_ready"), core.sem("a1_at_lo_ready")
        y_done, x_ready = core.sem("a1_y_done"), core.sem("a1_x_ready")
        S_BANK, T_BANK = 4, 5
        PER_HALF = 2 * NC

        with nc.Block() as block:
            @block.sync
            def _(sp):
                sp.dma_start(bias[:, :, :], dram["a1_bias"]).then_inc(bias_loaded, 16)
                weights.load(sp)

            @block.gpsimd
            def _(pool):
                weights.split_lo(pool)
                ahead.pool(pool)

            @block.scalar
            def _(act):
                def proj_hi(n):
                    half, which, m = n // PER_HALF, n % PER_HALF // NC, n % NC
                    act.wait_ge(proj_done, n + 1)
                    if half:
                        act.wait_ge(scores_done, half)
                    act.activation(kq_hi[which][:, m, :], ps[:, 2 + n % 2, :], ACT.Identity,
                                   bias=bias[:, which, m:m + 1], scale=1.0).then_inc(hi_ready, 1)

                def softmax(half):
                    for i in range(HB):
                        b = half * HB + i
                        act.wait_ge(shift_ready, half + 1)
                        if half:
                            act.wait_ge(attn_turned, half)
                        act.activation(e[:, i, :], ps[:, S_BANK, i * P:(i + 1) * P], ACT.Exp,
                                       bias=shift[:, b:b + 1], scale=scale,
                                       accum_out=total[:, b:b + 1]).then_inc(exp_ready, 1)

                def attn_hi(half):
                    act.wait_ge(attn_turned, half + 1)
                    if half:
                        act.wait_ge(y_done, HB * half)
                    act.copy(at_hi[:, :], ps[:, T_BANK, :]).then_inc(at_hi_ready, 1)

                weights.split_hi(act, [WK, CT0])
                turned.act(act, range(0, 4))
                act.wait_ge(bias_loaded, 16)
                for n in range(NC):
                    proj_hi(n)
                weights.split_hi(act, [WQ])
                turned.act(act, range(4, B))
                weights.split_hi(act, [C0])
                for n in range(NC, 2 * NC):
                    proj_hi(n)
                act.wait_ge(proj_done, NC)
                weights.split_hi(act, [CT1])
                softmax(0)
                attn_hi(0)
                for n in range(2 * NC, 3 * NC):
                    proj_hi(n)
                act.wait_ge(y_done, HB)
                weights.split_hi(act, [C1])
                for n in range(3 * NC, 4 * NC):
                    proj_hi(n)
                softmax(1)
                attn_hi(1)

            @block.tensor
            def _(pe):
                def project(n):
                    half, which, m = n // PER_HALF, n % PER_HALF // NC, n % NC
                    if n >= 2:
                        pe.wait_ge(lo_ready, n - 1)
                    for c in range(NC):
                        if which == 0:
                            mov = ct_hi[:, c, :], ct_lo[:, c, :]
                        else:
                            rows = slice(half * HT, (half + 1) * HT)
                            mov = hi[:, c, rows], lo[:, c, rows]
                        mm = matmul_split(pe, ps[:, 2 + n % 2, :], w_hi[which][:, c, m * P:(m + 1) * P],
                                          w_lo[which][:, c, m * P:(m + 1) * P], *mov, c == 0, c == NC - 1)
                    mm.then_inc(proj_done, 1)

                def scores(half):
                    pe.wait_ge(lo_ready, PER_HALF * (half + 1))
                    if half:
                        pe.wait_ge(exp_ready, HB * half)
                    for i in range(HB):
                        rows = slice(i * P, (i + 1) * P)
                        for c in range(NC):
                            mm = matmul_split(pe, ps[:, S_BANK, rows], kq_hi[1][:, c, rows],
                                              kq_lo[1][:, c, rows], kq_hi[0][:, c, rows],
                                              kq_lo[0][:, c, rows], c == 0, c == NC - 1)
                    mm.then_inc(scores_done, 1)

                def turn(half):
                    pe.wait_ge(exp_ready, HB * (half + 1))
                    if half:
                        pe.wait_ge(at_lo_ready, half)
                    for i in range(HB):
                        mm = pe.transpose(ps[:, T_BANK, i * P:(i + 1) * P], e[:, i, :], core.ident[:, :])
                    mm.then_inc(attn_turned, 1)

                def attend(half):
                    pe.wait_ge(at_lo_ready, half + 1)
                    weights.wait(pe, C1 if half else C0)
                    for i in range(HB):
                        b = half * HB + i
                        if b >= 2:
                            pe.wait_ge(x_ready, b - 1)
                        matmul_split(pe, ps[:, 6 + b % 2, :], at_hi[:, i * P:(i + 1) * P],
                                     at_lo[:, i * P:(i + 1) * P], c_hi[:, i, :], c_lo[:, i, :],
                                     True, True).then_inc(y_done, 1)

                turned.pe(pe, range(0, 4))
                weights.wait(pe, CT0)
                for n in range(NC):
                    project(n)
                turned.pe(pe, range(4, B))
                weights.wait(pe, WQ)
                pe.wait_ge(turned.lo_ready, B)
                for n in range(NC, 2 * NC):
                    project(n)
                scores(0)
                weights.wait(pe, CT1)
                turn(0)
                for n in range(2 * NC, 3 * NC):
                    project(n)
                attend(0)
                for n in range(3 * NC, 4 * NC):
                    project(n)
                scores(1)
                turn(1)
                attend(1)

            @block.vector
            def _(dve):
                def proj_lo(n):
                    which, m = n % PER_HALF // NC, n % NC
                    dve.wait_ge(hi_ready, n + 1)
                    dve.scalar_tensor_tensor(out=kq_lo[which][:, m, :], in0=ps[:, 2 + n % 2, :],
                                             scalar=bias[:, which, m:m + 1],
                                             in1=kq_hi[which][:, m, :].bitcast(F32),
                                             op0=ALU.add, op1=ALU.subtract).then_inc(lo_ready, 1)

                def maxima(half):
                    cols = slice(half * HB, (half + 1) * HB)
                    dve.wait_ge(scores_done, half + 1)
                    dve.tensor_reduce(negmax[:, cols], ps[:, S_BANK, :].rearrange("p (b k) -> p b k", b=HB),
                                      AX.X, ALU.max, negate=True).then_inc(negmax_ready, 1)
                    dve.wait_ge(negmax_ready, half + 1)
                    dve.tensor_scalar(shift[:, cols], negmax[:, cols], scale, None, ALU.mult)\
                       .then_inc(shift_ready, 1)

                def attn_lo(half):
                    cols = slice(half * HB, (half + 1) * HB)
                    dve.wait_ge(exp_ready, HB * (half + 1))
                    dve.reciprocal(inv[:, cols], total[:, cols]).then_inc(inv_ready, 1)
                    dve.wait_ge(at_hi_ready, half + 1)
                    dve.tensor_tensor(at_lo[:, :], ps[:, T_BANK, :], at_hi[:, :].bitcast(F32),
                                      ALU.subtract).then_inc(at_lo_ready, 1)

                def add(half):
                    dve.wait_ge(inv_ready, half + 1)
                    for i in range(HB):
                        b = half * HB + i
                        dve.wait_ge(y_done, b + 1)
                        dve.scalar_tensor_tensor(out=core.x[:, b, :], in0=ps[:, 6 + b % 2, :],
                                                 scalar=inv[:, b:b + 1], in1=core.x[:, b, :],
                                                 op0=ALU.mult, op1=ALU.add).then_inc(x_ready, 1)
                        dve.wait_ge(x_ready, b + 1)
                        ahead.dve(dve, b)

                turned.dve(dve, range(0, 5))
                for n in range(NC):
                    proj_lo(n)
                turned.dve(dve, range(5, B))
                for n in range(NC, 2 * NC):
                    proj_lo(n)
                maxima(0)
                attn_lo(0)
                for n in range(2 * NC, 3 * NC):
                    proj_lo(n)
                add(0)
                for n in range(3 * NC, 4 * NC):
                    proj_lo(n)
                maxima(1)
                attn_lo(1)
                add(1)


QW, QA = 127.0, 255.0
ROUND = 1.5 * 2.0 ** 23


def l1_ffn(core):
    nc, dram, ps = core.nc, core.dram, core.psum
    with ExitStack() as lay:
        w = sbuf(nc, lay, "f1_w", [P, NC, D])
        wr = sbuf(nc, lay, "f1_wr", [P, NC, D])
        wq = sbuf(nc, lay, "f1_wq", [P, NC, D], BF16)
        wt = sbuf(nc, lay, "f1_wt", [P, NC, D], BF16)
        wide = sbuf(nc, lay, "f1_wide", [P, NC, P])
        bias = sbuf(nc, lay, "f1_bias", [P, D])
        low = sbuf(nc, lay, "f1_low", [P, D])
        high = sbuf(nc, lay, "f1_high", [P, D])
        row_scale = sbuf(nc, lay, "f1_row_scale", [P, D])
        rs = sbuf(nc, lay, "f1_rs", [P, NC])
        rs_inv = sbuf(nc, lay, "f1_rs_inv", [P, NC])
        identb = sbuf(nc, lay, "f1_identb", [P, P], BF16)
        xn = sbuf(nc, lay, "f1_xn", [P, B, D])
        xr = sbuf(nc, lay, "f1_xr", [P, 2, D])
        xq = sbuf(nc, lay, "f1_xq", [P, 2, D], BF16)
        xt = sbuf(nc, lay, "f1_xt", [P, 2, NC, P], BF16)
        y = sbuf(nc, lay, "f1_y", [P, 3, D])
        negmean = sbuf(nc, lay, "f1_negmean", [P, B])
        mn = sbuf(nc, lay, "f1_mn", [P, B])
        mxm = sbuf(nc, lay, "f1_mx", [P, B])
        cs = sbuf(nc, lay, "f1_cs", [P, B])
        flat_row = sbuf(nc, lay, "f1_flat_row", [P, B])
        cs_inv = sbuf(nc, lay, "f1_cs_inv", [P, B])
        zp = sbuf(nc, lay, "f1_zp", [P, B])
        ends = sbuf(nc, lay, "f1_ends", [P, 2, B])
        ahead = Ahead(core, lay, "f1")
        loaded, w_loaded = core.sem("f1_loaded"), core.sem("f1_w_loaded")
        identb_ready = core.sem("f1_identb_ready")
        step = core.sem("f1_step")
        w_turned, wt_ready = core.sem("f1_w_turned"), core.sem("f1_wt_ready")
        wide_ready, rs_spread, rs_ready = (core.sem(f"f1_{n}") for n in ("wide_ready", "rs_spread", "rs_ready"))
        wq_ready = core.sem("f1_wq_ready")
        xq_ready, x_turned, xt_ready = (core.sem(f"f1_{n}") for n in ("xq_ready", "x_turned", "xt_ready"))
        y_done, y_taken = core.sem("f1_y_done"), core.sem("f1_y_taken")
        negmean_ready, centred = core.sem("f1_negmean_ready"), core.sem("f1_centred")
        wide_ones, y_scaled, y_ready = (core.sem(f"f1_{n}") for n in ("wide_ones", "y_scaled", "y_ready"))
        x_ready, late_scaled = core.sem("f1_x_ready"), core.sem("f1_late_scaled")

        def turned_bank(i):
            return ps[:, i % 2, 0:D // 2].bitcast(BF16).rearrange("p (c n) -> p c n", c=NC)

        with nc.Block() as block:
            @block.sync
            def _(sp):
                for dst, name in ((low, "f1_low"), (high, "f1_high"), (bias, "f1_bias")):
                    sp.dma_start(dst[:, :], dram[name]).then_inc(loaded, 16)
                sp.dma_start(w[:, :, :], dram["f1_w"]).then_inc(w_loaded, 16)

            @block.gpsimd
            def _(pool):
                pool.tensor_copy(identb[:, :], core.ident[:, :]).then_inc(identb_ready, 1)
                pool.memset(wide[:, :, :], 1.0).then_inc(wide_ones, 1)
                pool.wait_ge(loaded, 48)
                pool.wait_ge(rs_ready, 1)
                for b in range(B):
                    if b < HB:
                        pool.wait_ge(y_taken, b + 1)
                        pool.tensor_tensor(y[:, b % 3, :], y[:, b % 3, :], row_scale[:, :], ALU.mult)\
                            .then_inc(y_scaled, 1)
                        pool.wait_ge(y_scaled, b + 1)
                    else:
                        pool.wait_ge(late_scaled, b + 1 - HB)
                    pool.tensor_tensor(y[:, b % 3, :], y[:, b % 3, :], bias[:, :], ALU.add)\
                        .then_inc(y_ready, 1)
                    if b >= 1:
                        ahead.scale(pool, b - 1)
                ahead.scale(pool, B - 1)

            @block.tensor
            def _(pe):
                pe.wait_ge(identb_ready, 1)
                pe.wait_ge(wq_ready, 1)
                for c in range(NC):
                    if c >= 2:
                        pe.wait_ge(wt_ready, c - 1)
                    for m in range(NC):
                        mm = pe.transpose(turned_bank(c)[:, m, :], wq[:, m, c * P:(c + 1) * P], identb[:, :])
                    mm.then_inc(w_turned, 1)
                pe.wait_ge(wide_ready, 1)
                for m in range(NC):
                    mm = pe.matmul(ps[:, 2, m * P:(m + 1) * P], wide[:, m, :], core.ident[:, :],
                                   start=True, stop=True)
                mm.then_inc(rs_spread, 1)
                pe.wait_ge(wt_ready, NC)

                def product(b):
                    pe.wait_ge(xt_ready, b + 1)
                    if b >= 2:
                        if b - 2 < HB:
                            pe.wait_ge(y_taken, b - 1)
                        else:
                            pe.wait_ge(late_scaled, b - 1 - HB)
                    for c in range(NC):
                        mm = pe.matmul(ps[:, 4 + b % 2, :], xt[:, b % 2, c, :], wt[:, c, :],
                                       start=(c == 0), stop=(c == NC - 1))
                    mm.then_inc(y_done, 1)

                for b in range(B):
                    pe.wait_ge(xq_ready, b + 1)
                    if b >= 2:
                        pe.wait_ge(xt_ready, b - 1)
                    for c in range(NC):
                        mm = pe.transpose(turned_bank(b)[:, c, :], xq[:, b % 2, c * P:(c + 1) * P], identb[:, :])
                    mm.then_inc(x_turned, 1)
                    if b >= 1:
                        product(b - 1)
                product(B - 1)

            @block.scalar
            def _(act):
                act.wait_ge(negmean_ready, 1)
                for b in range(B):
                    act.activation(xn[:, b, :], core.x[:, b, :], ACT.Identity, bias=negmean[:, b:b + 1],
                                   scale=1.0).then_inc(centred, 1)
                for c in range(NC):
                    act.wait_ge(w_turned, c + 1)
                    act.copy(wt[:, c, :].rearrange("p (m n) -> p m n", m=NC), turned_bank(c)).then_inc(wt_ready, 1)
                act.wait_ge(rs_spread, 1)
                act.copy(row_scale[:, :], ps[:, 2, :]).then_inc(rs_ready, 1)

                def take_product(b):
                    act.wait_ge(y_done, b + 1)
                    if b >= 3:
                        act.wait_ge(x_ready, b - 2)
                    act.mul(y[:, b % 3, :], ps[:, 4 + b % 2, :], cs[:, b:b + 1]).then_inc(y_taken, 1)

                for b in range(B):
                    act.wait_ge(x_turned, b + 1)
                    if b >= 2:
                        act.wait_ge(y_done, b - 1)
                    act.copy(xt[:, b % 2, :, :], turned_bank(b)).then_inc(xt_ready, 1)
                    if 1 <= b <= HB:
                        take_product(b - 1)

            @block.vector
            def _(dve):
                steps = 0

                def after(instruction):
                    nonlocal steps
                    steps += 1
                    instruction.then_inc(step, 1)
                    dve.wait_ge(step, steps)

                dve.tensor_scalar(negmean[:, :], core.means(), -1.0, None, ALU.mult).then_inc(negmean_ready, 1)
                dve.wait_ge(loaded, 48)
                def weights():
                    dve.wait_ge(w_loaded, 16)
                    after(dve.tensor_reduce(rs[:, :], w[:, :, :], AX.X, ALU.max, apply_absolute_value=True))
                    after(dve.tensor_scalar(rs[:, :], rs[:, :], 1.0 / QW, None, ALU.mult))
                    dve.wait_ge(wide_ones, 1)
                    for m in range(NC):
                        ins = dve.tensor_scalar(wide[:, m, :], wide[:, m, :], rs[:, m:m + 1], None, ALU.mult)
                    ins.then_inc(wide_ready, 1)
                    after(dve.reciprocal(rs_inv[:, :], rs[:, :]))
                    for m in range(NC):
                        ins = dve.tensor_scalar(wr[:, m, :], w[:, m, :], rs_inv[:, m:m + 1], ROUND,
                                                ALU.mult, ALU.add)
                    after(ins)
                    after(dve.tensor_scalar(wr[:, :, :], wr[:, :, :], ROUND, QW, ALU.subtract, ALU.min))
                    dve.tensor_scalar(wq[:, :, :], wr[:, :, :], -QW, None, ALU.max).then_inc(wq_ready, 1)

                def clip(half):
                    for b in range(half * HB, (half + 1) * HB):
                        dve.wait_ge(centred, b + 1)
                        after(dve.scalar_tensor_tensor(out=xn[:, b, :], in0=xn[:, b, :], scalar=core.rstd(b),
                                                       in1=low[:, :], op0=ALU.mult, op1=ALU.max))
                        after(dve.tensor_tensor(xn[:, b, :], xn[:, b, :], high[:, :], ALU.min))
                        dve.tensor_reduce(mn[:, b:b + 1], xn[:, b, :], AX.X, ALU.min)
                        ins = dve.tensor_reduce(mxm[:, b:b + 1], xn[:, b, :], AX.X, ALU.max)
                    after(ins)

                def scales(half):
                    h = slice(half * HB, (half + 1) * HB)
                    after(dve.tensor_tensor(cs[:, h], mxm[:, h], mn[:, h], ALU.subtract))
                    after(dve.tensor_scalar(cs[:, h], cs[:, h], 1.0 / QA, None, ALU.mult))
                    after(dve.tensor_scalar(flat_row[:, h], cs[:, h], 0.0, None, ALU.is_le))
                    after(dve.tensor_tensor(cs[:, h], cs[:, h], flat_row[:, h], ALU.add))
                    after(dve.reciprocal(cs_inv[:, h], cs[:, h]))
                    after(dve.tensor_tensor(zp[:, h], mn[:, h], cs_inv[:, h], ALU.mult))
                    after(dve.tensor_scalar(zp[:, h], zp[:, h], -1.0, -128.0, ALU.mult, ALU.add))
                    after(dve.tensor_scalar(zp[:, h], zp[:, h], ROUND, ROUND, ALU.add, ALU.subtract))
                    dve.tensor_scalar(ends[:, 0, h], zp[:, h], -1.0, -128.0, ALU.mult, ALU.add)
                    after(dve.tensor_scalar(ends[:, 1, h], zp[:, h], -1.0, 127.0, ALU.mult, ALU.add))

                def quantise(b):
                    p, one = b % 2, slice(b, b + 1)
                    if b >= 2:
                        dve.wait_ge(xq_ready, b - 1)
                    after(dve.tensor_scalar(xr[:, p, :], xn[:, b, :], cs_inv[:, one], ROUND, ALU.mult, ALU.add))
                    after(dve.tensor_scalar(xr[:, p, :], xr[:, p, :], ROUND, ends[:, 0, one], ALU.subtract,
                                            ALU.max))
                    if b >= 2:
                        dve.wait_ge(x_turned, b - 1)
                    dve.tensor_scalar(xq[:, p, :], xr[:, p, :], ends[:, 1, one], None, ALU.min)\
                       .then_inc(xq_ready, 1)

                def finish(b):
                    dve.wait_ge(y_ready, b + 1)
                    dve.tensor_tensor(core.x[:, b, :], core.x[:, b, :], y[:, b % 3, :], ALU.add)\
                       .then_inc(x_ready, 1)
                    dve.wait_ge(x_ready, b + 1)
                    ahead.dve(dve, b)

                def scale_product(b):
                    dve.wait_ge(y_done, b + 1)
                    dve.wait_ge(rs_ready, 1)
                    dve.wait_ge(x_ready, b - 2)
                    dve.scalar_tensor_tensor(out=y[:, b % 3, :], in0=ps[:, 4 + b % 2, :],
                                             scalar=cs[:, b:b + 1], in1=row_scale[:, :],
                                             op0=ALU.mult, op1=ALU.mult).then_inc(late_scaled, 1)

                clip(0)
                weights()
                for half in range(HALVES):
                    if half:
                        clip(1)
                    scales(half)
                    for b in range(half * HB, (half + 1) * HB):
                        quantise(b)
                        if half:
                            finish(b - HB)
                scale_product(HB)
                for b in range(HB, B):
                    if b + 1 < B:
                        scale_product(b + 1)
                    finish(b)


A2_KV, A2_REP, A2_DH = 8, 4, 16
A2_SLOT, A2_MAX_ROW = 64, 48
A2_PAIRS = A2_KV // 2
A2_KVD = A2_KV * A2_DH
A2_VSLOT = 32
A2_GROUPS, A2_PER_GROUP = 2, 4
A2_UNITS = B * A2_GROUPS
A2_RAW = 1024


def l2_attention(core):
    with ExitStack() as lay:
        nc = core.nc
        q_st = sbuf(nc, lay, "a2_q_st", [P, A2_PAIRS * A2_REP, T], F32R)
        k_st = sbuf(nc, lay, "a2_k_st", [P, A2_PAIRS, T], F32R)
        v = sbuf(nc, lay, "a2_v", [P, B, A2_KV, A2_VSLOT])
        l2_project(core, q_st, k_st, v)
        l2_attend(core, q_st, k_st, v)


def l2_project(core, q_st, k_st, v):
    nc, dram, ps = core.nc, core.dram, core.psum
    with ExitStack() as part:
        hi = sbuf(nc, part, "a2_xn_hi", [P, NC, T], F32R)
        lo = sbuf(nc, part, "a2_xn_lo", [P, NC, T], F32R)
        turned = NormTurned(core, part, "a2", hi, lo)
        ct_hi = sbuf(nc, part, "a2_ct_hi", [P, NC, HT], F32R)
        ct_lo = sbuf(nc, part, "a2_ct_lo", [P, NC, HT], F32R)
        wq_hi = sbuf(nc, part, "a2_wq_hi", [P, NC, D], F32R)
        wq_lo = sbuf(nc, part, "a2_wq_lo", [P, NC, D], F32R)
        wkv_hi = sbuf(nc, part, "a2_wkv_hi", [P, NC, 2 * A2_KVD], F32R)
        wkv_lo = sbuf(nc, part, "a2_wkv_lo", [P, NC, 2 * A2_KVD], F32R)
        sel_k = sbuf(nc, part, "a2_sel_k", [P, 2, A2_PAIRS, P], F32R)
        sel_q = sbuf(nc, part, "a2_sel_q", [P, 2, A2_REP, P], F32R)
        part_hi = sbuf(nc, part, "a2_part_hi", [P, 2, HT], F32R)
        part_lo = sbuf(nc, part, "a2_part_lo", [P, 2, HT], F32R)
        ones_row = sbuf(nc, part, "a2_ones_row", [P, 1])

        def flat(w, a, b):
            return chunked(w[:, a:b, :])

        ct, wq = dram["ctx_turned"], dram["a2_wq"]
        pieces = [(dram["a2_wkv"], flat(wkv_hi, 0, NC), flat(wkv_lo, 0, NC)),
                  (ct[0][:, 0:A2_RAW], flat(ct_hi, 0, 2), flat(ct_lo, 0, 2)),
                  (ct[0][:, A2_RAW:], flat(ct_hi, 2, NC), flat(ct_lo, 2, NC)),
                  (dram["a2_sel_k"], sel_k[:, :, :, :].rearrange("p a b c -> p (a b c)"), None),
                  (dram["a2_sel_q"], sel_q[:, :, :, :].rearrange("p a b c -> p (a b c)"), None),
                  (wq[:, 0:A2_RAW], flat(wq_hi, 0, 2), flat(wq_lo, 0, 2)),
                  (wq[:, A2_RAW:], flat(wq_hi, 2, NC), flat(wq_lo, 2, NC)),
                  (ct[1][:, 0:A2_RAW], flat(ct_hi, 0, 2), flat(ct_lo, 0, 2)),
                  (ct[1][:, A2_RAW:], flat(ct_hi, 2, NC), flat(ct_lo, 2, NC))]
        WKV, CT0A, CT0B, SELK, SELQ, WQA, WQB, CT1A, CT1B = range(9)
        weights = Weights(core, part, "a2", pieces, A2_RAW)
        jobs = [("k", 0, 0)] + [("q", h, m) for h in range(HALVES) for m in range(NC)] + [("k", 1, 0)]
        row_loaded = core.sem("a2_row_loaded")
        proj_done = core.sem("a2_proj_done")
        hi_ready, lo_ready = core.sem("a2_hi_ready"), core.sem("a2_lo_ready")
        stack_done = core.sem("a2_stack_done")
        even_ready, odd_ready = core.sem("a2_even_ready"), core.sem("a2_odd_ready")
        v_done, v_ready, v_zeroed = core.sem("a2_v_done"), core.sem("a2_v_ready"), core.sem("a2_v_zeroed")

        def stack_tile(n, i):
            kind, half, m = jobs[n]
            rows = slice(half * HT, (half + 1) * HT)
            return k_st[:, i, rows] if kind == "k" else q_st[:, m * A2_REP + i, rows]

        with nc.Block() as block:
            @block.sync
            def _(sp):
                sp.dma_start(ones_row[:, :], dram["a2_ones_row"]).then_inc(row_loaded, 16)
                weights.load(sp)

            @block.gpsimd
            def _(pool):
                weights.split_lo(pool, [WKV, CT0A, CT0B, SELK, SELQ, WQA, WQB])
                pool.memset(v[:, :, :, :], 0.0).then_inc(v_zeroed, 1)
                pool.wait_ge(v_zeroed, 1)
                pool.memset(v[:, :, :, A2_DH:A2_DH + 1], 1.0).then_inc(v_zeroed, 1)
                weights.split_lo(pool, [CT1A, CT1B])

            @block.scalar
            def _(act):
                def part_of(n):
                    act.wait_ge(proj_done, n + 1)
                    if n >= 2:
                        act.wait_ge(stack_done, 4 * (n - 1))
                    act.copy(part_hi[:, n % 2, :], ps[:, 2 + n % 2, :]).then_inc(hi_ready, 1)

                def stacks(n):
                    for i in (0, 2):
                        act.wait_ge(stack_done, 4 * n + i + 1)
                        if jobs[n][0] == "k":
                            ins = act.activation(stack_tile(n, i), ps[:, 4 + i, :], ACT.Identity,
                                                 bias=ones_row[:, 0:1], scale=1.0)
                        else:
                            ins = act.copy(stack_tile(n, i), ps[:, 4 + i, :])
                        ins.then_inc(even_ready, 1)

                weights.split_hi(act, [WKV, CT0A])
                turned.act(act, range(0, 2))
                weights.split_hi(act, [CT0B])
                turned.act(act, range(2, 4))
                weights.split_hi(act, [SELK])
                turned.act(act, range(4, 6))
                weights.split_hi(act, [SELQ])
                turned.act(act, range(6, B))
                weights.split_hi(act, [WQA, WQB])
                act.wait_ge(row_loaded, 16)
                for n in range(len(jobs)):
                    part_of(n)
                    if n >= 1:
                        stacks(n - 1)
                    if n == 1:
                        act.wait_ge(v_done, 1)
                        weights.split_hi(act, [CT1A, CT1B])
                stacks(len(jobs) - 1)

            @block.vector
            def _(dve):
                def part_of(n):
                    dve.wait_ge(hi_ready, n + 1)
                    dve.tensor_tensor(part_lo[:, n % 2, :], ps[:, 2 + n % 2, :],
                                      part_hi[:, n % 2, :].bitcast(F32), ALU.subtract)\
                       .then_inc(lo_ready, 1)

                def stacks(n):
                    for i in (1, 3):
                        dve.wait_ge(stack_done, 4 * n + i + 1)
                        if jobs[n][0] == "k":
                            ins = dve.tensor_scalar(stack_tile(n, i), ps[:, 4 + i, :], ones_row[:, 0:1],
                                                    None, ALU.add)
                        else:
                            ins = dve.tensor_copy(stack_tile(n, i), ps[:, 4 + i, :])
                        ins.then_inc(odd_ready, 1)

                def values(half):
                    dve.wait_ge(v_done, half + 1)
                    dve.wait_ge(v_zeroed, 2)
                    dve.tensor_copy(v[:, half * HB:(half + 1) * HB, :, 0:A2_DH].rearrange(
                                        "p b c d -> p (b c) d"),
                                    ps[:, half, :].rearrange("p (n d) -> p n d", d=A2_DH)).then_inc(v_ready, 1)

                turned.dve(dve)
                dve.wait_ge(row_loaded, 16)
                for n in range(len(jobs)):
                    part_of(n)
                    if n == 0:
                        values(0)
                    if n >= 1:
                        stacks(n - 1)
                values(1)
                stacks(len(jobs) - 1)

            @block.tensor
            def _(pe):
                def project(n):
                    kind, half, m = jobs[n]
                    if n >= 2:
                        pe.wait_ge(lo_ready, n - 1)
                    for c in range(NC):
                        w = slice(m * P, (m + 1) * P)
                        if kind == "k":
                            ops = wkv_hi[:, c, w], wkv_lo[:, c, w], ct_hi[:, c, :], ct_lo[:, c, :]
                        else:
                            rows = slice(half * HT, (half + 1) * HT)
                            ops = wq_hi[:, c, w], wq_lo[:, c, w], hi[:, c, rows], lo[:, c, rows]
                        mm = matmul_split(pe, ps[:, 2 + n % 2, :], *ops, c == 0, c == NC - 1)
                    mm.then_inc(proj_done, 1)

                def stacks(n):
                    kind = jobs[n][0]
                    pe.wait_ge(lo_ready, n + 1)
                    sel = sel_k if kind == "k" else sel_q
                    for i in range(4):
                        if n >= 1:
                            pe.wait_ge(odd_ready if i % 2 else even_ready, 2 * (n - 1) + i // 2 + 1)
                        pe.matmul(ps[:, 4 + i, :], sel[:, 0, i, :], part_hi[:, n % 2, :], start=True,
                                  stop=False)
                        pe.matmul(ps[:, 4 + i, :], sel[:, 1, i, :], part_lo[:, n % 2, :], start=False,
                                  stop=True).then_inc(stack_done, 1)

                def values(half):
                    for i in range(HB):
                        rows = slice(i * P, (i + 1) * P)
                        for c in range(NC):
                            mm = matmul_split(pe, ps[:, half, i * A2_KVD:(i + 1) * A2_KVD],
                                              ct_hi[:, c, rows], ct_lo[:, c, rows],
                                              wkv_hi[:, c, A2_KVD:], wkv_lo[:, c, A2_KVD:],
                                              c == 0, c == NC - 1)
                    mm.then_inc(v_done, 1)

                turned.pe(pe)
                weights.wait(pe, CT0B)
                project(0)
                pe.wait_ge(turned.lo_ready, B)
                values(0)
                weights.wait(pe, WQB)
                for n in range(1, len(jobs)):
                    if n == len(jobs) - 1:
                        weights.wait(pe, CT1B)
                    project(n)
                    if n == len(jobs) - 1:
                        values(1)
                    stacks(n - 1)
                stacks(len(jobs) - 1)


def l2_attend(core, q_st, k_st, v):
    nc, dram, ps = core.nc, core.dram, core.psum
    scale = float(A2_DH) ** -0.5
    with ExitStack() as part:
        e = sbuf(nc, part, "a2_e", [P, 2, A2_PER_GROUP, A2_REP * P])
        osb = sbuf(nc, part, "a2_osb", [P, 2, A2_REP * P])
        rec = sbuf(nc, part, "a2_rec", [P, A2_REP, A2_PER_GROUP])
        on = sbuf(nc, part, "a2_on", [P, 2, A2_KV, A2_REP, A2_DH])
        ot_hi = sbuf(nc, part, "a2_ot_hi", [P, NC, T], F32R)
        ot_lo = sbuf(nc, part, "a2_ot_lo", [P, NC, T], F32R)
        wo_hi = sbuf(nc, part, "a2_wo_hi", [P, NC, D], F32R)
        wo_lo = sbuf(nc, part, "a2_wo_lo", [P, NC, D], F32R)
        mx = sbuf(nc, part, "a2_mx", [P, 2 * A2_REP, P])
        wo = dram["a2_wo"]
        pieces = [(wo[:, 0:A2_RAW], chunked(wo_hi[:, 0:2, :]), chunked(wo_lo[:, 0:2, :])),
                  (wo[:, A2_RAW:], chunked(wo_hi[:, 2:, :]), chunked(wo_lo[:, 2:, :]))]
        weights = Weights(core, part, "a2o", pieces, A2_RAW)
        ahead = Ahead(core, part, "a2")
        zeroed = core.sem("a2_zeroed")
        scores_done, max_ready = core.sem("a2_scores_done"), core.sem("a2_max_ready")
        max_turned, q_ready = core.sem("a2_max_turned"), core.sem("a2_q_ready")
        keyed_done, exp_ready = core.sem("a2_keyed_done"), core.sem("a2_exp_ready")
        pv_done, o_ready = core.sem("a2_pv_done"), core.sem("a2_o_ready")
        o_turned, rec_ready, on_ready = (core.sem(f"a2_{n}") for n in ("o_turned", "rec_ready", "on_ready"))
        on_turned, ot_hi_ready, ot_lo_ready = (core.sem(f"a2_{n}") for n in
                                               ("on_turned", "ot_hi_ready", "ot_lo_ready"))
        y_done, x_ready = core.sem("a2_y_done"), core.sem("a2_x_ready")
        M_BANK, O_BANK, S_BANK, ON_BANK = 0, 2, 4, 3

        def rows_of(b):
            return slice(b * P, (b + 1) * P)

        STEPS = 2 * A2_UNITS

        def s_bank(s):
            return S_BANK + 2 * (s % 2)

        def batch_pair(s):
            return divmod(s, A2_PAIRS)

        with nc.Block() as block:
            @block.sync
            def _(sp):
                weights.load(sp)

            @block.gpsimd
            def _(pool):
                pool.memset(mx[:, :, :], 0.0).then_inc(zeroed, 1)
                weights.split_lo(pool)
                ahead.pool(pool)

            @block.scalar
            def _(act):
                def take_out(u):
                    act.wait_ge(pv_done, u + 1)
                    if u >= 2:
                        act.wait_ge(o_turned, u - 1)
                    act.copy(osb[:, u % 2, :], ps[:, O_BANK + u % 2, :]).then_inc(o_ready, 1)

                def turned_hi(b):
                    act.wait_ge(on_turned, b + 1)
                    act.copy(ot_hi[:, :, rows_of(b)], ps[:, ON_BANK, :].rearrange("p (c t) -> p c t", c=NC))\
                       .then_inc(ot_hi_ready, 1)

                weights.split_hi(act)
                for s in range(STEPS + 4):
                    u = s // 2
                    if s < STEPS:
                        act.wait_ge(keyed_done, s + 1)
                        if u >= 2:
                            act.wait_ge(pv_done, u - 1)
                        act.activation(e[:, u % 2, 2 * (s % 2):2 * (s % 2) + 2, :],
                                       ps[:, s_bank(s):s_bank(s) + 2, :],
                                       ACT.Exp, scale=scale).then_inc(exp_ready, 1)
                    if s % 2 == 0 and 1 <= u <= A2_UNITS:
                        take_out(u - 1)
                    if s % A2_PAIRS == 2 and s >= 6:
                        turned_hi((s - 6) // A2_PAIRS)

            @block.vector
            def _(dve):
                def take_on(u):
                    b, g = divmod(u, A2_GROUPS)
                    dve.wait_ge(o_turned, u + 1)
                    if u >= 1:
                        dve.wait_ge(on_ready, u)
                    o = ps[:, O_BANK + u % 2, :].rearrange("p (m c d) -> p m c d", m=A2_REP, c=A2_PER_GROUP)
                    dve.reciprocal(rec[:, :, :], o[:, :, :, A2_DH]).then_inc(rec_ready, 1)
                    dve.wait_ge(rec_ready, u + 1)
                    if b >= 2:
                        dve.wait_ge(on_turned, b - 1)
                    dve.tensor_tensor(
                        on[:, b % 2, g * A2_PER_GROUP:(g + 1) * A2_PER_GROUP, :, :].rearrange(
                            "p c m d -> p m c d"),
                        o[:, :, :, 0:A2_DH],
                        rec[:, :, :].unsqueeze(3).broadcast_to([P, A2_REP, A2_PER_GROUP, A2_DH]),
                        ALU.mult).then_inc(on_ready, 1)

                def turned_lo(b):
                    dve.wait_ge(ot_hi_ready, b + 1)
                    dve.tensor_tensor(ot_lo[:, :, rows_of(b)],
                                      ps[:, ON_BANK, :].rearrange("p (c t) -> p c t", c=NC),
                                      ot_hi[:, :, rows_of(b)].bitcast(F32), ALU.subtract)\
                       .then_inc(ot_lo_ready, 1)

                def maximum(s):
                    dve.wait_ge(scores_done, s + 1)
                    tiles = slice(A2_REP * (s % 2), A2_REP * (s % 2 + 1))
                    dve.tensor_reduce(
                        mx[:, tiles, A2_MAX_ROW:P:A2_SLOT].rearrange("p m r -> p r m"),
                        ps[:, s_bank(s):s_bank(s) + 2, :].rearrange("p r (m j) -> p r m j", m=A2_REP),
                        AX.X, ALU.max, negate=True).then_inc(max_ready, 1)

                def lower(s):
                    b, pair = batch_pair(s)
                    dve.wait_ge(max_turned, s + 1)
                    tiles = q_st[:, pair * A2_REP:(pair + 1) * A2_REP, rows_of(b)]
                    dve.tensor_tensor(tiles, ps[:, M_BANK + s % 2, :].rearrange("p (m t) -> p m t", m=A2_REP),
                                      tiles.bitcast(F32), ALU.add).then_inc(q_ready, 1)

                dve.wait_ge(zeroed, 1)
                maximum(0)
                lower(0)
                maximum(1)
                for s in range(STEPS + 4):
                    if s + 1 < STEPS:
                        lower(s + 1)
                    if s % A2_PAIRS == 2 and s >= 6:
                        turned_lo((s - 6) // A2_PAIRS)
                    if s + 2 < STEPS:
                        maximum(s + 2)
                    if s % 2 == 1 and 3 <= s < STEPS + 2:
                        take_on((s - 3) // 2)
                for b in range(B):
                    dve.wait_ge(y_done, b + 1)
                    dve.tensor_tensor(core.x[:, b, :], ps[:, S_BANK + b % 4, :], core.x[:, b, :], ALU.add)\
                       .then_inc(x_ready, 1)
                    dve.wait_ge(x_ready, b + 1)
                    ahead.dve(dve, b)
                dve.wait_ge(x_ready, B)

            @block.tensor
            def _(pe):
                def slot(i):
                    return slice(A2_SLOT * (i % 2), A2_SLOT * (i % 2 + 1))

                def scores(s):
                    b, pair = batch_pair(s)
                    if s >= 2:
                        pe.wait_ge(exp_ready, s - 1)
                    for m in range(A2_REP):
                        for i in range(2):
                            mm = pe.matmul(ps[:, s_bank(s) + i, m * P:(m + 1) * P],
                                           q_st[slot(i), pair * A2_REP + m, rows_of(b)],
                                           k_st[slot(i), pair, rows_of(b)], start=True, stop=True)
                    mm.then_inc(scores_done, 1)

                def turn_max(s):
                    pe.wait_ge(max_ready, s + 1)
                    if s >= 2:
                        pe.wait_ge(q_ready, s - 1)
                    for m in range(A2_REP):
                        mm = pe.transpose(ps[:, M_BANK + s % 2, m * P:(m + 1) * P],
                                          mx[:, A2_REP * (s % 2) + m, :], core.ident[:, :])
                    mm.then_inc(max_turned, 1)

                def keyed(s):
                    b, pair = batch_pair(s)
                    pe.wait_ge(q_ready, s + 1)
                    for i in range(2):
                        mm = pe.matmul(ps[:, s_bank(s) + i, :], k_st[slot(i), pair, rows_of(b)],
                                       q_st[slot(i), pair * A2_REP:(pair + 1) * A2_REP, rows_of(b)],
                                       start=True, stop=True)
                    mm.then_inc(keyed_done, 1)

                def values(s):
                    u = s // 2
                    b, g = divmod(u, A2_GROUPS)
                    pe.wait_ge(exp_ready, s + 1)
                    if u >= 2:
                        pe.wait_ge(on_ready, u - 1)
                    if u % 2 == 1 and b >= 1:
                        pe.wait_ge(ot_lo_ready, b)
                    for i in range(2 * (s % 2), 2 * (s % 2) + 2):
                        mm = pe.matmul(ps[A2_VSLOT * i:A2_VSLOT * (i + 1), O_BANK + u % 2, :],
                                       v[:, b, g * A2_PER_GROUP + i, :], e[:, u % 2, i, :],
                                       start=True, stop=True)
                    if s % 2 == 1:
                        mm.then_inc(pv_done, 1)

                def turn_o(u):
                    pe.wait_ge(o_ready, u + 1)
                    for m in range(A2_REP):
                        mm = pe.transpose(ps[:, O_BANK + u % 2, m * P:(m + 1) * P],
                                          osb[:, u % 2, m * P:(m + 1) * P], core.ident[:, :])
                    mm.then_inc(o_turned, 1)

                def turn_on(b):
                    pe.wait_ge(on_ready, A2_GROUPS * (b + 1))
                    rows = on[:, b % 2, :, :, :].rearrange("p c m d -> p (c m d)")
                    for c in range(NC):
                        mm = pe.transpose(ps[:, ON_BANK, c * P:(c + 1) * P], rows[:, c * P:(c + 1) * P],
                                          core.ident[:, :])
                    mm.then_inc(on_turned, 1)

                scores(0)
                turn_max(0)
                scores(1)
                for s in range(STEPS + 4):
                    if s < STEPS:
                        keyed(s)
                    if 1 <= s <= STEPS:
                        values(s - 1)
                    if s + 1 < STEPS:
                        turn_max(s + 1)
                    if s % 2 == 1 and 3 <= s < STEPS + 2:
                        turn_o((s - 3) // 2)
                    if s % A2_PAIRS == 2 and s >= 6:
                        turn_on((s - 6) // A2_PAIRS)
                    if s + 2 < STEPS:
                        scores(s + 2)
                weights.wait(pe, 1)
                pe.wait_ge(ot_lo_ready, B)
                for b in range(B):
                    if b >= 4:
                        pe.wait_ge(x_ready, b - 3)
                    for c in range(NC):
                        mm = matmul_split(pe, ps[:, S_BANK + b % 4, :], ot_hi[:, c, rows_of(b)],
                                          ot_lo[:, c, rows_of(b)], wo_hi[:, c, :], wo_lo[:, c, :],
                                          c == 0, c == NC - 1)
                    mm.then_inc(y_done, 1)


F2_H, F2_R = 8, 16
F2_HR = F2_H * F2_R
F2_N = F2_HR + F2_H
F2_SCALING = 2.0


def l2_ffn(core):
    nc, dram, ps = core.nc, core.dram, core.psum
    with ExitStack() as lay:
        hi = sbuf(nc, lay, "f2_xn_hi", [P, NC, T], F32R)
        lo = sbuf(nc, lay, "f2_xn_lo", [P, NC, T], F32R)
        turned = NormTurned(core, lay, "f2", hi, lo)
        a_hi = sbuf(nc, lay, "f2_a_hi", [P, NC, F2_N], F32R)
        a_lo = sbuf(nc, lay, "f2_a_lo", [P, NC, F2_N], F32R)
        b_hi = sbuf(nc, lay, "f2_b_hi", [P, D], F32R)
        b_lo = sbuf(nc, lay, "f2_b_lo", [P, D], F32R)
        br = sbuf(nc, lay, "f2_br", [P, F2_H])
        low = sbuf(nc, lay, "f2_low", [P, B, F2_HR])
        logit = sbuf(nc, lay, "f2_logit", [P, B, F2_H])
        weight = sbuf(nc, lay, "f2_weight", [P, B, F2_H])
        col = sbuf(nc, lay, "f2_col", [P, B])
        lt_hi = sbuf(nc, lay, "f2_lt_hi", [P, T], F32R)
        lt_lo = sbuf(nc, lay, "f2_lt_lo", [P, T], F32R)
        pieces = [(dram["f2_a"], chunked(a_hi[:, :, :]), chunked(a_lo[:, :, :])),
                  (dram["f2_b"], b_hi[:, :], b_lo[:, :])]
        weights = Weights(core, lay, "f2", pieces)
        ahead = Ahead(core, lay, "f2")
        br_loaded = core.sem("f2_br_loaded")
        low_done, low_ready, logit_ready = (core.sem(f"f2_{n}") for n in
                                            ("low_done", "low_ready", "logit_ready"))
        shifted_ready, exp_ready, step = (core.sem(f"f2_{n}") for n in ("shifted_ready", "exp_ready", "step"))
        scaled_ready, low_turned = core.sem("f2_scaled_ready"), core.sem("f2_low_turned")
        lt_hi_ready, lt_lo_ready = core.sem("f2_lt_hi_ready"), core.sem("f2_lt_lo_ready")
        y_done, x_ready = core.sem("f2_y_done"), core.sem("f2_x_ready")
        LOW_BANK, T_BANK, Y_BANK = 2, 4, 6

        with nc.Block() as block:
            @block.sync
            def _(sp):
                weights.load(sp)
                sp.dma_start(br[:, :], dram["f2_br"]).then_inc(br_loaded, 16)

            @block.gpsimd
            def _(pool):
                weights.split_lo(pool)
                ahead.pool(pool)

            @block.scalar
            def _(act):
                def take_low(b):
                    act.wait_ge(low_done, b + 1)
                    act.copy(low[:, b, :], ps[:, LOW_BANK + b % 2, 0:F2_HR]).then_inc(low_ready, 1)

                weights.split_hi(act)
                for b in range(B):
                    turned.act(act, [b])
                    if b >= 1:
                        take_low(b - 1)
                take_low(B - 1)
                act.wait_ge(shifted_ready, 1)
                act.activation(weight[:, :, :], weight[:, :, :], ACT.Exp).then_inc(exp_ready, 1)
                for h in range(HALVES):
                    act.wait_ge(low_turned, h + 1)
                    act.copy(lt_hi[:, h * HT:(h + 1) * HT], ps[:, T_BANK + h, :]).then_inc(lt_hi_ready, 1)

            @block.tensor
            def _(pe):
                def lower(b):
                    if b == 0:
                        weights.wait(pe, 0)
                    pe.wait_ge(turned.lo_ready, b + 1)
                    if b >= 2:
                        pe.wait_ge(logit_ready, b - 1)
                    rows = slice(b * P, (b + 1) * P)
                    for c in range(NC):
                        mm = matmul_split(pe, ps[:, LOW_BANK + b % 2, 0:F2_N], hi[:, c, rows], lo[:, c, rows],
                                          a_hi[:, c, :], a_lo[:, c, :], c == 0, c == NC - 1)
                    mm.then_inc(low_done, 1)

                for b in range(B):
                    turned.pe(pe, [b])
                    if b >= 1:
                        lower(b - 1)
                lower(B - 1)
                for h in range(HALVES):
                    pe.wait_ge(scaled_ready, h + 1)
                    for i in range(HB):
                        mm = pe.transpose(ps[:, T_BANK + h, i * P:(i + 1) * P], low[:, h * HB + i, :],
                                          core.ident[:, :])
                    mm.then_inc(low_turned, 1)
                weights.wait(pe, 1)
                for b in range(B):
                    pe.wait_ge(lt_lo_ready, b // HB + 1)
                    if b >= 2:
                        pe.wait_ge(x_ready, b - 1)
                    rows = slice(b * P, (b + 1) * P)
                    matmul_split(pe, ps[:, Y_BANK + b % 2, :], lt_hi[:, rows], lt_lo[:, rows], b_hi[:, :],
                                 b_lo[:, :], True, True).then_inc(y_done, 1)

            @block.vector
            def _(dve):
                steps = 0

                def after(instruction):
                    nonlocal steps
                    steps += 1
                    instruction.then_inc(step, 1)
                    dve.wait_ge(step, steps)

                def take_logit(b):
                    dve.wait_ge(low_ready, b + 1)
                    dve.tensor_tensor(logit[:, b, :], ps[:, LOW_BANK + b % 2, F2_HR:F2_N], br[:, :],
                                      ALU.add).then_inc(logit_ready, 1)

                def by_batch(c):
                    return c[:, :].unsqueeze(2).broadcast_to([P, B, F2_H])

                for b in range(B):
                    turned.dve(dve, [b])
                    if b == 1:
                        dve.wait_ge(br_loaded, 16)
                    if b >= 2:
                        take_logit(b - 2)
                take_logit(B - 2)
                take_logit(B - 1)
                dve.wait_ge(logit_ready, B)
                after(dve.tensor_reduce(col[:, :], logit[:, :, :], AX.X, ALU.max))
                dve.tensor_tensor(weight[:, :, :], logit[:, :, :], by_batch(col), ALU.subtract)\
                   .then_inc(shifted_ready, 1)
                dve.wait_ge(exp_ready, 1)
                after(dve.tensor_reduce(col[:, :], weight[:, :, :], AX.X, ALU.add))
                after(dve.reciprocal(col[:, :], col[:, :]))
                after(dve.scalar_tensor_tensor(out=weight[:, :, :], in0=weight[:, :, :],
                                               scalar=F2_SCALING * F2_H, in1=by_batch(col),
                                               op0=ALU.mult, op1=ALU.mult))
                for h in range(HALVES):
                    half = low[:, h * HB:(h + 1) * HB, :].rearrange("p b (h r) -> p (b h) r", h=F2_H)
                    w = weight[:, h * HB:(h + 1) * HB, :].rearrange("p b h -> p (b h)")
                    dve.tensor_tensor(half, half, w.unsqueeze(2).broadcast_to([P, HB * F2_H, F2_R]),
                                      ALU.mult).then_inc(scaled_ready, 1)
                for h in range(HALVES):
                    rows = slice(h * HT, (h + 1) * HT)
                    dve.wait_ge(lt_hi_ready, h + 1)
                    dve.tensor_tensor(lt_lo[:, rows], ps[:, T_BANK + h, :], lt_hi[:, rows].bitcast(F32),
                                      ALU.subtract).then_inc(lt_lo_ready, 1)
                for b in range(B):
                    dve.wait_ge(y_done, b + 1)
                    dve.tensor_tensor(core.x[:, b, :], ps[:, Y_BANK + b % 2, :], core.x[:, b, :], ALU.add)\
                       .then_inc(x_ready, 1)
                    dve.wait_ge(x_ready, b + 1)
                    ahead.dve(dve, b)


A3_JOBS = B * NC


def l3_attention(core):
    nc, dram, ps = core.nc, core.dram, core.psum
    scale = float(P) ** -0.5
    with ExitStack() as lay:
        c_hi = sbuf(nc, lay, "a3_c_hi", [P, B, D], F32R)
        c_lo = sbuf(nc, lay, "a3_c_lo", [P, B, D], F32R)
        v_hi = [sbuf(nc, lay, f"a3_v{h}_hi", [P, NC, HT], F32R) for h in range(HALVES)]
        v_lo = [sbuf(nc, lay, f"a3_v{h}_lo", [P, NC, HT], F32R) for h in range(HALVES)]
        pieces = []
        for h in range(HALVES):
            batches = slice(h * HB, (h + 1) * HB)
            pieces += [(dram["ctx_rows"][h], chunked(c_hi[:, batches, :]), chunked(c_lo[:, batches, :])),
                       (dram["ctx_turned"][h], chunked(v_hi[h][:, :, :]), chunked(v_lo[h][:, :, :]))]
        weights = Weights(core, lay, "a3", pieces)
        xn = sbuf(nc, lay, "a3_xn", [P, 2, D])
        q_hi = sbuf(nc, lay, "a3_q_hi", [P, 2, D], F32R)
        q_lo = sbuf(nc, lay, "a3_q_lo", [P, 2, D], F32R)
        e = sbuf(nc, lay, "a3_e", [P, 2, D])
        et_hi = sbuf(nc, lay, "a3_et_hi", [P, 2, NC, D], F32R)
        et_lo = sbuf(nc, lay, "a3_et_lo", [P, 2, NC, D], F32R)
        negmax = sbuf(nc, lay, "a3_negmax", [P, A3_JOBS])
        shift = sbuf(nc, lay, "a3_shift", [P, A3_JOBS])
        total = sbuf(nc, lay, "a3_total", [P, A3_JOBS])
        inv = sbuf(nc, lay, "a3_inv", [P, A3_JOBS])
        ahead = Ahead(core, lay, "a3")
        xn_ready, q_hi_ready, q_lo_ready = (core.sem(f"a3_{n}") for n in ("xn_ready", "q_hi_ready", "q_lo_ready"))
        scores_done, negmax_ready, shift_ready = (core.sem(f"a3_{n}") for n in
                                                  ("scores_done", "negmax_ready", "shift_ready"))
        exp_ready, inv_ready, e_ready = (core.sem(f"a3_{n}") for n in ("exp_ready", "inv_ready", "e_ready"))
        e_turned, et_hi_ready, et_lo_ready = (core.sem(f"a3_{n}") for n in
                                              ("e_turned", "et_hi_ready", "et_lo_ready"))
        y_done, x_ready = core.sem("a3_y_done"), core.sem("a3_x_ready")
        S_BANK, T_BANK, Y_BANK = 0, 2, 4

        def turned_bank(j):
            return ps[:, T_BANK + j % 2, :].rearrange("p (m n) -> p m n", m=NC)

        def columns(part, j):
            b, n = divmod(j, NC)
            return part[:, b % 2, :, n * P:(n + 1) * P]

        with nc.Block() as block:
            @block.sync
            def _(sp):
                weights.load(sp)

            @block.gpsimd
            def _(pool):
                def query_lo(b):
                    pool.wait_ge(q_hi_ready, b + 1)
                    if b >= 2:
                        pool.wait_ge(scores_done, NC * (b - 1))
                    pool.tensor_tensor(q_lo[:, b % 2, :], xn[:, b % 2, :], q_hi[:, b % 2, :].bitcast(F32),
                                       ALU.subtract).then_inc(q_lo_ready, 1)

                weights.split_lo(pool, [0])
                query_lo(0)
                weights.split_lo(pool, [1])
                for b in range(1, B):
                    query_lo(b)
                    if b <= HALVES:
                        weights.split_lo(pool, [1 + b])
                ahead.pool(pool)

            @block.scalar
            def _(act):
                def query_hi(b):
                    act.wait_ge(xn_ready, b + 1)
                    if b >= 2:
                        act.wait_ge(scores_done, NC * (b - 1))
                    act.copy(q_hi[:, b % 2, :], xn[:, b % 2, :]).then_inc(q_hi_ready, 1)

                def exp(j):
                    act.wait_ge(shift_ready, j + 1)
                    if j >= 2:
                        act.wait_ge(e_turned, j - 1)
                    act.activation(e[:, j % 2, :], ps[:, S_BANK + j % 2, :], ACT.Exp,
                                   bias=shift[:, j:j + 1], scale=scale,
                                   accum_out=total[:, j:j + 1]).then_inc(exp_ready, 1)

                def turned_hi(j):
                    act.wait_ge(e_turned, j + 1)
                    if j // NC >= 2:
                        act.wait_ge(y_done, j // NC - 1)
                    act.copy(columns(et_hi, j), turned_bank(j)).then_inc(et_hi_ready, 1)

                weights.split_hi(act, [0])
                query_hi(0)
                weights.split_hi(act, [1])
                for j in range(A3_JOBS):
                    exp(j)
                    if j >= 1:
                        turned_hi(j - 1)
                    if j % NC == 1 and j // NC + 1 < B:
                        query_hi(j // NC + 1)
                    if j in (0, 4):
                        weights.split_hi(act, [2 + j // 4])
                turned_hi(A3_JOBS - 1)

            @block.vector
            def _(dve):
                def query(b):
                    if b >= 2:
                        dve.wait_ge(q_lo_ready, b - 1)
                    dve.tensor_scalar(xn[:, b % 2, :], core.x[:, b, :], core.mean(b), core.rstd(b),
                                      ALU.subtract, ALU.mult).then_inc(xn_ready, 1)

                def maximum(j):
                    dve.wait_ge(scores_done, j + 1)
                    dve.tensor_reduce(negmax[:, j:j + 1], ps[:, S_BANK + j % 2, :], AX.X, ALU.max,
                                      negate=True).then_inc(negmax_ready, 1)
                    dve.wait_ge(negmax_ready, j + 1)
                    dve.tensor_scalar(shift[:, j:j + 1], negmax[:, j:j + 1], scale, None, ALU.mult)\
                       .then_inc(shift_ready, 1)

                def invert(j):
                    dve.wait_ge(exp_ready, j + 1)
                    dve.reciprocal(inv[:, j:j + 1], total[:, j:j + 1]).then_inc(inv_ready, 1)

                def divide(j):
                    dve.wait_ge(inv_ready, j + 1)
                    dve.tensor_scalar(e[:, j % 2, :], e[:, j % 2, :], inv[:, j:j + 1], None, ALU.mult)\
                       .then_inc(e_ready, 1)

                def turned_lo(j):
                    dve.wait_ge(et_hi_ready, j + 1)
                    dve.tensor_tensor(columns(et_lo, j), turned_bank(j), columns(et_hi, j).bitcast(F32),
                                      ALU.subtract).then_inc(et_lo_ready, 1)

                def add(b):
                    dve.wait_ge(y_done, b + 1)
                    dve.tensor_tensor(core.x[:, b, :], ps[:, Y_BANK + b % 2, :], core.x[:, b, :], ALU.add)\
                       .then_inc(x_ready, 1)
                    dve.wait_ge(x_ready, b + 1)
                    ahead.dve(dve, b)

                query(0)
                for j in range(A3_JOBS):
                    b, n = divmod(j, NC)
                    maximum(j)
                    if j >= 1:
                        invert(j - 1)
                        divide(j - 1)
                    if n == 0 and b + 1 < B:
                        query(b + 1)
                    if j >= 2:
                        turned_lo(j - 2)
                    if n == 0 and b >= 2:
                        add(b - 2)
                invert(A3_JOBS - 1)
                divide(A3_JOBS - 1)
                turned_lo(A3_JOBS - 2)
                turned_lo(A3_JOBS - 1)
                add(B - 2)
                add(B - 1)

            @block.tensor
            def _(pe):
                def scores(j):
                    b, n = divmod(j, NC)
                    if n == 0:
                        pe.wait_ge(q_lo_ready, b + 1)
                        if b % HB == 0:
                            weights.wait(pe, 2 * (b // HB))
                    if j >= 2:
                        pe.wait_ge(exp_ready, j - 1)
                    cols = slice(n * P, (n + 1) * P)
                    matmul_split(pe, ps[:, S_BANK + j % 2, :], c_hi[:, b, cols], c_lo[:, b, cols],
                                 q_hi[:, b % 2, :], q_lo[:, b % 2, :], True, True).then_inc(scores_done, 1)

                def turn(j):
                    pe.wait_ge(e_ready, j + 1)
                    if j >= 2:
                        pe.wait_ge(et_lo_ready, j - 1)
                    for m in range(NC):
                        mm = pe.transpose(turned_bank(j)[:, m, :], e[:, j % 2, m * P:(m + 1) * P],
                                          core.ident[:, :])
                    mm.then_inc(e_turned, 1)

                def attend(b, chunks):
                    h, i = divmod(b, HB)
                    if i == 0:
                        weights.wait(pe, 2 * h + 1)
                    pe.wait_ge(et_lo_ready, NC * (b + 1))
                    if b >= 2:
                        pe.wait_ge(x_ready, b - 1)
                    for m in chunks:
                        mm = matmul_split(pe, ps[:, Y_BANK + b % 2, :], v_hi[h][:, m, i * P:(i + 1) * P],
                                          v_lo[h][:, m, i * P:(i + 1) * P], et_hi[:, b % 2, m, :],
                                          et_lo[:, b % 2, m, :], m == 0, m == NC - 1)
                    if NC - 1 in chunks:
                        mm.then_inc(y_done, 1)

                scores(0)
                for j in range(A3_JOBS):
                    if j + 1 < A3_JOBS:
                        scores(j + 1)
                    if j >= 1:
                        turn(j - 1)
                    if j % NC >= 2 and j // NC >= 1:
                        attend(j // NC - 1, (0, 1) if j % NC == 2 else (2, 3))
                turn(A3_JOBS - 1)
                attend(B - 1, range(NC))


F3_INT, F3_LAT, F3_E = 1024, 256, 8
F3_IC, F3_LC = F3_INT // P, F3_LAT // P
F3_RAW = 1024


def l3_ffn(core):
    nc, dram, ps = core.nc, core.dram, core.psum
    with ExitStack() as lay:
        hi = sbuf(nc, lay, "f3_xn_hi", [P, NC, T], F32R)
        lo = sbuf(nc, lay, "f3_xn_lo", [P, NC, T], F32R)
        turned = NormTurned(core, lay, "f3", hi, lo)

        def pair(name, shape):
            return (sbuf(nc, lay, f"f3_{name}_hi", shape, F32R), sbuf(nc, lay, f"f3_{name}_lo", shape, F32R))

        up, down = pair("up", [P, NC, F3_INT]), pair("down", [P, F3_IC, D])
        fc1, fc2 = pair("fc1", [P, NC, F3_LAT]), pair("fc2", [P, F3_LC, D])
        expert, gate = pair("expert", [P, F3_LC, F3_LAT]), pair("gate", [P, NC, F3_E])
        latent, routed = pair("latent", [P, F3_LC, HT]), pair("routed", [P, F3_LC, HT])
        h = pair("h", [P, F3_IC, HT])
        relu = sbuf(nc, lay, "f3_relu", [P, 2, HT])
        gamma = sbuf(nc, lay, "f3_gamma", [P, D])
        beta = sbuf(nc, lay, "f3_beta", [P, D])
        side = sbuf(nc, lay, "f3_side", [P, D])
        both = turned.xn
        top = sbuf(nc, lay, "f3_top", [P, B, F3_E])
        rw = sbuf(nc, lay, "f3_rw", [P, B])
        norm = Norm(core, lay, "f3o")

        def piece(name, parts, a, b):
            n = parts[0].shape[2]
            return (dram[name][:, a * n:b * n], chunked(parts[0][:, a:b, :]), chunked(parts[1][:, a:b, :]))

        pieces = [piece("f3_fc1", fc1, 0, NC), piece("f3_gate", gate, 0, NC),
                  piece("f3_expert", expert, 0, F3_LC)]
        pieces += [piece("f3_up", up, c, c + 1) for c in range(NC)]
        pieces += [piece("f3_fc2", fc2, 0, F3_LC)]
        pieces += [piece("f3_down", down, c, c + 2) for c in range(0, F3_IC, 2)]
        FC1, GATE, EXPERT, UP, FC2, DOWN = 0, 1, 2, 3, 3 + NC, 4 + NC
        LAST_UP, LAST = FC2 - 1, len(pieces) - 1
        weights = Weights(core, lay, "f3", pieces, F3_RAW)
        order = [("fc1", 0), ("fc1", 1), ("up", 0), ("expert", 0), ("expert", 1)]
        order += [("up", m) for m in range(1, F3_IC)]
        jobs = [(half, kind, m) for half in range(HALVES) for kind, m in order]
        PER_HALF = len(order)
        SPLIT_AT = range(F3_LC, F3_LC + len(pieces) - FC2)

        def before(n, kinds):
            return sum(k in kinds for _, k, _ in jobs[:n])

        cols_loaded = core.sem("f3_cols_loaded")
        logits_done, top_ready, rw_ready = (core.sem(f"f3_{n}") for n in ("logits_done", "top_ready", "rw_ready"))
        job_done = core.sem("f3_job_done")
        hi_ready, lo_ready = core.sem("f3_hi_ready"), core.sem("f3_lo_ready")
        relu_ready, square_ready = core.sem("f3_relu_ready"), core.sem("f3_square_ready")
        h_hi_ready, h_lo_ready = core.sem("f3_h_hi_ready"), core.sem("f3_h_lo_ready")
        side_done, side_ready = core.sem("f3_side_done"), core.sem("f3_side_ready")
        main_done, both_ready = core.sem("f3_main_done"), core.sem("f3_both_ready")
        unit_ready, gain_ready, out_ready = (core.sem(f"f3_{n}") for n in ("unit_ready", "gain_ready", "out_ready"))
        x_ready = core.sem("f3_x_ready")
        JOB_BANK, G_BANK, SIDE_BANK, MAIN_BANK = 2, 4, 5, 6
        SPLIT = ("fc1", "expert")

        def split_out(kind):
            return latent if kind == "fc1" else routed

        with nc.Block() as block:
            @block.sync
            def _(sp):
                weights.load(sp)
                sp.dma_start(gamma[:, :], dram["f3_gamma"]).then_inc(cols_loaded, 16)
                sp.dma_start(beta[:, :], dram["f3_beta"]).then_inc(cols_loaded, 16)

            @block.gpsimd
            def _(pool):
                weights.split_lo(pool, range(LAST_UP + 1))

                def square_lo(n):
                    i = before(n, ("up",))
                    pool.wait_ge(h_hi_ready, i + 1)
                    pool.tensor_tensor(h[1][:, jobs[n][2], :], relu[:, i % 2, :],
                                       h[0][:, jobs[n][2], :].bitcast(F32), ALU.subtract).then_inc(h_lo_ready, 1)

                def gain(b):
                    norm.scale(pool, b)
                    pool.wait_ge(cols_loaded, 32)
                    pool.wait_ge(unit_ready, b + 1)
                    pool.tensor_tensor(both[:, b % 2, :], both[:, b % 2, :], gamma[:, :], ALU.mult)\
                        .then_inc(gain_ready, 1)
                    pool.wait_ge(gain_ready, b + 1)
                    pool.tensor_tensor(both[:, b % 2, :], both[:, b % 2, :], beta[:, :], ALU.add)\
                        .then_inc(out_ready, 1)

                for half in range(HALVES):
                    for n in range(half * PER_HALF, (half + 1) * PER_HALF):
                        if n in SPLIT_AT:
                            weights.split_lo(pool, [FC2 + n - SPLIT_AT[0]])
                        if jobs[n][1] == "up":
                            square_lo(n)
                    for b in range(half * HB, (half + 1) * HB):
                        gain(b)

            @block.scalar
            def _(act):
                def evacuate(n):
                    half, kind, m = jobs[n]
                    act.wait_ge(job_done, n + 1)
                    if kind in SPLIT:
                        if half:
                            act.wait_ge(side_done, HB)
                        act.copy(split_out(kind)[0][:, m, :], ps[:, JOB_BANK + n % 2, :]).then_inc(hi_ready, 1)
                    else:
                        i = before(n, ("up",))
                        if i >= 2:
                            act.wait_ge(h_lo_ready, i - 1)
                        act.activation(relu[:, i % 2, :], ps[:, JOB_BANK + n % 2, :], ACT.Relu)\
                           .then_inc(relu_ready, 1)
                        act.wait_ge(square_ready, i + 1)
                        if half:
                            act.wait_ge(main_done, HB)
                        act.copy(h[0][:, m, :], relu[:, i % 2, :]).then_inc(h_hi_ready, 1)

                def take_side(b):
                    act.wait_ge(side_done, b + 1)
                    act.wait_ge(rw_ready, 1)
                    if b >= 1:
                        act.wait_ge(both_ready, b)
                    act.mul(side[:, :], ps[:, SIDE_BANK, :], rw[:, b:b + 1]).then_inc(side_ready, 1)

                weights.split_hi(act, [FC1])
                turned.act(act, range(0, 2))
                weights.split_hi(act, [GATE, EXPERT])
                turned.act(act, range(2, HB))
                weights.split_hi(act, [UP])
                for half in range(HALVES):
                    for n in range(half * PER_HALF, (half + 1) * PER_HALF):
                        evacuate(n)
                        if n == F3_LC - 1:
                            for b in range(HB, B):
                                turned.act(act, [b])
                                if UP + b - HB + 1 <= LAST_UP:
                                    weights.split_hi(act, [UP + b - HB + 1])
                        if n in SPLIT_AT:
                            weights.split_hi(act, [FC2 + n - SPLIT_AT[0]])
                    for b in range(half * HB, (half + 1) * HB):
                        take_side(b)

            @block.vector
            def _(dve):
                def evacuate(n):
                    half, kind, m = jobs[n]
                    if kind in SPLIT:
                        dve.wait_ge(hi_ready, before(n, SPLIT) + 1)
                        dve.tensor_tensor(split_out(kind)[1][:, m, :], ps[:, JOB_BANK + n % 2, :],
                                          split_out(kind)[0][:, m, :].bitcast(F32), ALU.subtract)\
                           .then_inc(lo_ready, 1)
                    else:
                        i = before(n, ("up",))
                        dve.wait_ge(relu_ready, i + 1)
                        dve.tensor_tensor(relu[:, i % 2, :], relu[:, i % 2, :], relu[:, i % 2, :], ALU.mult)\
                           .then_inc(square_ready, 1)

                def add_side(b):
                    dve.wait_ge(main_done, b + 1)
                    dve.wait_ge(side_ready, b + 1)
                    if b >= 2:
                        dve.wait_ge(x_ready, b - 1)
                    dve.tensor_tensor(both[:, b % 2, :], ps[:, MAIN_BANK + b % 2, :], side[:, :], ALU.add)\
                       .then_inc(both_ready, 1)
                    dve.wait_ge(both_ready, b + 1)
                    norm.stats(dve, b, both[:, b % 2, :])
                    dve.wait_ge(norm.rstd_ready, b + 1)
                    dve.tensor_scalar(both[:, b % 2, :], both[:, b % 2, :], norm.mean(b), norm.rstd(b),
                                      ALU.subtract, ALU.mult).then_inc(unit_ready, 1)

                def add_x(b):
                    dve.wait_ge(out_ready, b + 1)
                    dve.tensor_tensor(core.x[:, b, :], both[:, b % 2, :], core.x[:, b, :], ALU.add)\
                       .then_inc(x_ready, 1)

                def routing():
                    dve.wait_ge(logits_done, 1)
                    for b in range(B):
                        ins = dve.max(top[:, b, :], ps[:, G_BANK, b * F3_E:(b + 1) * F3_E])
                    ins.then_inc(top_ready, 1)
                    dve.wait_ge(top_ready, 1)
                    dve.tensor_tensor(rw[:, :], top[:, :, 0], top[:, :, 1], ALU.add).then_inc(rw_ready, 1)

                turned.dve(dve, range(0, HB + 1))
                for half in range(HALVES):
                    for n in range(half * PER_HALF, (half + 1) * PER_HALF):
                        evacuate(n)
                        if n == F3_LC - 1:
                            turned.dve(dve, range(HB + 1, B))
                        if n == PER_HALF - 1:
                            routing()
                    for b in range(half * HB, (half + 1) * HB):
                        add_side(b)
                        if b % HB >= 1:
                            add_x(b - 1)
                    add_x((half + 1) * HB - 1)

            @block.tensor
            def _(pe):
                def product(n):
                    half, kind, m = jobs[n]
                    if n >= 2:
                        if jobs[n - 2][1] in SPLIT:
                            pe.wait_ge(lo_ready, before(n - 2, SPLIT) + 1)
                        else:
                            pe.wait_ge(relu_ready, before(n - 2, ("up",)) + 1)
                    rows = slice(half * HT, (half + 1) * HT)
                    w = slice(m * P, (m + 1) * P)
                    if kind == "expert":
                        pe.wait_ge(lo_ready, F3_LC + 2 * F3_LC * half)
                    parts, count = {"fc1": (fc1, NC), "expert": (expert, F3_LC), "up": (up, NC)}[kind]
                    for c in range(count):
                        mov = ((latent[0][:, c, :], latent[1][:, c, :]) if kind == "expert"
                               else (hi[:, c, rows], lo[:, c, rows]))
                        mm = matmul_split(pe, ps[:, JOB_BANK + n % 2, :], parts[0][:, c, w], parts[1][:, c, w],
                                          *mov, c == 0, c == count - 1)
                    mm.then_inc(job_done, 1)

                def outputs(half):
                    pe.wait_ge(lo_ready, 2 * F3_LC * (half + 1))
                    for i in range(HB):
                        b = half * HB + i
                        rows = slice(i * P, (i + 1) * P)
                        if b >= 1:
                            pe.wait_ge(side_ready, b)
                        for c in range(F3_LC):
                            mm = matmul_split(pe, ps[:, SIDE_BANK, :], routed[0][:, c, rows],
                                              routed[1][:, c, rows], fc2[0][:, c, :], fc2[1][:, c, :],
                                              c == 0, c == F3_LC - 1)
                        mm.then_inc(side_done, 1)
                        if b >= 2:
                            pe.wait_ge(both_ready, b - 1)
                        if i == 0:
                            pe.wait_ge(h_lo_ready, F3_IC * (half + 1))
                        for c in range(F3_IC):
                            mm = matmul_split(pe, ps[:, MAIN_BANK + b % 2, :], h[0][:, c, rows], h[1][:, c, rows],
                                              down[0][:, c, :], down[1][:, c, :], c == 0, c == F3_IC - 1)
                        mm.then_inc(main_done, 1)

                def logits():
                    for b in range(B):
                        rows = slice(b * P, (b + 1) * P)
                        for c in range(NC):
                            mm = matmul_split(pe, ps[:, G_BANK, b * F3_E:(b + 1) * F3_E], hi[:, c, rows],
                                              lo[:, c, rows], gate[0][:, c, :], gate[1][:, c, :],
                                              c == 0, c == NC - 1)
                    mm.then_inc(logits_done, 1)

                turned.pe(pe, range(0, HB))
                weights.wait(pe, FC1)
                pe.wait_ge(turned.lo_ready, HB)
                for n in range(F3_LC):
                    product(n)
                turned.pe(pe, range(HB, B))
                weights.wait(pe, LAST_UP)
                for n in range(F3_LC, PER_HALF):
                    product(n)
                    if n == F3_LC:
                        pe.wait_ge(turned.lo_ready, B)
                        logits()
                weights.wait(pe, LAST)
                outputs(0)
                for n in range(PER_HALF, 2 * PER_HALF):
                    product(n)
                outputs(1)


def more_layouts(a, out, np):
    f32 = np.float32

    def rows(w):
        return w.reshape(-1, P, w.shape[1]).transpose(1, 0, 2).reshape(P, -1)

    wg = np.concatenate([a["L0_ffn_Sg"][None], a["L0_ffn_Wg"]])
    wu = np.concatenate([a["L0_ffn_Su"][None], a["L0_ffn_Wu"]])
    wd = np.concatenate([a["L0_ffn_Sd"][None], a["L0_ffn_Wd"]])
    gu = np.stack([wg, wu], 1).reshape(F0_ALL, 2, F0_I, NC, P)
    out["f0_gu"] = gu.transpose(0, 4, 3, 1, 2).reshape(F0_ALL, P, F0_GU)
    out["f0_dn"] = wd.transpose(0, 2, 1).reshape(F0_ALL, F0_IC, P, D).transpose(0, 2, 1, 3)\
        .reshape(F0_ALL, P, F0_IC * D)
    out["f0_gate"] = a["L0_ffn_gate_w"].T.reshape(NC, P, F0_E).transpose(1, 0, 2)
    out["f0_bias"] = np.broadcast_to(a["L0_ffn_bias"], (P, F0_E))
    out["f0_rank"] = np.broadcast_to(np.arange(F0_E, 0, -1, dtype=f32), (P, F0_E))

    halves = a["ctx_4096"].reshape(HALVES, HB, P, D)
    out["ctx_turned"] = np.stack([rows(h.reshape(HT, D).T) for h in halves])
    out["ctx_rows"] = halves.transpose(0, 2, 1, 3).reshape(HALVES, P, HB * D)
    out["a1_wk"], out["a1_wq"] = rows(a["L1_xattn_Wk"].T), rows(a["L1_xattn_Wq"].T)
    out["a1_bias"] = np.stack([a["L1_xattn_bk"].reshape(NC, P).T, a["L1_xattn_bq"].reshape(NC, P).T], 1)
    out["f1_w"] = a["L1_ffn_W"].reshape(NC, P, D).transpose(1, 0, 2)
    for name, key in (("f1_bias", "L1_ffn_bias"), ("f1_low", "L1_ffn_calib_min"), ("f1_high", "L1_ffn_calib_max")):
        out[name] = np.broadcast_to(a[key], (P, D))

    sel_k = np.zeros((A2_KV, A2_DH, 2, A2_PAIRS, 2, A2_SLOT), f32)
    sel_q = np.zeros((2, A2_REP, A2_DH, 2, A2_REP, 2, A2_SLOT), f32)
    for d in range(A2_DH):
        for part in range(3):
            for c in range(A2_KV):
                sel_k[c, d, int(part == 1), c // 2, c % 2, part * A2_DH + d] = 1.0
            for r in range(2):
                for m in range(A2_REP):
                    sel_q[r, m, d, int(part == 2), m, r, part * A2_DH + d] = 1.0
    out["a2_sel_k"], out["a2_sel_q"] = sel_k.reshape(P, -1), sel_q.reshape(P, -1)
    ones_row = np.zeros((2, A2_SLOT, 1), f32)
    ones_row[:, A2_MAX_ROW] = 1.0
    out["a2_ones_row"] = ones_row.reshape(P, 1)
    out["a2_wq"], out["a2_wo"] = rows(a["L2_xattn_Wq"]), rows(a["L2_xattn_Wo"])
    out["a2_wkv"] = rows(np.concatenate([a["L2_xattn_Wk"], a["L2_xattn_Wv"]], 1))

    out["f2_a"] = rows(np.concatenate([a["L2_ffn_A"].reshape(F2_HR, D), a["L2_ffn_Wr"]]).T)
    out["f2_b"] = a["L2_ffn_B"].transpose(0, 2, 1).reshape(F2_HR, D)
    out["f2_br"] = np.broadcast_to(a["L2_ffn_br"], (P, F2_H))
    for name, key in (("f3_up", "up_w"), ("f3_down", "down_w"), ("f3_fc1", "fc1_w"), ("f3_fc2", "fc2_w"),
                      ("f3_expert", "expert_w"), ("f3_gate", "gate_w")):
        out[name] = rows(a[f"L3_ffn_{key}"])
    for name in ("gamma", "beta"):
        out[f"f3_{name}"] = np.broadcast_to(a[f"L3_ffn_ln_{name}"], (P, D))


LAYERS = [l0_attention, l0_ffn, l1_attention, l1_ffn, l2_attention, l2_ffn,
          l3_attention, l3_ffn]


def build(nc, dram):
    with ExitStack() as ctx:
        core = Core(nc, ctx, dram)
        load_inputs(core)
        for layer in LAYERS:
            layer(core)
            core.end_layer()
        store_output(core)


def laid_out(inputs):
    import numpy as np

    a = {k: np.asarray(v) for k, v in inputs.items()}
    f32 = np.float32
    out = {"x": a["x"], "ctx": a["ctx_4096"], "mask": a["mask_Bx1x4096_ff1"].reshape(B, D)}

    wq = np.zeros((P, A0_GROUPS, A0_PER_GROUP, A0_SLOT), f32)
    wk, cols = np.zeros_like(wq), np.zeros((A0_PER_GROUP, A0_SLOT, A0_COLS), f32)
    for h in range(A0_HEADS):
        g, r = divmod(h, A0_PER_GROUP)
        e = slice(h * A0_DH, (h + 1) * A0_DH)
        for part in range(3):
            rows = slice(part * A0_DH, (part + 1) * A0_DH)
            wq[:, g, r, rows] = a["L0_xattn_Wq"].T[:, e]
            wk[:, g, r, rows] = a["L0_xattn_Wk"].T[:, e]
            cols[r, rows, C_BQ + g] = a["L0_xattn_bq"][e]
            cols[r, rows, C_BK + g] = a["L0_xattn_bk"][e]
            if part == 2:
                cols[r, rows, C_SBQ + g] = a["L0_xattn_bq"][e]
    cols[:, 2 * A0_DH:3 * A0_DH, C_SELQ] = 1.0
    cols[:, A0_DH:2 * A0_DH, C_SELK] = 1.0
    cols[:, 0:3 * A0_DH, C_MASKC] = 1.0
    cols[:, A0_MAX_ROW, C_MASKA] = 1.0
    cols[:, A0_MASK_ROW, C_MASKC] = -1.0
    cols[:, A0_MASK_ROW, C_MASKA] = 1.0
    cols[:, A0_MAX_ROW, C_BK:C_BK + A0_GROUPS] = 1.0
    cols[:, A0_MASK_ROW, C_BK:C_BK + A0_GROUPS] = A0_OFF
    cols[:, A0_MASK_ROW, C_BQ:C_BQ + A0_GROUPS] = 1.0
    cols = cols.reshape(P, A0_COLS)
    cols[:, C_BO] = a["L0_xattn_bo"]
    out["a0_wq"], out["a0_wk"] = (w.reshape(P, A0_GROUPS, P) for w in (wq, wk))
    out["a0_wo"], out["a0_cols"] = a["L0_xattn_Wo"].T, cols
    out["a0_wv"] = a["L0_xattn_Wv"].T
    out["a0_bv"] = np.broadcast_to(a["L0_xattn_bv"], (P, A0_DK))
    more_layouts(a, out, np)
    return {k: np.ascontiguousarray(v) for k, v in out.items()}


def kernel(**inputs):
    import concourse.bacc as bacc
    from concourse.bass_utils import run_bass_kernel_spmd

    nc = bacc.Bacc("TRN2", target_bir_lowering=False, num_devices=1)
    arrays = {f"in_{k}": v for k, v in laid_out(inputs).items()}
    dram = {k[3:]: nc.dram_tensor(k, v.shape, mybir.dt.from_np(v.dtype), kind="ExternalInput").ap()
            for k, v in arrays.items()}
    dram["out"] = nc.dram_tensor("out", (B, P, D), F32, kind="ExternalOutput").ap()
    build(nc, dram)
    return run_bass_kernel_spmd(nc, [arrays], core_ids=[0]).results[0]["out"]
```

```python
import concourse.bass as bass
from concourse import mybir
from contextlib import ExitStack

F32 = mybir.dt.float32
F32R = mybir.dt.float32r
BF16 = mybir.dt.bfloat16
ALU = mybir.AluOpType
ACT = mybir.ActivationFunctionType
AX = mybir.AxisListType

P = 128
B = 8
D = 512
NC = D // P
T = B * P
HALVES = 2
HB = B // HALVES
HT = HB * P
BANK = 512
RAW = 2048
LN_EPS = 1e-5


class Core:

    def __init__(self, nc, ctx, dram):
        self.nc, self.ctx, self.dram, self.sems = nc, ctx, dram, []
        self.x = ctx.enter_context(nc.sbuf_tensor("x_res", [P, B, D], F32))
        self.ident = ctx.enter_context(nc.sbuf_tensor("ident", [P, P], F32))
        self.eps = ctx.enter_context(nc.sbuf_tensor("eps", [P, B], F32))
        self.neg_half = ctx.enter_context(nc.sbuf_tensor("neg_half", [P, B], F32))
        self.stat = ctx.enter_context(nc.sbuf_tensor("stat", [P, B, 6], F32))
        self.mv = [ctx.enter_context(nc.sbuf_tensor(f"mean_var_{i}", [P, B, 2], F32)) for i in range(2)]
        self.rs = [ctx.enter_context(nc.sbuf_tensor(f"rstd_{i}", [P, B], F32)) for i in range(2)]
        self.next = 0
        self.raw = ctx.enter_context(nc.sbuf_tensor("raw", [P, 2, RAW], F32))
        self.upcoming = []
        self.psum = ctx.enter_context(nc.psum_tensor("banks", [P, 8, BANK], F32))

    def sem(self, name):
        self.sems.append(self.nc.alloc_semaphore(name=name))
        return self.sems[-1]

    def prefetch(self, sp, name, sources=None):
        sources = self.upcoming if sources is None else sources
        if sources:
            prefetched = self.sem(f"{name}_prefetched")
            for i, src in enumerate(sources):
                sp.dma_start(self.raw[:, i, 0:src.shape[1]], src).then_inc(prefetched, 16)
            sp.wait_ge(prefetched, 16 * len(sources))

    def mean(self, b):
        return self.mv[1 - self.next][:, b, 0:1]

    def means(self):
        return self.mv[1 - self.next][:, :, 0]

    def rstd(self, b):
        return self.rs[1 - self.next][:, b:b + 1]

    def end_layer(self):
        self.next = 1 - self.next
        self.nc.clear_and_free_semaphores(self.sems)
        self.nc.all_engine_barrier()
        self.sems = []


def sbuf(nc, scope, name, shape, dt=F32):
    return scope.enter_context(nc.sbuf_tensor(name, shape, dt))


class Norm:

    def __init__(self, core, scope, name, stat=None, mv=None, rs=None):
        self.core = core
        self.stat = sbuf(core.nc, scope, f"{name}_stat", [P, B, 6]) if stat is None else stat
        self.mv = sbuf(core.nc, scope, f"{name}_mv", [P, B, 2]) if mv is None else mv
        self.ve = sbuf(core.nc, scope, f"{name}_var_eps", [P, B])
        self.rs = sbuf(core.nc, scope, f"{name}_rstd", [P, B]) if rs is None else rs
        self.stat_ready = core.sem(f"{name}_stat_ready")
        self.mv_ready = core.sem(f"{name}_mv_ready")
        self.ve_ready = core.sem(f"{name}_ve_ready")
        self.rstd_ready = core.sem(f"{name}_rstd_ready")

    def stats(self, dve, b, src):
        dve.bn_stats(self.stat[:, b, :], src).then_inc(self.stat_ready, 1)
        dve.wait_ge(self.stat_ready, b + 1)
        dve.bn_aggr(self.mv[:, b, :], self.stat[:, b, :]).then_inc(self.mv_ready, 1)

    def scale(self, pool, b):
        pool.wait_ge(self.mv_ready, b + 1)
        pool.tensor_tensor(self.ve[:, b:b + 1], self.mv[:, b, 1:2], self.core.eps[:, 0:1],
                           ALU.add).then_inc(self.ve_ready, 1)
        pool.wait_ge(self.ve_ready, b + 1)
        pool.tensor_tensor(self.rs[:, b:b + 1], self.ve[:, b:b + 1], self.core.neg_half[:, 0:1],
                           ALU.pow).then_inc(self.rstd_ready, 1)

    def mean(self, b):
        return self.mv[:, b, 0:1]

    def rstd(self, b):
        return self.rs[:, b:b + 1]


class Ahead(Norm):

    def __init__(self, core, scope, name):
        super().__init__(core, scope, f"{name}_ahead", core.stat, core.mv[core.next], core.rs[core.next])

    def dve(self, dve, b):
        self.stats(dve, b, self.core.x[:, b, :])

    def pool(self, pool):
        for b in range(B):
            self.scale(pool, b)


def load_inputs(core):
    with ExitStack() as lay:
        load_inputs_in(core, lay)
    core.end_layer()


def load_inputs_in(core, lay):
    nc = core.nc
    ahead = Ahead(core, lay, "in")
    loaded = [core.sem(f"x_loaded_{b}") for b in range(B)]
    const_ready = core.sem("const_ready")
    with nc.Block() as block:
        @block.sync
        def _(sp):
            for b in range(B):
                sp.dma_start(core.x[:, b, :], core.dram["x"][b]).then_inc(loaded[b], 16)
            core.prefetch(sp, "first")

        @block.vector
        def _(dve):
            for b in range(B):
                dve.wait_ge(loaded[b], 16)
                ahead.dve(dve, b)

        @block.gpsimd
        def _(pool):
            pool.memset(core.ident[:, :], 0.0).then_inc(const_ready, 1)
            pool.memset(core.eps[:, :], LN_EPS).then_inc(const_ready, 1)
            pool.memset(core.neg_half[:, :], -0.5).then_inc(const_ready, 1)
            pool.wait_ge(const_ready, 3)
            pool.affine_select(out=core.ident[:, :], in_=core.ident[:, :],
                               compare_op=ALU.not_equal, fill=1.0, base=0,
                               pattern=[[-1, P]], channel_multiplier=1)
            ahead.pool(pool)


def store_output(core):
    stored = core.sem("stored")
    with core.nc.Block() as block:
        @block.sync
        def _(sp):
            for b in range(B):
                sp.dma_start(core.dram["out"][b], core.x[:, b, :]).then_inc(stored, 16)
            sp.wait_ge(stored, 16 * B)


class NormTurned:

    def __init__(self, core, scope, name, hi, lo, bank=0):
        self.core, self.hi, self.lo, self.first_bank = core, hi, lo, bank
        self.xn = sbuf(core.nc, scope, f"{name}_turn_xn", [P, 2, D])
        self.xn_ready = core.sem(f"{name}_xn_ready")
        self.turned = core.sem(f"{name}_turned")
        self.hi_ready = core.sem(f"{name}_turned_hi_ready")
        self.lo_ready = core.sem(f"{name}_turned_lo_ready")

    def tile(self, part, b):
        return part[:, :, b * P:(b + 1) * P]

    def bank(self, b):
        return self.core.psum[:, self.first_bank + b % 2, :].rearrange("p (c t) -> p c t", c=NC)

    def act(self, act, batches=range(B)):
        for b in batches:
            act.wait_ge(self.turned, b + 1)
            act.copy(self.tile(self.hi, b), self.bank(b)).then_inc(self.hi_ready, 1)

    def pe(self, pe, batches=range(B)):
        for b in batches:
            pe.wait_ge(self.xn_ready, b + 1)
            if b >= 2:
                pe.wait_ge(self.lo_ready, b - 1)
            for c in range(NC):
                mm = pe.transpose(self.core.psum[:, self.first_bank + b % 2, c * P:(c + 1) * P],
                                  self.xn[:, b % 2, c * P:(c + 1) * P], self.core.ident[:, :])
            mm.then_inc(self.turned, 1)

    def dve(self, dve, batches=range(B)):
        for b in batches:
            if b >= 2:
                dve.wait_ge(self.turned, b - 1)
            dve.tensor_scalar(self.xn[:, b % 2, :], self.core.x[:, b, :], self.core.mean(b),
                              self.core.rstd(b), ALU.subtract, ALU.mult)\
               .then_inc(self.xn_ready, 1)
            if b >= 1:
                self.rest(dve, b - 1)
            if b == B - 1:
                self.rest(dve, b)

    def rest(self, dve, b):
        dve.wait_ge(self.hi_ready, b + 1)
        dve.tensor_tensor(self.tile(self.lo, b), self.bank(b), self.tile(self.hi, b).bitcast(F32),
                          ALU.subtract).then_inc(self.lo_ready, 1)


class Weights:

    def __init__(self, core, name, pieces):
        self.core, self.name, self.pieces, self.raw = core, name, pieces, core.raw
        self.loaded = [core.sem(f"{name}_loaded_{i}") for i in range(2)]
        self.hi_ready = core.sem(f"{name}_w_hi_ready")
        self.lo_ready = core.sem(f"{name}_w_lo_ready")

    def load(self, sp):
        for i, (src, _, _) in enumerate(self.pieces):
            if i >= 2:
                sp.wait_ge(self.lo_ready, i - 1)
                sp.dma_start(self.raw[:, i % 2, 0:src.shape[1]], src).then_inc(self.loaded[i % 2], 16)

    def prefetch(self, sp, sources=None):
        sp.wait_ge(self.lo_ready, len(self.pieces))
        self.core.prefetch(sp, self.name, sources)

    def split_hi(self, act, pieces=None):
        for i in range(len(self.pieces)) if pieces is None else pieces:
            src, hi, _ = self.pieces[i]
            if i >= 2:
                act.wait_ge(self.loaded[i % 2], 16 * (i // 2))
            act.copy(hi, self.raw[:, i % 2, 0:src.shape[1]]).then_inc(self.hi_ready, 1)

    def first_lo(self, dve):
        src, hi, lo = self.pieces[0]
        dve.wait_ge(self.hi_ready, 1)
        dve.tensor_tensor(lo, self.raw[:, 0, 0:src.shape[1]], hi.bitcast(F32),
                          ALU.subtract).then_inc(self.lo_ready, 1)

    def split_lo(self, pool, pieces=None):
        for i in range(len(self.pieces)) if pieces is None else pieces:
            src, hi, lo = self.pieces[i]
            if i == 1:
                pool.wait_ge(self.lo_ready, 1)
            pool.wait_ge(self.hi_ready, i + 1)
            if lo is None:
                if i:
                    pool.wait_ge(self.lo_ready, i)
                pool.sem_inc(self.lo_ready, 1)
            else:
                pool.tensor_tensor(lo, self.raw[:, i % 2, 0:src.shape[1]], hi.bitcast(F32),
                                   ALU.subtract).then_inc(self.lo_ready, 1)

    def wait(self, pe, i):
        pe.wait_ge(self.lo_ready, i + 1)


def matmul_split(pe, out, w_hi, w_lo, m_hi, m_lo, start, stop):
    pe.matmul(out, w_hi, m_hi, start=start, stop=False)
    pe.matmul(out, w_hi, m_lo, start=False, stop=False)
    return pe.matmul(out, w_lo, m_hi, start=False, stop=stop)


A0_WIN, A0_HEADS, A0_DH = 128, 8, 8
A0_DK = A0_HEADS * A0_DH
A0_SLOT, A0_GROUPS = 32, 2
A0_PER_GROUP = A0_HEADS // A0_GROUPS
A0_WINS = D // A0_WIN
A0_MAX_ROW, A0_MASK_ROW = 24, 25
A0_OFF = -float(2 ** 31)
C_SELQ, C_SELK, C_MASKC, C_MASKA, C_BO = 0, 1, 2, 3, 4
C_BQ, C_SBQ, C_BK = 5, 7, 9
A0_COLS = 11
A0_FIRST = (0, A0_GROUPS * P, 2 * A0_GROUPS * P, 2 * A0_GROUPS * P + A0_DK,
            2 * A0_GROUPS * P + 2 * A0_DK, 2 * A0_GROUPS * P + 2 * A0_DK + A0_COLS)


def l0_attention(core):
    nc, dram, ps = core.nc, core.dram, core.psum
    scale = float(A0_DH) ** -0.5
    with ExitStack() as lay:
        on_all = sbuf(nc, lay, "a0_on_all", [P, B, A0_WINS, A0_DK])
        wo = sbuf(nc, lay, "a0_wo", [A0_DK, P])
        out_mask = sbuf(nc, lay, "a0_out_mask", [P, B, D])
        gl = sbuf(nc, lay, "a0_gelu", [A0_DK, 2, D])
        tmp = sbuf(nc, lay, "a0_tmp", [P, 2, D])
        cols = sbuf(nc, lay, "a0_cols", [P, A0_COLS])
        loaded = core.sem("a0_loaded")
        ctx_loaded = [core.sem(f"a0_ctx_loaded_{h}") for h in range(HALVES)]
        mask_loaded, cols_ready = core.sem("a0_mask_loaded"), core.sem("a0_cols_ready")
        out_mask_loaded = core.sem("a0_out_mask_loaded")
        with ExitStack() as part:
            wq, wk, wv, bv, first_cols = (core.raw[:, 0, a:b] for a, b in zip(A0_FIRST, A0_FIRST[1:]))
            ctx = sbuf(nc, part, "a0_ctx", [P, B, D])
            late_mask = sbuf(nc, part, "a0_mask", [P, HB, D])
            xn = sbuf(nc, part, "a0_xn", [P, 2, D])
            q_lo = sbuf(nc, part, "a0_q_sel", [P, D], F32R)
            q = sbuf(nc, part, "a0_q", [P, 2, D], F32R)
            kf = sbuf(nc, part, "a0_kf", [P, 2, D])
            k_hi = sbuf(nc, part, "a0_k_sel", [P, 2, D], F32R)
            k = sbuf(nc, part, "a0_k", [P, 2, D], F32R)
            v = sbuf(nc, part, "a0_v", [P, 2, A0_WINS, A0_HEADS, A0_SLOT])
            mx = sbuf(nc, part, "a0_mx", [P, 2, A0_WINS, P])
            e = sbuf(nc, part, "a0_e", [P, 2, A0_PER_GROUP, D])
            osb = sbuf(nc, part, "a0_osb", [P, 2, D])
            rec = sbuf(nc, part, "a0_rec", [P, A0_WINS, A0_PER_GROUP])
            ahead = Ahead(core, part, "a0")
            zeroed = core.sem("a0_zeroed")
            xn_ready = core.sem("a0_xn_ready")
            mask_ready = core.sem("a0_mask_ready")
            first_mask_ready = core.sem("a0_first_mask_ready")
            proj_done = core.sem("a0_proj_done")
            v_done = core.sem("a0_v_done")
            q_sel_ready = core.sem("a0_q_sel_ready")
            q_ready = core.sem("a0_q_ready")
            kf_ready = core.sem("a0_kf_ready")
            k_sel_ready = core.sem("a0_k_sel_ready")
            k_ready = core.sem("a0_k_ready")
            v_ready = core.sem("a0_v_ready")
            scores_done = core.sem("a0_scores_done")
            max_ready = core.sem("a0_max_ready")
            max_turned = core.sem("a0_max_turned")
            q_max_ready = core.sem("a0_q_max_ready")
            keyed_done = core.sem("a0_keyed_done")
            exp_ready = core.sem("a0_exp_ready")
            pv_done = core.sem("a0_pv_done")
            o_ready = core.sem("a0_o_ready")
            o_turned = core.sem("a0_o_turned")
            rec_ready = core.sem("a0_rec_ready")
            on_ready = core.sem("a0_on_ready")
            on_turned = core.sem("a0_on_turned")
            gelu_ready = core.sem("a0_gelu_ready")
            out_done = core.sem("a0_out_done")
            tmp_ready = core.sem("a0_tmp_ready")
            x_ready = core.sem("a0_x_ready")
            Q_BANK, K_BANK, V_BANK, M_BANK, S_BANK = 0, 1, 2, 3, 4
            GELU_BANK, OUT_BANK = 4, 6
            UNITS = B * A0_GROUPS

            STEPS = 2 * UNITS
            PAIR = 2 * A0_SLOT

            def mask_of(b):
                if b < HB:
                    return core.raw[:, 1, b * D:(b + 1) * D]
                return late_mask[:, b - HB, :]

            def key_mask(eng, b, ready, before):
                eng.tensor_scalar(mask_of(b), mask_of(b), 0.0, cols[:, C_MASKC:C_MASKC + 1], ALU.is_gt,
                                  ALU.mult).then_inc(ready, 1)
                eng.wait_ge(ready, before + 1)
                eng.tensor_scalar(mask_of(b), mask_of(b), cols[:, C_MASKA:C_MASKA + 1], None,
                                  ALU.add).then_inc(ready, 1)

            def pair_rows(s):
                return slice(PAIR * (s % 2), PAIR * (s % 2 + 1))

            def s_banks(s):
                return slice(S_BANK + 2 * (s % 2), S_BANK + 2 * (s % 2) + 2)

            def turned_o():
                return ps[:, Q_BANK, :].rearrange("p (w r s) -> p w r s", w=A0_WINS, r=A0_PER_GROUP)

            with nc.Block() as block:
                @block.sync
                def _(sp):
                    for h in range(HALVES):
                        part_b = slice(h * B // HALVES, (h + 1) * B // HALVES)
                        sp.dma_start(ctx[:, part_b, :], dram["ctx"][part_b].rearrange("b p s -> p b s"))\
                          .then_inc(ctx_loaded[h], 16)
                        if h == 0:
                            sp.dma_start(late_mask[:, :, :], dram["mask"][HB:].partition_broadcast(P))\
                              .then_inc(mask_loaded, 16)
                    sp.dma_start(wo[:, :], dram["a0_wo"]).then_inc(loaded, 16)
                    sp.dma_start(out_mask[:, :, :], dram["mask"].partition_broadcast(P))\
                      .then_inc(out_mask_loaded, 16)
                    sp.wait_ge(proj_done, UNITS)
                    sp.wait_ge(v_ready, B)
                    sp.wait_ge(kf_ready, UNITS)
                    core.prefetch(sp, "a0")

                @block.gpsimd
                def _(pool):
                    pool.tensor_copy(cols[:, :], first_cols).then_inc(cols_ready, 1)
                    for i in range(2):
                        pool.memset(v[:, i, :, :, :], 0.0)
                    pool.memset(mx[:, :, :, :], 0.0).then_inc(zeroed, 1)
                    pool.wait_ge(zeroed, 1)
                    for i in range(2):
                        pool.memset(v[:, i, :, :, A0_DH:A0_DH + 1], 1.0).then_inc(zeroed, 1)
                    pool.wait_ge(cols_ready, 1)
                    for b in range(B):
                        if b >= HB:
                            pool.wait_ge(mask_loaded, 16)
                        if b >= 1:
                            key_mask(pool, b, mask_ready, 2 * b - 2)
                        for g in range(A0_GROUPS):
                            u = A0_GROUPS * b + g
                            pool.wait_ge(k_sel_ready, u + 1)
                            if u >= 2:
                                pool.wait_ge(keyed_done, 2 * u - 2)
                            pool.tensor_tensor(k[:, u % 2, :], kf[:, u % 2, :],
                                               k_hi[:, u % 2, :].bitcast(F32),
                                               ALU.subtract).then_inc(k_ready, 1)
                    ahead.pool(pool)

                @block.scalar
                def _(act):
                    act.wait_ge(cols_ready, 1)

                    def split(u):
                        g = u % A0_GROUPS
                        act.wait_ge(proj_done, u + 1)
                        if u >= 1:
                            act.wait_ge(q_ready, u)
                        act.activation(q_lo[:, :], ps[:, Q_BANK, :], ACT.Identity,
                                       bias=cols[:, C_SBQ + g:C_SBQ + g + 1],
                                       scale=cols[:, C_SELQ:C_SELQ + 1]).then_inc(q_sel_ready, 1)
                        act.wait_ge(kf_ready, u + 1)
                        if u >= 2:
                            act.wait_ge(k_ready, u - 1)
                        act.activation(k_hi[:, u % 2, :], kf[:, u % 2, :], ACT.Copy,
                                       scale=cols[:, C_SELK:C_SELK + 1]).then_inc(k_sel_ready, 1)

                    def take_out(u):
                        act.wait_ge(pv_done, u + 1)
                        if u >= 2:
                            act.wait_ge(o_turned, u - 1)
                        act.copy(osb[:, u % 2, :], ps[:, V_BANK, :]).then_inc(o_ready, 1)

                    split(0)
                    split(1)
                    for s in range(STEPS + 1):
                        u = s // 2
                        if s < STEPS:
                            act.wait_ge(keyed_done, s + 1)
                            if u >= 2:
                                act.wait_ge(pv_done, u - 1)
                            act.activation(e[:, u % 2, 2 * (s % 2):2 * (s % 2) + 2, :], ps[:, s_banks(s), :],
                                           ACT.Exp, scale=scale).then_inc(exp_ready, 1)
                        if s % 2 == 0 and s >= 2:
                            take_out(u - 1)
                        if s % 2 == 1 and u + 2 < UNITS:
                            split(u + 2)
                    for b in range(B):
                        act.wait_ge(on_turned, b + 1)
                        if b >= 2:
                            act.wait_ge(out_done, b - 1)
                        act.activation(gl[:, b % 2, :], ps[0:A0_DK, GELU_BANK + b % 2, :], ACT.Gelu)\
                           .then_inc(gelu_ready, 1)

                @block.vector
                def _(dve):
                    def normalise(b):
                        if b >= 2:
                            dve.wait_ge(proj_done, A0_GROUPS * (b - 1))
                        dve.tensor_scalar(xn[:, b % 2, :], core.x[:, b, :], core.mean(b),
                                          core.rstd(b), ALU.subtract, ALU.mult).then_inc(xn_ready, 1)

                    def stack(u):
                        b, g = divmod(u, A0_GROUPS)
                        dve.wait_ge(proj_done, u + 1)
                        if b == 0:
                            dve.wait_ge(first_mask_ready, 2)
                        else:
                            dve.wait_ge(mask_ready, 2 * b)
                        if u >= 2:
                            dve.wait_ge(k_ready, u - 1)
                        dve.scalar_tensor_tensor(out=kf[:, u % 2, :], in0=ps[:, K_BANK, :],
                                                 scalar=cols[:, C_BK + g:C_BK + g + 1],
                                                 in1=mask_of(b), op0=ALU.add,
                                                 op1=ALU.mult).then_inc(kf_ready, 1)
                        dve.wait_ge(q_sel_ready, u + 1)
                        if u >= 2:
                            dve.wait_ge(keyed_done, 2 * u - 2)
                        dve.scalar_tensor_tensor(out=q[:, u % 2, :], in0=ps[:, Q_BANK, :],
                                                 scalar=cols[:, C_BQ + g:C_BQ + g + 1],
                                                 in1=q_lo[:, :].bitcast(F32), op0=ALU.add,
                                                 op1=ALU.subtract).then_inc(q_ready, 1)

                    def values_biased(b):
                        dve.wait_ge(v_done, b + 1)
                        dve.wait_ge(zeroed, 3)
                        if b >= 2:
                            dve.wait_ge(pv_done, A0_GROUPS * (b - 1))
                        dve.tensor_tensor(
                            v[:, b % 2, :, :, 0:A0_DH],
                            ps[:, K_BANK, 0:A0_WINS * A0_DK].rearrange(
                                "p (w h d) -> p w h d", w=A0_WINS, h=A0_HEADS),
                            bv.rearrange("p (h d) -> p h d", h=A0_HEADS).unsqueeze(1)
                            .broadcast_to([P, A0_WINS, A0_HEADS, A0_DH]),
                            ALU.add).then_inc(v_ready, 1)

                    def divide(u):
                        b, g = divmod(u, A0_GROUPS)
                        dve.wait_ge(o_turned, u + 1)
                        dve.reciprocal(rec[:, :, :], turned_o()[:, :, :, A0_DH]).then_inc(rec_ready, 1)
                        dve.wait_ge(rec_ready, u + 1)
                        dve.tensor_tensor(
                            on_all[:, b, :, :].rearrange("p w (h d) -> p w h d", h=A0_HEADS)
                            [:, :, A0_PER_GROUP * g:A0_PER_GROUP * (g + 1), :],
                            turned_o()[:, :, :, 0:A0_DH],
                            rec[:, :, :].unsqueeze(3).broadcast_to([P, A0_WINS, A0_PER_GROUP, A0_DH]),
                            ALU.mult).then_inc(on_ready, 1)

                    def maximum(s):
                        dve.wait_ge(scores_done, s + 1)
                        dve.tensor_reduce(
                            mx[:, s % 2, :, PAIR * (s % 2) + A0_MAX_ROW:PAIR * (s % 2 + 1):A0_SLOT].rearrange(
                                "p w r -> p r w"),
                            ps[:, s_banks(s), :].rearrange("p r (w j) -> p r w j", w=A0_WINS),
                            AX.X, ALU.max, negate=True).then_inc(max_ready, 1)

                    def lower(s):
                        u = s // 2
                        dve.wait_ge(max_turned, s + 1)
                        dve.wait_ge(q_ready, u + 1)
                        half = q[pair_rows(s), u % 2, :]
                        dve.tensor_tensor(half, ps[pair_rows(s), M_BANK, :], half.bitcast(F32), ALU.add)\
                           .then_inc(q_max_ready, 1)

                    normalise(0)
                    dve.wait_ge(cols_ready, 1)
                    key_mask(dve, 0, first_mask_ready, 0)
                    stack(0)
                    maximum(0)
                    lower(0)
                    stack(1)
                    maximum(1)
                    values_biased(0)
                    for s in range(STEPS + 3):
                        if s + 1 < STEPS:
                            lower(s + 1)
                        if s % 2 == 1 and s // 2 + 2 < UNITS:
                            stack(s // 2 + 2)
                        if s + 2 < STEPS:
                            maximum(s + 2)
                        if s % 4 == 2 and (s + 2) // 4 < B:
                            values_biased((s + 2) // 4)
                        if s % 4 == 0 and s // 4 + 1 < B:
                            normalise(s // 4 + 1)
                        if s % 2 == 0 and s >= 4:
                            divide((s - 4) // 2)
                    dve.wait_ge(out_mask_loaded, 16)
                    for b in range(B):
                        dve.wait_ge(out_done, b + 1)
                        dve.scalar_tensor_tensor(out=tmp[:, b % 2, :], in0=ps[:, OUT_BANK + b % 2, :],
                                                 scalar=cols[:, C_BO:C_BO + 1], in1=out_mask[:, b, :],
                                                 op0=ALU.add, op1=ALU.mult).then_inc(tmp_ready, 1)
                        dve.wait_ge(tmp_ready, b + 1)
                        dve.tensor_tensor(core.x[:, b, :], core.x[:, b, :], tmp[:, b % 2, :],
                                          ALU.add).then_inc(x_ready, 1)
                        dve.wait_ge(x_ready, b + 1)
                        ahead.dve(dve, b)

                @block.tensor
                def _(pe):
                    def project(u):
                        b, g = divmod(u, A0_GROUPS)
                        pe.wait_ge(xn_ready, b + 1)
                        if u >= 1:
                            pe.wait_ge(q_ready, u)
                            pe.wait_ge(kf_ready, u)
                        if u >= 2:
                            pe.wait_ge(v_ready, (u + 1) // 2)
                        if u >= 4:
                            pe.wait_ge(on_ready, u - 3)
                        pe.matmul(ps[:, K_BANK, :], wk[:, g * P:(g + 1) * P], xn[:, b % 2, :], start=True, stop=True)
                        pe.matmul(ps[:, Q_BANK, :], wq[:, g * P:(g + 1) * P], xn[:, b % 2, :], start=True,
                                  stop=True).then_inc(proj_done, 1)

                    def project_values(b):
                        pe.wait_ge(ctx_loaded[b * HALVES // B], 16)
                        pe.wait_ge(kf_ready, max(2 * b + 1, 2))
                        for w in range(A0_WINS):
                            mm = pe.matmul(ps[:, K_BANK, w * A0_DK:(w + 1) * A0_DK],
                                           ctx[:, b, w * A0_WIN:(w + 1) * A0_WIN], wv,
                                           start=True, stop=True)
                        mm.then_inc(v_done, 1)

                    def heads(s):
                        for w in range(A0_WINS):
                            for r in (2 * (s % 2), 2 * (s % 2) + 1):
                                yield (slice(A0_SLOT * r, A0_SLOT * (r + 1)), r, w,
                                       slice(w * A0_WIN, (w + 1) * A0_WIN))

                    def scores(s):
                        u = s // 2
                        pe.wait_ge(q_ready, u + 1)
                        pe.wait_ge(k_ready, u + 1)
                        if s >= 2:
                            pe.wait_ge(exp_ready, s - 1)
                        for rows, r, w, win in heads(s):
                            mm = pe.matmul(ps[:, S_BANK + r, win], q[rows, u % 2, win],
                                           k[rows, u % 2, win], start=True, stop=True)
                        mm.then_inc(scores_done, 1)

                    def turn_max(s):
                        pe.wait_ge(max_ready, s + 1)
                        if s >= 1:
                            pe.wait_ge(q_max_ready, s)
                        for w in range(A0_WINS):
                            mm = pe.transpose(ps[:, M_BANK, w * A0_WIN:(w + 1) * A0_WIN],
                                              mx[:, s % 2, w, :], core.ident[:, :])
                        mm.then_inc(max_turned, 1)

                    def keyed(s):
                        u = s // 2
                        pe.wait_ge(q_max_ready, s + 1)
                        for rows, r, w, win in heads(s):
                            mm = pe.matmul(ps[:, S_BANK + r, win], k[rows, u % 2, win],
                                           q[rows, u % 2, win], start=True, stop=True)
                        mm.then_inc(keyed_done, 1)

                    def values(s):
                        u = s // 2
                        b, g = divmod(u, A0_GROUPS)
                        pe.wait_ge(exp_ready, s + 1)
                        pe.wait_ge(v_ready, b + 1)
                        if u >= 1:
                            pe.wait_ge(o_ready, u)
                        for rows, r, w, win in heads(s):
                            mm = pe.matmul(ps[rows, V_BANK, win], v[:, b % 2, w, A0_PER_GROUP * g + r, :],
                                           e[:, u % 2, r, win], start=True, stop=True)
                        if s % 2 == 1:
                            mm.then_inc(pv_done, 1)

                    def turn_outputs(u):
                        pe.wait_ge(o_ready, u + 1)
                        pe.wait_ge(q_ready, min(u + 4, UNITS))
                        if u >= 1:
                            pe.wait_ge(on_ready, u)
                        for w in range(A0_WINS):
                            mm = pe.transpose(ps[:, Q_BANK, w * A0_WIN:(w + 1) * A0_WIN],
                                              osb[:, u % 2, w * A0_WIN:(w + 1) * A0_WIN], core.ident[:, :])
                        mm.then_inc(o_turned, 1)

                    def turn_back(b):
                        pe.wait_ge(on_ready, A0_GROUPS * (b + 1))
                        if b >= 2:
                            pe.wait_ge(gelu_ready, b - 1)
                        for w in range(A0_WINS):
                            mm = pe.transpose(ps[0:A0_DK, GELU_BANK + b % 2, w * A0_WIN:(w + 1) * A0_WIN],
                                              on_all[:, b, w, :], core.ident[:, :])
                        mm.then_inc(on_turned, 1)

                    def project_out(b):
                        pe.wait_ge(gelu_ready, b + 1)
                        if b >= 2:
                            pe.wait_ge(tmp_ready, b - 1)
                        pe.matmul(ps[:, OUT_BANK + b % 2, :], wo[:, :], gl[:, b % 2, :], start=True,
                                  stop=True).then_inc(out_done, 1)

                    project(0)
                    scores(0)
                    project(1)
                    turn_max(0)
                    scores(1)
                    project_values(0)
                    for s in range(STEPS + 3):
                        if s < STEPS:
                            keyed(s)
                        if 1 <= s <= STEPS:
                            values(s - 1)
                        if s + 1 < STEPS:
                            turn_max(s + 1)
                        if s % 2 == 1 and s // 2 + 2 < UNITS:
                            project(s // 2 + 2)
                        if s % 4 == 2 and (s + 2) // 4 < B:
                            project_values((s + 2) // 4)
                        if s + 2 < STEPS:
                            scores(s + 2)
                        if s % 2 == 0 and s >= 4:
                            turn_outputs((s - 4) // 2)
                    pe.wait_ge(loaded, 16)
                    turn_back(0)
                    for b in range(B):
                        if b + 1 < B:
                            turn_back(b + 1)
                        project_out(b)


F0_E, F0_TOPK, F0_I = 16, 4, 256
F0_ALL = F0_E + 1
F0_IC = F0_I // P
F0_HALF = T // 2
F0_GU = NC * 2 * F0_I
F0_JOBS = 2 * F0_IC
FIRST, LAST = 0, F0_ALL - 1
TAKEN = -1e30


def l0_ffn(core):
    nc, dram, ps = core.nc, core.dram, core.psum
    with ExitStack() as lay:
        hi = sbuf(nc, lay, "f0_xn_hi", [P, NC, T], F32R)
        lo = sbuf(nc, lay, "f0_xn_lo", [P, NC, T], F32R)
        weight = sbuf(nc, lay, "f0_weight", [P, B, F0_ALL])
        turned = NormTurned(core, lay, "f0", hi, lo, bank=4)
        ahead = Ahead(core, lay, "f0")
        gate = sbuf(nc, lay, "f0_gate", [P, NC, F0_E])
        gate_hi = sbuf(nc, lay, "f0_gate_hi", [P, NC, F0_E], F32R)
        gate_lo = sbuf(nc, lay, "f0_gate_lo", [P, NC, F0_E], F32R)
        bias = sbuf(nc, lay, "f0_bias", [P, F0_E])
        rank = sbuf(nc, lay, "f0_rank", [P, F0_E])
        score = sbuf(nc, lay, "f0_score", [P, B, F0_E])
        left = sbuf(nc, lay, "f0_left", [P, B, F0_E])
        pick = sbuf(nc, lay, "f0_pick", [P, B, F0_E])
        chosen = sbuf(nc, lay, "f0_chosen", [P, B, F0_E])
        top = sbuf(nc, lay, "f0_top", [P, B])
        logit = sbuf(nc, lay, "f0_logit", [F0_E, T])
        gu, dn = core.raw[:, 0, :], core.raw[:, 1, 0:F0_IC * D]
        gu_hi = sbuf(nc, lay, "f0_gu_hi", [P, NC, 2, F0_I], F32R)
        gu_lo = sbuf(nc, lay, "f0_gu_lo", [P, NC, 2, F0_I], F32R)
        dn_hi = sbuf(nc, lay, "f0_dn_hi", [P, F0_IC, D], F32R)
        dn_lo = sbuf(nc, lay, "f0_dn_lo", [P, F0_IC, D], F32R)
        sil = sbuf(nc, lay, "f0_sil", [P, 2, F0_HALF])
        z = sbuf(nc, lay, "f0_z", [P, 2, F0_HALF])
        z_hi = sbuf(nc, lay, "f0_z_hi", [P, F0_IC, T], F32R)
        z_lo = sbuf(nc, lay, "f0_z_lo", [P, F0_IC, T], F32R)
        loaded = core.sem("f0_gate_loaded")
        gate_hi_ready = core.sem("f0_gate_hi_ready")
        gate_lo_ready = core.sem("f0_gate_lo_ready")
        logits_done = core.sem("f0_logits_done")
        logit_ready, logits_turned = core.sem("f0_logit_ready"), core.sem("f0_logits_turned")
        sigmoid_ready = core.sem("f0_sigmoid_ready")
        step = core.sem("f0_route_step")
        gu_loaded, dn_loaded = core.sem("f0_gu_loaded"), core.sem("f0_dn_loaded")
        gu_hi_ready, gu_lo_ready = core.sem("f0_gu_hi_ready"), core.sem("f0_gu_lo_ready")
        dn_hi_ready, dn_lo_ready = core.sem("f0_dn_hi_ready"), core.sem("f0_dn_lo_ready")
        gu_done = core.sem("f0_gu_done")
        sil_ready, z_ready = core.sem("f0_sil_ready"), core.sem("f0_z_ready")
        z_hi_ready, z_lo_ready = core.sem("f0_z_hi_ready"), core.sem("f0_z_lo_ready")
        y_done = core.sem("f0_y_done")
        y_added = core.sem("f0_y_added")
        Y_BANK, Y_BANKS, LOGITS = 4, 4, 7

        def flat(w):
            return w[:, :, :, :].rearrange("p c g i -> p (c g i)")

        def flat_dn(w):
            return w[:, :, :].rearrange("p c n -> p (c n)")

        def job_place(j):
            half, ic = divmod(j, F0_IC)
            return ic, slice(half * F0_HALF, (half + 1) * F0_HALF)

        with nc.Block() as block:
            @block.sync
            def _(sp):
                def load(e):
                    sp.wait_ge(gu_lo_ready, e)
                    sp.dma_start(gu, dram["f0_gu"][bass.ds(e, 1)].rearrange("e p n -> p (e n)"))\
                      .then_inc(gu_loaded, 16)
                    sp.wait_ge(dn_lo_ready, e)
                    sp.dma_start(dn, dram["f0_dn"][bass.ds(e, 1)].rearrange("e p n -> p (e n)"))\
                      .then_inc(dn_loaded, 16)

                sp.dma_start(gate[:, :, :], dram["f0_gate"]).then_inc(loaded, 16)
                sp.dma_start(bias[:, :], dram["f0_bias"]).then_inc(loaded, 16)
                sp.dma_start(rank[:, :], dram["f0_rank"]).then_inc(loaded, 16)
                with sp.Fori(1, F0_ALL) as e:
                    load(e)
                sp.wait_ge(gu_lo_ready, F0_ALL)
                sp.wait_ge(dn_lo_ready, F0_ALL)
                core.prefetch(sp, "f0")

            @block.scalar
            def _(act):
                def gu_split(e):
                    if e is not FIRST:
                        act.wait_ge(gu_loaded, 16 * e)
                        act.wait_ge(gu_done, F0_JOBS * e)
                    act.copy(flat(gu_hi), gu).then_inc(gu_hi_ready, 1)

                def job(e, j):
                    ic, cols = job_place(j)
                    act.wait_ge(gu_done, F0_JOBS * e + (j + 1))
                    if j >= 2:
                        act.wait_ge(z_ready, F0_JOBS * e + (j - 1))
                    act.activation(sil[:, j % 2, :], ps[:, 2 * (j % 2), :], ACT.Silu)\
                       .then_inc(sil_ready, 1)
                    if j == 0:
                        if e is not FIRST:
                            act.wait_ge(dn_loaded, 16 * e)
                        act.copy(flat_dn(dn_hi), dn).then_inc(dn_hi_ready, 1)
                    act.wait_ge(z_ready, F0_JOBS * e + (j + 1))
                    act.copy(z_hi[:, ic, cols], z[:, j % 2, :]).then_inc(z_hi_ready, 1)

                def expert(e):
                    gu_split(e)
                    for j in range(F0_JOBS):
                        job(e, j)

                gu_split(FIRST)
                turned.act(act, range(0, 2))
                act.wait_ge(loaded, 48)
                act.copy(gate_hi[:, :, :], gate[:, :, :]).then_inc(gate_hi_ready, 1)
                turned.act(act, range(2, HB))
                job(FIRST, 0)
                job(FIRST, 1)
                turned.act(act, range(HB, B))
                for h in range(HALVES):
                    act.wait_ge(logits_done, h + 1)
                    act.copy(logit[:, h * HT:(h + 1) * HT], ps[0:F0_E, LOGITS - h, :]).then_inc(logit_ready, 1)
                job(FIRST, 2)
                act.wait_ge(logits_turned, 1)
                act.activation(left[:, :, :], ps[:, LOGITS, 0:B * F0_E].rearrange(
                    "p (b e) -> p b e", b=B), ACT.Sigmoid).then_inc(sigmoid_ready, 1)
                job(FIRST, 3)
                with act.Fori(1, F0_ALL) as e:
                    expert(e)

            @block.gpsimd
            def _(pool):
                def expert(e):
                    pool.wait_ge(gu_hi_ready, e + 1)
                    pool.tensor_tensor(flat(gu_lo), gu, flat(gu_hi).bitcast(F32),
                                       ALU.subtract).then_inc(gu_lo_ready, 1)
                    for j in range(F0_JOBS):
                        ic, cols = job_place(j)
                        pool.wait_ge(z_hi_ready, F0_JOBS * e + (j + 1))
                        pool.tensor_tensor(z_lo[:, ic, cols], z[:, j % 2, :],
                                           z_hi[:, ic, cols].bitcast(F32),
                                           ALU.subtract).then_inc(z_lo_ready, 1)
                        if j == 0:
                            pool.wait_ge(dn_hi_ready, e + 1)
                            pool.tensor_tensor(flat_dn(dn_lo), dn, flat_dn(dn_hi).bitcast(F32),
                                               ALU.subtract).then_inc(dn_lo_ready, 1)

                expert(FIRST)
                with pool.Fori(1, F0_ALL) as e:
                    expert(e)
                ahead.pool(pool)

            @block.vector
            def _(dve):
                def gated(e, j):
                    dve.wait_ge(sil_ready, F0_JOBS * e + (j + 1))
                    if j >= 2:
                        dve.wait_ge(z_lo_ready, F0_JOBS * e + (j - 1))
                    dve.tensor_tensor(z[:, j % 2, :], sil[:, j % 2, :], ps[:, 2 * (j % 2) + 1, :],
                                      ALU.mult).then_inc(z_ready, 1)

                def add(e, b):
                    dve.wait_ge(y_done, B * e + (b + 1))
                    dve.scalar_tensor_tensor(out=core.x[:, b, :], in0=ps[:, Y_BANK + b % Y_BANKS, :],
                                             scalar=weight[:, b, bass.ds(e, 1)], in1=core.x[:, b, :],
                                             op0=ALU.mult, op1=ALU.add).then_inc(y_added, 1)

                steps = 0

                def after(instruction):
                    nonlocal steps
                    steps += 1
                    instruction.then_inc(step, 1)
                    dve.wait_ge(step, steps)

                def by_expert(row):
                    return row[:, :].unsqueeze(1).broadcast_to([P, B, F0_E])

                def by_batch(col):
                    return col[:, :].unsqueeze(2).broadcast_to([P, B, F0_E])

                def biased():
                    dve.wait_ge(sigmoid_ready, 1)
                    after(dve.tensor_tensor(score[:, :, :], left[:, :, :], by_expert(bias), ALU.add))
                    after(dve.tensor_copy(left[:, :, :], score[:, :, :]))

                def choose(k):
                    after(dve.tensor_reduce(top[:, :], left[:, :, :], AX.X, ALU.max))
                    after(dve.tensor_tensor(pick[:, :, :], left[:, :, :], by_batch(top), ALU.is_equal))
                    after(dve.tensor_tensor(pick[:, :, :], pick[:, :, :], by_expert(rank), ALU.mult))
                    after(dve.tensor_reduce(top[:, :], pick[:, :, :], AX.X, ALU.max))
                    after(dve.tensor_tensor(pick[:, :, :], by_expert(rank), by_batch(top), ALU.is_equal))
                    after(dve.scalar_tensor_tensor(out=left[:, :, :], in0=pick[:, :, :], scalar=TAKEN,
                                                   in1=left[:, :, :], op0=ALU.mult, op1=ALU.add))
                    if k == 0:
                        after(dve.tensor_copy(chosen[:, :, :], pick[:, :, :]))
                    else:
                        after(dve.tensor_tensor(chosen[:, :, :], chosen[:, :, :], pick[:, :, :], ALU.add))

                def weigh():
                    after(dve.tensor_tensor(score[:, :, :], score[:, :, :], chosen[:, :, :], ALU.mult))
                    after(dve.tensor_reduce(top[:, :], score[:, :, :], AX.X, ALU.add))
                    after(dve.tensor_scalar(top[:, :], top[:, :], 1e-20, None, ALU.add))
                    after(dve.reciprocal(top[:, :], top[:, :]))
                    after(dve.tensor_tensor(weight[:, :, 1:], score[:, :, :], by_batch(top), ALU.mult))

                turned.dve(dve, range(0, HB + 1))
                dve.wait_ge(gate_hi_ready, 1)
                dve.tensor_tensor(gate_lo[:, :, :], gate[:, :, :], gate_hi[:, :, :].bitcast(F32),
                                  ALU.subtract).then_inc(gate_lo_ready, 1)
                after(dve.memset(weight[:, :, 0:1], 1.0))
                dve.wait_ge(loaded, 48)
                gated(FIRST, 0)
                gated(FIRST, 1)
                turned.dve(dve, range(HB + 1, B))
                gated(FIRST, 2)
                biased()
                choose(0)
                choose(1)
                gated(FIRST, 3)
                for b in range(B):
                    add(FIRST, b)
                    if b % HB == HB - 1:
                        choose(2 + b // HB)
                weigh()
                with dve.Fori(1, F0_ALL - 1) as e:
                    for j in range(F0_JOBS):
                        gated(e, j)
                    for b in range(B):
                        add(e, b)
                for j in range(F0_JOBS):
                    gated(LAST, j)
                for b in range(B):
                    add(LAST, b)
                    dve.wait_ge(y_added, B * LAST + b + 1)
                    ahead.dve(dve, b)

            @block.tensor
            def _(pe):
                def job(e, j):
                    ic, cols = job_place(j)
                    if j >= 2:
                        pe.wait_ge(z_ready, F0_JOBS * e + (j - 1))
                    for n in range(2):
                        out = ps[:, 2 * (j % 2) + n, :]
                        w = slice(ic * P, (ic + 1) * P)
                        for c in range(NC):
                            mm = matmul_split(pe, out, gu_hi[:, c, n, w], gu_lo[:, c, n, w],
                                              hi[:, c, cols], lo[:, c, cols], c == 0, c == NC - 1)
                    mm.then_inc(gu_done, 1)

                def down(e):
                    if e is not FIRST:
                        pe.wait_ge(y_added, B * e)
                    pe.wait_ge(dn_lo_ready, e + 1)
                    for b in range(B):
                        if b % (B // 2) == 0:
                            pe.wait_ge(z_lo_ready, F0_JOBS * e + F0_IC * (b // (B // 2) + 1))
                        if b >= Y_BANKS:
                            pe.wait_ge(y_added, B * e + (b - Y_BANKS + 1))
                        rows = slice(b * P, (b + 1) * P)
                        for ic in range(F0_IC):
                            mm = matmul_split(pe, ps[:, Y_BANK + b % Y_BANKS, :], z_hi[:, ic, rows],
                                              z_lo[:, ic, rows], dn_hi[:, ic, :], dn_lo[:, ic, :],
                                              ic == 0, ic == F0_IC - 1)
                        mm.then_inc(y_done, 1)

                def logits():
                    pe.wait_ge(gate_lo_ready, 1)
                    pe.wait_ge(turned.lo_ready, B)
                    for h in range(HALVES):
                        rows = slice(h * HT, (h + 1) * HT)
                        for c in range(NC):
                            mm = matmul_split(pe, ps[0:F0_E, LOGITS - h, :], gate_hi[:, c, :], gate_lo[:, c, :],
                                              hi[:, c, rows], lo[:, c, rows], c == 0, c == NC - 1)
                        mm.then_inc(logits_done, 1)

                def turn_logits():
                    pe.wait_ge(logit_ready, HALVES)
                    for b in range(B):
                        mm = pe.transpose(ps[:, LOGITS, b * F0_E:(b + 1) * F0_E],
                                          logit[:, b * P:(b + 1) * P], core.ident[0:F0_E, 0:F0_E])
                    mm.then_inc(logits_turned, 1)

                turned.pe(pe, range(0, HB))
                pe.wait_ge(gu_lo_ready, 1)
                pe.wait_ge(turned.lo_ready, HB)
                job(FIRST, 0)
                job(FIRST, 1)
                turned.pe(pe, range(HB, B))
                logits()
                job(FIRST, 2)
                turn_logits()
                job(FIRST, 3)
                pe.wait_ge(sigmoid_ready, 1)
                down(FIRST)
                with pe.Fori(1, F0_ALL) as e:
                    pe.wait_ge(gu_lo_ready, e + 1)
                    for j in range(F0_JOBS):
                        job(e, j)
                    down(e)




def chunked(w):
    return w.rearrange("p c n -> p (c n)")


def l1_attention(core):
    nc, dram, ps = core.nc, core.dram, core.psum
    scale = float(D) ** -0.5
    with ExitStack() as lay:
        hi = sbuf(nc, lay, "a1_xn_hi", [P, NC, T], F32R)
        lo = sbuf(nc, lay, "a1_xn_lo", [P, NC, T], F32R)
        turned = NormTurned(core, lay, "a1", hi, lo)
        w_hi = [sbuf(nc, lay, f"a1_w{i}_hi", [P, NC, D], F32R) for i in range(2)]
        w_lo = [sbuf(nc, lay, f"a1_w{i}_lo", [P, NC, D], F32R) for i in range(2)]
        ct_hi = sbuf(nc, lay, "a1_ct_hi", [P, NC, HT], F32R)
        ct_lo = sbuf(nc, lay, "a1_ct_lo", [P, NC, HT], F32R)
        kq_hi = [sbuf(nc, lay, f"a1_kq{i}_hi", [P, NC, HT], F32R) for i in range(2)]
        kq_lo = [sbuf(nc, lay, f"a1_kq{i}_lo", [P, NC, HT], F32R) for i in range(2)]
        c_hi = sbuf(nc, lay, "a1_c_hi", [P, HB, D], F32R)
        c_lo = sbuf(nc, lay, "a1_c_lo", [P, HB, D], F32R)
        bias = sbuf(nc, lay, "a1_bias", [P, 2, NC])
        negmax = sbuf(nc, lay, "a1_negmax", [P, B])
        shift = sbuf(nc, lay, "a1_shift", [P, B])
        total = sbuf(nc, lay, "a1_total", [P, B])
        inv = sbuf(nc, lay, "a1_inv", [P, B])
        e = sbuf(nc, lay, "a1_e", [P, HB, P])
        at_hi = sbuf(nc, lay, "a1_at_hi", [P, HT], F32R)
        at_lo = sbuf(nc, lay, "a1_at_lo", [P, HT], F32R)
        pieces = [(dram["a1_wk"], chunked(w_hi[0][:, :, :]), chunked(w_lo[0][:, :, :])),
                  (dram["ctx_turned"][0], chunked(ct_hi[:, :, :]), chunked(ct_lo[:, :, :])),
                  (dram["a1_wq"], chunked(w_hi[1][:, :, :]), chunked(w_lo[1][:, :, :])),
                  (dram["ctx_rows"][0], chunked(c_hi[:, :, :]), chunked(c_lo[:, :, :])),
                  (dram["ctx_turned"][1], chunked(ct_hi[:, :, :]), chunked(ct_lo[:, :, :])),
                  (dram["ctx_rows"][1], chunked(c_hi[:, :, :]), chunked(c_lo[:, :, :]))]
        WK, CT0, WQ, C0, CT1, C1 = range(6)
        weights = Weights(core, "a1", pieces)
        ahead = Ahead(core, lay, "a1")
        bias_loaded = core.sem("a1_bias_loaded")
        proj_done = core.sem("a1_proj_done")
        hi_ready, lo_ready = core.sem("a1_hi_ready"), core.sem("a1_lo_ready")
        scores_done = core.sem("a1_scores_done")
        negmax_ready, shift_ready = core.sem("a1_negmax_ready"), core.sem("a1_shift_ready")
        exp_ready, inv_ready = core.sem("a1_exp_ready"), core.sem("a1_inv_ready")
        attn_turned = core.sem("a1_attn_turned")
        at_hi_ready, at_lo_ready = core.sem("a1_at_hi_ready"), core.sem("a1_at_lo_ready")
        y_done, x_ready = core.sem("a1_y_done"), core.sem("a1_x_ready")
        S_BANK, T_BANK = 4, 5
        PER_HALF = 2 * NC

        with nc.Block() as block:
            @block.sync
            def _(sp):
                sp.dma_start(bias[:, :, :], dram["a1_bias"]).then_inc(bias_loaded, 16)
                weights.load(sp)
                weights.prefetch(sp)

            @block.gpsimd
            def _(pool):
                weights.split_lo(pool, range(CT0, len(pieces)))
                ahead.pool(pool)

            @block.scalar
            def _(act):
                def proj_hi(n):
                    half, which, m = n // PER_HALF, n % PER_HALF // NC, n % NC
                    act.wait_ge(proj_done, n + 1)
                    if half:
                        act.wait_ge(scores_done, half)
                    act.activation(kq_hi[which][:, m, :], ps[:, 2 + n % 2, :], ACT.Identity,
                                   bias=bias[:, which, m:m + 1], scale=1.0).then_inc(hi_ready, 1)

                def softmax(half):
                    for i in range(HB):
                        b = half * HB + i
                        act.wait_ge(shift_ready, half + 1)
                        if half:
                            act.wait_ge(attn_turned, half)
                        act.activation(e[:, i, :], ps[:, S_BANK, i * P:(i + 1) * P], ACT.Exp,
                                       bias=shift[:, b:b + 1], scale=scale,
                                       accum_out=total[:, b:b + 1]).then_inc(exp_ready, 1)

                def attn_hi(half):
                    act.wait_ge(attn_turned, half + 1)
                    if half:
                        act.wait_ge(y_done, HB * half)
                    act.copy(at_hi[:, :], ps[:, T_BANK, :]).then_inc(at_hi_ready, 1)

                weights.split_hi(act, [WK])
                turned.act(act, range(0, 2))
                weights.split_hi(act, [CT0])
                turned.act(act, range(2, 4))
                act.wait_ge(bias_loaded, 16)
                for n in range(NC):
                    proj_hi(n)
                weights.split_hi(act, [WQ])
                turned.act(act, range(4, B))
                weights.split_hi(act, [C0])
                for n in range(NC, 2 * NC):
                    proj_hi(n)
                act.wait_ge(proj_done, NC)
                weights.split_hi(act, [CT1])
                softmax(0)
                attn_hi(0)
                for n in range(2 * NC, 3 * NC):
                    proj_hi(n)
                act.wait_ge(y_done, HB)
                weights.split_hi(act, [C1])
                for n in range(3 * NC, 4 * NC):
                    proj_hi(n)
                softmax(1)
                attn_hi(1)

            @block.tensor
            def _(pe):
                def project(n):
                    half, which, m = n // PER_HALF, n % PER_HALF // NC, n % NC
                    if n >= 2:
                        pe.wait_ge(lo_ready, n - 1)
                    for c in range(NC):
                        if which == 0:
                            mov = ct_hi[:, c, :], ct_lo[:, c, :]
                        else:
                            rows = slice(half * HT, (half + 1) * HT)
                            mov = hi[:, c, rows], lo[:, c, rows]
                        mm = matmul_split(pe, ps[:, 2 + n % 2, :], w_hi[which][:, c, m * P:(m + 1) * P],
                                          w_lo[which][:, c, m * P:(m + 1) * P], *mov, c == 0, c == NC - 1)
                    mm.then_inc(proj_done, 1)

                def scores(half):
                    pe.wait_ge(lo_ready, PER_HALF * (half + 1))
                    if half:
                        pe.wait_ge(exp_ready, HB * half)
                    for i in range(HB):
                        rows = slice(i * P, (i + 1) * P)
                        for c in range(NC):
                            mm = matmul_split(pe, ps[:, S_BANK, rows], kq_hi[1][:, c, rows],
                                              kq_lo[1][:, c, rows], kq_hi[0][:, c, rows],
                                              kq_lo[0][:, c, rows], c == 0, c == NC - 1)
                    mm.then_inc(scores_done, 1)

                def turn(half):
                    pe.wait_ge(exp_ready, HB * (half + 1))
                    if half:
                        pe.wait_ge(at_lo_ready, half)
                    for i in range(HB):
                        mm = pe.transpose(ps[:, T_BANK, i * P:(i + 1) * P], e[:, i, :], core.ident[:, :])
                    mm.then_inc(attn_turned, 1)

                def attend(half):
                    pe.wait_ge(at_lo_ready, half + 1)
                    weights.wait(pe, C1 if half else C0)
                    for i in range(HB):
                        b = half * HB + i
                        if b >= 2:
                            pe.wait_ge(x_ready, b - 1)
                        matmul_split(pe, ps[:, 6 + b % 2, :], at_hi[:, i * P:(i + 1) * P],
                                     at_lo[:, i * P:(i + 1) * P], c_hi[:, i, :], c_lo[:, i, :],
                                     True, True).then_inc(y_done, 1)

                turned.pe(pe, range(0, 4))
                weights.wait(pe, CT0)
                for n in range(NC):
                    project(n)
                turned.pe(pe, range(4, B))
                weights.wait(pe, WQ)
                pe.wait_ge(turned.lo_ready, B)
                for n in range(NC, 2 * NC):
                    project(n)
                scores(0)
                weights.wait(pe, CT1)
                for n in (2 * NC, 2 * NC + 1):
                    project(n)
                turn(0)
                for n in range(2 * NC + 2, 3 * NC):
                    project(n)
                attend(0)
                for n in range(3 * NC, 4 * NC):
                    project(n)
                scores(1)
                turn(1)
                attend(1)

            @block.vector
            def _(dve):
                def proj_lo(n):
                    which, m = n % PER_HALF // NC, n % NC
                    dve.wait_ge(hi_ready, n + 1)
                    dve.scalar_tensor_tensor(out=kq_lo[which][:, m, :], in0=ps[:, 2 + n % 2, :],
                                             scalar=bias[:, which, m:m + 1],
                                             in1=kq_hi[which][:, m, :].bitcast(F32),
                                             op0=ALU.add, op1=ALU.subtract).then_inc(lo_ready, 1)

                def maxima(half):
                    cols = slice(half * HB, (half + 1) * HB)
                    dve.wait_ge(scores_done, half + 1)
                    dve.tensor_reduce(negmax[:, cols], ps[:, S_BANK, :].rearrange("p (b k) -> p b k", b=HB),
                                      AX.X, ALU.max, negate=True).then_inc(negmax_ready, 1)
                    dve.wait_ge(negmax_ready, half + 1)
                    dve.tensor_scalar(shift[:, cols], negmax[:, cols], scale, None, ALU.mult)\
                       .then_inc(shift_ready, 1)

                def attn_lo(half):
                    cols = slice(half * HB, (half + 1) * HB)
                    dve.wait_ge(exp_ready, HB * (half + 1))
                    dve.reciprocal(inv[:, cols], total[:, cols]).then_inc(inv_ready, 1)
                    dve.wait_ge(at_hi_ready, half + 1)
                    dve.tensor_tensor(at_lo[:, :], ps[:, T_BANK, :], at_hi[:, :].bitcast(F32),
                                      ALU.subtract).then_inc(at_lo_ready, 1)

                def add(half):
                    dve.wait_ge(inv_ready, half + 1)
                    for i in range(HB):
                        b = half * HB + i
                        dve.wait_ge(y_done, b + 1)
                        dve.scalar_tensor_tensor(out=core.x[:, b, :], in0=ps[:, 6 + b % 2, :],
                                                 scalar=inv[:, b:b + 1], in1=core.x[:, b, :],
                                                 op0=ALU.mult, op1=ALU.add).then_inc(x_ready, 1)
                        dve.wait_ge(x_ready, b + 1)
                        ahead.dve(dve, b)

                turned.dve(dve, range(0, 2))
                weights.first_lo(dve)
                turned.dve(dve, range(2, 5))
                for n in range(NC):
                    proj_lo(n)
                turned.dve(dve, range(5, B))
                for n in range(NC, 2 * NC):
                    proj_lo(n)
                maxima(0)
                attn_lo(0)
                for n in range(2 * NC, 3 * NC):
                    proj_lo(n)
                add(0)
                for n in range(3 * NC, 4 * NC):
                    proj_lo(n)
                maxima(1)
                attn_lo(1)
                add(1)


QW, QA = 127.0, 255.0
ROUND = 1.5 * 2.0 ** 23


def l1_ffn(core):
    nc, dram, ps = core.nc, core.dram, core.psum
    with ExitStack() as lay:
        w = core.raw[:, 0, :].rearrange("p (c n) -> p c n", c=NC)
        low, high, bias = (core.raw[:, 1, i * D:(i + 1) * D] for i in range(3))
        wr = sbuf(nc, lay, "f1_wr", [P, NC, D])
        wq = sbuf(nc, lay, "f1_wq", [P, NC, D], BF16)
        wt = sbuf(nc, lay, "f1_wt", [P, NC, D], BF16)
        wide = sbuf(nc, lay, "f1_wide", [P, NC, P])
        row_scale = sbuf(nc, lay, "f1_row_scale", [P, D])
        rs = sbuf(nc, lay, "f1_rs", [P, NC])
        rs_inv = sbuf(nc, lay, "f1_rs_inv", [P, NC])
        identb = sbuf(nc, lay, "f1_identb", [P, P], BF16)
        xn = sbuf(nc, lay, "f1_xn", [P, B, D])
        xr = sbuf(nc, lay, "f1_xr", [P, 2, D])
        xq = sbuf(nc, lay, "f1_xq", [P, 2, D], BF16)
        xt = sbuf(nc, lay, "f1_xt", [P, 2, NC, P], BF16)
        y = sbuf(nc, lay, "f1_y", [P, 3, D])
        negmean = sbuf(nc, lay, "f1_negmean", [P, B])
        mn = sbuf(nc, lay, "f1_mn", [P, B])
        mxm = sbuf(nc, lay, "f1_mx", [P, B])
        cs = sbuf(nc, lay, "f1_cs", [P, B])
        flat_row = sbuf(nc, lay, "f1_flat_row", [P, B])
        cs_inv = sbuf(nc, lay, "f1_cs_inv", [P, B])
        zp = sbuf(nc, lay, "f1_zp", [P, B])
        ends = sbuf(nc, lay, "f1_ends", [P, 2, B])
        ahead = Ahead(core, lay, "f1")
        identb_ready = core.sem("f1_identb_ready")
        step = core.sem("f1_step")
        w_turned, wt_ready = core.sem("f1_w_turned"), core.sem("f1_wt_ready")
        wide_ready, rs_spread, rs_ready = (core.sem(f"f1_{n}") for n in ("wide_ready", "rs_spread", "rs_ready"))
        wq_ready = core.sem("f1_wq_ready")
        xq_ready, x_turned, xt_ready = (core.sem(f"f1_{n}") for n in ("xq_ready", "x_turned", "xt_ready"))
        y_done, y_taken = core.sem("f1_y_done"), core.sem("f1_y_taken")
        negmean_ready, centred = core.sem("f1_negmean_ready"), core.sem("f1_centred")
        wide_ones, y_scaled, y_ready = (core.sem(f"f1_{n}") for n in ("wide_ones", "y_scaled", "y_ready"))
        x_ready, late_scaled = core.sem("f1_x_ready"), core.sem("f1_late_scaled")

        def turned_bank(i):
            return ps[:, i % 2, 0:D // 2].bitcast(BF16).rearrange("p (c n) -> p c n", c=NC)

        with nc.Block() as block:
            @block.sync
            def _(sp):
                sp.wait_ge(y_ready, B)
                core.prefetch(sp, "f1")

            @block.gpsimd
            def _(pool):
                pool.tensor_copy(identb[:, :], core.ident[:, :]).then_inc(identb_ready, 1)
                pool.memset(wide[:, :, :], 1.0).then_inc(wide_ones, 1)
                pool.wait_ge(rs_ready, 1)
                for b in range(B):
                    if b < HB:
                        pool.wait_ge(y_taken, b + 1)
                        pool.tensor_tensor(y[:, b % 3, :], y[:, b % 3, :], row_scale[:, :], ALU.mult)\
                            .then_inc(y_scaled, 1)
                        pool.wait_ge(y_scaled, b + 1)
                    else:
                        pool.wait_ge(late_scaled, b + 1 - HB)
                    pool.tensor_tensor(y[:, b % 3, :], y[:, b % 3, :], bias, ALU.add)\
                        .then_inc(y_ready, 1)
                    if b >= 1:
                        ahead.scale(pool, b - 1)
                ahead.scale(pool, B - 1)

            @block.tensor
            def _(pe):
                pe.wait_ge(identb_ready, 1)
                pe.wait_ge(wq_ready, 1)
                for c in range(NC):
                    if c >= 2:
                        pe.wait_ge(wt_ready, c - 1)
                    for m in range(NC):
                        mm = pe.transpose(turned_bank(c)[:, m, :], wq[:, m, c * P:(c + 1) * P], identb[:, :])
                    mm.then_inc(w_turned, 1)
                pe.wait_ge(wide_ready, 1)
                for m in range(NC):
                    mm = pe.matmul(ps[:, 2, m * P:(m + 1) * P], wide[:, m, :], core.ident[:, :],
                                   start=True, stop=True)
                mm.then_inc(rs_spread, 1)
                pe.wait_ge(wt_ready, NC)

                def product(b):
                    pe.wait_ge(xt_ready, b + 1)
                    if b >= 2:
                        if b - 2 < HB:
                            pe.wait_ge(y_taken, b - 1)
                        else:
                            pe.wait_ge(late_scaled, b - 1 - HB)
                    for c in range(NC):
                        mm = pe.matmul(ps[:, 4 + b % 2, :], xt[:, b % 2, c, :], wt[:, c, :],
                                       start=(c == 0), stop=(c == NC - 1))
                    mm.then_inc(y_done, 1)

                for b in range(B):
                    pe.wait_ge(xq_ready, b + 1)
                    if b >= 2:
                        pe.wait_ge(xt_ready, b - 1)
                    for c in range(NC):
                        mm = pe.transpose(turned_bank(b)[:, c, :], xq[:, b % 2, c * P:(c + 1) * P], identb[:, :])
                    mm.then_inc(x_turned, 1)
                    if b >= 1:
                        product(b - 1)
                product(B - 1)

            @block.scalar
            def _(act):
                act.wait_ge(negmean_ready, 1)
                for b in range(B):
                    act.activation(xn[:, b, :], core.x[:, b, :], ACT.Identity, bias=negmean[:, b:b + 1],
                                   scale=1.0).then_inc(centred, 1)
                for c in range(NC):
                    act.wait_ge(w_turned, c + 1)
                    act.copy(wt[:, c, :].rearrange("p (m n) -> p m n", m=NC), turned_bank(c)).then_inc(wt_ready, 1)
                act.wait_ge(rs_spread, 1)
                act.copy(row_scale[:, :], ps[:, 2, :]).then_inc(rs_ready, 1)

                def take_product(b):
                    act.wait_ge(y_done, b + 1)
                    if b >= 3:
                        act.wait_ge(x_ready, b - 2)
                    act.mul(y[:, b % 3, :], ps[:, 4 + b % 2, :], cs[:, b:b + 1]).then_inc(y_taken, 1)

                for b in range(B):
                    act.wait_ge(x_turned, b + 1)
                    if b >= 2:
                        act.wait_ge(y_done, b - 1)
                    act.copy(xt[:, b % 2, :, :], turned_bank(b)).then_inc(xt_ready, 1)
                    if 1 <= b <= HB:
                        take_product(b - 1)

            @block.vector
            def _(dve):
                steps = 0

                def after(instruction):
                    nonlocal steps
                    steps += 1
                    instruction.then_inc(step, 1)
                    dve.wait_ge(step, steps)

                dve.tensor_scalar(negmean[:, :], core.means(), -1.0, None, ALU.mult).then_inc(negmean_ready, 1)
                def weights():
                    after(dve.tensor_reduce(rs[:, :], w[:, :, :], AX.X, ALU.max, apply_absolute_value=True))
                    after(dve.tensor_scalar(rs[:, :], rs[:, :], 1.0 / QW, None, ALU.mult))
                    dve.wait_ge(wide_ones, 1)
                    for m in range(NC):
                        ins = dve.tensor_scalar(wide[:, m, :], wide[:, m, :], rs[:, m:m + 1], None, ALU.mult)
                    ins.then_inc(wide_ready, 1)
                    after(dve.reciprocal(rs_inv[:, :], rs[:, :]))
                    for m in range(NC):
                        ins = dve.tensor_scalar(wr[:, m, :], w[:, m, :], rs_inv[:, m:m + 1], ROUND,
                                                ALU.mult, ALU.add)
                    after(ins)
                    after(dve.tensor_scalar(wr[:, :, :], wr[:, :, :], ROUND, QW, ALU.subtract, ALU.min))
                    dve.tensor_scalar(wq[:, :, :], wr[:, :, :], -QW, None, ALU.max).then_inc(wq_ready, 1)

                def clip(half):
                    for b in range(half * HB, (half + 1) * HB):
                        dve.wait_ge(centred, b + 1)
                        after(dve.scalar_tensor_tensor(out=xn[:, b, :], in0=xn[:, b, :], scalar=core.rstd(b),
                                                       in1=low, op0=ALU.mult, op1=ALU.max))
                        after(dve.tensor_tensor(xn[:, b, :], xn[:, b, :], high, ALU.min))
                        dve.tensor_reduce(mn[:, b:b + 1], xn[:, b, :], AX.X, ALU.min)
                        ins = dve.tensor_reduce(mxm[:, b:b + 1], xn[:, b, :], AX.X, ALU.max)
                    after(ins)

                def scales(half):
                    h = slice(half * HB, (half + 1) * HB)
                    after(dve.tensor_tensor(cs[:, h], mxm[:, h], mn[:, h], ALU.subtract))
                    after(dve.tensor_scalar(cs[:, h], cs[:, h], 1.0 / QA, None, ALU.mult))
                    after(dve.tensor_scalar(flat_row[:, h], cs[:, h], 0.0, None, ALU.is_le))
                    after(dve.tensor_tensor(cs[:, h], cs[:, h], flat_row[:, h], ALU.add))
                    after(dve.reciprocal(cs_inv[:, h], cs[:, h]))
                    after(dve.tensor_tensor(zp[:, h], mn[:, h], cs_inv[:, h], ALU.mult))
                    after(dve.tensor_scalar(zp[:, h], zp[:, h], -1.0, -128.0, ALU.mult, ALU.add))
                    after(dve.tensor_scalar(zp[:, h], zp[:, h], ROUND, ROUND, ALU.add, ALU.subtract))
                    dve.tensor_scalar(ends[:, 0, h], zp[:, h], -1.0, -128.0, ALU.mult, ALU.add)
                    after(dve.tensor_scalar(ends[:, 1, h], zp[:, h], -1.0, 127.0, ALU.mult, ALU.add))

                def quantise(b):
                    p, one = b % 2, slice(b, b + 1)
                    if b >= 2:
                        dve.wait_ge(xq_ready, b - 1)
                    after(dve.tensor_scalar(xr[:, p, :], xn[:, b, :], cs_inv[:, one], ROUND, ALU.mult, ALU.add))
                    after(dve.tensor_scalar(xr[:, p, :], xr[:, p, :], ROUND, ends[:, 0, one], ALU.subtract,
                                            ALU.max))
                    if b >= 2:
                        dve.wait_ge(x_turned, b - 1)
                    dve.tensor_scalar(xq[:, p, :], xr[:, p, :], ends[:, 1, one], None, ALU.min)\
                       .then_inc(xq_ready, 1)

                def finish(b):
                    dve.wait_ge(y_ready, b + 1)
                    dve.tensor_tensor(core.x[:, b, :], core.x[:, b, :], y[:, b % 3, :], ALU.add)\
                       .then_inc(x_ready, 1)
                    dve.wait_ge(x_ready, b + 1)
                    ahead.dve(dve, b)

                def scale_product(b):
                    dve.wait_ge(y_done, b + 1)
                    dve.wait_ge(rs_ready, 1)
                    dve.wait_ge(x_ready, b - 2)
                    dve.scalar_tensor_tensor(out=y[:, b % 3, :], in0=ps[:, 4 + b % 2, :],
                                             scalar=cs[:, b:b + 1], in1=row_scale[:, :],
                                             op0=ALU.mult, op1=ALU.mult).then_inc(late_scaled, 1)

                clip(0)
                weights()
                for half in range(HALVES):
                    if half:
                        clip(1)
                    scales(half)
                    for b in range(half * HB, (half + 1) * HB):
                        quantise(b)
                        if half:
                            finish(b - HB)
                scale_product(HB)
                for b in range(HB, B):
                    if b + 1 < B:
                        scale_product(b + 1)
                    finish(b)


A2_KV, A2_REP, A2_DH = 8, 4, 16
A2_SLOT, A2_MAX_ROW = 64, 48
A2_PAIRS = A2_KV // 2
A2_KVD = A2_KV * A2_DH
A2_VSLOT = 32
A2_GROUPS, A2_PER_GROUP = 2, 4
A2_UNITS = B * A2_GROUPS
A2_RAW = 1024


def halves_of(w):
    return [w[:, 0:A2_RAW], w[:, A2_RAW:]]


def l2_attention(core):
    with ExitStack() as lay:
        nc = core.nc
        q_st = sbuf(nc, lay, "a2_q_st", [P, A2_PAIRS * A2_REP, T], F32R)
        k_st = sbuf(nc, lay, "a2_k_st", [P, A2_PAIRS, T], F32R)
        v = core.raw[:, :, A2_RAW:].rearrange("p h (b c d) -> p h b c d", b=HB, c=A2_KV)
        l2_project(core, q_st, k_st, v)
        l2_attend(core, q_st, k_st, v)


def l2_project(core, q_st, k_st, v):
    nc, dram, ps = core.nc, core.dram, core.psum
    with ExitStack() as part:
        hi = sbuf(nc, part, "a2_xn_hi", [P, NC, T], F32R)
        lo = sbuf(nc, part, "a2_xn_lo", [P, NC, T], F32R)
        turned = NormTurned(core, part, "a2", hi, lo)
        ct_hi = sbuf(nc, part, "a2_ct_hi", [P, NC, HT], F32R)
        ct_lo = sbuf(nc, part, "a2_ct_lo", [P, NC, HT], F32R)
        wq_hi = sbuf(nc, part, "a2_wq_hi", [P, NC, D], F32R)
        wq_lo = sbuf(nc, part, "a2_wq_lo", [P, NC, D], F32R)
        wkv_hi = sbuf(nc, part, "a2_wkv_hi", [P, NC, 2 * A2_KVD], F32R)
        wkv_lo = sbuf(nc, part, "a2_wkv_lo", [P, NC, 2 * A2_KVD], F32R)
        sel_k = sbuf(nc, part, "a2_sel_k", [P, 2, A2_PAIRS, P], F32R)
        sel_q = sbuf(nc, part, "a2_sel_q", [P, 2, A2_REP, P], F32R)
        part_hi = sbuf(nc, part, "a2_part_hi", [P, 2, HT], F32R)
        part_lo = sbuf(nc, part, "a2_part_lo", [P, 2, HT], F32R)
        ones_row = sbuf(nc, part, "a2_ones_row", [P, 1])

        def flat(w, a, b):
            return chunked(w[:, a:b, :])

        ct, wq = dram["ctx_turned"], dram["a2_wq"]
        pieces = [(dram["a2_wkv"], flat(wkv_hi, 0, NC), flat(wkv_lo, 0, NC)),
                  (ct[0][:, 0:A2_RAW], flat(ct_hi, 0, 2), flat(ct_lo, 0, 2)),
                  (ct[0][:, A2_RAW:], flat(ct_hi, 2, NC), flat(ct_lo, 2, NC)),
                  (dram["a2_sel_k"], sel_k[:, :, :, :].rearrange("p a b c -> p (a b c)"), None),
                  (dram["a2_sel_q"], sel_q[:, :, :, :].rearrange("p a b c -> p (a b c)"), None),
                  (wq[:, 0:A2_RAW], flat(wq_hi, 0, 2), flat(wq_lo, 0, 2)),
                  (wq[:, A2_RAW:], flat(wq_hi, 2, NC), flat(wq_lo, 2, NC)),
                  (ct[1][:, 0:A2_RAW], flat(ct_hi, 0, 2), flat(ct_lo, 0, 2)),
                  (ct[1][:, A2_RAW:], flat(ct_hi, 2, NC), flat(ct_lo, 2, NC))]
        WKV, CT0A, CT0B, SELK, SELQ, WQA, WQB, CT1A, CT1B = range(9)
        weights = Weights(core, "a2", pieces)
        jobs = [("k", 0, 0)] + [("q", h, m) for h in range(HALVES) for m in range(NC)] + [("k", 1, 0)]
        row_loaded = core.sem("a2_row_loaded")
        proj_done = core.sem("a2_proj_done")
        hi_ready, lo_ready = core.sem("a2_hi_ready"), core.sem("a2_lo_ready")
        stack_done = core.sem("a2_stack_done")
        even_ready, odd_ready = core.sem("a2_even_ready"), core.sem("a2_odd_ready")
        v_done, v_ready, v_zeroed = core.sem("a2_v_done"), core.sem("a2_v_ready"), core.sem("a2_v_zeroed")

        def stack_tile(n, i):
            kind, half, m = jobs[n]
            rows = slice(half * HT, (half + 1) * HT)
            return k_st[:, i, rows] if kind == "k" else q_st[:, m * A2_REP + i, rows]

        with nc.Block() as block:
            @block.sync
            def _(sp):
                sp.dma_start(ones_row[:, :], dram["a2_ones_row"]).then_inc(row_loaded, 16)
                weights.load(sp)
                weights.prefetch(sp, halves_of(dram["a2_wo"]))

            @block.gpsimd
            def _(pool):
                weights.split_lo(pool, [CT0A, CT0B, SELK, SELQ, WQA, WQB])
                pool.memset(core.raw[:, :, A2_RAW:], 0.0).then_inc(v_zeroed, 1)
                pool.wait_ge(v_zeroed, 1)
                for half in range(HALVES):
                    ones = pool.memset(v[:, half, :, :, A2_DH:A2_DH + 1], 1.0)
                ones.then_inc(v_zeroed, 1)
                weights.split_lo(pool, [CT1A, CT1B])

            @block.scalar
            def _(act):
                def part_of(n):
                    act.wait_ge(proj_done, n + 1)
                    if n >= 2:
                        act.wait_ge(stack_done, 4 * (n - 1))
                    act.copy(part_hi[:, n % 2, :], ps[:, 2 + n % 2, :]).then_inc(hi_ready, 1)

                def stacks(n):
                    for i in (0, 2):
                        act.wait_ge(stack_done, 4 * n + i + 1)
                        if jobs[n][0] == "k":
                            ins = act.activation(stack_tile(n, i), ps[:, 4 + i, :], ACT.Identity,
                                                 bias=ones_row[:, 0:1], scale=1.0)
                        else:
                            ins = act.copy(stack_tile(n, i), ps[:, 4 + i, :])
                        ins.then_inc(even_ready, 1)

                weights.split_hi(act, [WKV, CT0A])
                turned.act(act, range(0, 2))
                weights.split_hi(act, [CT0B])
                turned.act(act, range(2, 4))
                weights.split_hi(act, [SELK])
                turned.act(act, range(4, 6))
                weights.split_hi(act, [SELQ])
                turned.act(act, range(6, B))
                weights.split_hi(act, [WQA, WQB])
                act.wait_ge(row_loaded, 16)
                for n in range(len(jobs)):
                    part_of(n)
                    if n >= 1:
                        stacks(n - 1)
                    if n == 1:
                        act.wait_ge(v_done, 1)
                        weights.split_hi(act, [CT1A, CT1B])
                stacks(len(jobs) - 1)

            @block.vector
            def _(dve):
                def part_of(n):
                    dve.wait_ge(hi_ready, n + 1)
                    dve.tensor_tensor(part_lo[:, n % 2, :], ps[:, 2 + n % 2, :],
                                      part_hi[:, n % 2, :].bitcast(F32), ALU.subtract)\
                       .then_inc(lo_ready, 1)

                def stacks(n):
                    for i in (1, 3):
                        dve.wait_ge(stack_done, 4 * n + i + 1)
                        if jobs[n][0] == "k":
                            ins = dve.tensor_scalar(stack_tile(n, i), ps[:, 4 + i, :], ones_row[:, 0:1],
                                                    None, ALU.add)
                        else:
                            ins = dve.tensor_copy(stack_tile(n, i), ps[:, 4 + i, :])
                        ins.then_inc(odd_ready, 1)

                def values(half):
                    dve.wait_ge(v_done, half + 1)
                    dve.wait_ge(v_zeroed, 2)
                    dve.tensor_copy(v[:, half, :, :, 0:A2_DH].rearrange(
                                        "p b c d -> p (b c) d"),
                                    ps[:, half, :].rearrange("p (n d) -> p n d", d=A2_DH)).then_inc(v_ready, 1)

                turned.dve(dve, range(0, 2))
                weights.first_lo(dve)
                turned.dve(dve, range(2, B))
                dve.wait_ge(row_loaded, 16)
                for n in range(len(jobs)):
                    part_of(n)
                    if n == 0:
                        values(0)
                    if n >= 1:
                        stacks(n - 1)
                values(1)
                stacks(len(jobs) - 1)

            @block.tensor
            def _(pe):
                def project(n):
                    kind, half, m = jobs[n]
                    if n >= 2:
                        pe.wait_ge(lo_ready, n - 1)
                    for c in range(NC):
                        w = slice(m * P, (m + 1) * P)
                        if kind == "k":
                            ops = wkv_hi[:, c, w], wkv_lo[:, c, w], ct_hi[:, c, :], ct_lo[:, c, :]
                        else:
                            rows = slice(half * HT, (half + 1) * HT)
                            ops = wq_hi[:, c, w], wq_lo[:, c, w], hi[:, c, rows], lo[:, c, rows]
                        mm = matmul_split(pe, ps[:, 2 + n % 2, :], *ops, c == 0, c == NC - 1)
                    mm.then_inc(proj_done, 1)

                def stacks(n):
                    kind = jobs[n][0]
                    pe.wait_ge(lo_ready, n + 1)
                    sel = sel_k if kind == "k" else sel_q
                    for i in range(4):
                        if n >= 1:
                            pe.wait_ge(odd_ready if i % 2 else even_ready, 2 * (n - 1) + i // 2 + 1)
                        pe.matmul(ps[:, 4 + i, :], sel[:, 0, i, :], part_hi[:, n % 2, :], start=True,
                                  stop=False)
                        pe.matmul(ps[:, 4 + i, :], sel[:, 1, i, :], part_lo[:, n % 2, :], start=False,
                                  stop=True).then_inc(stack_done, 1)

                def values(half):
                    for i in range(HB):
                        rows = slice(i * P, (i + 1) * P)
                        for c in range(NC):
                            mm = matmul_split(pe, ps[:, half, i * A2_KVD:(i + 1) * A2_KVD],
                                              ct_hi[:, c, rows], ct_lo[:, c, rows],
                                              wkv_hi[:, c, A2_KVD:], wkv_lo[:, c, A2_KVD:],
                                              c == 0, c == NC - 1)
                    mm.then_inc(v_done, 1)

                turned.pe(pe)
                weights.wait(pe, CT0B)
                project(0)
                pe.wait_ge(turned.lo_ready, B)
                values(0)
                weights.wait(pe, WQB)
                for n in range(1, len(jobs)):
                    if n == len(jobs) - 1:
                        weights.wait(pe, CT1B)
                    project(n)
                    if n == len(jobs) - 1:
                        values(1)
                    stacks(n - 1)
                stacks(len(jobs) - 1)


def l2_attend(core, q_st, k_st, v):
    nc, dram, ps = core.nc, core.dram, core.psum
    scale = float(A2_DH) ** -0.5
    with ExitStack() as part:
        e = sbuf(nc, part, "a2_e", [P, 2, A2_PER_GROUP, A2_REP * P])
        osb = sbuf(nc, part, "a2_osb", [P, 2, A2_REP * P])
        rec = sbuf(nc, part, "a2_rec", [P, A2_REP, A2_PER_GROUP])
        on = sbuf(nc, part, "a2_on", [P, 2, A2_KV, A2_REP, A2_DH])
        ot_hi = sbuf(nc, part, "a2_ot_hi", [P, NC, T], F32R)
        ot_lo = sbuf(nc, part, "a2_ot_lo", [P, NC, T], F32R)
        wo_hi = sbuf(nc, part, "a2_wo_hi", [P, NC, D], F32R)
        wo_lo = sbuf(nc, part, "a2_wo_lo", [P, NC, D], F32R)
        mx = sbuf(nc, part, "a2_mx", [P, 2 * A2_REP, P])
        wo = halves_of(dram["a2_wo"])
        pieces = [(wo[0], chunked(wo_hi[:, 0:2, :]), chunked(wo_lo[:, 0:2, :])),
                  (wo[1], chunked(wo_hi[:, 2:, :]), chunked(wo_lo[:, 2:, :]))]
        weights = Weights(core, "a2o", pieces)
        ahead = Ahead(core, part, "a2")
        zeroed = core.sem("a2_zeroed")
        scores_done, max_ready = core.sem("a2_scores_done"), core.sem("a2_max_ready")
        max_turned, q_ready = core.sem("a2_max_turned"), core.sem("a2_q_ready")
        keyed_done, exp_ready = core.sem("a2_keyed_done"), core.sem("a2_exp_ready")
        pv_done, o_ready = core.sem("a2_pv_done"), core.sem("a2_o_ready")
        o_turned, rec_ready, on_ready = (core.sem(f"a2_{n}") for n in ("o_turned", "rec_ready", "on_ready"))
        on_turned, ot_hi_ready, ot_lo_ready = (core.sem(f"a2_{n}") for n in
                                               ("on_turned", "ot_hi_ready", "ot_lo_ready"))
        y_done, x_ready = core.sem("a2_y_done"), core.sem("a2_x_ready")
        M_BANK, O_BANK, S_BANK, ON_BANK = 0, 2, 4, 3

        def rows_of(b):
            return slice(b * P, (b + 1) * P)

        STEPS = 2 * A2_UNITS

        def s_bank(s):
            return S_BANK + 2 * (s % 2)

        def batch_pair(s):
            return divmod(s, A2_PAIRS)

        with nc.Block() as block:
            @block.sync
            def _(sp):
                weights.prefetch(sp)

            @block.gpsimd
            def _(pool):
                pool.memset(mx[:, :, :], 0.0).then_inc(zeroed, 1)
                weights.split_lo(pool)
                ahead.pool(pool)

            @block.scalar
            def _(act):
                def take_out(u):
                    act.wait_ge(pv_done, u + 1)
                    if u >= 2:
                        act.wait_ge(o_turned, u - 1)
                    act.copy(osb[:, u % 2, :], ps[:, O_BANK + u % 2, :]).then_inc(o_ready, 1)

                def turned_hi(b):
                    act.wait_ge(on_turned, b + 1)
                    act.copy(ot_hi[:, :, rows_of(b)], ps[:, ON_BANK, :].rearrange("p (c t) -> p c t", c=NC))\
                       .then_inc(ot_hi_ready, 1)

                weights.split_hi(act)
                for s in range(STEPS + 4):
                    u = s // 2
                    if s < STEPS:
                        act.wait_ge(keyed_done, s + 1)
                        if u >= 2:
                            act.wait_ge(pv_done, u - 1)
                        act.activation(e[:, u % 2, 2 * (s % 2):2 * (s % 2) + 2, :],
                                       ps[:, s_bank(s):s_bank(s) + 2, :],
                                       ACT.Exp, scale=scale).then_inc(exp_ready, 1)
                    if s % 2 == 0 and 1 <= u <= A2_UNITS:
                        take_out(u - 1)
                    if s % A2_PAIRS == 2 and s >= 6:
                        turned_hi((s - 6) // A2_PAIRS)

            @block.vector
            def _(dve):
                def take_on(u):
                    b, g = divmod(u, A2_GROUPS)
                    dve.wait_ge(o_turned, u + 1)
                    if u >= 1:
                        dve.wait_ge(on_ready, u)
                    o = ps[:, O_BANK + u % 2, :].rearrange("p (m c d) -> p m c d", m=A2_REP, c=A2_PER_GROUP)
                    dve.reciprocal(rec[:, :, :], o[:, :, :, A2_DH]).then_inc(rec_ready, 1)
                    dve.wait_ge(rec_ready, u + 1)
                    if b >= 2:
                        dve.wait_ge(on_turned, b - 1)
                    dve.tensor_tensor(
                        on[:, b % 2, g * A2_PER_GROUP:(g + 1) * A2_PER_GROUP, :, :].rearrange(
                            "p c m d -> p m c d"),
                        o[:, :, :, 0:A2_DH],
                        rec[:, :, :].unsqueeze(3).broadcast_to([P, A2_REP, A2_PER_GROUP, A2_DH]),
                        ALU.mult).then_inc(on_ready, 1)

                def turned_lo(b):
                    dve.wait_ge(ot_hi_ready, b + 1)
                    dve.tensor_tensor(ot_lo[:, :, rows_of(b)],
                                      ps[:, ON_BANK, :].rearrange("p (c t) -> p c t", c=NC),
                                      ot_hi[:, :, rows_of(b)].bitcast(F32), ALU.subtract)\
                       .then_inc(ot_lo_ready, 1)

                def maximum(s):
                    dve.wait_ge(scores_done, s + 1)
                    tiles = slice(A2_REP * (s % 2), A2_REP * (s % 2 + 1))
                    dve.tensor_reduce(
                        mx[:, tiles, A2_MAX_ROW:P:A2_SLOT].rearrange("p m r -> p r m"),
                        ps[:, s_bank(s):s_bank(s) + 2, :].rearrange("p r (m j) -> p r m j", m=A2_REP),
                        AX.X, ALU.max, negate=True).then_inc(max_ready, 1)

                def lower(s):
                    b, pair = batch_pair(s)
                    dve.wait_ge(max_turned, s + 1)
                    tiles = q_st[:, pair * A2_REP:(pair + 1) * A2_REP, rows_of(b)]
                    dve.tensor_tensor(tiles, ps[:, M_BANK + s % 2, :].rearrange("p (m t) -> p m t", m=A2_REP),
                                      tiles.bitcast(F32), ALU.add).then_inc(q_ready, 1)

                dve.wait_ge(zeroed, 1)
                maximum(0)
                lower(0)
                maximum(1)
                for s in range(STEPS + 4):
                    if s + 1 < STEPS:
                        lower(s + 1)
                    if s % A2_PAIRS == 2 and s >= 6:
                        turned_lo((s - 6) // A2_PAIRS)
                    if s + 2 < STEPS:
                        maximum(s + 2)
                    if s % 2 == 1 and 3 <= s < STEPS + 2:
                        take_on((s - 3) // 2)
                for b in range(B):
                    dve.wait_ge(y_done, b + 1)
                    dve.tensor_tensor(core.x[:, b, :], ps[:, S_BANK + b % 4, :], core.x[:, b, :], ALU.add)\
                       .then_inc(x_ready, 1)
                    dve.wait_ge(x_ready, b + 1)
                    ahead.dve(dve, b)
                dve.wait_ge(x_ready, B)

            @block.tensor
            def _(pe):
                def slot(i):
                    return slice(A2_SLOT * (i % 2), A2_SLOT * (i % 2 + 1))

                def scores(s):
                    b, pair = batch_pair(s)
                    if s >= 2:
                        pe.wait_ge(exp_ready, s - 1)
                    for m in range(A2_REP):
                        for i in range(2):
                            mm = pe.matmul(ps[:, s_bank(s) + i, m * P:(m + 1) * P],
                                           q_st[slot(i), pair * A2_REP + m, rows_of(b)],
                                           k_st[slot(i), pair, rows_of(b)], start=True, stop=True)
                    mm.then_inc(scores_done, 1)

                def turn_max(s):
                    pe.wait_ge(max_ready, s + 1)
                    if s >= 2:
                        pe.wait_ge(q_ready, s - 1)
                    for m in range(A2_REP):
                        mm = pe.transpose(ps[:, M_BANK + s % 2, m * P:(m + 1) * P],
                                          mx[:, A2_REP * (s % 2) + m, :], core.ident[:, :])
                    mm.then_inc(max_turned, 1)

                def keyed(s):
                    b, pair = batch_pair(s)
                    pe.wait_ge(q_ready, s + 1)
                    for i in range(2):
                        mm = pe.matmul(ps[:, s_bank(s) + i, :], k_st[slot(i), pair, rows_of(b)],
                                       q_st[slot(i), pair * A2_REP:(pair + 1) * A2_REP, rows_of(b)],
                                       start=True, stop=True)
                    mm.then_inc(keyed_done, 1)

                def values(s):
                    u = s // 2
                    b, g = divmod(u, A2_GROUPS)
                    pe.wait_ge(exp_ready, s + 1)
                    if u >= 2:
                        pe.wait_ge(on_ready, u - 1)
                    if u % 2 == 1 and b >= 1:
                        pe.wait_ge(ot_lo_ready, b)
                    for i in range(2 * (s % 2), 2 * (s % 2) + 2):
                        mm = pe.matmul(ps[A2_VSLOT * i:A2_VSLOT * (i + 1), O_BANK + u % 2, :],
                                       v[:, b // HB, b % HB, g * A2_PER_GROUP + i, :], e[:, u % 2, i, :],
                                       start=True, stop=True)
                    if s % 2 == 1:
                        mm.then_inc(pv_done, 1)

                def turn_o(u):
                    pe.wait_ge(o_ready, u + 1)
                    for m in range(A2_REP):
                        mm = pe.transpose(ps[:, O_BANK + u % 2, m * P:(m + 1) * P],
                                          osb[:, u % 2, m * P:(m + 1) * P], core.ident[:, :])
                    mm.then_inc(o_turned, 1)

                def turn_on(b):
                    pe.wait_ge(on_ready, A2_GROUPS * (b + 1))
                    rows = on[:, b % 2, :, :, :].rearrange("p c m d -> p (c m d)")
                    for c in range(NC):
                        mm = pe.transpose(ps[:, ON_BANK, c * P:(c + 1) * P], rows[:, c * P:(c + 1) * P],
                                          core.ident[:, :])
                    mm.then_inc(on_turned, 1)

                scores(0)
                turn_max(0)
                scores(1)
                for s in range(STEPS + 4):
                    if s < STEPS:
                        keyed(s)
                    if 1 <= s <= STEPS:
                        values(s - 1)
                    if s + 1 < STEPS:
                        turn_max(s + 1)
                    if s % 2 == 1 and 3 <= s < STEPS + 2:
                        turn_o((s - 3) // 2)
                    if s % A2_PAIRS == 2 and s >= 6:
                        turn_on((s - 6) // A2_PAIRS)
                    if s + 2 < STEPS:
                        scores(s + 2)
                weights.wait(pe, 1)
                pe.wait_ge(ot_lo_ready, B)
                for b in range(B):
                    if b >= 4:
                        pe.wait_ge(x_ready, b - 3)
                    for c in range(NC):
                        mm = matmul_split(pe, ps[:, S_BANK + b % 4, :], ot_hi[:, c, rows_of(b)],
                                          ot_lo[:, c, rows_of(b)], wo_hi[:, c, :], wo_lo[:, c, :],
                                          c == 0, c == NC - 1)
                    mm.then_inc(y_done, 1)


F2_H, F2_R = 8, 16
F2_HR = F2_H * F2_R
F2_N = F2_HR + F2_H
F2_SCALING = 2.0


def l2_ffn(core):
    nc, dram, ps = core.nc, core.dram, core.psum
    with ExitStack() as lay:
        hi = sbuf(nc, lay, "f2_xn_hi", [P, NC, T], F32R)
        lo = sbuf(nc, lay, "f2_xn_lo", [P, NC, T], F32R)
        turned = NormTurned(core, lay, "f2", hi, lo)
        a_hi = sbuf(nc, lay, "f2_a_hi", [P, NC, F2_N], F32R)
        a_lo = sbuf(nc, lay, "f2_a_lo", [P, NC, F2_N], F32R)
        b_hi = sbuf(nc, lay, "f2_b_hi", [P, D], F32R)
        b_lo = sbuf(nc, lay, "f2_b_lo", [P, D], F32R)
        br = sbuf(nc, lay, "f2_br", [F2_H, 1])
        low = sbuf(nc, lay, "f2_low", [P, T])
        logit = sbuf(nc, lay, "f2_logit", [F2_H, T])
        weight = sbuf(nc, lay, "f2_weight", [P, B, F2_H])
        wide = sbuf(nc, lay, "f2_wide", [P, B, F2_H, F2_R])
        col = sbuf(nc, lay, "f2_col", [P, B])
        lt = sbuf(nc, lay, "f2_lt", [P, T])
        lt_hi = sbuf(nc, lay, "f2_lt_hi", [P, T], F32R)
        lt_lo = sbuf(nc, lay, "f2_lt_lo", [P, T], F32R)
        pieces = [(dram["f2_a"], chunked(a_hi[:, :, :]), chunked(a_lo[:, :, :])),
                  (dram["f2_b"], b_hi[:, :], b_lo[:, :])]
        weights = Weights(core, "f2", pieces)
        ahead = Ahead(core, lay, "f2")
        br_loaded = core.sem("f2_br_loaded")
        low_done, low_ready = core.sem("f2_low_done"), core.sem("f2_low_ready")
        logits_done, logit_ready, logits_turned = (core.sem(f"f2_{n}") for n in
                                                   ("logits_done", "logit_ready", "logits_turned"))
        shifted_ready, exp_ready, step = (core.sem(f"f2_{n}") for n in ("shifted_ready", "exp_ready", "step"))
        wide_ready, wide_turned = core.sem("f2_wide_ready"), core.sem("f2_wide_turned")
        lt_ready, lt_hi_ready, lt_lo_ready = (core.sem(f"f2_{n}") for n in
                                              ("lt_ready", "lt_hi_ready", "lt_lo_ready"))
        y_done, x_ready = core.sem("f2_y_done"), core.sem("f2_x_ready")
        LOW_BANK, G_BANK, T_BANK, Y_BANK = 2, 4, 6, 0

        def rows_of(h):
            return slice(h * HT, (h + 1) * HT)

        def by_row():
            return ps[:, T_BANK, 0:B * F2_H].rearrange("p (b h) -> p b h", b=B)

        with nc.Block() as block:
            @block.sync
            def _(sp):
                sp.dma_start(br[:, :], dram["f2_br"]).then_inc(br_loaded, 16)
                weights.load(sp)
                weights.prefetch(sp)

            @block.gpsimd
            def _(pool):
                weights.split_lo(pool, [1])
                ahead.pool(pool)

            @block.scalar
            def _(act):
                def take_low(h):
                    act.wait_ge(low_done, h + 1)
                    act.copy(low[:, rows_of(h)], ps[:, LOW_BANK + h, :]).then_inc(low_ready, 1)

                def take_logit(h):
                    act.wait_ge(logits_done, h + 1)
                    act.activation(logit[:, rows_of(h)], ps[0:F2_H, G_BANK + h, :], ACT.Identity,
                                   bias=br[:, 0:1], scale=1.0).then_inc(logit_ready, 1)

                weights.split_hi(act, [0])
                turned.act(act, range(0, HB))
                weights.split_hi(act, [1])
                act.wait_ge(br_loaded, 16)
                take_logit(0)
                take_low(0)
                turned.act(act, range(HB, B))
                take_logit(1)
                act.wait_ge(shifted_ready, 1)
                act.activation(weight[:, :, :], weight[:, :, :], ACT.Exp).then_inc(exp_ready, 1)
                take_low(1)
                for h in range(HALVES):
                    act.wait_ge(lt_ready, h + 1)
                    act.copy(lt_hi[:, rows_of(h)], lt[:, rows_of(h)]).then_inc(lt_hi_ready, 1)

            @block.tensor
            def _(pe):
                def product(out, cols, h):
                    for c in range(NC):
                        mm = matmul_split(pe, out, a_hi[:, c, cols], a_lo[:, c, cols],
                                          hi[:, c, rows_of(h)], lo[:, c, rows_of(h)], c == 0, c == NC - 1)
                    return mm

                def logits(h):
                    pe.wait_ge(turned.lo_ready, HB * (h + 1))
                    product(ps[0:F2_H, G_BANK + h, :], slice(F2_HR, F2_N), h).then_inc(logits_done, 1)

                def lower(h):
                    product(ps[:, LOW_BANK + h, :], slice(0, F2_HR), h).then_inc(low_done, 1)

                turned.pe(pe, range(0, HB))
                weights.wait(pe, 0)
                logits(0)
                lower(0)
                turned.pe(pe, range(HB, B))
                logits(1)
                pe.wait_ge(logit_ready, HALVES)
                for b in range(B):
                    mm = pe.transpose(ps[:, T_BANK, b * F2_H:(b + 1) * F2_H], logit[:, b * P:(b + 1) * P],
                                      core.ident[0:F2_H, 0:F2_H])
                mm.then_inc(logits_turned, 1)
                lower(1)
                for h in range(HALVES):
                    pe.wait_ge(wide_ready, h + 1)
                    for i in range(HB):
                        mm = pe.transpose(ps[:, G_BANK + h, i * P:(i + 1) * P],
                                          wide[:, h * HB + i, :, :].rearrange("p h r -> p (h r)"),
                                          core.ident[:, :])
                    mm.then_inc(wide_turned, 1)
                weights.wait(pe, 1)
                for b in range(B):
                    pe.wait_ge(lt_lo_ready, b // HB + 1)
                    if b >= 2:
                        pe.wait_ge(x_ready, b - 1)
                    rows = slice(b * P, (b + 1) * P)
                    matmul_split(pe, ps[:, Y_BANK + b % 2, :], lt_hi[:, rows], lt_lo[:, rows], b_hi[:, :],
                                 b_lo[:, :], True, True).then_inc(y_done, 1)

            @block.vector
            def _(dve):
                steps = 0

                def after(instruction):
                    nonlocal steps
                    steps += 1
                    instruction.then_inc(step, 1)
                    dve.wait_ge(step, steps)

                def by_batch(c):
                    return c[:, :].unsqueeze(2).broadcast_to([P, B, F2_H])

                turned.dve(dve, range(0, 2))
                weights.first_lo(dve)
                turned.dve(dve, range(2, B))
                dve.wait_ge(logits_turned, 1)
                after(dve.tensor_reduce(col[:, :], by_row(), AX.X, ALU.max))
                dve.tensor_tensor(weight[:, :, :], by_row(), by_batch(col), ALU.subtract)\
                   .then_inc(shifted_ready, 1)
                dve.wait_ge(exp_ready, 1)
                after(dve.tensor_reduce(col[:, :], weight[:, :, :], AX.X, ALU.add))
                after(dve.reciprocal(col[:, :], col[:, :]))
                after(dve.scalar_tensor_tensor(out=weight[:, :, :], in0=weight[:, :, :],
                                               scalar=F2_SCALING * F2_H, in1=by_batch(col),
                                               op0=ALU.mult, op1=ALU.mult))
                for h in range(HALVES):
                    batches = slice(h * HB, (h + 1) * HB)
                    w = weight[:, batches, :].unsqueeze(3).broadcast_to([P, HB, F2_H, F2_R])
                    dve.tensor_copy(wide[:, batches, :, :], w).then_inc(wide_ready, 1)
                dve.wait_ge(low_ready, HALVES)
                for h in range(HALVES):
                    dve.wait_ge(wide_turned, h + 1)
                    dve.tensor_tensor(lt[:, rows_of(h)], low[:, rows_of(h)], ps[:, G_BANK + h, :],
                                      ALU.mult).then_inc(lt_ready, 1)
                for h in range(HALVES):
                    dve.wait_ge(lt_hi_ready, h + 1)
                    dve.tensor_tensor(lt_lo[:, rows_of(h)], lt[:, rows_of(h)], lt_hi[:, rows_of(h)].bitcast(F32),
                                      ALU.subtract).then_inc(lt_lo_ready, 1)
                for b in range(B):
                    dve.wait_ge(y_done, b + 1)
                    dve.tensor_tensor(core.x[:, b, :], ps[:, Y_BANK + b % 2, :], core.x[:, b, :], ALU.add)\
                       .then_inc(x_ready, 1)
                    dve.wait_ge(x_ready, b + 1)
                    ahead.dve(dve, b)


A3_JOBS = B * NC


def l3_attention(core):
    nc, dram, ps = core.nc, core.dram, core.psum
    scale = float(P) ** -0.5
    with ExitStack() as lay:
        c_hi = sbuf(nc, lay, "a3_c_hi", [P, B, D], F32R)
        c_lo = sbuf(nc, lay, "a3_c_lo", [P, B, D], F32R)
        v_hi = [sbuf(nc, lay, f"a3_v{h}_hi", [P, NC, HT], F32R) for h in range(HALVES)]
        v_lo = [sbuf(nc, lay, f"a3_v{h}_lo", [P, NC, HT], F32R) for h in range(HALVES)]
        pieces = []
        for h in range(HALVES):
            batches = slice(h * HB, (h + 1) * HB)
            pieces += [(dram["ctx_rows"][h], chunked(c_hi[:, batches, :]), chunked(c_lo[:, batches, :])),
                       (dram["ctx_turned"][h], chunked(v_hi[h][:, :, :]), chunked(v_lo[h][:, :, :]))]
        weights = Weights(core, "a3", pieces)
        xn = sbuf(nc, lay, "a3_xn", [P, 2, D])
        q_hi = sbuf(nc, lay, "a3_q_hi", [P, 2, D], F32R)
        q_lo = sbuf(nc, lay, "a3_q_lo", [P, 2, D], F32R)
        e = sbuf(nc, lay, "a3_e", [P, 2, D])
        et_hi = sbuf(nc, lay, "a3_et_hi", [P, 2, NC, D], F32R)
        et_lo = sbuf(nc, lay, "a3_et_lo", [P, 2, NC, D], F32R)
        negmax = sbuf(nc, lay, "a3_negmax", [P, A3_JOBS])
        shift = sbuf(nc, lay, "a3_shift", [P, A3_JOBS])
        total = sbuf(nc, lay, "a3_total", [P, A3_JOBS])
        inv = sbuf(nc, lay, "a3_inv", [P, A3_JOBS])
        ahead = Ahead(core, lay, "a3")
        xn_ready, q_hi_ready, q_lo_ready = (core.sem(f"a3_{n}") for n in ("xn_ready", "q_hi_ready", "q_lo_ready"))
        scores_done, negmax_ready, shift_ready = (core.sem(f"a3_{n}") for n in
                                                  ("scores_done", "negmax_ready", "shift_ready"))
        exp_ready, inv_ready, e_ready = (core.sem(f"a3_{n}") for n in ("exp_ready", "inv_ready", "e_ready"))
        e_turned, et_hi_ready, et_lo_ready = (core.sem(f"a3_{n}") for n in
                                              ("e_turned", "et_hi_ready", "et_lo_ready"))
        y_done, x_ready = core.sem("a3_y_done"), core.sem("a3_x_ready")
        S_BANK, T_BANK, Y_BANK = 0, 2, 4

        def turned_bank(j):
            return ps[:, T_BANK + j % 2, :].rearrange("p (m n) -> p m n", m=NC)

        def columns(part, j):
            b, n = divmod(j, NC)
            return part[:, b % 2, :, n * P:(n + 1) * P]

        with nc.Block() as block:
            @block.sync
            def _(sp):
                weights.load(sp)
                weights.prefetch(sp)

            @block.gpsimd
            def _(pool):
                def query_lo(b):
                    pool.wait_ge(q_hi_ready, b + 1)
                    if b >= 2:
                        pool.wait_ge(scores_done, NC * (b - 1))
                    pool.tensor_tensor(q_lo[:, b % 2, :], xn[:, b % 2, :], q_hi[:, b % 2, :].bitcast(F32),
                                       ALU.subtract).then_inc(q_lo_ready, 1)

                query_lo(0)
                weights.split_lo(pool, [1])
                for b in range(1, B):
                    query_lo(b)
                    if b <= HALVES:
                        weights.split_lo(pool, [1 + b])
                ahead.pool(pool)

            @block.scalar
            def _(act):
                def query_hi(b):
                    act.wait_ge(xn_ready, b + 1)
                    if b >= 2:
                        act.wait_ge(scores_done, NC * (b - 1))
                    act.copy(q_hi[:, b % 2, :], xn[:, b % 2, :]).then_inc(q_hi_ready, 1)

                def exp(j):
                    act.wait_ge(shift_ready, j + 1)
                    if j >= 2:
                        act.wait_ge(e_turned, j - 1)
                    act.activation(e[:, j % 2, :], ps[:, S_BANK + j % 2, :], ACT.Exp,
                                   bias=shift[:, j:j + 1], scale=scale,
                                   accum_out=total[:, j:j + 1]).then_inc(exp_ready, 1)

                def turned_hi(j):
                    act.wait_ge(e_turned, j + 1)
                    if j // NC >= 2:
                        act.wait_ge(y_done, j // NC - 1)
                    act.copy(columns(et_hi, j), turned_bank(j)).then_inc(et_hi_ready, 1)

                weights.split_hi(act, [0])
                query_hi(0)
                weights.split_hi(act, [1])
                for j in range(A3_JOBS):
                    exp(j)
                    if j >= 1:
                        turned_hi(j - 1)
                    if j % NC == 1 and j // NC + 1 < B:
                        query_hi(j // NC + 1)
                    if j in (0, 4):
                        weights.split_hi(act, [2 + j // 4])
                turned_hi(A3_JOBS - 1)

            @block.vector
            def _(dve):
                def query(b):
                    if b >= 2:
                        dve.wait_ge(q_lo_ready, b - 1)
                    dve.tensor_scalar(xn[:, b % 2, :], core.x[:, b, :], core.mean(b), core.rstd(b),
                                      ALU.subtract, ALU.mult).then_inc(xn_ready, 1)

                def maximum(j):
                    dve.wait_ge(scores_done, j + 1)
                    dve.tensor_reduce(negmax[:, j:j + 1], ps[:, S_BANK + j % 2, :], AX.X, ALU.max,
                                      negate=True).then_inc(negmax_ready, 1)
                    dve.wait_ge(negmax_ready, j + 1)
                    dve.tensor_scalar(shift[:, j:j + 1], negmax[:, j:j + 1], scale, None, ALU.mult)\
                       .then_inc(shift_ready, 1)

                def invert(j):
                    dve.wait_ge(exp_ready, j + 1)
                    dve.reciprocal(inv[:, j:j + 1], total[:, j:j + 1]).then_inc(inv_ready, 1)

                def divide(j):
                    dve.wait_ge(inv_ready, j + 1)
                    dve.tensor_scalar(e[:, j % 2, :], e[:, j % 2, :], inv[:, j:j + 1], None, ALU.mult)\
                       .then_inc(e_ready, 1)

                def turned_lo(j):
                    dve.wait_ge(et_hi_ready, j + 1)
                    dve.tensor_tensor(columns(et_lo, j), turned_bank(j), columns(et_hi, j).bitcast(F32),
                                      ALU.subtract).then_inc(et_lo_ready, 1)

                def add(b):
                    dve.wait_ge(y_done, b + 1)
                    dve.tensor_tensor(core.x[:, b, :], ps[:, Y_BANK + b % 2, :], core.x[:, b, :], ALU.add)\
                       .then_inc(x_ready, 1)
                    dve.wait_ge(x_ready, b + 1)
                    ahead.dve(dve, b)

                query(0)
                weights.first_lo(dve)
                for j in range(A3_JOBS):
                    b, n = divmod(j, NC)
                    maximum(j)
                    if j >= 1:
                        invert(j - 1)
                        divide(j - 1)
                    if n == 0 and b + 1 < B:
                        query(b + 1)
                    if j >= 2:
                        turned_lo(j - 2)
                    if n == 0 and b >= 2:
                        add(b - 2)
                invert(A3_JOBS - 1)
                divide(A3_JOBS - 1)
                turned_lo(A3_JOBS - 2)
                turned_lo(A3_JOBS - 1)
                add(B - 2)
                add(B - 1)

            @block.tensor
            def _(pe):
                def scores(j):
                    b, n = divmod(j, NC)
                    if n == 0:
                        pe.wait_ge(q_lo_ready, b + 1)
                        if b % HB == 0:
                            weights.wait(pe, 2 * (b // HB))
                    if j >= 2:
                        pe.wait_ge(exp_ready, j - 1)
                    cols = slice(n * P, (n + 1) * P)
                    matmul_split(pe, ps[:, S_BANK + j % 2, :], c_hi[:, b, cols], c_lo[:, b, cols],
                                 q_hi[:, b % 2, :], q_lo[:, b % 2, :], True, True).then_inc(scores_done, 1)

                def turn(j):
                    pe.wait_ge(e_ready, j + 1)
                    if j >= 2:
                        pe.wait_ge(et_lo_ready, j - 1)
                    for m in range(NC):
                        mm = pe.transpose(turned_bank(j)[:, m, :], e[:, j % 2, m * P:(m + 1) * P],
                                          core.ident[:, :])
                    mm.then_inc(e_turned, 1)

                def attend(b, chunks):
                    h, i = divmod(b, HB)
                    if i == 0:
                        weights.wait(pe, 2 * h + 1)
                    pe.wait_ge(et_lo_ready, NC * (b + 1))
                    if b >= 2:
                        pe.wait_ge(x_ready, b - 1)
                    for m in chunks:
                        mm = matmul_split(pe, ps[:, Y_BANK + b % 2, :], v_hi[h][:, m, i * P:(i + 1) * P],
                                          v_lo[h][:, m, i * P:(i + 1) * P], et_hi[:, b % 2, m, :],
                                          et_lo[:, b % 2, m, :], m == 0, m == NC - 1)
                    if NC - 1 in chunks:
                        mm.then_inc(y_done, 1)

                scores(0)
                for j in range(A3_JOBS):
                    if j + 1 < A3_JOBS:
                        scores(j + 1)
                    if j >= 1:
                        turn(j - 1)
                    if j % NC >= 2 and j // NC >= 1:
                        attend(j // NC - 1, (0, 1) if j % NC == 2 else (2, 3))
                turn(A3_JOBS - 1)
                attend(B - 1, range(NC))


F3_INT, F3_LAT, F3_E = 1024, 256, 8
F3_IC, F3_LC = F3_INT // P, F3_LAT // P


def l3_ffn(core):
    nc, dram, ps = core.nc, core.dram, core.psum
    with ExitStack() as lay:
        hi = sbuf(nc, lay, "f3_xn_hi", [P, NC, T], F32R)
        lo = sbuf(nc, lay, "f3_xn_lo", [P, NC, T], F32R)
        turned = NormTurned(core, lay, "f3", hi, lo)

        def pair(name, shape):
            return (sbuf(nc, lay, f"f3_{name}_hi", shape, F32R), sbuf(nc, lay, f"f3_{name}_lo", shape, F32R))

        UP_N = 2 * P
        up, down = pair("up", [P, F3_INT // UP_N, NC * UP_N]), pair("down", [P, F3_IC, D])
        fc1, fc2 = pair("fc1", [P, NC, F3_LAT]), pair("fc2", [P, F3_LC, D])
        expert, gate = pair("expert", [P, F3_LC, F3_LAT]), pair("gate", [P, NC, F3_E])
        latent, routed = pair("latent", [P, F3_LC, HT]), pair("routed", [P, F3_LC, HT])
        h = pair("h", [P, F3_IC, HT])
        relu = sbuf(nc, lay, "f3_relu", [P, 2, HT])
        gamma, beta = core.raw[:, 0, RAW // 2:RAW // 2 + D], core.raw[:, 1, RAW // 2:RAW // 2 + D]
        side = core.raw[:, 0, RAW - D:]
        both = turned.xn
        top = sbuf(nc, lay, "f3_top", [P, B, F3_E])
        rw = sbuf(nc, lay, "f3_rw", [P, B])
        logit = turned.xn[0:F3_E, :, :].rearrange("p i n -> p (i n)")
        norm = Norm(core, lay, "f3o")

        def piece(name, parts, a, b):
            n = parts[0].shape[2]
            return (dram[name][:, a * n:b * n], chunked(parts[0][:, a:b, :]), chunked(parts[1][:, a:b, :]))

        pieces = [piece("f3_fc1", fc1, 0, NC), piece("f3_gate", gate, 0, NC),
                  piece("f3_expert", expert, 0, F3_LC)]
        pieces += [piece("f3_up", up, i, i + 1) for i in range(F3_INT // UP_N)]
        pieces += [piece("f3_fc2", fc2, 0, F3_LC)]
        pieces += [piece("f3_down", down, c, c + 2) for c in range(0, F3_IC, 2)]
        FC1, GATE, EXPERT, UP, FC2 = 0, 1, 2, 3, 3 + F3_INT // UP_N
        LAST_UP, LAST = FC2 - 1, len(pieces) - 1
        weights = Weights(core, "f3", pieces)
        order = [("fc1", 0), ("fc1", 1), ("up", 0), ("expert", 0), ("expert", 1)]
        order += [("up", m) for m in range(1, F3_IC)]
        jobs = [(half, kind, m) for half in range(HALVES) for kind, m in order]
        PER_HALF = len(order)
        SPLIT_AT = range(F3_LC, F3_LC + len(pieces) - FC2)

        def before(n, kinds):
            return sum(k in kinds for _, k, _ in jobs[:n])

        cols_loaded = core.sem("f3_cols_loaded")
        logits_done, top_ready, rw_ready = (core.sem(f"f3_{n}") for n in ("logits_done", "top_ready", "rw_ready"))
        logit_ready, logits_turned = core.sem("f3_logit_ready"), core.sem("f3_logits_turned")
        job_done = core.sem("f3_job_done")
        hi_ready, lo_ready = core.sem("f3_hi_ready"), core.sem("f3_lo_ready")
        relu_ready, square_ready = core.sem("f3_relu_ready"), core.sem("f3_square_ready")
        h_hi_ready, h_lo_ready = core.sem("f3_h_hi_ready"), core.sem("f3_h_lo_ready")
        side_done, side_ready = core.sem("f3_side_done"), core.sem("f3_side_ready")
        main_done, both_ready = core.sem("f3_main_done"), core.sem("f3_both_ready")
        unit_ready, gain_ready, out_ready = (core.sem(f"f3_{n}") for n in ("unit_ready", "gain_ready", "out_ready"))
        x_ready = core.sem("f3_x_ready")
        JOB_BANK, G_BANK, SIDE_BANK, MAIN_BANK = 2, 4, 5, 6
        SPLIT = ("fc1", "expert")

        def split_out(kind):
            return latent if kind == "fc1" else routed

        with nc.Block() as block:
            @block.sync
            def _(sp):
                weights.load(sp)
                sp.dma_start(gamma, dram["f3_gamma"]).then_inc(cols_loaded, 16)
                sp.dma_start(beta, dram["f3_beta"]).then_inc(cols_loaded, 16)

            @block.gpsimd
            def _(pool):
                weights.split_lo(pool, range(GATE, LAST_UP + 1))

                def square_lo(n):
                    i = before(n, ("up",))
                    pool.wait_ge(h_hi_ready, i + 1)
                    pool.tensor_tensor(h[1][:, jobs[n][2], :], relu[:, i % 2, :],
                                       h[0][:, jobs[n][2], :].bitcast(F32), ALU.subtract).then_inc(h_lo_ready, 1)

                def gain(b):
                    norm.scale(pool, b)
                    pool.wait_ge(cols_loaded, 32)
                    pool.wait_ge(unit_ready, b + 1)
                    pool.tensor_tensor(both[:, b % 2, :], both[:, b % 2, :], gamma, ALU.mult)\
                        .then_inc(gain_ready, 1)
                    pool.wait_ge(gain_ready, b + 1)
                    pool.tensor_tensor(both[:, b % 2, :], both[:, b % 2, :], beta, ALU.add)\
                        .then_inc(out_ready, 1)

                for half in range(HALVES):
                    for n in range(half * PER_HALF, (half + 1) * PER_HALF):
                        if n in SPLIT_AT:
                            weights.split_lo(pool, [FC2 + n - SPLIT_AT[0]])
                        if jobs[n][1] == "up":
                            square_lo(n)
                    for b in range(half * HB, (half + 1) * HB):
                        gain(b)

            @block.scalar
            def _(act):
                def evacuate(n):
                    half, kind, m = jobs[n]
                    act.wait_ge(job_done, n + 1)
                    if kind in SPLIT:
                        if half:
                            act.wait_ge(side_done, HB)
                        act.copy(split_out(kind)[0][:, m, :], ps[:, JOB_BANK + n % 2, :]).then_inc(hi_ready, 1)
                    else:
                        i = before(n, ("up",))
                        if i >= 2:
                            act.wait_ge(h_lo_ready, i - 1)
                        act.activation(relu[:, i % 2, :], ps[:, JOB_BANK + n % 2, :], ACT.Relu)\
                           .then_inc(relu_ready, 1)
                        act.wait_ge(square_ready, i + 1)
                        if half:
                            act.wait_ge(main_done, HB)
                        act.copy(h[0][:, m, :], relu[:, i % 2, :]).then_inc(h_hi_ready, 1)

                def take_side(b):
                    act.wait_ge(side_done, b + 1)
                    act.wait_ge(rw_ready, 1)
                    if b >= 1:
                        act.wait_ge(both_ready, b)
                    act.mul(side, ps[:, SIDE_BANK, :], rw[:, b:b + 1]).then_inc(side_ready, 1)

                weights.split_hi(act, [FC1])
                turned.act(act, range(0, 2))
                weights.split_hi(act, [GATE, EXPERT])
                turned.act(act, range(2, HB))
                weights.split_hi(act, [UP])
                for half in range(HALVES):
                    for n in range(half * PER_HALF, (half + 1) * PER_HALF):
                        evacuate(n)
                        if n == F3_LC - 1:
                            for b in range(HB, B):
                                turned.act(act, [b])
                                if UP + b - HB + 1 <= LAST_UP:
                                    weights.split_hi(act, [UP + b - HB + 1])
                        if n in SPLIT_AT:
                            weights.split_hi(act, [FC2 + n - SPLIT_AT[0]])
                        if n == PER_HALF - 3:
                            for i in range(HALVES):
                                act.wait_ge(logits_done, i + 1)
                                act.copy(logit[:, i * HT:(i + 1) * HT], ps[0:F3_E, G_BANK + i, :])\
                                   .then_inc(logit_ready, 1)
                    for b in range(half * HB, (half + 1) * HB):
                        take_side(b)

            @block.vector
            def _(dve):
                def evacuate(n):
                    half, kind, m = jobs[n]
                    if kind in SPLIT:
                        dve.wait_ge(hi_ready, before(n, SPLIT) + 1)
                        dve.tensor_tensor(split_out(kind)[1][:, m, :], ps[:, JOB_BANK + n % 2, :],
                                          split_out(kind)[0][:, m, :].bitcast(F32), ALU.subtract)\
                           .then_inc(lo_ready, 1)
                    else:
                        i = before(n, ("up",))
                        dve.wait_ge(relu_ready, i + 1)
                        dve.tensor_tensor(relu[:, i % 2, :], relu[:, i % 2, :], relu[:, i % 2, :], ALU.mult)\
                           .then_inc(square_ready, 1)

                def add_side(b):
                    dve.wait_ge(main_done, b + 1)
                    dve.wait_ge(side_ready, b + 1)
                    if b >= 2:
                        dve.wait_ge(x_ready, b - 1)
                    dve.tensor_tensor(both[:, b % 2, :], ps[:, MAIN_BANK + b % 2, :], side, ALU.add)\
                       .then_inc(both_ready, 1)
                    dve.wait_ge(both_ready, b + 1)
                    norm.stats(dve, b, both[:, b % 2, :])
                    dve.wait_ge(norm.rstd_ready, b + 1)
                    dve.tensor_scalar(both[:, b % 2, :], both[:, b % 2, :], norm.mean(b), norm.rstd(b),
                                      ALU.subtract, ALU.mult).then_inc(unit_ready, 1)

                def add_x(b):
                    dve.wait_ge(out_ready, b + 1)
                    dve.tensor_tensor(core.x[:, b, :], both[:, b % 2, :], core.x[:, b, :], ALU.add)\
                       .then_inc(x_ready, 1)

                def routing():
                    dve.wait_ge(logits_turned, 1)
                    for b in range(B):
                        ins = dve.max(top[:, b, :], ps[:, G_BANK, b * F3_E:(b + 1) * F3_E])
                    ins.then_inc(top_ready, 1)
                    dve.wait_ge(top_ready, 1)
                    dve.tensor_tensor(rw[:, :], top[:, :, 0], top[:, :, 1], ALU.add).then_inc(rw_ready, 1)

                turned.dve(dve, range(0, 2))
                weights.first_lo(dve)
                turned.dve(dve, range(2, HB + 1))
                for half in range(HALVES):
                    for n in range(half * PER_HALF, (half + 1) * PER_HALF):
                        evacuate(n)
                        if n == F3_LC - 1:
                            turned.dve(dve, range(HB + 1, B))
                        if n == PER_HALF - 1:
                            routing()
                    for b in range(half * HB, (half + 1) * HB):
                        add_side(b)
                        if b % HB >= 1:
                            add_x(b - 1)
                    add_x((half + 1) * HB - 1)

            @block.tensor
            def _(pe):
                def product(n):
                    half, kind, m = jobs[n]
                    if n >= 2:
                        if jobs[n - 2][1] in SPLIT:
                            pe.wait_ge(lo_ready, before(n - 2, SPLIT) + 1)
                        else:
                            pe.wait_ge(relu_ready, before(n - 2, ("up",)) + 1)
                    rows = slice(half * HT, (half + 1) * HT)
                    w = slice(m * P, (m + 1) * P)
                    if kind == "expert":
                        pe.wait_ge(lo_ready, F3_LC + 2 * F3_LC * half)
                    parts, count = {"fc1": (fc1, NC), "expert": (expert, F3_LC), "up": (up, NC)}[kind]
                    for c in range(count):
                        if kind == "up":
                            stat = [u[:, m * P // UP_N, c * UP_N + m * P % UP_N:][:, 0:P] for u in up]
                        else:
                            stat = [part[:, c, w] for part in parts]
                        mov = ((latent[0][:, c, :], latent[1][:, c, :]) if kind == "expert"
                               else (hi[:, c, rows], lo[:, c, rows]))
                        mm = matmul_split(pe, ps[:, JOB_BANK + n % 2, :], *stat,
                                          *mov, c == 0, c == count - 1)
                    mm.then_inc(job_done, 1)

                def outputs(half):
                    pe.wait_ge(lo_ready, 2 * F3_LC * (half + 1))
                    for i in range(HB):
                        b = half * HB + i
                        rows = slice(i * P, (i + 1) * P)
                        if b >= 1:
                            pe.wait_ge(side_ready, b)
                        for c in range(F3_LC):
                            mm = matmul_split(pe, ps[:, SIDE_BANK, :], routed[0][:, c, rows],
                                              routed[1][:, c, rows], fc2[0][:, c, :], fc2[1][:, c, :],
                                              c == 0, c == F3_LC - 1)
                        mm.then_inc(side_done, 1)
                        if b >= 2:
                            pe.wait_ge(both_ready, b - 1)
                        if i == 0:
                            pe.wait_ge(h_lo_ready, F3_IC * (half + 1))
                        for c in range(F3_IC):
                            mm = matmul_split(pe, ps[:, MAIN_BANK + b % 2, :], h[0][:, c, rows], h[1][:, c, rows],
                                              down[0][:, c, :], down[1][:, c, :], c == 0, c == F3_IC - 1)
                        mm.then_inc(main_done, 1)

                def logits():
                    for half in range(HALVES):
                        rows = slice(half * HT, (half + 1) * HT)
                        for c in range(NC):
                            mm = matmul_split(pe, ps[0:F3_E, G_BANK + half, :], gate[0][:, c, :], gate[1][:, c, :],
                                              hi[:, c, rows], lo[:, c, rows], c == 0, c == NC - 1)
                        mm.then_inc(logits_done, 1)

                def turn_logits():
                    pe.wait_ge(logit_ready, HALVES)
                    for b in range(B):
                        mm = pe.transpose(ps[:, G_BANK, b * F3_E:(b + 1) * F3_E],
                                          logit[:, b * P:(b + 1) * P], core.ident[0:F3_E, 0:F3_E])
                    mm.then_inc(logits_turned, 1)

                turned.pe(pe, range(0, HB))
                weights.wait(pe, FC1)
                pe.wait_ge(turned.lo_ready, HB)
                for n in range(F3_LC):
                    product(n)
                turned.pe(pe, range(HB, B))
                for n in range(F3_LC, PER_HALF):
                    weights.wait(pe, UP + jobs[n][2] * P // UP_N if jobs[n][1] == "up" else EXPERT)
                    product(n)
                    if n == F3_LC:
                        pe.wait_ge(turned.lo_ready, B)
                        logits()
                    if n == PER_HALF - 2:
                        turn_logits()
                weights.wait(pe, LAST)
                outputs(0)
                for n in range(PER_HALF, 2 * PER_HALF):
                    product(n)
                outputs(1)


def more_layouts(a, out, np):
    f32 = np.float32

    def rows(w):
        return w.reshape(-1, P, w.shape[1]).transpose(1, 0, 2).reshape(P, -1)

    wg = np.concatenate([a["L0_ffn_Sg"][None], a["L0_ffn_Wg"]])
    wu = np.concatenate([a["L0_ffn_Su"][None], a["L0_ffn_Wu"]])
    wd = np.concatenate([a["L0_ffn_Sd"][None], a["L0_ffn_Wd"]])
    gu = np.stack([wg, wu], 1).reshape(F0_ALL, 2, F0_I, NC, P)
    out["f0_gu"] = gu.transpose(0, 4, 3, 1, 2).reshape(F0_ALL, P, F0_GU)
    out["f0_dn"] = wd.transpose(0, 2, 1).reshape(F0_ALL, F0_IC, P, D).transpose(0, 2, 1, 3)\
        .reshape(F0_ALL, P, F0_IC * D)
    out["f0_gate"] = a["L0_ffn_gate_w"].T.reshape(NC, P, F0_E).transpose(1, 0, 2)
    out["f0_bias"] = np.broadcast_to(a["L0_ffn_bias"], (P, F0_E))
    out["f0_rank"] = np.broadcast_to(np.arange(F0_E, 0, -1, dtype=f32), (P, F0_E))

    halves = a["ctx_4096"].reshape(HALVES, HB, P, D)
    out["ctx_turned"] = np.stack([rows(h.reshape(HT, D).T) for h in halves])
    out["ctx_rows"] = halves.transpose(0, 2, 1, 3).reshape(HALVES, P, HB * D)
    out["a1_wk"], out["a1_wq"] = rows(a["L1_xattn_Wk"].T), rows(a["L1_xattn_Wq"].T)
    out["a1_bias"] = np.stack([a["L1_xattn_bk"].reshape(NC, P).T, a["L1_xattn_bq"].reshape(NC, P).T], 1)
    out["f1_w"] = a["L1_ffn_W"].reshape(NC, P, D).transpose(1, 0, 2).reshape(P, NC * D)
    out["f1_cols"] = np.broadcast_to(np.concatenate(
        [a[f"L1_ffn_{key}"] for key in ("calib_min", "calib_max", "bias")]), (P, 3 * D))

    sel_k = np.zeros((A2_KV, A2_DH, 2, A2_PAIRS, 2, A2_SLOT), f32)
    sel_q = np.zeros((2, A2_REP, A2_DH, 2, A2_REP, 2, A2_SLOT), f32)
    for d in range(A2_DH):
        for part in range(3):
            for c in range(A2_KV):
                sel_k[c, d, int(part == 1), c // 2, c % 2, part * A2_DH + d] = 1.0
            for r in range(2):
                for m in range(A2_REP):
                    sel_q[r, m, d, int(part == 2), m, r, part * A2_DH + d] = 1.0
    out["a2_sel_k"], out["a2_sel_q"] = sel_k.reshape(P, -1), sel_q.reshape(P, -1)
    ones_row = np.zeros((2, A2_SLOT, 1), f32)
    ones_row[:, A2_MAX_ROW] = 1.0
    out["a2_ones_row"] = ones_row.reshape(P, 1)
    out["a2_wq"], out["a2_wo"] = rows(a["L2_xattn_Wq"]), rows(a["L2_xattn_Wo"])
    out["a2_wkv"] = rows(np.concatenate([a["L2_xattn_Wk"], a["L2_xattn_Wv"]], 1))

    out["f2_a"] = rows(np.concatenate([a["L2_ffn_A"].reshape(F2_HR, D), a["L2_ffn_Wr"]]).T)
    out["f2_b"] = a["L2_ffn_B"].transpose(0, 2, 1).reshape(F2_HR, D)
    out["f2_br"] = a["L2_ffn_br"][:, None]
    for name, key in (("f3_up", "up_w"), ("f3_down", "down_w"), ("f3_fc1", "fc1_w"), ("f3_fc2", "fc2_w"),
                      ("f3_expert", "expert_w"), ("f3_gate", "gate_w")):
        out[name] = rows(a[f"L3_ffn_{key}"])
    up = out["f3_up"].reshape(P, NC, F3_IC // 2, 2 * P)
    out["f3_up"] = up.transpose(0, 2, 1, 3).reshape(P, -1)
    for name in ("gamma", "beta"):
        out[f"f3_{name}"] = np.broadcast_to(a[f"L3_ffn_ln_{name}"], (P, D))


def first_loads(dram):
    ct, rows = dram["ctx_turned"], dram["ctx_rows"]
    mask = dram["mask"][0:HB].rearrange("b s -> (b s)").partition_broadcast(P)
    return {l0_attention: [dram["a0_first"], mask],
            l0_ffn: [dram["f0_gu"][FIRST], dram["f0_dn"][FIRST]],
            l1_attention: [dram["a1_wk"], ct[0]], l1_ffn: [dram["f1_w"], dram["f1_cols"]],
            l2_attention: [dram["a2_wkv"], ct[0][:, 0:A2_RAW]], l2_ffn: [dram["f2_a"], dram["f2_b"]],
            l3_attention: [rows[0], ct[0]], l3_ffn: [dram["f3_fc1"], dram["f3_gate"]]}


LAYERS = [l0_attention, l0_ffn, l1_attention, l1_ffn, l2_attention, l2_ffn,
          l3_attention, l3_ffn]


def build(nc, dram):
    with ExitStack() as ctx:
        core = Core(nc, ctx, dram)
        loads = first_loads(dram)
        core.upcoming = loads[LAYERS[0]]
        load_inputs(core)
        for layer, following in zip(LAYERS, LAYERS[1:] + [None]):
            core.upcoming = loads.get(following, [])
            layer(core)
            core.end_layer()
        store_output(core)


def laid_out(inputs):
    import numpy as np

    a = {k: np.asarray(v) for k, v in inputs.items()}
    f32 = np.float32
    out = {"x": a["x"], "ctx": a["ctx_4096"], "mask": a["mask_Bx1x4096_ff1"].reshape(B, D)}

    wq = np.zeros((P, A0_GROUPS, A0_PER_GROUP, A0_SLOT), f32)
    wk, cols = np.zeros_like(wq), np.zeros((A0_PER_GROUP, A0_SLOT, A0_COLS), f32)
    for h in range(A0_HEADS):
        g, r = divmod(h, A0_PER_GROUP)
        e = slice(h * A0_DH, (h + 1) * A0_DH)
        for part in range(3):
            rows = slice(part * A0_DH, (part + 1) * A0_DH)
            wq[:, g, r, rows] = a["L0_xattn_Wq"].T[:, e]
            wk[:, g, r, rows] = a["L0_xattn_Wk"].T[:, e]
            cols[r, rows, C_BQ + g] = a["L0_xattn_bq"][e]
            cols[r, rows, C_BK + g] = a["L0_xattn_bk"][e]
            if part == 2:
                cols[r, rows, C_SBQ + g] = a["L0_xattn_bq"][e]
    cols[:, 2 * A0_DH:3 * A0_DH, C_SELQ] = 1.0
    cols[:, A0_DH:2 * A0_DH, C_SELK] = 1.0
    cols[:, 0:3 * A0_DH, C_MASKC] = 1.0
    cols[:, A0_MAX_ROW, C_MASKA] = 1.0
    cols[:, A0_MASK_ROW, C_MASKC] = -1.0
    cols[:, A0_MASK_ROW, C_MASKA] = 1.0
    cols[:, A0_MAX_ROW, C_BK:C_BK + A0_GROUPS] = 1.0
    cols[:, A0_MASK_ROW, C_BK:C_BK + A0_GROUPS] = A0_OFF
    cols[:, A0_MASK_ROW, C_BQ:C_BQ + A0_GROUPS] = 1.0
    cols = cols.reshape(P, A0_COLS)
    cols[:, C_BO] = a["L0_xattn_bo"]
    out["a0_wo"] = a["L0_xattn_Wo"].T
    out["a0_first"] = np.concatenate([wq.reshape(P, -1), wk.reshape(P, -1), a["L0_xattn_Wv"].T,
                                      np.broadcast_to(a["L0_xattn_bv"], (P, A0_DK)), cols], 1)
    more_layouts(a, out, np)
    return {k: np.ascontiguousarray(v) for k, v in out.items()}


def kernel(**inputs):
    import concourse.bacc as bacc
    from concourse.bass_utils import run_bass_kernel_spmd

    nc = bacc.Bacc("TRN2", target_bir_lowering=False, num_devices=1)
    arrays = {f"in_{k}": v for k, v in laid_out(inputs).items()}
    dram = {k[3:]: nc.dram_tensor(k, v.shape, mybir.dt.from_np(v.dtype), kind="ExternalInput").ap()
            for k, v in arrays.items()}
    dram["out"] = nc.dram_tensor("out", (B, P, D), F32, kind="ExternalOutput").ap()
    build(nc, dram)
    return run_bass_kernel_spmd(nc, [arrays], core_ids=[0]).results[0]["out"]
```
